# Optimizing a Trainium2 kernel written in Bass

```python
import numpy as np
import jax
import jax.numpy as jnp

def _softmax(x, axis=-1):
    return jax.nn.softmax(x, axis=axis)

def _gelu(x):
    return jax.nn.gelu(x, approximate=True)

def _silu(x):
    return jax.nn.silu(x)

def _sigmoid(x):
    return jax.nn.sigmoid(x)

def _layernorm(x, axis=-1, eps=1e-05):
    m = jnp.mean(x, axis=axis, keepdims=True)
    v = jnp.var(x, axis=axis, keepdims=True)
    return (x - m) / jnp.sqrt(v + eps)

def _scatter_add(tgt, idx, src, axis=0):
    return tgt.at[idx].add(src)

def _segment_sum(src, seg, n):
    return jax.ops.segment_sum(src, seg, n)
kernel_name = 'mk_decoder_preln_d4_seqx_r8_9bbc5f'

def setup_inputs(seed: int=0):
    np.random.seed(seed)
    _w = jnp.asarray

    def _rec_inputs():
        import jax
        import jax.numpy as jnp
        _rk = jax.random.key(seed)
        x = -0.0003929 + 0.9999 * jax.random.normal(jax.random.fold_in(_rk, 1), (8, 128, 128), jnp.float32)
        _lenS = 128 - jax.random.randint(jax.random.fold_in(_rk, 7), (8,), 0, max(1, 128 // 4) + 1, jnp.int32)
        _lenS2 = 120 - jax.random.randint(jax.random.fold_in(_rk, 8), (8,), 0, max(1, 120 // 4) + 1, jnp.int32)
        _ctx_2048P = jax.random.normal(jax.random.fold_in(_rk, 11), (8, 16, 256), jnp.float32)
        _ctx_2048c = jax.random.dirichlet(jax.random.fold_in(_rk, 511), 0.3 * jnp.ones((16,), jnp.float32), (8, 120))
        _ctx_2048t = jnp.einsum('bsk,bkd->bsd', _ctx_2048c, _ctx_2048P)
        _ctx_2048t = _ctx_2048t * jax.lax.rsqrt(jnp.mean(jnp.square(_ctx_2048t)) + 1e-12) * 0.953939
        ctx_2048 = 4.13588e-05 + 0.999923 * (_ctx_2048t + 0.3 * jax.random.normal(jax.random.fold_in(_rk, 611), (8, 120, 256), jnp.float32))
        _validS = jnp.arange(128)[None, :] < _lenS[:, None]
        _validS2 = jnp.arange(120)[None, :] < _lenS2[:, None]
        _causal = jnp.tril(jnp.ones((128, 128), dtype=bool))
        mask_BxS2_if0 = jnp.where(jnp.ones((8, 120), dtype=bool), 4, 0).astype(jnp.int32)
        mask_BxS2_ik0 = jnp.where(jnp.broadcast_to(_validS2[:, :], (8, 120)), 0, 1).astype(jnp.int32)
        return (x, ctx_2048, mask_BxS2_if0, mask_BxS2_ik0)
    x, ctx_2048, mask_BxS2_if0, mask_BxS2_ik0 = _rec_inputs()

    def _L0_attn_setup():
        import jax, jax.numpy as jnp
        import numpy as np
        NUM_HEADS = 16
        D_MODEL = 128
        D_K = D_MODEL // NUM_HEADS
        MAX_SEQ_LEN = 512
        ROPE_BASE = 10000.0
        BATCH = 2
        SEQ_LEN = 256

        def _rope_tables(seq_len, d_k, base=ROPE_BASE):
            theta = 1.0 / base ** (jnp.arange(0, d_k, 2, dtype=jnp.float32) / d_k)
            m = jnp.arange(seq_len, dtype=jnp.float32)
            m_theta = jnp.outer(m, theta)
            ang = jnp.concatenate([m_theta, m_theta], axis=-1)
            return (jnp.cos(ang), jnp.sin(ang))

        def _apply_rope(x, cos, sin):
            d2 = x.shape[-1] // 2
            x1, x2 = (x[..., :d2], x[..., d2:])
            x_flip = jnp.concatenate([-x2, x1], axis=-1)
            return x * cos + x_flip * sin
        key = jax.random.key(seed)
        kx, kq, kk, kv, ko = jax.random.split(key, 5)
        s = 1.0 / np.sqrt(D_MODEL)
        x = jax.random.normal(kx, (BATCH, SEQ_LEN, D_MODEL), dtype=jnp.float32)
        W_Q = jax.random.uniform(kq, (D_MODEL, D_MODEL), jnp.float32, -s, s)
        W_K = jax.random.uniform(kk, (D_MODEL, D_MODEL), jnp.float32, -s, s)
        W_V = jax.random.uniform(kv, (D_MODEL, D_MODEL), jnp.float32, -s, s)
        W_O = jax.random.uniform(ko, (D_MODEL, D_MODEL), jnp.float32, -s, s)
        return {'x': x, 'W_Q': W_Q, 'W_K': W_K, 'W_V': W_V, 'W_O': W_O}
    _L0_attn_all = _L0_attn_setup()
    _L0_attn_in = {k: v for k, v in _L0_attn_all.items() if k in ('W_Q', 'W_K', 'W_V', 'W_O')}
    del _L0_attn_all

    def _L0_xattn_setup():
        import jax, jax.numpy as jnp
        import numpy as np
        B, L, P = (4, 512, 128)
        D_MODEL = 128
        D_GLOBAL = 256
        HEADDIM = 32
        EPSILON = 0.001
        RMS_EPS = 1e-05

        def rmsnorm(x, g, eps=RMS_EPS):
            var = jnp.mean(jnp.square(x), axis=-1, keepdims=True)
            return x * jax.lax.rsqrt(var + eps) * g

        def _hnet_depool(h, h_patch_full, patch_lens):
            h_patch = h_patch_full[..., :D_MODEL]
            bsz, plen = (h_patch.shape[0], h_patch.shape[1])
            seqlen = h.shape[1]
            logp = jnp.full((bsz, plen), -EPSILON, dtype=jnp.float32)
            bidx = jnp.cumsum(patch_lens, axis=1) - 1
            boundary_mask = jnp.zeros((bsz, seqlen), dtype=jnp.int32)
            boundary_mask = boundary_mask.at[jnp.arange(bsz)[:, None], bidx].set(1)
            dt = (-jnp.log(-jnp.expm1(logp))).astype(h_patch.dtype)
            x = h_patch / dt[..., None]
            n_heads = D_MODEL // HEADDIM
            A = -jnp.ones((n_heads,), dtype=jnp.float32)
            bcoef = jnp.exp(logp).astype(h_patch.dtype)
            x4 = x.reshape(bsz, plen, n_heads, HEADDIM)
            a = jnp.exp(dt[:, :, None] * A[None, None, :])
            u = (dt * bcoef)[:, :, None, None] * x4
            a_b = jnp.broadcast_to(a[..., None], u.shape)

            def comb(lft, rgt):
                aL, uL = lft
                aR, uR = rgt
                return (aL * aR, uL * aR + uR)
            _, s = jax.lax.associative_scan(comb, (a_b, u), axis=1)
            depool = s.reshape(bsz, plen, D_MODEL)
            plug = jnp.clip(jnp.cumsum(boundary_mask, axis=1) - 1, 0, plen - 1)
            depool_out = depool[jnp.arange(bsz)[:, None], plug]
            return depool_out + h
        key = jax.random.key(seed)
        k1, k2, k3, k4 = jax.random.split(key, 4)
        embeds = jax.random.normal(k1, (B, L, D_MODEL), dtype=jnp.float32)
        patch_embeds = jax.random.normal(k2, (B, P, D_GLOBAL), dtype=jnp.float32)
        patch_lens = jnp.full((B, P), L // P, dtype=jnp.int64)
        W_in = jax.random.normal(k3, (D_MODEL, D_MODEL), dtype=jnp.float32) * 0.02
        b_in = jnp.zeros((D_MODEL,), dtype=jnp.float32)
        g_res = jnp.ones((D_MODEL,), dtype=jnp.float32)
        g_init = jnp.ones((D_GLOBAL,), dtype=jnp.float32)
        return {'embeds': embeds, 'patch_embeds': patch_embeds, 'patch_lens': patch_lens, 'W_in': W_in, 'b_in': b_in, 'g_res': g_res, 'g_init': g_init}
    _L0_xattn_all = _L0_xattn_setup()
    _L0_xattn_in = {k: v for k, v in _L0_xattn_all.items() if k in ('W_in', 'b_in', 'g_res', 'g_init')}
    del _L0_xattn_all

    def _L0_ffn_setup():
        import jax, jax.numpy as jnp
        import numpy as np
        HIDDEN = 128
        FFN = 4 * HIDDEN
        NUM_EXPERTS = 8
        TOP_K = 2
        B, S = (4, 256)
        key = jax.random.key(seed)
        ks = jax.random.split(key, 7)
        scale = 0.02
        return {'x': jax.random.normal(ks[0], (B, S, HIDDEN), dtype=jnp.float32), 'gate_w': jax.random.normal(ks[1], (HIDDEN, NUM_EXPERTS), dtype=jnp.float32) * scale, 'gate_b': jnp.zeros((NUM_EXPERTS,), dtype=jnp.float32), 'w1': jax.random.normal(ks[2], (NUM_EXPERTS, HIDDEN, FFN), dtype=jnp.float32) * scale, 'b1': jnp.zeros((NUM_EXPERTS, FFN), dtype=jnp.float32), 'w2': jax.random.normal(ks[3], (NUM_EXPERTS, FFN, HIDDEN), dtype=jnp.float32) * scale, 'b2': jnp.zeros((NUM_EXPERTS, HIDDEN), dtype=jnp.float32)}
    _L0_ffn_all = _L0_ffn_setup()
    _L0_ffn_in = {k: v for k, v in _L0_ffn_all.items() if k in ('gate_w', 'gate_b', 'w1', 'b1', 'w2', 'b2')}
    del _L0_ffn_all

    def _L1_attn_setup():
        import jax, jax.numpy as jnp
        import numpy as np
        H = 16
        W = 32
        D_MODEL = 128
        D_FF = 512
        EPS = 1e-05

        def _layernorm(x, g, b):
            mu = jnp.mean(x, axis=-1, keepdims=True)
            var = jnp.mean(jnp.square(x - mu), axis=-1, keepdims=True)
            return (x - mu) * jax.lax.rsqrt(var + EPS) * g + b

        def _sliding_attn(q, k, v, w):
            B, Hh, S, d = q.shape
            nc = S // w
            qc = q.reshape(B, Hh, nc, w, d)
            kp = jnp.pad(k, ((0, 0), (0, 0), (w, w), (0, 0)))
            vp = jnp.pad(v, ((0, 0), (0, 0), (w, w), (0, 0)))
            idx = (jnp.arange(nc) * w)[:, None] + jnp.arange(3 * w)[None, :]
            kc = kp[:, :, idx, :]
            vc = vp[:, :, idx, :]
            scores = jnp.einsum('bhcqd,bhckd->bhcqk', qc, kc)
            q_pos = jnp.arange(nc)[:, None, None] * w + jnp.arange(w)[None, :, None]
            k_pos = jnp.arange(nc)[:, None, None] * w - w + jnp.arange(3 * w)[None, None, :]
            rel = k_pos - q_pos
            valid = (jnp.abs(rel) <= w) & (k_pos >= 0) & (k_pos < S)
            scores = jnp.where(valid[None, None], scores, jnp.float32(-1000000000.0))
            p = jax.nn.softmax(scores, axis=-1)
            out = jnp.einsum('bhcqk,bhckd->bhcqd', p, vc)
            return out.reshape(B, Hh, S, d)
        key = jax.random.key(seed)
        ks = jax.random.split(key, 8)
        B, S = (2, 512)
        src = jax.random.normal(ks[0], (B, S, D_MODEL), dtype=jnp.float32)
        ln1_g = jnp.ones((D_MODEL,), jnp.float32)
        ln1_b = jnp.zeros((D_MODEL,), jnp.float32)
        ln2_g = jnp.ones((D_MODEL,), jnp.float32)
        ln2_b = jnp.zeros((D_MODEL,), jnp.float32)
        W1 = jax.random.normal(ks[1], (D_MODEL, D_FF), jnp.float32) * 0.02
        b1 = jnp.zeros((D_FF,), jnp.float32)
        W2 = jax.random.normal(ks[2], (D_FF, D_MODEL), jnp.float32) * 0.02
        b2 = jnp.zeros((D_MODEL,), jnp.float32)
        return {'src': src, 'ln1_g': ln1_g, 'ln1_b': ln1_b, 'ln2_g': ln2_g, 'ln2_b': ln2_b, 'W1': W1, 'b1': b1, 'W2': W2, 'b2': b2}
    _L1_attn_all = _L1_attn_setup()
    _L1_attn_in = {k: v for k, v in _L1_attn_all.items() if k in ('ln1_g', 'ln1_b', 'ln2_g', 'ln2_b', 'W1', 'b1', 'W2', 'b2')}
    del _L1_attn_all

    def _L1_xattn_setup():
        import jax, jax.numpy as jnp
        import numpy as np
        UNITS = 128
        NUM_HEADS = 8

        def _split_heads(x, n):
            B, S, D = x.shape
            return x.reshape(B, S, n, D // n).transpose(0, 2, 1, 3)
        key = jax.random.key(seed)
        k1, k2, k3 = jax.random.split(key, 3)
        B, S = (8, 128)
        memory = jax.random.normal(k1, (B, S, 2 * UNITS), dtype=jnp.float32)
        query = jax.random.normal(k2, (B, S, UNITS), dtype=jnp.float32)
        seq_mask = jax.random.randint(k3, (B, S), 0, 2, dtype=jnp.int32)
        b = jnp.zeros((1,), dtype=jnp.float32)
        return {'memory': memory, 'query': query, 'seq_mask': seq_mask, 'b': b}
    _L1_xattn_all = _L1_xattn_setup()
    _L1_xattn_in = {k: v for k, v in _L1_xattn_all.items() if k in ('b',)}
    del _L1_xattn_all

    def _L1_ffn_setup():
        import jax, jax.numpy as jnp
        import numpy as np
        NUM_EXPERTS = 8
        NUM_LANGS = 4
        TOP_K = 2
        D_MODEL = 128
        EXPERT_SIZE = 512
        B, S = (2, 256)
        key = jax.random.key(seed)
        ks = jax.random.split(key, 6)

        def xavier(k, shape, fan_in, fan_out):
            a = float(np.sqrt(6.0 / (fan_in + fan_out)))
            return jax.random.uniform(k, shape, jnp.float32, -a, a)
        return {'x': jax.random.normal(ks[0], (B, S, D_MODEL), jnp.float32), 'router_w': xavier(ks[1], (NUM_EXPERTS, D_MODEL), D_MODEL, NUM_EXPERTS), 'router_b': jnp.zeros((NUM_EXPERTS,), jnp.float32), 'lang_w': xavier(ks[2], (NUM_LANGS, D_MODEL), D_MODEL, NUM_LANGS), 'lang_b': jnp.zeros((NUM_LANGS,), jnp.float32), 'w1': xavier(ks[3], (NUM_EXPERTS, D_MODEL, EXPERT_SIZE), D_MODEL, EXPERT_SIZE), 'b1': jnp.zeros((NUM_EXPERTS, EXPERT_SIZE), jnp.float32), 'w2': xavier(ks[4], (NUM_EXPERTS, EXPERT_SIZE, D_MODEL), EXPERT_SIZE, D_MODEL), 'b2': jnp.zeros((NUM_EXPERTS, D_MODEL), jnp.float32)}
    _L1_ffn_all = _L1_ffn_setup()
    _L1_ffn_in = {k: v for k, v in _L1_ffn_all.items() if k in ('router_w', 'router_b', 'lang_w', 'lang_b', 'w1', 'b1', 'w2', 'b2')}
    del _L1_ffn_all

    def _L2_attn_setup():
        import jax, jax.numpy as jnp
        import numpy as np
        D_MODEL = 128
        D_IN = 256
        K = 4
        DT_RANK = 64
        N = 16
        B_SZ = 2
        L = 256

        def _silu(v):
            return v * jax.nn.sigmoid(v)

        def _mamba_forward(x, W_in, conv_w, conv_b, W_x, W_dt, b_dt, A_log, D, W_out):
            B, Lseq, _ = x.shape
            d_in = A_log.shape[0]
            k = conv_w.shape[0]
            x_and_res = x @ W_in
            u, res = jnp.split(x_and_res, [d_in], axis=-1)
            u = jax.lax.conv_general_dilated(u, conv_w, window_strides=(1,), padding=((k - 1, k - 1),), dimension_numbers=('NWC', 'WIO', 'NWC'))[:, :Lseq, :] + conv_b
            u = _silu(u)
            A = -jnp.exp(A_log)
            x_dbl = u @ W_x
            delta, Bm, Cm = jnp.split(x_dbl, [DT_RANK, DT_RANK + N], axis=-1)
            delta = jax.nn.softplus(delta @ W_dt + b_dt)
            deltaA = jnp.exp(jnp.einsum('bld,dn->bldn', delta, A))
            deltaB_u = jnp.einsum('bld,bln,bld->bldn', delta, Bm, u)

            def step(s, inp):
                dA_t, dBu_t, C_t = inp
                s = dA_t * s + dBu_t
                y_t = jnp.einsum('bdn,bn->bd', s, C_t)
                return (s, y_t)
            s0 = jnp.zeros((B, d_in, N), dtype=u.dtype)
            s_final, ys = jax.lax.scan(step, s0, (deltaA.transpose(1, 0, 2, 3), deltaB_u.transpose(1, 0, 2, 3), Cm.transpose(1, 0, 2)))
            y = ys.transpose(1, 0, 2)
            residual = jnp.einsum('bdn,d->bd', s_final, D)
            y = y + residual[:, None, :]
            y = y * _silu(res)
            return y @ W_out
        key = jax.random.key(seed)
        ks = jax.random.split(key, 10)
        x = jax.random.normal(ks[0], (B_SZ, L, D_MODEL), dtype=jnp.float32)
        W_in = jax.random.normal(ks[1], (D_MODEL, 2 * D_IN), dtype=jnp.float32) * 0.02
        conv_w = jax.random.normal(ks[2], (K, D_IN, D_IN), dtype=jnp.float32) * 0.02
        conv_b = jax.random.normal(ks[3], (D_IN,), dtype=jnp.float32) * 0.01
        W_x = jax.random.normal(ks[4], (D_IN, DT_RANK + 2 * N), dtype=jnp.float32) * 0.02
        W_dt = jax.random.normal(ks[5], (DT_RANK, D_IN), dtype=jnp.float32) * 0.02
        b_dt = jax.random.normal(ks[6], (D_IN,), dtype=jnp.float32) * 0.01
        A_log = jnp.log(jnp.broadcast_to(jnp.arange(1, N + 1, dtype=jnp.float32), (D_IN, N)))
        D = jnp.ones((D_IN,), dtype=jnp.float32)
        W_out = jax.random.normal(ks[7], (D_IN, D_MODEL), dtype=jnp.float32) * 0.02
        return {'x': x, 'W_in': W_in, 'conv_w': conv_w, 'conv_b': conv_b, 'W_x': W_x, 'W_dt': W_dt, 'b_dt': b_dt, 'A_log': A_log, 'D': D, 'W_out': W_out}
    _L2_attn_all = _L2_attn_setup()
    _L2_attn_in = {k: v for k, v in _L2_attn_all.items() if k in ('W_in', 'conv_w', 'conv_b', 'W_x', 'W_dt', 'b_dt', 'A_log', 'D', 'W_out')}
    del _L2_attn_all

    def _L2_xattn_setup():
        import jax, jax.numpy as jnp
        import numpy as np
        B, N, DIM = (8, 512, 128)
        M, CTX = (32, 256)
        HEADS, DH = (16, 64)
        INNER = HEADS * DH
        EPS = 1e-06

        def _split_heads(t):
            b, n, _ = t.shape
            return t.reshape(b, n, HEADS, DH).transpose(0, 2, 1, 3)
        key = jax.random.key(seed)
        ks = jax.random.split(key, 6)
        x = jax.random.normal(ks[0], (B, N, DIM), dtype=jnp.float32)
        context = jax.random.normal(ks[1], (B, M, CTX), dtype=jnp.float32)
        Wq = jax.random.normal(ks[2], (DIM, INNER), dtype=jnp.float32) / np.sqrt(DIM)
        Wkv = jax.random.normal(ks[3], (CTX, 2 * INNER), dtype=jnp.float32) / np.sqrt(CTX)
        null_kv = jax.random.normal(ks[4], (2, DH), dtype=jnp.float32) / np.sqrt(2.0)
        Wout = jax.random.normal(ks[5], (INNER, DIM), dtype=jnp.float32) / np.sqrt(INNER)
        ln_scale = jnp.ones((DIM,), dtype=jnp.float32)
        ln_bias = jnp.zeros((DIM,), dtype=jnp.float32)
        return {'x': x, 'context': context, 'Wq': Wq, 'Wkv': Wkv, 'null_kv': null_kv, 'Wout': Wout, 'ln_scale': ln_scale, 'ln_bias': ln_bias}
    _L2_xattn_all = _L2_xattn_setup()
    _L2_xattn_in = {k: v for k, v in _L2_xattn_all.items() if k in ('Wq', 'Wkv', 'null_kv', 'Wout', 'ln_scale', 'ln_bias')}
    del _L2_xattn_all

    def _L2_ffn_setup():
        import jax, jax.numpy as jnp
        import numpy as np
        D_MODEL = 128
        EXPERT_DIM = 256
        N_EXPERTS = 8
        LN_EPS = 1e-05

        def _bit_quant(W):
            scale = jnp.clip(jnp.mean(jnp.abs(W), axis=-1, keepdims=True), 1e-05, None)
            w_q = jnp.clip(jnp.round(W / scale), -1.0, 1.0) * scale
            return W + jax.lax.stop_gradient(w_q - W)
        key = jax.random.key(seed)
        ks = jax.random.split(key, 7)
        x = jax.random.normal(ks[0], (4, 256, D_MODEL), dtype=jnp.float32)
        shared_w1 = jax.random.normal(ks[1], (EXPERT_DIM, D_MODEL), dtype=jnp.float32) / np.sqrt(EXPERT_DIM)
        shared_w2 = jax.random.normal(ks[2], (D_MODEL, EXPERT_DIM), dtype=jnp.float32) / np.sqrt(D_MODEL)
        expert_w1 = jax.random.normal(ks[3], (N_EXPERTS, EXPERT_DIM, D_MODEL), dtype=jnp.float32) / np.sqrt(EXPERT_DIM)
        expert_w2 = jax.random.normal(ks[4], (N_EXPERTS, D_MODEL, EXPERT_DIM), dtype=jnp.float32) / np.sqrt(D_MODEL)
        router_w = 0.02 * jax.random.normal(ks[5], (N_EXPERTS, D_MODEL), dtype=jnp.float32)
        ln_gamma = jnp.ones((D_MODEL,), dtype=jnp.float32)
        ln_beta = jnp.zeros((D_MODEL,), dtype=jnp.float32)
        return {'x': x, 'shared_w1': shared_w1, 'shared_w2': shared_w2, 'expert_w1': expert_w1, 'expert_w2': expert_w2, 'router_w': router_w, 'ln_gamma': ln_gamma, 'ln_beta': ln_beta}
    _L2_ffn_all = _L2_ffn_setup()
    _L2_ffn_in = {k: v for k, v in _L2_ffn_all.items() if k in ('shared_w1', 'shared_w2', 'expert_w1', 'expert_w2', 'router_w', 'ln_gamma', 'ln_beta')}
    del _L2_ffn_all

    def _L3_attn_setup():
        import jax, jax.numpy as jnp
        import numpy as np
        B, S, E, H = (2, 256, 128, 16)
        D = E // H
        key = jax.random.key(seed)
        k1, k2, k3 = jax.random.split(key, 3)
        x = jax.random.normal(k1, (B, S, E), dtype=jnp.float32)
        lim_qkv = np.sqrt(6.0 / (E + 3 * E)).astype(np.float32)
        lim_out = np.sqrt(6.0 / (E + E)).astype(np.float32)
        w_qkv = jax.random.uniform(k2, (E, 3 * E), jnp.float32, -lim_qkv, lim_qkv)
        w_out = jax.random.uniform(k3, (E, E), jnp.float32, -lim_out, lim_out)
        return {'x': x, 'w_qkv': w_qkv, 'w_out': w_out}
    _L3_attn_all = _L3_attn_setup()
    _L3_attn_in = {k: v for k, v in _L3_attn_all.items() if k in ('w_qkv', 'w_out')}
    del _L3_attn_all

    def _L3_xattn_setup():
        import jax, jax.numpy as jnp
        import numpy as np
        B, L, P = (4, 512, 128)
        D_MODEL = 128
        D_GLOBAL = 256
        HEADDIM = 32
        EPSILON = 0.001
        RMS_EPS = 1e-05

        def rmsnorm(x, g, eps=RMS_EPS):
            var = jnp.mean(jnp.square(x), axis=-1, keepdims=True)
            return x * jax.lax.rsqrt(var + eps) * g

        def _hnet_depool(h, h_patch_full, patch_lens):
            h_patch = h_patch_full[..., :D_MODEL]
            bsz, plen = (h_patch.shape[0], h_patch.shape[1])
            seqlen = h.shape[1]
            logp = jnp.full((bsz, plen), -EPSILON, dtype=jnp.float32)
            bidx = jnp.cumsum(patch_lens, axis=1) - 1
            boundary_mask = jnp.zeros((bsz, seqlen), dtype=jnp.int32)
            boundary_mask = boundary_mask.at[jnp.arange(bsz)[:, None], bidx].set(1)
            dt = (-jnp.log(-jnp.expm1(logp))).astype(h_patch.dtype)
            x = h_patch / dt[..., None]
            n_heads = D_MODEL // HEADDIM
            A = -jnp.ones((n_heads,), dtype=jnp.float32)
            bcoef = jnp.exp(logp).astype(h_patch.dtype)
            x4 = x.reshape(bsz, plen, n_heads, HEADDIM)
            a = jnp.exp(dt[:, :, None] * A[None, None, :])
            u = (dt * bcoef)[:, :, None, None] * x4
            a_b = jnp.broadcast_to(a[..., None], u.shape)

            def comb(lft, rgt):
                aL, uL = lft
                aR, uR = rgt
                return (aL * aR, uL * aR + uR)
            _, s = jax.lax.associative_scan(comb, (a_b, u), axis=1)
            depool = s.reshape(bsz, plen, D_MODEL)
            plug = jnp.clip(jnp.cumsum(boundary_mask, axis=1) - 1, 0, plen - 1)
            depool_out = depool[jnp.arange(bsz)[:, None], plug]
            return depool_out + h
        key = jax.random.key(seed)
        k1, k2, k3, k4 = jax.random.split(key, 4)
        embeds = jax.random.normal(k1, (B, L, D_MODEL), dtype=jnp.float32)
        patch_embeds = jax.random.normal(k2, (B, P, D_GLOBAL), dtype=jnp.float32)
        patch_lens = jnp.full((B, P), L // P, dtype=jnp.int64)
        W_in = jax.random.normal(k3, (D_MODEL, D_MODEL), dtype=jnp.float32) * 0.02
        b_in = jnp.zeros((D_MODEL,), dtype=jnp.float32)
        g_res = jnp.ones((D_MODEL,), dtype=jnp.float32)
        g_init = jnp.ones((D_GLOBAL,), dtype=jnp.float32)
        return {'embeds': embeds, 'patch_embeds': patch_embeds, 'patch_lens': patch_lens, 'W_in': W_in, 'b_in': b_in, 'g_res': g_res, 'g_init': g_init}
    _L3_xattn_all = _L3_xattn_setup()
    _L3_xattn_in = {k: v for k, v in _L3_xattn_all.items() if k in ('W_in', 'b_in', 'g_res', 'g_init')}
    del _L3_xattn_all

    def _L3_ffn_setup():
        import jax, jax.numpy as jnp
        import numpy as np
        B, S, D, H, E = (4, 256, 128, 512, 8)
        THRESHOLD = 0.5
        key = jax.random.key(seed)
        ks = jax.random.split(key, 7)
        s_in = 1.0 / np.sqrt(D)
        s_h = 1.0 / np.sqrt(H)
        return {'x': jax.random.normal(ks[0], (B, S, D), dtype=jnp.float32), 'Wg': jax.random.uniform(ks[1], (D, E), jnp.float32, -s_in, s_in), 'bg': jax.random.uniform(ks[2], (E,), jnp.float32, -s_in, s_in), 'W1': jax.random.uniform(ks[3], (E, D, H), jnp.float32, -s_in, s_in), 'b1': jax.random.uniform(ks[4], (E, H), jnp.float32, -s_in, s_in), 'W2': jax.random.uniform(ks[5], (E, H, D), jnp.float32, -s_h, s_h), 'b2': jax.random.uniform(ks[6], (E, D), jnp.float32, -s_h, s_h)}
    _L3_ffn_all = _L3_ffn_setup()
    _L3_ffn_in = {k: v for k, v in _L3_ffn_all.items() if k in ('Wg', 'bg', 'W1', 'b1', 'W2', 'b2')}
    del _L3_ffn_all
    return {'x': x, 'ctx_2048': ctx_2048, 'mask_BxS2_if0': mask_BxS2_if0, 'mask_BxS2_ik0': mask_BxS2_ik0, 'L0_attn_W_Q': _L0_attn_in['W_Q'], 'L0_attn_W_K': _L0_attn_in['W_K'], 'L0_attn_W_V': _L0_attn_in['W_V'], 'L0_attn_W_O': _L0_attn_in['W_O'], 'L0_xattn_W_in': _L0_xattn_in['W_in'], 'L0_xattn_b_in': _L0_xattn_in['b_in'], 'L0_xattn_g_res': _L0_xattn_in['g_res'], 'L0_xattn_g_init': _L0_xattn_in['g_init'], 'L0_ffn_gate_w': _L0_ffn_in['gate_w'], 'L0_ffn_gate_b': _L0_ffn_in['gate_b'], 'L0_ffn_w1': _L0_ffn_in['w1'], 'L0_ffn_b1': _L0_ffn_in['b1'], 'L0_ffn_w2': _L0_ffn_in['w2'], 'L0_ffn_b2': _L0_ffn_in['b2'], 'L1_attn_ln1_g': _L1_attn_in['ln1_g'], 'L1_attn_ln1_b': _L1_attn_in['ln1_b'], 'L1_attn_ln2_g': _L1_attn_in['ln2_g'], 'L1_attn_ln2_b': _L1_attn_in['ln2_b'], 'L1_attn_W1': _L1_attn_in['W1'], 'L1_attn_b1': _L1_attn_in['b1'], 'L1_attn_W2': _L1_attn_in['W2'], 'L1_attn_b2': _L1_attn_in['b2'], 'L1_xattn_b': _L1_xattn_in['b'], 'L1_ffn_router_w': _L1_ffn_in['router_w'], 'L1_ffn_router_b': _L1_ffn_in['router_b'], 'L1_ffn_lang_w': _L1_ffn_in['lang_w'], 'L1_ffn_lang_b': _L1_ffn_in['lang_b'], 'L1_ffn_w1': _L1_ffn_in['w1'], 'L1_ffn_b1': _L1_ffn_in['b1'], 'L1_ffn_w2': _L1_ffn_in['w2'], 'L1_ffn_b2': _L1_ffn_in['b2'], 'L2_attn_W_in': _L2_attn_in['W_in'], 'L2_attn_conv_w': _L2_attn_in['conv_w'], 'L2_attn_conv_b': _L2_attn_in['conv_b'], 'L2_attn_W_x': _L2_attn_in['W_x'], 'L2_attn_W_dt': _L2_attn_in['W_dt'], 'L2_attn_b_dt': _L2_attn_in['b_dt'], 'L2_attn_A_log': _L2_attn_in['A_log'], 'L2_attn_D': _L2_attn_in['D'], 'L2_attn_W_out': _L2_attn_in['W_out'], 'L2_xattn_Wq': _L2_xattn_in['Wq'], 'L2_xattn_Wkv': _L2_xattn_in['Wkv'], 'L2_xattn_null_kv': _L2_xattn_in['null_kv'], 'L2_xattn_Wout': _L2_xattn_in['Wout'], 'L2_xattn_ln_scale': _L2_xattn_in['ln_scale'], 'L2_xattn_ln_bias': _L2_xattn_in['ln_bias'], 'L2_ffn_shared_w1': _L2_ffn_in['shared_w1'], 'L2_ffn_shared_w2': _L2_ffn_in['shared_w2'], 'L2_ffn_expert_w1': _L2_ffn_in['expert_w1'], 'L2_ffn_expert_w2': _L2_ffn_in['expert_w2'], 'L2_ffn_router_w': _L2_ffn_in['router_w'], 'L2_ffn_ln_gamma': _L2_ffn_in['ln_gamma'], 'L2_ffn_ln_beta': _L2_ffn_in['ln_beta'], 'L3_attn_w_qkv': _L3_attn_in['w_qkv'], 'L3_attn_w_out': _L3_attn_in['w_out'], 'L3_xattn_W_in': _L3_xattn_in['W_in'], 'L3_xattn_b_in': _L3_xattn_in['b_in'], 'L3_xattn_g_res': _L3_xattn_in['g_res'], 'L3_xattn_g_init': _L3_xattn_in['g_init'], 'L3_ffn_Wg': _L3_ffn_in['Wg'], 'L3_ffn_bg': _L3_ffn_in['bg'], 'L3_ffn_W1': _L3_ffn_in['W1'], 'L3_ffn_b1': _L3_ffn_in['b1'], 'L3_ffn_W2': _L3_ffn_in['W2'], 'L3_ffn_b2': _L3_ffn_in['b2']}

def reference(x, ctx_2048, mask_BxS2_if0, mask_BxS2_ik0, L0_attn_W_Q, L0_attn_W_K, L0_attn_W_V, L0_attn_W_O, L0_xattn_W_in, L0_xattn_b_in, L0_xattn_g_res, L0_xattn_g_init, L0_ffn_gate_w, L0_ffn_gate_b, L0_ffn_w1, L0_ffn_b1, L0_ffn_w2, L0_ffn_b2, L1_attn_ln1_g, L1_attn_ln1_b, L1_attn_ln2_g, L1_attn_ln2_b, L1_attn_W1, L1_attn_b1, L1_attn_W2, L1_attn_b2, L1_xattn_b, L1_ffn_router_w, L1_ffn_router_b, L1_ffn_lang_w, L1_ffn_lang_b, L1_ffn_w1, L1_ffn_b1, L1_ffn_w2, L1_ffn_b2, L2_attn_W_in, L2_attn_conv_w, L2_attn_conv_b, L2_attn_W_x, L2_attn_W_dt, L2_attn_b_dt, L2_attn_A_log, L2_attn_D, L2_attn_W_out, L2_xattn_Wq, L2_xattn_Wkv, L2_xattn_null_kv, L2_xattn_Wout, L2_xattn_ln_scale, L2_xattn_ln_bias, L2_ffn_shared_w1, L2_ffn_shared_w2, L2_ffn_expert_w1, L2_ffn_expert_w2, L2_ffn_router_w, L2_ffn_ln_gamma, L2_ffn_ln_beta, L3_attn_w_qkv, L3_attn_w_out, L3_xattn_W_in, L3_xattn_b_in, L3_xattn_g_res, L3_xattn_g_init, L3_ffn_Wg, L3_ffn_bg, L3_ffn_W1, L3_ffn_b1, L3_ffn_W2, L3_ffn_b2):
    import jax
    import jax.numpy as jnp

    def _L0_attn_ref(x, W_Q, W_K, W_V, W_O):
        import jax, jax.numpy as jnp
        import numpy as np
        NUM_HEADS = 16
        D_MODEL = 128
        D_K = D_MODEL // NUM_HEADS
        MAX_SEQ_LEN = 512
        ROPE_BASE = 10000.0
        BATCH = 2
        SEQ_LEN = 256

        def _rope_tables(seq_len, d_k, base=ROPE_BASE):
            theta = 1.0 / base ** (jnp.arange(0, d_k, 2, dtype=jnp.float32) / d_k)
            m = jnp.arange(seq_len, dtype=jnp.float32)
            m_theta = jnp.outer(m, theta)
            ang = jnp.concatenate([m_theta, m_theta], axis=-1)
            return (jnp.cos(ang), jnp.sin(ang))

        def _apply_rope(x, cos, sin):
            d2 = x.shape[-1] // 2
            x1, x2 = (x[..., :d2], x[..., d2:])
            x_flip = jnp.concatenate([-x2, x1], axis=-1)
            return x * cos + x_flip * sin
        B, S, _ = x.shape

        def proj(W):
            y = jnp.einsum('bsd,ed->bse', x, W)
            return y.reshape(B, S, NUM_HEADS, D_K).transpose(0, 2, 1, 3)
        Q, K, V = (proj(W_Q), proj(W_K), proj(W_V))
        cos, sin = _rope_tables(S, D_K)
        Q = _apply_rope(Q, cos, sin)
        K = _apply_rope(K, cos, sin)
        scores = jnp.einsum('bhsd,bhtd->bhst', Q, K) / jnp.sqrt(jnp.float32(D_K))
        causal = jnp.tril(jnp.ones((S, S), dtype=bool))
        scores = jnp.where(causal[None, None], scores, -jnp.inf)
        attn = jax.nn.softmax(scores, axis=-1)
        out = jnp.einsum('bhst,bhtd->bhsd', attn, V)
        out = out.transpose(0, 2, 1, 3).reshape(B, S, D_MODEL)
        return jnp.einsum('bsd,ed->bse', out, W_O)

    def _L0_xattn_ref(embeds, patch_embeds, patch_lens, W_in, b_in, g_res, g_init):
        import jax, jax.numpy as jnp
        import numpy as np
        B, L, P = (4, 512, 128)
        D_MODEL = 128
        D_GLOBAL = 256
        HEADDIM = 32
        EPSILON = 0.001
        RMS_EPS = 1e-05

        def rmsnorm(x, g, eps=RMS_EPS):
            var = jnp.mean(jnp.square(x), axis=-1, keepdims=True)
            return x * jax.lax.rsqrt(var + eps) * g

        def _hnet_depool(h, h_patch_full, patch_lens):
            h_patch = h_patch_full[..., :D_MODEL]
            bsz, plen = (h_patch.shape[0], h_patch.shape[1])
            seqlen = h.shape[1]
            logp = jnp.full((bsz, plen), -EPSILON, dtype=jnp.float32)
            bidx = jnp.cumsum(patch_lens, axis=1) - 1
            boundary_mask = jnp.zeros((bsz, seqlen), dtype=jnp.int32)
            boundary_mask = boundary_mask.at[jnp.arange(bsz)[:, None], bidx].set(1)
            dt = (-jnp.log(-jnp.expm1(logp))).astype(h_patch.dtype)
            x = h_patch / dt[..., None]
            n_heads = D_MODEL // HEADDIM
            A = -jnp.ones((n_heads,), dtype=jnp.float32)
            bcoef = jnp.exp(logp).astype(h_patch.dtype)
            x4 = x.reshape(bsz, plen, n_heads, HEADDIM)
            a = jnp.exp(dt[:, :, None] * A[None, None, :])
            u = (dt * bcoef)[:, :, None, None] * x4
            a_b = jnp.broadcast_to(a[..., None], u.shape)

            def comb(lft, rgt):
                aL, uL = lft
                aR, uR = rgt
                return (aL * aR, uL * aR + uR)
            _, s = jax.lax.associative_scan(comb, (a_b, u), axis=1)
            depool = s.reshape(bsz, plen, D_MODEL)
            plug = jnp.clip(jnp.cumsum(boundary_mask, axis=1) - 1, 0, plen - 1)
            depool_out = depool[jnp.arange(bsz)[:, None], plug]
            return depool_out + h
        h = rmsnorm(embeds, g_res)
        h = jnp.einsum('bld,ed->ble', h, W_in) + b_in
        h_patch = rmsnorm(patch_embeds, g_init)
        return _hnet_depool(h, h_patch, patch_lens)

    def _L0_ffn_ref(x, gate_w, gate_b, w1, b1, w2, b2):
        import jax, jax.numpy as jnp
        import numpy as np
        HIDDEN = 128
        FFN = 4 * HIDDEN
        NUM_EXPERTS = 8
        TOP_K = 2
        B, S = (4, 256)
        b, s, h = x.shape
        xt = x.reshape(b * s, h)
        probs = jax.nn.softmax(xt @ gate_w + gate_b, axis=-1)
        _, idx = jax.lax.top_k(probs, TOP_K)
        one_hot = jax.nn.one_hot(idx, NUM_EXPERTS, dtype=xt.dtype)
        mask = (one_hot.sum(axis=1) > 0).astype(xt.dtype)
        h1 = jax.nn.relu(jnp.einsum('th,ehf->etf', xt, w1) + b1[:, None, :])
        out_e = jnp.einsum('etf,efh->eth', h1, w2) + b2[:, None, :]
        out = jnp.einsum('eth,te->th', out_e, mask)
        return out.reshape(b, s, h)

    def _L1_attn_ref(src, ln1_g, ln1_b, ln2_g, ln2_b, W1, b1, W2, b2):
        import jax, jax.numpy as jnp
        import numpy as np
        H = 16
        W = 32
        D_MODEL = 128
        D_FF = 512
        EPS = 1e-05

        def _layernorm(x, g, b):
            mu = jnp.mean(x, axis=-1, keepdims=True)
            var = jnp.mean(jnp.square(x - mu), axis=-1, keepdims=True)
            return (x - mu) * jax.lax.rsqrt(var + EPS) * g + b

        def _sliding_attn(q, k, v, w):
            B, Hh, S, d = q.shape
            nc = S // w
            qc = q.reshape(B, Hh, nc, w, d)
            kp = jnp.pad(k, ((0, 0), (0, 0), (w, w), (0, 0)))
            vp = jnp.pad(v, ((0, 0), (0, 0), (w, w), (0, 0)))
            idx = (jnp.arange(nc) * w)[:, None] + jnp.arange(3 * w)[None, :]
            kc = kp[:, :, idx, :]
            vc = vp[:, :, idx, :]
            scores = jnp.einsum('bhcqd,bhckd->bhcqk', qc, kc)
            q_pos = jnp.arange(nc)[:, None, None] * w + jnp.arange(w)[None, :, None]
            k_pos = jnp.arange(nc)[:, None, None] * w - w + jnp.arange(3 * w)[None, None, :]
            rel = k_pos - q_pos
            valid = (jnp.abs(rel) <= w) & (k_pos >= 0) & (k_pos < S)
            scores = jnp.where(valid[None, None], scores, jnp.float32(-1000000000.0))
            p = jax.nn.softmax(scores, axis=-1)
            out = jnp.einsum('bhcqk,bhckd->bhcqd', p, vc)
            return out.reshape(B, Hh, S, d)
        B, S, _ = src.shape
        d_head = D_MODEL // H
        qkv = src.reshape(B, S, H, d_head).transpose(0, 2, 1, 3)
        attn = _sliding_attn(qkv, qkv, qkv, W)
        attn = attn.transpose(0, 2, 1, 3).reshape(B, S, D_MODEL)
        x = _layernorm(src + attn, ln1_g, ln1_b)
        ff = jnp.maximum(x @ W1 + b1, 0.0) @ W2 + b2
        return _layernorm(x + ff, ln2_g, ln2_b)

    def _L1_xattn_ref(memory, query, seq_mask, b):
        import jax, jax.numpy as jnp
        import numpy as np
        UNITS = 128
        NUM_HEADS = 8

        def _split_heads(x, n):
            B, S, D = x.shape
            return x.reshape(B, S, n, D // n).transpose(0, 2, 1, 3)
        H = NUM_HEADS
        depth = UNITS // H
        Q = _split_heads(query, H) * depth ** (-0.5)
        k_mem, v_mem = jnp.split(memory, 2, axis=2)
        K = _split_heads(k_mem, H)
        V = _split_heads(v_mem, H)
        logits = jnp.einsum('bhqd,bhkd->bhqk', Q, K) + b[0]
        mask = seq_mask.astype(jnp.float32)[:, None, None, :]
        logits = logits + -1e+30 * (1.0 - mask)
        weights = jax.nn.softmax(logits, axis=-1)
        out = jnp.einsum('bhqk,bhkd->bhqd', weights, V)
        B, _, S, _ = out.shape
        return out.transpose(0, 2, 1, 3).reshape(B, S, UNITS)

    def _L1_ffn_ref(x, router_w, router_b, lang_w, lang_b, w1, b1, w2, b2):
        import jax, jax.numpy as jnp
        import numpy as np
        NUM_EXPERTS = 8
        NUM_LANGS = 4
        TOP_K = 2
        D_MODEL = 128
        EXPERT_SIZE = 512
        B, S = (2, 256)
        lang_logits = x @ lang_w.T + lang_b
        lang_probs = jax.nn.softmax(lang_logits, axis=-1)
        lp_pad = jnp.pad(lang_probs, ((0, 0), (0, 0), (0, 1)))
        idx = jnp.arange(NUM_EXPERTS) % NUM_LANGS
        expert_weights = lp_pad[..., idx] + lp_pad[..., idx + 1]
        router_logits = x @ router_w.T + router_b + 0.1 * expert_weights
        router_probs = jax.nn.softmax(router_logits, axis=-1)
        top_p, top_i = jax.lax.top_k(router_probs, TOP_K)
        top_p = top_p / top_p.sum(axis=-1, keepdims=True)
        h = jax.nn.gelu(jnp.einsum('bsd,edh->bseh', x, w1) + b1, approximate=False)
        expert_out = jnp.einsum('bseh,ehd->bsed', h, w2) + b2
        sel = jnp.take_along_axis(expert_out, top_i[..., None], axis=2)
        return (top_p[..., None] * sel).sum(axis=2)

    def _L2_attn_ref(x, W_in, conv_w, conv_b, W_x, W_dt, b_dt, A_log, D, W_out):
        import jax, jax.numpy as jnp
        import numpy as np
        D_MODEL = 128
        D_IN = 256
        K = 4
        DT_RANK = 64
        N = 16
        B_SZ = 2
        L = 256

        def _silu(v):
            return v * jax.nn.sigmoid(v)

        def _mamba_forward(x, W_in, conv_w, conv_b, W_x, W_dt, b_dt, A_log, D, W_out):
            B, Lseq, _ = x.shape
            d_in = A_log.shape[0]
            k = conv_w.shape[0]
            x_and_res = x @ W_in
            u, res = jnp.split(x_and_res, [d_in], axis=-1)
            u = jax.lax.conv_general_dilated(u, conv_w, window_strides=(1,), padding=((k - 1, k - 1),), dimension_numbers=('NWC', 'WIO', 'NWC'))[:, :Lseq, :] + conv_b
            u = _silu(u)
            A = -jnp.exp(A_log)
            x_dbl = u @ W_x
            delta, Bm, Cm = jnp.split(x_dbl, [DT_RANK, DT_RANK + N], axis=-1)
            delta = jax.nn.softplus(delta @ W_dt + b_dt)
            deltaA = jnp.exp(jnp.einsum('bld,dn->bldn', delta, A))
            deltaB_u = jnp.einsum('bld,bln,bld->bldn', delta, Bm, u)

            def step(s, inp):
                dA_t, dBu_t, C_t = inp
                s = dA_t * s + dBu_t
                y_t = jnp.einsum('bdn,bn->bd', s, C_t)
                return (s, y_t)
            s0 = jnp.zeros((B, d_in, N), dtype=u.dtype)
            s_final, ys = jax.lax.scan(step, s0, (deltaA.transpose(1, 0, 2, 3), deltaB_u.transpose(1, 0, 2, 3), Cm.transpose(1, 0, 2)))
            y = ys.transpose(1, 0, 2)
            residual = jnp.einsum('bdn,d->bd', s_final, D)
            y = y + residual[:, None, :]
            y = y * _silu(res)
            return y @ W_out
        return _mamba_forward(x, W_in, conv_w, conv_b, W_x, W_dt, b_dt, A_log, D, W_out)

    def _L2_xattn_ref(x, context, Wq, Wkv, null_kv, Wout, ln_scale, ln_bias):
        import jax, jax.numpy as jnp
        import numpy as np
        B, N, DIM = (8, 512, 128)
        M, CTX = (32, 256)
        HEADS, DH = (16, 64)
        INNER = HEADS * DH
        EPS = 1e-06

        def _split_heads(t):
            b, n, _ = t.shape
            return t.reshape(b, n, HEADS, DH).transpose(0, 2, 1, 3)
        scale = DH ** (-0.5)
        b = x.shape[0]
        q = _split_heads(jnp.einsum('bnd,df->bnf', x, Wq))
        kv = jnp.einsum('bmc,cf->bmf', context, Wkv)
        k, v = jnp.split(kv, 2, axis=-1)
        k, v = (_split_heads(k), _split_heads(v))
        nk = jnp.broadcast_to(null_kv[0], (b, HEADS, 1, DH))
        nv = jnp.broadcast_to(null_kv[1], (b, HEADS, 1, DH))
        k = jnp.concatenate((nk, k), axis=-2)
        v = jnp.concatenate((nv, v), axis=-2)
        q = q * scale
        sim = jnp.einsum('bhid,bhjd->bhij', q, k)
        attn = jax.nn.softmax(sim, axis=-1)
        out = jnp.einsum('bhij,bhjd->bhid', attn, v)
        out = out.transpose(0, 2, 1, 3).reshape(b, -1, INNER)
        out = jnp.einsum('bnf,fd->bnd', out, Wout)
        mu = jnp.mean(out, axis=-1, keepdims=True)
        var = jnp.var(out, axis=-1, keepdims=True)
        out = (out - mu) * jax.lax.rsqrt(var + EPS) * ln_scale + ln_bias
        return out

    def _L2_ffn_ref(x, shared_w1, shared_w2, expert_w1, expert_w2, router_w, ln_gamma, ln_beta):
        import jax, jax.numpy as jnp
        import numpy as np
        D_MODEL = 128
        EXPERT_DIM = 256
        N_EXPERTS = 8
        LN_EPS = 1e-05

        def _bit_quant(W):
            scale = jnp.clip(jnp.mean(jnp.abs(W), axis=-1, keepdims=True), 1e-05, None)
            w_q = jnp.clip(jnp.round(W / scale), -1.0, 1.0) * scale
            return W + jax.lax.stop_gradient(w_q - W)
        mu = jnp.mean(x, axis=-1, keepdims=True)
        var = jnp.mean(jnp.square(x - mu), axis=-1, keepdims=True)
        h = (x - mu) / jnp.sqrt(var + LN_EPS) * ln_gamma + ln_beta
        sw1, sw2 = (_bit_quant(shared_w1), _bit_quant(shared_w2))
        shared_out = jax.nn.silu(jnp.einsum('btd,fd->btf', h, sw1)) @ sw2.T
        probs = jax.nn.softmax(h @ router_w.T, axis=-1)
        top_prob = jnp.max(probs, axis=-1)
        top_idx = jnp.argmax(probs, axis=-1)
        ew1, ew2 = (_bit_quant(expert_w1), _bit_quant(expert_w2))
        h1 = jax.nn.silu(jnp.einsum('btd,efd->ebtf', h, ew1))
        eo = jnp.einsum('ebtf,edf->ebtd', h1, ew2)
        gate = jax.nn.one_hot(top_idx, N_EXPERTS, dtype=h.dtype) * top_prob[..., None]
        routed_out = jnp.einsum('ebtd,bte->btd', eo, gate)
        return shared_out + routed_out

    def _L3_attn_ref(x, w_qkv, w_out):
        import jax, jax.numpy as jnp
        import numpy as np
        B, S, E, H = (2, 256, 128, 16)
        D = E // H
        b, s, e = x.shape
        qkv = jnp.einsum('bse,ef->bsf', x, w_qkv)
        qkv = qkv.reshape(b, s, 3, H, D).transpose(2, 0, 3, 1, 4)
        q, k, v = (qkv[0], qkv[1], qkv[2])
        scale = 1.0 / np.sqrt(D).astype(np.float32)
        scores = jnp.einsum('bhsd,bhtd->bhst', q, k) * scale
        attn = jax.nn.softmax(scores, axis=-1)
        out = jnp.einsum('bhst,bhtd->bhsd', attn, v)
        out = out.transpose(0, 2, 1, 3).reshape(b, s, e)
        return jnp.einsum('bse,ef->bsf', out, w_out)

    def _L3_xattn_ref(embeds, patch_embeds, patch_lens, W_in, b_in, g_res, g_init):
        import jax, jax.numpy as jnp
        import numpy as np
        B, L, P = (4, 512, 128)
        D_MODEL = 128
        D_GLOBAL = 256
        HEADDIM = 32
        EPSILON = 0.001
        RMS_EPS = 1e-05

        def rmsnorm(x, g, eps=RMS_EPS):
            var = jnp.mean(jnp.square(x), axis=-1, keepdims=True)
            return x * jax.lax.rsqrt(var + eps) * g

        def _hnet_depool(h, h_patch_full, patch_lens):
            h_patch = h_patch_full[..., :D_MODEL]
            bsz, plen = (h_patch.shape[0], h_patch.shape[1])
            seqlen = h.shape[1]
            logp = jnp.full((bsz, plen), -EPSILON, dtype=jnp.float32)
            bidx = jnp.cumsum(patch_lens, axis=1) - 1
            boundary_mask = jnp.zeros((bsz, seqlen), dtype=jnp.int32)
            boundary_mask = boundary_mask.at[jnp.arange(bsz)[:, None], bidx].set(1)
            dt = (-jnp.log(-jnp.expm1(logp))).astype(h_patch.dtype)
            x = h_patch / dt[..., None]
            n_heads = D_MODEL // HEADDIM
            A = -jnp.ones((n_heads,), dtype=jnp.float32)
            bcoef = jnp.exp(logp).astype(h_patch.dtype)
            x4 = x.reshape(bsz, plen, n_heads, HEADDIM)
            a = jnp.exp(dt[:, :, None] * A[None, None, :])
            u = (dt * bcoef)[:, :, None, None] * x4
            a_b = jnp.broadcast_to(a[..., None], u.shape)

            def comb(lft, rgt):
                aL, uL = lft
                aR, uR = rgt
                return (aL * aR, uL * aR + uR)
            _, s = jax.lax.associative_scan(comb, (a_b, u), axis=1)
            depool = s.reshape(bsz, plen, D_MODEL)
            plug = jnp.clip(jnp.cumsum(boundary_mask, axis=1) - 1, 0, plen - 1)
            depool_out = depool[jnp.arange(bsz)[:, None], plug]
            return depool_out + h
        h = rmsnorm(embeds, g_res)
        h = jnp.einsum('bld,ed->ble', h, W_in) + b_in
        h_patch = rmsnorm(patch_embeds, g_init)
        return _hnet_depool(h, h_patch, patch_lens)

    def _L3_ffn_ref(x, Wg, bg, W1, b1, W2, b2):
        import jax, jax.numpy as jnp
        import numpy as np
        B, S, D, H, E = (4, 256, 128, 512, 8)
        THRESHOLD = 0.5
        b, s, d = x.shape
        x_flat = x.reshape(-1, d)
        probs = jax.nn.sigmoid(x_flat @ Wg + bg)
        mask = (probs > THRESHOLD).astype(x_flat.dtype)
        weights = probs * mask
        h = jax.nn.relu(jnp.einsum('td,edh->eth', x_flat, W1) + b1[:, None, :])
        expert_out = jnp.einsum('eth,ehd->etd', h, W2) + b2[:, None, :]
        combined = jnp.einsum('te,etd->td', weights, expert_out)
        return combined.reshape(b, s, d)
    x = x + _L0_attn_ref(_layernorm(x, axis=-1), L0_attn_W_Q, L0_attn_W_K, L0_attn_W_V, L0_attn_W_O)
    x = x + _L0_xattn_ref(_layernorm(x, axis=-1), ctx_2048, mask_BxS2_if0, L0_xattn_W_in, L0_xattn_b_in, L0_xattn_g_res, L0_xattn_g_init)
    x = x + _L0_ffn_ref(_layernorm(x, axis=-1), L0_ffn_gate_w, L0_ffn_gate_b, L0_ffn_w1, L0_ffn_b1, L0_ffn_w2, L0_ffn_b2)
    x = x + _L1_attn_ref(_layernorm(x, axis=-1), L1_attn_ln1_g, L1_attn_ln1_b, L1_attn_ln2_g, L1_attn_ln2_b, L1_attn_W1, L1_attn_b1, L1_attn_W2, L1_attn_b2)
    x = x + _L1_xattn_ref(ctx_2048, _layernorm(x, axis=-1), mask_BxS2_ik0, L1_xattn_b)
    x = x + _L1_ffn_ref(_layernorm(x, axis=-1), L1_ffn_router_w, L1_ffn_router_b, L1_ffn_lang_w, L1_ffn_lang_b, L1_ffn_w1, L1_ffn_b1, L1_ffn_w2, L1_ffn_b2)
    x = x + _L2_attn_ref(_layernorm(x, axis=-1), L2_attn_W_in, L2_attn_conv_w, L2_attn_conv_b, L2_attn_W_x, L2_attn_W_dt, L2_attn_b_dt, L2_attn_A_log, L2_attn_D, L2_attn_W_out)
    x = x + _L2_xattn_ref(_layernorm(x, axis=-1), ctx_2048, L2_xattn_Wq, L2_xattn_Wkv, L2_xattn_null_kv, L2_xattn_Wout, L2_xattn_ln_scale, L2_xattn_ln_bias)
    x = x + _L2_ffn_ref(_layernorm(x, axis=-1), L2_ffn_shared_w1, L2_ffn_shared_w2, L2_ffn_expert_w1, L2_ffn_expert_w2, L2_ffn_router_w, L2_ffn_ln_gamma, L2_ffn_ln_beta)
    x = x + _L3_attn_ref(_layernorm(x, axis=-1), L3_attn_w_qkv, L3_attn_w_out)
    x = x + _L3_xattn_ref(_layernorm(x, axis=-1), ctx_2048, mask_BxS2_if0, L3_xattn_W_in, L3_xattn_b_in, L3_xattn_g_res, L3_xattn_g_init)
    x = x + _L3_ffn_ref(_layernorm(x, axis=-1), L3_ffn_Wg, L3_ffn_bg, L3_ffn_W1, L3_ffn_b1, L3_ffn_W2, L3_ffn_b2)
    return x

_drawn_inputs = setup_inputs


def setup_inputs(seed=0):
    import zlib

    import numpy as np

    out = dict(_drawn_inputs(seed))
    spreads = {'L0_xattn_b_in': (0.0, 0.1),
     'L0_xattn_g_res': (1.0, 0.2),
     'L0_xattn_g_init': (1.0, 0.2),
     'L0_ffn_gate_b': (0.0, 0.1),
     'L0_ffn_b1': (0.0, 0.1),
     'L0_ffn_b2': (0.0, 0.1),
     'L1_attn_ln1_g': (1.0, 0.2),
     'L1_attn_ln1_b': (0.0, 0.1),
     'L1_attn_ln2_g': (1.0, 0.2),
     'L1_attn_ln2_b': (0.0, 0.1),
     'L1_attn_b1': (0.0, 0.1),
     'L1_attn_b2': (0.0, 0.1),
     'L1_ffn_router_b': (0.0, 0.1),
     'L1_ffn_lang_b': (0.0, 0.1),
     'L1_ffn_b1': (0.0, 0.1),
     'L1_ffn_b2': (0.0, 0.1),
     'L2_attn_D': (1.0, 0.2),
     'L2_xattn_ln_scale': (1.0, 0.2),
     'L2_xattn_ln_bias': (0.0, 0.1),
     'L2_ffn_ln_gamma': (1.0, 0.2),
     'L2_ffn_ln_beta': (0.0, 0.1),
     'L3_xattn_b_in': (0.0, 0.1),
     'L3_xattn_g_res': (1.0, 0.2),
     'L3_xattn_g_init': (1.0, 0.2)}
    factors = {}
    for name, (base, spread) in spreads.items():
        noise = np.random.default_rng([zlib.crc32(name.encode()), seed]).standard_normal(out[name].shape)
        drawn = base * np.exp(spread * noise) if base else spread * noise
        out[name] = jnp.asarray(drawn.astype(out[name].dtype))
    for name, factor in factors.items():
        out[name] = (out[name] * factor).astype(out[name].dtype)
    return out
```

```python
from contextlib import ExitStack

import numpy as np

import concourse.bass as bass
from concourse import mybir

F32 = mybir.dt.float32
BF16 = mybir.dt.bfloat16
I32 = mybir.dt.int32
U16 = mybir.dt.uint16
ACT = mybir.ActivationFunctionType
ALU = mybir.AluOpType
AX = mybir.AxisListType

P = 128
B, S, D = 8, 128, 128
TOK = B * S
M, CTX = 120, 256
LN_EPS = 1e-5
HALF = 512
DEPOOL_EPS = 0.001
NEG = -1e30

PT0, OB, MB = 4, 6, 7


class Signal:

    def __init__(self, sem):
        self.sem, self.total = sem, 0

    def take(self, count):
        base = self.total
        self.total += count
        return Share(self.sem, base)


class Share:
    def __init__(self, sem, base):
        self.sem, self.base = sem, base

    def upto(self, n):
        return self.sem, n + self.base


class Chain:

    def __init__(self, eng, sem):
        self.eng, self.sem, self.base, self.n = eng, sem, 0, 0
        self.i, self.per = None, 0

    def step(self, ins):
        ins.then_inc(self.sem, 1)
        self.n += 1

    def settle(self):
        if self.i is None:
            if self.base + self.n:
                self.eng.wait_ge(self.sem, self.base + self.n)
        else:
            self.eng.wait_ge(self.sem, self.i * self.per + (self.base + self.n))

    def link(self, ins):
        self.step(ins)
        self.settle()

    def enter(self, i, per):
        self.base, self.n, self.i, self.per = self.base + self.n, 0, i, per

    def leave(self, trips):
        assert self.n == self.per, (self.n, self.per)
        self.base, self.n, self.i = self.base + trips * self.per, 0, None


def bcast(ap, axis, n):
    new = ap.unsqueeze(axis)
    shape = list(new.shape)
    shape[axis] = n
    return new.to_broadcast(shape)


class Norm:

    def __init__(self, k, src=None, again=False, eps=LN_EPS):
        self.k, self.src, self.again, self.eps = k, k.x if src is None else src, again, eps
        self.var_ready = k.sig["var_ready"].take(1)
        self.rstd_ready = k.sig["rstd_ready"].take(1)
        self.xn_ready = k.sig["xn_ready"].take(B)

    def vector(self, dve):
        k = self.k
        k.dchain.settle()
        dve.tensor_scalar(k.var_eps[:, :], k.mv[:, :, 1], self.eps, None, ALU.add).then_inc(self.var_ready.sem, 1)
        dve.wait_ge(*self.rstd_ready.upto(1))
        for b in range(B):
            dve.tensor_scalar(k.xn[:, b, :], self.src[:, b, :], k.mv[:, b, 0:1], k.rstd[:, b:b + 1],
                              ALU.subtract, ALU.mult).then_inc(self.xn_ready.sem, 1)

    def pool(self, pool):
        k = self.k
        pool.wait_ge(*self.var_ready.upto(1))
        root = lambda out, v: pool.tensor_tensor(out, v, bcast(k.minus_half[:, 0], 1, B), ALU.pow)
        if not self.again:
            root(k.rstd[:, :], k.var_eps[:, :]).then_inc(self.rstd_ready.sem, 1)
            return
        k.pchain.link(root(k.root1[:, :], k.var_eps[:, :]))
        k.pchain.link(pool.tensor_tensor(k.ms[:, :], k.root1[:, :], k.root1[:, :], ALU.mult))
        k.pchain.link(pool.tensor_tensor(k.ms[:, :], k.ms[:, :], k.mv[:, :, 1], ALU.mult))
        k.pchain.link(pool.tensor_scalar(k.ms[:, :], k.ms[:, :], LN_EPS, None, ALU.add))
        k.pchain.link(root(k.root2[:, :], k.ms[:, :]))
        pool.tensor_tensor(k.rstd[:, :], k.root1[:, :], k.root2[:, :], ALU.mult).then_inc(self.rstd_ready.sem, 1)


def token_stats(k, dve, src, bs):
    for b in bs:
        k.dchain.step(dve.bn_stats(k.bn[:, b, :], src[:, b, :]))
    k.dchain.settle()
    for b in bs:
        k.dchain.step(dve.bn_aggr(k.mv[:, b, :], k.bn[:, b, :]))


class Turn:

    def __init__(self, k, norm):
        self.k, self.norm = k, norm
        self.turned = k.sig["x_turned"].take(2)
        self.xT_ready = k.sig["xnT_ready"].take(2)

    def tensor(self, pe):
        k = self.k
        for b in range(B):
            pe.wait_ge(*self.norm.xn_ready.upto(b + 1))
            t = pe.transpose(k.ps[:, PT0 + b // 4, b % 4 * P:(b % 4 + 1) * P], k.xn[:, b, :], k.ident)
            if b % 4 == 3:
                t.then_inc(self.turned.sem, 1)

    def scalar(self, act, scale=1.0, bias=0.0):
        k = self.k
        for h in range(2):
            act.wait_ge(*self.turned.upto(h + 1))
            act.activation(k.xnT[:, h * HALF:(h + 1) * HALF], k.ps[:, PT0 + h, :], ACT.Identity,
                           scale=scale, bias=bias).then_inc(self.xT_ready.sem, 1)


class Attention:

    UNITS = 4

    def __init__(self, k, norm, turn, kind):
        self.k, self.norm, self.turn, self.kind = k, norm, turn, kind
        self.H = 8 if kind == "context" else 16
        self.dh = D // self.H
        self.per = self.H // self.UNITS
        self.T = M if kind == "context" else S
        self.scale = 1.0 / np.sqrt(8.0) if kind in ("rope", "packed") else 1.0
        self.proj = kind in ("rope", "packed")
        self.v = k.v8 if kind == "context" else k.v16
        sig = k.sig
        self.v_clear = sig["at_v_clear"].take(1)
        self.xT_ready = sig["at_xT_ready"].take(B)
        self.kv_ready = sig["at_kv_ready"].take(B)
        self.v_ready = sig["at_v_ready"].take(B)
        self.s_done = sig["at_s_done"].take(4 * B)
        self.max_ready = sig["at_max_ready"].take(4 * B)
        self.p_ready = sig["at_p_ready"].take(4 * B)
        self.pt_done = sig["at_pt_done"].take(4 * B)
        self.ptv_ready = sig["at_ptv_ready"].take(2 * B)
        self.pta_ready = sig["at_pta_ready"].take(2 * B)
        self.av_even = sig["at_av_even"].take(2 * B)
        self.av_odd = sig["at_av_odd"].take(2 * B)
        self.o_ready = sig["at_o_ready"].take(B)
        if self.proj:
            self.qkv_done = sig["at_qkv_done"].take(B)
            self.oT_done = sig["at_oT_done"].take(B)
            self.oT_ready = sig["at_oT_ready"].take(B)
            self.y_done = sig["at_y_done"].take(B)
            self.res_done = sig["at_res_done"].take(B)

    def tensor(self, pe):
        k = self.k
        with pe.Fori(0, B // 2) as i:
            if self.proj:
                for p in range(2):
                    self.project(pe, i, p)
            self.scores(pe, i, 0, range(4))
            self.values(pe, i, 0)
            self.scores(pe, i, 1, range(2))
            if self.proj:
                self.turn_out(pe, i, 0)
            self.scores(pe, i, 1, range(2, 4))
            self.values(pe, i, 1)
            if self.proj:
                self.turn_out(pe, i, 1)
                self.out(pe, i, 1)

    def project(self, pe, i, p):
        k = self.k
        b = 2 * i + p
        pe.wait_ge(*self.xT_ready.upto(b + 1))
        pe.wait_ge(*self.p_ready.upto(8 * i))
        for j, w in enumerate(k.l0_qk if self.kind == "rope" else k.l3_qk):
            pe.matmul(k.ps[:, 2 * p, j * P:(j + 1) * P], w, k.xT[p][:, :], start=True, stop=True)
        wv = k.l0_wvT if self.kind == "rope" else k.l3_wv
        pe.matmul(k.ps[:, 2 * p + 1, 0:P], k.xT[p][:, :], wv, start=True, stop=True).then_inc(self.qkv_done.sem, 1)

    def scores(self, pe, i, p, units):
        k = self.k
        b = 2 * i + p
        q = k.q[p] if self.proj else k.xT[p]
        for u in units:
            need = b + 1 if p or u < 2 or not self.proj else 2 * i + 2
            pe.wait_ge(*self.kv_ready.upto(need))
            if self.proj:
                pe.wait_ge(*self.v_ready.upto(need))
            if p:
                pe.wait_ge(*self.p_ready.upto(8 * i + u + 1))
            else:
                pe.wait_ge(*self.p_ready.upto(8 * i))
            out = k.ps[:, u, :].rearrange("q (h t) -> q h t", t=P)[:, 0:self.per, 0:self.T]
            g = slice(32 * u, 32 * u + 32)
            mask = self.kind != "packed"
            if self.kind == "context":
                pe.matmul(out, k.ones, bcast(k.key_row[:, bass.ts(b, M)], 1, self.per), start=True, stop=False)
            elif mask:
                pe.matmul(out, k.ident16, bcast(k.causal if self.kind == "rope" else k.band, 1, self.per),
                          start=True, stop=False)
            pe.matmul(out, q[g, :], k.kb[p][g, 0:self.per, 0:self.T], start=not mask, stop=True)\
                .then_inc(self.s_done.sem, 1)

    def values(self, pe, i, p):
        k = self.k
        b = 2 * i + p

        def turn(u):
            pe.wait_ge(*self.p_ready.upto(4 * b + u + 1))
            ready = self.pta_ready if u % 2 else self.ptv_ready
            pe.wait_ge(*ready.upto(2 * b + u // 2))
            for j in range(self.per):
                t = pe.transpose(k.ps[0:self.T, PT0 + u % 2, j * P:(j + 1) * P],
                                 k.p[p][:, u * self.per + j, 0:self.T], k.ident)
            t.then_inc(self.pt_done.sem, 1)

        def times_v(u):
            if u == 0:
                pe.wait_ge(*self.o_ready.upto(b))
                pe.wait_ge(*self.v_ready.upto(b + 1))
            ready = self.pta_ready if u % 2 else self.ptv_ready
            pe.wait_ge(*ready.upto(2 * b + u // 2 + 1))
            w = self.dh + 1
            for j in range(self.per):
                h = u * self.per + j
                m = pe.matmul(k.ps[:, OB, h * w:(h + 1) * w], k.pT[u % 2][0:self.T, j, :],
                              self.v[p][0:self.T, h * w:(h + 1) * w], start=True, stop=True)
            m.then_inc((self.av_odd if u % 2 else self.av_even).sem, 1)

        turn(0)
        turn(1)
        if p and self.proj:
            self.out(pe, i, 0)
        times_v(0)
        turn(2)
        times_v(1)
        turn(3)
        times_v(2)
        times_v(3)

    def turn_out(self, pe, i, p):
        k = self.k
        b = 2 * i + p
        pe.wait_ge(*self.o_ready.upto(b + 1))
        pe.wait_ge(*self.oT_ready.upto(b))
        pe.transpose(k.ps[:, MB, 2 * P:3 * P], k.o[:, :], k.ident).then_inc(self.oT_done.sem, 1)

    def out(self, pe, i, p):
        k = self.k
        b = 2 * i + p
        pe.wait_ge(*self.oT_ready.upto(b + 1))
        pe.wait_ge(*self.res_done.upto(b))
        pe.matmul(k.ps[:, MB, 3 * P:4 * P], k.oT[:, :], k.l0_woT if self.kind == "rope" else k.l3_wo,
                  start=True, stop=True).then_inc(self.y_done.sem, 1)

    def vector(self, dve):
        k = self.k
        c = k.dchain
        per = 2 * ({"rope": 6, "packed": 1}.get(self.kind, 0) + 4 + (1 if self.proj else 2))
        with dve.Fori(0, B // 2) as i:
            c.enter(i, per)
            for p in range(2):
                self.keys(dve, i, p)
            for p in range(2):
                b = 2 * i + p
                for u in range(4):
                    self.maxima(dve, b, p, u)
                if p and self.proj:
                    self.residual(dve, 2 * i)
                for u in (0, 2):
                    dve.wait_ge(*self.pt_done.upto(4 * b + u + 1))
                    dve.wait_ge(*self.av_even.upto(2 * b + u // 2))
                    n = self.per * P
                    dve.tensor_copy(k.pT[0][0:self.T, :, :].rearrange("t h q -> t (h q)")[:, 0:n],
                                    k.ps[0:self.T, PT0, 0:n]).then_inc(self.ptv_ready.sem, 1)
                self.outputs(dve, b)
                if p and self.proj:
                    self.residual(dve, b)
        c.leave(B // 2)
        if self.proj:
            dve.wait_ge(*self.res_done.upto(B))
        else:
            c.settle()
        token_stats(k, dve, k.r if self.kind == "self" else k.x, range(B))

    def keys(self, dve, i, p):
        k, c = self.k, self.k.dchain
        b = 2 * i + p
        if self.proj:
            dve.wait_ge(*self.qkv_done.upto(b + 1))
            dve.wait_ge(*self.s_done.upto(8 * i))
            slot = lambda j: k.ps[:, 2 * p, j * P:(j + 1) * P]
        if self.kind == "rope":
            c.step(dve.tensor_tensor(k.t1[p][:, :], slot(0), k.cosT, ALU.mult))
            c.step(dve.tensor_tensor(k.t2[p][:, :], slot(1), k.sinT, ALU.mult))
            c.step(dve.tensor_tensor(k.t3[p][:, :], slot(2), k.cosT, ALU.mult))
            c.link(dve.tensor_tensor(k.t4[p][:, :], slot(3), k.sinT, ALU.mult))
            c.step(dve.tensor_tensor(k.q[p][:, :], k.t1[p][:, :], k.t2[p][:, :], ALU.add))
            c.link(dve.tensor_tensor(k.t3[p][:, :], k.t3[p][:, :], k.t4[p][:, :], ALU.add))
            keys = k.t3[p][:, :]
        elif self.kind == "packed":
            c.step(dve.tensor_copy(k.q[p][:, :], slot(0)))
            keys = slot(1)
        else:
            dve.wait_ge(*self.xT_ready.upto(b + 1))
            dve.wait_ge(*self.s_done.upto(8 * i))
            keys = k.xT[p][:, :] if self.kind == "self" else k.ctxT[:, 0, bass.ts(b, M)]
        hm = k.head_of4 if self.per == 4 else k.head_of2
        dve.tensor_tensor(k.kb[p][:, 0:self.per, 0:self.T], bcast(keys, 1, self.per), bcast(hm, 2, self.T),
                          ALU.mult).then_inc(self.kv_ready.sem, 1)

    def maxima(self, dve, b, p, u):
        k, c = self.k, self.k.dchain
        dve.wait_ge(*self.s_done.upto(4 * b + u + 1))
        hs = slice(u * self.per, (u + 1) * self.per)
        src = k.ps[:, u, :].rearrange("q (h t) -> q h t", t=P)[:, 0:self.per, 0:self.T]
        c.link(dve.tensor_reduce(k.mx[p][:, hs], src, AX.X, ALU.max))
        dve.tensor_scalar(k.nmx[p][:, hs], k.mx[p][:, hs], -self.scale, None, ALU.mult)\
            .then_inc(self.max_ready.sem, 1)

    def outputs(self, dve, b):
        k, c = self.k, self.k.dchain
        w = self.dh + 1
        dve.wait_ge(*self.av_odd.upto(2 * b + 2))
        O = k.ps[:, OB, 0:self.H * w].rearrange("q (h w) -> q h w", w=w)
        c.link(dve.reciprocal(k.rec[:, 0:self.H], O[:, :, self.dh]))
        if self.proj:
            dve.wait_ge(*self.oT_done.upto(b))
        dve.tensor_tensor(k.o[:, :].rearrange("q (h w) -> q h w", w=self.dh), O[:, :, 0:self.dh],
                          bcast(k.rec[:, 0:self.H], 2, self.dh), ALU.mult).then_inc(self.o_ready.sem, 1)
        if not self.proj:
            dve.wait_ge(*self.o_ready.upto(b + 1))
            base, dst = (k.xn, k.r) if self.kind == "self" else (k.x, k.x)
            c.step(dve.tensor_tensor(dst[:, b, :], base[:, b, :], k.o[:, :], ALU.add))

    def residual(self, dve, b):
        k, c = self.k, self.k.dchain
        dve.wait_ge(*self.y_done.upto(b + 1))
        dve.tensor_tensor(k.x[:, b, :], k.x[:, b, :], k.ps[:, MB, 3 * P:4 * P], ALU.add)\
            .then_inc(self.res_done.sem, 1)

    def pool(self, pool):
        k = self.k
        pool.wait_ge(*self.turn.xT_ready.upto(1))
        for p in range(2):
            t = pool.memset(self.v[p], 1.0)
        t.then_inc(self.v_clear.sem, 1)
        pool.wait_ge(*self.turn.xT_ready.upto(2))
        with pool.Fori(0, B // 2) as i:
            for p in range(2):
                b = 2 * i + p
                if self.proj:
                    pool.wait_ge(*self.qkv_done.upto(2 * i))
                else:
                    pool.wait_ge(*self.s_done.upto(8 * i))
                    pool.wait_ge(*self.kv_ready.upto(2 * i))
                pool.tensor_copy(k.xT[p][:, :], k.xnT[:, bass.ts(b, P)]).then_inc(self.xT_ready.sem, 1)

    def scalar(self, act):
        k = self.k
        with act.Fori(0, B // 2) as i:
            for p in range(2):
                b = 2 * i + p
                if self.proj:
                    act.wait_ge(*self.qkv_done.upto(b + 1))
                    src = k.ps[:, 2 * p + 1, 0:P]
                elif self.kind == "self":
                    act.wait_ge(*self.norm.xn_ready.upto(b + 1))
                    src = k.xn[:, b, :]
                else:
                    src = k.ctx[:, bass.ts(b, CTX)][0:M, P:CTX]
                act.wait_ge(*self.av_odd.upto(4 * i))
                act.wait_ge(*self.v_clear.upto(1))
                w = self.dh + 1
                dst = self.v[p][0:self.T, 0:self.H * w].rearrange("t (h w) -> t h w", w=w)[:, :, 0:self.dh]
                act.activation(dst, src.rearrange("t (h w) -> t h w", w=self.dh), ACT.Copy)\
                    .then_inc(self.v_ready.sem, 1)
            for p in range(2):
                b = 2 * i + p
                for u in range(4):
                    self.weights(act, i, b, p, u)
                    if p and u == 1 and self.proj:
                        self.turned_out(act, 2 * i)
                for u in (1, 3):
                    act.wait_ge(*self.pt_done.upto(4 * b + u + 1))
                    act.wait_ge(*self.av_odd.upto(2 * b + u // 2))
                    n = self.per * P
                    act.activation(k.pT[1][0:self.T, :, :].rearrange("t h q -> t (h q)")[:, 0:n],
                                   k.ps[0:self.T, PT0 + 1, 0:n], ACT.Copy).then_inc(self.pta_ready.sem, 1)
                if p and self.proj:
                    self.turned_out(act, b)

    def weights(self, act, i, b, p, u):
        k = self.k
        act.wait_ge(*self.max_ready.upto(4 * b + u + 1))
        act.wait_ge(*self.pt_done.upto(8 * i))
        for j in range(self.per):
            h = u * self.per + j
            e = act.activation(k.p[p][:, h, 0:self.T], k.ps[:, u, j * P:j * P + self.T], ACT.Exp,
                               bias=k.nmx[p][:, h:h + 1], scale=float(self.scale))
        e.then_inc(self.p_ready.sem, 1)

    def turned_out(self, act, b):
        k = self.k
        act.wait_ge(*self.oT_done.upto(b + 1))
        act.wait_ge(*self.y_done.upto(b))
        act.activation(k.oT[:, :], k.ps[:, MB, 2 * P:3 * P], ACT.Copy).then_inc(self.oT_ready.sem, 1)


class Experts:

    def __init__(self, k, norm, turn, kind):
        self.k, self.norm, self.turn, self.kind = k, norm, turn, kind
        self.nf = 2 if kind == "bit" else 4
        self.func = {"gelu": ACT.Gelu, "bit": ACT.Silu}.get(kind, ACT.Relu)
        self.routed = kind != "dense"
        self.b2 = kind in ("relu", "gelu", "gate")
        self.first = {"dense": -2, "bit": 2}.get(kind, 0)
        self.items = {"dense": 2, "bit": 18}.get(kind, 16)
        sig = k.sig
        self.h_done = sig["ff_h_done"].take(self.items * self.nf)
        self.h_ready = sig["ff_h_ready"].take(self.items * self.nf)
        self.o_done = sig["ff_o_done"].take(self.items)
        self.acc_done = sig["ff_acc_done"].take(self.items)
        if self.routed:
            self.router_done = sig["ff_router_done"].take(1)
        if kind in ("relu", "gelu", "gate"):
            self.loaded = [s.take(4 * 32) for s in k.ring_loaded]
        elif kind == "bit":
            self.loaded = [s.take(4) for s in k.ring_copied]
        else:
            self.loaded = [None, k.ring_loaded[1].take(32)]
        if self.b2:
            self.w_ready = sig["ff_w_ready"].take(1)
            self.w_turned = sig["ff_w_turned"].take(1)
            self.wT_ready = sig["ff_wT_ready"].take(1)
            self.b2_done = sig["ff_b2_done"].take(1)
        if kind == "gate":
            self.result = sig["result"].take(2)
        if kind in ("gelu", "gate", "bit"):
            self.l_ready = sig["ff_l_ready"].take(2 if kind == "gelu" else 1)
            self.e_ready = sig["ff_e_ready"].take(2 if kind == "gelu" else 1)

    def weights_in(self, p):
        if self.kind == "bit":
            return lambda i: self.loaded[p].upto(i + 1)
        return lambda i: self.loaded[p].upto(32 * (i + 1))

    def sync(self, sp, w1, w2):
        k = self.k
        if self.kind == "dense":
            sp.wait_ge(*self.o_done.upto(0))
            sp.dma_start(k.w1[1][:, :], w1).then_inc(self.loaded[1].sem, 16)
            sp.dma_start(k.w2[1][:, :, :], w2.rearrange("(c p) d -> p c d", p=P)).then_inc(self.loaded[1].sem, 16)
            return
        with sp.Fori(0, 4) as i:
            for p in range(2):
                e = 2 * i + p
                sp.wait_ge(*self.o_done.upto(2 * e - 2))
                sp.dma_start(k.w1[p][:, :], w1[bass.ds(e, 1)].rearrange("o d f -> d (o f)"))\
                    .then_inc(self.loaded[p].sem, 16)
                sp.dma_start(k.w2[p][:, :, :], w2[bass.ds(e, 1)].rearrange("o (c p) d -> p (o c) d", p=P))\
                    .then_inc(self.loaded[p].sem, 16)

    def pool(self, pool):
        k = self.k
        with pool.Fori(0, 4) as i:
            for p in range(2):
                e = 2 * i + p
                pool.wait_ge(*self.o_done.upto(2 * e))
                pool.tensor_copy(k.w1[p][:, 0:256], k.bit_w1T[:, bass.ts(e + 1, 256)])
                pool.tensor_copy(k.w2[p][:, 0:2, :].rearrange("f c d -> f (c d)"), k.bit_w2T[:, bass.ts(e + 1, 256)])\
                    .then_inc(self.loaded[p].sem, 1)

    def tensor(self, pe):
        k = self.k
        if self.routed:
            R = {"gelu": 12}.get(self.kind, 8)
            for t in range(B):
                pe.wait_ge(*self.turn.xT_ready.upto(t // 4 + 1))
                m = pe.matmul(k.ps[:, 6, 16 * t:16 * t + R], k.xnT[:, t * P:(t + 1) * P], k.router[self.kind],
                              start=True, stop=True)
            m.then_inc(self.router_done.sem, 1)
        else:
            pe.wait_ge(*self.turn.xT_ready.upto(2))
        if self.kind == "dense":
            self.block(pe, 0, [1])
        else:
            if self.kind == "bit":
                self.block(pe, 0, ["shared"])
            with pe.Fori(0, 4) as i:
                self.block(pe, i, [0, 1])
        if self.b2:
            pe.wait_ge(*self.w_ready.upto(1))
            pe.wait_ge(*self.h_ready.upto(self.items * self.nf))
            pe.transpose(k.ps[0:64, 0, 0:P], k.w[:, :], k.ident).then_inc(self.w_turned.sem, 1)
            pe.wait_ge(*self.wT_ready.upto(1))
            k.arrived(pe, "b2")
            for h in range(2):
                m = pe.matmul(k.ps[:, 6 + h, :], k.wT_small, k.b2_blocks[self.kind][:, h * HALF:(h + 1) * HALF],
                              start=True, stop=True)
            m.then_inc(self.b2_done.sem, 1)

    def item(self, i, p, h):
        return h if p == "shared" else self.first + 4 * i + 2 * p + h

    def block(self, pe, i, ps):
        items = [(p, h) for p in ps for h in range(2)]
        self.layer1(pe, i, *items[0])
        for n, it in enumerate(items):
            if n + 1 < len(items):
                self.layer1(pe, i, *items[n + 1])
            self.layer2(pe, i, *it)

    def layer1(self, pe, i, p, h):
        k = self.k
        n = self.item(i, p, h)
        shared = p == "shared"
        if h == 0 and not shared:
            pe.wait_ge(*self.weights_in(p)(i))
        w1 = k.bit_w1T[:, 0:256] if shared else k.w1[p][:, :]
        for c in range(self.nf):
            pe.wait_ge(*self.h_ready.upto(self.nf * (n - 1) + c + 1))
            pe.matmul(k.ps[:, c, :], w1[:, c * P:(c + 1) * P], k.xnT[:, h * HALF:(h + 1) * HALF],
                      start=True, stop=True).then_inc(self.h_done.sem, 1)

    def layer2(self, pe, i, p, h):
        k = self.k
        n = self.item(i, p, h)
        pe.wait_ge(*self.acc_done.upto(n - 1))
        pe.wait_ge(*self.h_ready.upto(self.nf * (n + 1)))
        for j in range(4):
            for c in range(self.nf):
                w2 = k.bit_w2T[:, c * P:(c + 1) * P] if p == "shared" else k.w2[p][:, c, :]
                m = pe.matmul(k.ps[:, 4 + h, j * P:(j + 1) * P], k.hT[h][:, c, j * P:(j + 1) * P], w2,
                              start=c == 0, stop=c == self.nf - 1)
        m.then_inc(self.o_done.sem, 1)

    def scalar(self, act):
        k = self.k
        if self.kind in ("gelu", "gate", "bit"):
            for r in range({"gelu": 2}.get(self.kind, 1)):
                act.wait_ge(*self.l_ready.upto(r + 1))
                arg = k.lang if self.kind == "gelu" and r == 0 else k.logit
                act.activation(arg[:, :, :], arg[:, :, :], ACT.Exp, scale=-1.0 if self.kind == "gate" else 1.0)\
                    .then_inc(self.e_ready.sem, 1)
        if self.kind == "dense":
            self.hidden(act, 0, [1])
        else:
            if self.kind == "bit":
                self.hidden(act, 0, ["shared"])
            with act.Fori(0, 4) as i:
                self.hidden(act, i, [0, 1])
        if self.b2:
            act.wait_ge(*self.w_turned.upto(1))
            act.activation(k.wT_small, k.ps[0:64, 0, 0:P], ACT.Copy).then_inc(self.wT_ready.sem, 1)

    def hidden(self, act, i, ps):
        k = self.k
        for p in ps:
            for h in range(2):
                n = self.item(i, p, h)
                act.wait_ge(*self.o_done.upto(n - 1))
                for c in range(self.nf):
                    act.wait_ge(*self.h_done.upto(self.nf * n + c + 1))
                    if self.kind == "bit":
                        bias = 0.0
                    elif self.kind == "dense":
                        bias = k.cols[:, k.col["dense_b1"] + c:k.col["dense_b1"] + c + 1]
                    else:
                        j = k.col[self.kind + "_b1"] + c
                        bias = k.cols[:, bass.ds((2 * i + p) * 4 + j if h == 0 else i * 8 + (4 * p + j), 1)]
                    act.activation(k.hT[h][:, c, :], k.ps[:, c, :], self.func, bias=bias)\
                        .then_inc(self.h_ready.sem, 1)

    def vector(self, dve, stats=True, between=None):
        k, c = self.k, self.k.dchain
        if self.routed:
            self.route(dve)
        if between is not None:
            between.vector(dve)
        if self.kind == "dense":
            self.add(dve, 0, 1, k.r)
        elif self.kind == "bit":
            self.add(dve, 0, "shared", k.x)
            with dve.Fori(0, 4) as i:
                for p in range(2):
                    self.add(dve, i, p, k.x)
        else:
            with dve.Fori(0, 4) as i:
                for p in range(2):
                    self.add(dve, i, p, k.x)
        dve.wait_ge(*self.acc_done.upto(self.items))
        acc = k.r if self.kind == "dense" else k.x
        for h in range(2):
            if self.b2:
                dve.wait_ge(*self.b2_done.upto(1))
                total = dve.tensor_tensor(k.x[:, 4 * h:4 * h + 4, :], k.x[:, 4 * h:4 * h + 4, :],
                                          k.ps[:, 6 + h, :].rearrange("s (b d) -> s b d", d=D), ALU.add)
                if stats:
                    c.link(total)
                else:
                    total.then_inc(self.result.sem, 1)
            if stats:
                token_stats(k, dve, acc, range(4 * h, 4 * h + 4))

    def add(self, dve, i, p, acc):
        k = self.k
        for h in range(2):
            n = self.item(i, p, h)
            dve.wait_ge(*self.o_done.upto(n + 1))
            dve.wait_ge(*self.acc_done.upto(n - 1))
            if p == "shared" or self.kind == "dense":
                ins = dve.tensor_tensor(acc[:, 4 * h:4 * h + 4, :], acc[:, 4 * h:4 * h + 4, :],
                                        k.ps[:, 4 + h, :].rearrange("s (b d) -> s b d", d=D), ALU.add)
            else:
                for j in range(4):
                    t = 4 * h + j
                    ins = dve.scalar_tensor_tensor(acc[:, t, :], k.ps[:, 4 + h, j * P:(j + 1) * P],
                                                   k.w[:, bass.ds(2 * i + (8 * t + p), 1)], acc[:, t, :],
                                                   ALU.mult, ALU.add)
            ins.then_inc(self.acc_done.sem, 1)

    def route(self, dve):
        k, c = self.k, self.k.dchain
        dve.wait_ge(*self.router_done.upto(1))
        G = k.ps[:, 6, 0:16 * B].rearrange("s (t r) -> s t r", r=16)
        L = k.logit[:, :, :]
        W = k.w[:, :].rearrange("s (t e) -> s t e", e=8)

        def exponentials(r):
            dve.wait_ge(*self.e_ready.upto(r + 1))

        c.link(dve.tensor_tensor(L, G[:, :, 0:8], bcast(k.router_b[self.kind], 1, B), ALU.add))
        if self.kind == "gate":
            dve.tensor_scalar(W, L, 0.0, None, ALU.is_gt).then_inc(self.l_ready.sem, 1)
            exponentials(0)
            c.link(dve.tensor_scalar(L, L, 1.0, None, ALU.add))
            c.link(dve.reciprocal(L, L))
            dve.tensor_tensor(W, W, L, ALU.mult).then_inc(self.w_ready.sem, 1)
            dve.wait_ge(*self.w_ready.upto(1))
            return
        if self.kind == "gelu":
            G4 = k.lang[:, :, :]
            c.link(dve.tensor_tensor(G4, G[:, :, 8:12], bcast(k.lang_b, 1, B), ALU.add))
            c.link(dve.tensor_reduce(k.peak[:, :], G4, AX.X, ALU.max))
            dve.tensor_tensor(G4, G4, bcast(k.peak[:, :], 2, 4), ALU.subtract).then_inc(self.l_ready.sem, 1)
            exponentials(0)
            c.link(dve.tensor_reduce(k.peak[:, :], G4, AX.X, ALU.add))
            c.link(dve.reciprocal(k.peak[:, :], k.peak[:, :]))
            c.link(dve.tensor_tensor(k.lp[:, :, 0:4], G4, bcast(k.peak[:, :], 2, 4), ALU.mult))
            c.link(dve.tensor_tensor(G4, k.lp[:, :, 0:4], k.lp[:, :, 1:5], ALU.add))
            for half in range(2):
                v = k.logit[:, :, 4 * half:4 * half + 4]
                c.link(dve.scalar_tensor_tensor(v, G4, 0.1, v, ALU.mult, ALU.add))
        c.link(dve.tensor_reduce(k.peak[:, :], L, AX.X, ALU.max))
        c.link(dve.tensor_tensor(L, L, bcast(k.peak[:, :], 2, 8), ALU.subtract))
        c.link(dve.tensor_scalar(L, L, -104.0, None, ALU.max))
        mine, other = bcast(L, 3, 8), bcast(L, 2, 8)
        c.step(dve.tensor_tensor(k.more[:, :, :, :], other, mine, ALU.is_gt))
        c.link(dve.tensor_tensor(k.same[:, :, :, :], other, mine, ALU.is_equal))
        c.link(dve.tensor_tensor(k.same[:, :, :, :], k.same[:, :, :, :], bcast(k.lower, 1, B), ALU.mult))
        c.link(dve.tensor_tensor(k.more[:, :, :, :], k.more[:, :, :, :], k.same[:, :, :, :], ALU.add))
        last = dve.tensor_reduce(k.rank[:, :, :], k.more[:, :, :, :], AX.X, ALU.add)
        if self.kind == "relu":
            c.link(last)
            dve.tensor_scalar(W, k.rank[:, :, :], 2.0, None, ALU.is_lt).then_inc(self.w_ready.sem, 1)
            dve.wait_ge(*self.w_ready.upto(1))
            return
        last.then_inc(self.l_ready.sem, 1)
        r = 1 if self.kind == "gelu" else 0
        exponentials(r)
        c.link(dve.tensor_scalar(W, k.rank[:, :, :], 2.0 if self.kind == "gelu" else 1.0, None, ALU.is_lt))
        if self.kind == "gelu":
            c.link(dve.tensor_tensor(L, L, W, ALU.mult))
        c.link(dve.tensor_reduce(k.peak[:, :], L, AX.X, ALU.add))
        c.link(dve.reciprocal(k.peak[:, :], k.peak[:, :]))
        if self.kind == "gelu":
            dve.tensor_tensor(W, L, bcast(k.peak[:, :], 2, 8), ALU.mult).then_inc(self.w_ready.sem, 1)
            dve.wait_ge(*self.w_ready.upto(1))
        else:
            c.link(dve.tensor_tensor(W, W, bcast(k.peak[:, :], 2, 8), ALU.mult))


class Depool:

    def __init__(self, k, norm, turn, w_inT, pooled, nth):
        self.k, self.norm, self.turn, self.w_inT, self.pooled, self.nth = k, norm, turn, w_inT, pooled, nth
        self.pooled_in = k.sig["dp_pooled_in"].take(1)
        self.y_done = k.sig["dp_y_done"].take(2)

    def pool(self, pool):
        k = self.k
        pool.wait_ge(*self.norm.xn_ready.upto(B))
        pool.wait_ge(*k.pooled_ready.upto(self.nth))
        pool.tensor_tensor(k.x[:, :, :], k.x[:, :, :], self.pooled[:, :, :], ALU.add).then_inc(self.pooled_in.sem, 1)

    def tensor(self, pe):
        k = self.k
        for b in range(B):
            pe.wait_ge(*self.turn.xT_ready.upto(b // 4 + 1))
            m = pe.matmul(k.ps[:, b // 4, b % 4 * P:(b % 4 + 1) * P], k.xnT[:, b * P:(b + 1) * P], self.w_inT,
                          start=True, stop=True)
            if b % 4 == 3:
                m.then_inc(self.y_done.sem, 1)

    def vector(self, dve):
        k = self.k
        dve.wait_ge(*self.pooled_in.upto(1))
        for h in range(2):
            dve.wait_ge(*self.y_done.upto(h + 1))
            k.dchain.link(dve.tensor_tensor(k.x[:, 4 * h:4 * h + 4, :], k.x[:, 4 * h:4 * h + 4, :],
                                            k.ps[:, h, :].rearrange("s (b d) -> s b d", d=D), ALU.add))
            token_stats(k, dve, k.x, range(4 * h, 4 * h + 4))


class AfterNorm:

    def __init__(self, k, norm, gain, bias):
        self.k, self.norm, self.gain, self.bias = k, norm, gain, bias
        self.bias_in = k.sig["an_bias_in"].take(1)

    def pool(self, pool):
        k = self.k
        pool.tensor_tensor(k.x[:, :, :], k.x[:, :, :], bcast(self.bias, 1, B), ALU.add).then_inc(self.bias_in.sem, 1)

    def vector(self, dve):
        k, c = self.k, self.k.dchain
        dve.wait_ge(*self.norm.xn_ready.upto(B))
        dve.wait_ge(*self.bias_in.upto(1))
        for h in range(2):
            q = slice(4 * h, 4 * h + 4)
            c.link(dve.tensor_tensor(k.xn[:, q, :], k.xn[:, q, :], bcast(self.gain, 1, 4), ALU.mult))
            c.link(dve.tensor_tensor(k.x[:, q, :], k.x[:, q, :], k.xn[:, q, :], ALU.add))
            token_stats(k, dve, k.x, range(4 * h, 4 * h + 4))


class DenseStart:

    def __init__(self, k, norm):
        self.k, self.norm = k, norm
        self.ready = k.sig["dense_start"].take(1)

    def pool(self, pool):
        k = self.k
        pool.wait_ge(*self.norm.xn_ready.upto(B))
        k.pchain.link(pool.tensor_tensor(k.r[:, :, :], k.xn[:, :, :], bcast(k.ln1_g, 1, B), ALU.mult))
        k.pchain.link(pool.tensor_tensor(k.r[:, :, :], k.r[:, :, :], bcast(k.ln1_b, 1, B), ALU.add))
        pool.tensor_tensor(k.r[:, :, :], k.r[:, :, :], bcast(k.dense_b2, 1, B), ALU.add).then_inc(self.ready.sem, 1)

    def vector(self, dve):
        dve.wait_ge(*self.ready.upto(1))


class Mamba:

    N, K, C = 16, 4, 2

    def __init__(self, k, norm, turn):
        self.k, self.norm, self.turn = k, norm, turn
        sig = k.sig
        t = lambda name, n: sig["mb_" + name].take(n)
        self.pad_ready = t("pad_ready", 1)
        self.started = t("started", 1)
        self.in_done = t("in_done", 8)
        self.u_in = t("u_in", 4)
        self.gate_ready = t("gate_ready", 4)
        self.conv_done = t("conv_done", 4)
        self.u_ready = t("u_ready", 4)
        self.dl_done = t("dl_done", 2)
        self.dl_ready = t("dl_ready", 2)
        self.bc_done = t("bc_done", 2)
        self.bc_ready = t("bc_ready", 1)
        self.dt_done = t("dt_done", 4)
        self.z_ready = t("z_ready", 2)
        self.lg_ready = t("lg_ready", 2)
        self.du_ready = t("du_ready", 2)
        self.a_exp = t("a_exp", 1)
        self.b_done = t("b_done", self.N)
        self.c_done = t("c_done", self.N)
        self.c_ready = t("c_ready", self.N)
        self.dA_ready = [t(f"dA_ready{c}", self.N) for c in range(2)]
        self.dbu_done = t("dbu_done", 2 * self.N)
        self.scanned = [t(f"scanned{c}", self.N) for c in range(2)]
        self.sc_ready = [t(f"sc_ready{c}", self.N) for c in range(2)]
        self.y_done = [t(f"y_done{c}", self.N) for c in range(2)]
        self.yg_ready = t("yg_ready", 2)
        self.out_done = t("out_done", 2)

    def tensor(self, pe):
        k = self.k
        pe.wait_ge(*self.turn.xT_ready.upto(2))
        k.arrived(pe, "mamba")
        k.arrived(pe, "masks")
        for c in range(4):
            for h in range(2):
                pe.matmul(k.ps[:, 2 * c + h, :], k.mb_win[:, c * P:(c + 1) * P], k.xnT[:, h * HALF:(h + 1) * HALF],
                          start=True, stop=True).then_inc(self.in_done.sem, 1)
        pe.wait_ge(*self.u_in.upto(4))
        pe.wait_ge(*self.pad_ready.upto(1))
        for o in range(2):
            for h in range(2):
                for n, (tap, c) in enumerate((tap, c) for tap in range(self.K) for c in range(2)):
                    m = pe.matmul(k.ps[:, 2 * o + h, :], k.mb_conv[:, 2 * tap + c, o * P:(o + 1) * P],
                                  k.upad[:, c, 4 * h:4 * h + 4, tap:tap + P], start=n == 0, stop=n == 2 * self.K - 1)
                m.then_inc(self.conv_done.sem, 1)
        pe.wait_ge(*self.gate_ready.upto(4))
        pe.wait_ge(*self.u_ready.upto(4))
        for out, w, rows, sig in ((4, k.mb_wx[:, :, 0:64], 64, self.dl_done), (6, k.wx3[:, :, :], 96, self.bc_done)):
            for h in range(2):
                for c in range(2):
                    m = pe.matmul(k.ps[0:rows, out + h, :], w[:, c, :], k.u[:, c, h * HALF:(h + 1) * HALF],
                                  start=c == 0, stop=c == 1)
                m.then_inc(sig.sem, 1)
        pe.wait_ge(*self.dl_ready.upto(2))
        for c in range(2):
            for h in range(2):
                pe.matmul(k.ps[:, 2 * c + h, :], k.mb_wdt[:, c * P:(c + 1) * P], k.dlT[:, h * HALF:(h + 1) * HALF],
                          start=True, stop=True).then_inc(self.dt_done.sem, 1)
        pe.wait_ge(*self.bc_ready.upto(1))
        for bank in range(4, 8):
            pe.matmul(k.ps[:, bank, :], k.ident, k.zeros, start=True, stop=False)
        pe.wait_ge(*self.du_ready.upto(2))
        self.spread(pe, 0)
        with pe.Fori(0, self.N // 2 - 1) as i:
            for q in range(2):
                self.spread(pe, 2 * i + (q + 1))
                self.sum_up(pe, 2 * i + q, False)
        self.spread(pe, self.N - 1)
        self.sum_up(pe, self.N - 2, False)
        self.sum_up(pe, self.N - 1, True)
        pe.wait_ge(*self.yg_ready.upto(2))
        for b in range(B):
            for c in range(2):
                m = pe.matmul(k.ps[:, b // 4, b % 4 * P:(b % 4 + 1) * P], k.yg[:, c, b * P:(b + 1) * P],
                              k.mb_wout[:, c, :], start=c == 0, stop=c == 1)
            if b % 4 == 3:
                m.then_inc(self.out_done.sem, 1)

    def spread(self, pe, n):
        k = self.k
        pe.wait_ge(*self.dbu_done.upto(2 * n))
        for h in range(2):
            m = pe.matmul(k.ps[:, h, :], k.sel[:, bass.ts(n, P)], k.bc3[:, h * HALF:(h + 1) * HALF],
                          start=True, stop=True)
        m.then_inc(self.b_done.sem, 1)
        pe.wait_ge(*self.c_ready.upto(n))
        for h in range(2):
            m = pe.matmul(k.ps[:, 2 + h, :], k.sel[:, bass.ts(n + self.N, P)], k.bc3[:, h * HALF:(h + 1) * HALF],
                          start=True, stop=True)
        m.then_inc(self.c_done.sem, 1)

    def sum_up(self, pe, n, last):
        k = self.k
        for c in range(2):
            pe.wait_ge(*self.sc_ready[c].upto(n + 1))
            for h in range(2):
                m = pe.matmul(k.ps[:, 4 + 2 * c + h, :], k.ident, k.sC[c][:, h * HALF:(h + 1) * HALF],
                              start=False, stop=last)
            m.then_inc(self.y_done[c].sem, 1)

    def scalar(self, act):
        k = self.k
        for c in range(2):
            for h in range(2):
                act.wait_ge(*self.in_done.upto(2 * c + h + 1))
                act.activation(k.upad[:, c, 4 * h:4 * h + 4, self.K - 1:self.K - 1 + P],
                               k.ps[:, 2 * c + h, :].rearrange("p (b t) -> p b t", t=P), ACT.Copy)\
                    .then_inc(self.u_in.sem, 1)
        for c in range(2):
            for h in range(2):
                act.wait_ge(*self.in_done.upto(4 + 2 * c + h + 1))
                act.activation(k.gate[:, c, h * HALF:(h + 1) * HALF], k.ps[:, 4 + 2 * c + h, :], ACT.Silu)\
                    .then_inc(self.gate_ready.sem, 1)
        for o in range(2):
            for h in range(2):
                act.wait_ge(*self.conv_done.upto(2 * o + h + 1))
                j = k.col["conv_b"] + o
                act.activation(k.u[:, o, h * HALF:(h + 1) * HALF], k.ps[:, 2 * o + h, :], ACT.Silu,
                               bias=k.cols[:, j:j + 1]).then_inc(self.u_ready.sem, 1)
        for h in range(2):
            act.wait_ge(*self.dl_done.upto(h + 1))
            act.activation(k.dlT[:, h * HALF:(h + 1) * HALF], k.ps[0:64, 4 + h, :], ACT.Copy)\
                .then_inc(self.dl_ready.sem, 1)
        k.arrived(act, "mamba")
        act.activation(k.a_exp[:, :, :], k.a_log[:, :, :], ACT.Exp).then_inc(self.a_exp.sem, 1)
        for c in range(2):
            act.wait_ge(*self.z_ready.upto(c + 1))
            k.achain.link(act.activation(k.sp[:, c, :], k.sp[:, c, :], ACT.Exp))
            act.activation(k.sp[:, c, :], k.sp[:, c, :], ACT.Ln, bias=k.one_col).then_inc(self.lg_ready.sem, 1)
        with act.Fori(0, self.N // 2) as i:
            for q in range(2):
                n = 2 * i + q
                for c in range(2):
                    act.wait_ge(*self.scanned[c].upto(n))
                    act.wait_ge(*self.started.upto(1))
                    act.activation(k.dA[c][:, :, 1:S], k.delta[:, c, :].rearrange("p (b t) -> p b t", t=S)[:, :, 1:S],
                                   ACT.Exp, scale=k.a_neg[:, bass.ds(n + 16 * c, 1)]).then_inc(self.dA_ready[c].sem, 1)
                    if c == 0:
                        act.wait_ge(*self.c_done.upto(n + 1))
                        act.wait_ge(*self.sc_ready[1].upto(n - 1))
                        act.activation(k.cb[q][:, :], k.ps[:, 2:4, :].rearrange("p a n -> p (a n)"), ACT.Copy)\
                            .then_inc(self.c_ready.sem, 1)

    def vector(self, dve):
        k, c_ = self.k, self.k.dchain
        dve.wait_ge(*self.bc_done.upto(2))
        src = k.ps[:, 6:8, :].rearrange("p a n -> p (a n)")
        c_.link(dve.tensor_copy(k.bc3[0:96, :], src[0:96, :]))
        c_.link(dve.tensor_tensor(k.rest[:, :], src[0:96, :], k.bc3[0:96, :], ALU.subtract))
        c_.step(dve.tensor_copy(k.bc3[32:64, :], k.rest[32:64, :]))
        c_.link(dve.tensor_copy(k.bc3[64:96, :], k.rest[64:96, :]))
        c_.link(dve.tensor_tensor(k.rest[64:96, :], k.rest[64:96, :], k.bc3[64:96, :], ALU.subtract))
        dve.tensor_copy(k.bc3[64:96, :], k.rest[64:96, :]).then_inc(self.bc_ready.sem, 1)
        dve.wait_ge(*self.a_exp.upto(1))
        c_.step(dve.tensor_scalar(k.a_neg[:, :], k.a_exp[:, :, :].rearrange("p c n -> p (c n)"), -1.0, None, ALU.mult))
        for c in range(2):
            dve.wait_ge(*self.dt_done.upto(2 * c + 2))
            z = k.ps[:, 2 * c:2 * c + 2, :].rearrange("p a n -> p (a n)")
            j = k.col["b_dt"] + c
            c_.link(dve.tensor_scalar(k.delta[:, c, :], z, k.cols[:, j:j + 1], None, ALU.add))
            dve.scalar_tensor_tensor(k.sp[:, c, :], k.delta[:, c, :], -1.0, k.delta[:, c, :], ALU.mult, ALU.min)\
                .then_inc(self.z_ready.sem, 1)
        for c in range(2):
            dve.wait_ge(*self.lg_ready.upto(c + 1))
            c_.link(dve.scalar_tensor_tensor(k.delta[:, c, :], k.delta[:, c, :], 0.0, k.sp[:, c, :], ALU.max, ALU.add))
            dve.wait_ge(*self.u_ready.upto(4))
            dve.tensor_tensor(k.du[:, c, :], k.delta[:, c, :], k.u[:, c, :], ALU.mult).then_inc(self.du_ready.sem, 1)
        dve.wait_ge(*self.du_ready.upto(2))
        for c in range(2):
            c_.step(dve.memset(k.dA[c][:, :, 0:1], 0.0))
        dve.memset(k.s_last[:, :, :], 0.0).then_inc(self.started.sem, 1)
        dve.wait_ge(*self.started.upto(1))
        with dve.Fori(0, self.N) as n:
            for c in range(2):
                dve.wait_ge(*self.b_done.upto(n + 1))
                dve.wait_ge(*self.scanned[c].upto(n))
                dve.tensor_tensor(k.dbu[c][:, :], k.ps[:, 0:2, :].rearrange("p a n -> p (a n)"), k.du[:, c, :],
                                  ALU.mult).then_inc(self.dbu_done.sem, 1)
                dve.wait_ge(*self.dbu_done.upto(2 * n + (c + 1)))
                dve.wait_ge(*self.dA_ready[c].upto(n + 1))
                dve.wait_ge(*self.sc_ready[c].upto(n))
                dve.tensor_tensor_scan(k.s[c][:, :], k.dA[c][:, :, :].rearrange("p b t -> p (b t)"), k.dbu[c][:, :],
                                       0.0, ALU.mult, ALU.add).then_inc(self.scanned[c].sem, 1)
        for c in range(2):
            j = k.col["ssm_d"] + c
            dve.wait_ge(*self.y_done[c].upto(self.N))
            dve.wait_ge(*self.sc_ready[c].upto(self.N))
            c_.link(dve.tensor_scalar(k.s_last[:, c, :], k.s_last[:, c, :], k.cols[:, j:j + 1], None, ALU.mult))
            y = k.ps[:, 4 + 2 * c:6 + 2 * c, :].rearrange("p a (b t) -> p (a b) t", t=S)
            c_.link(dve.tensor_tensor(k.yg[:, c, :].rearrange("p (b t) -> p b t", t=S), y,
                                      bcast(k.s_last[:, c, :], 2, S), ALU.add))
            dve.wait_ge(*self.gate_ready.upto(4))
            dve.tensor_tensor(k.yg[:, c, :], k.yg[:, c, :], k.gate[:, c, :], ALU.mult).then_inc(self.yg_ready.sem, 1)
        for h in range(2):
            dve.wait_ge(*self.out_done.upto(h + 1))
            c_.link(dve.tensor_tensor(k.x[:, 4 * h:4 * h + 4, :], k.x[:, 4 * h:4 * h + 4, :],
                                      k.ps[:, h, :].rearrange("s (b d) -> s b d", d=D), ALU.add))
            token_stats(k, dve, k.x, range(4 * h, 4 * h + 4))

    def pool(self, pool):
        k = self.k
        pool.wait_ge(*self.turn.xT_ready.upto(2))
        k.arrived(pool, "mamba")
        for j in range(3):
            pool.tensor_copy(k.wx3[:, :, 32 * j:32 * j + 32], k.mb_wx[:, :, 64:96])
        pool.memset(k.zeros, 0.0)
        pool.memset(k.upad[:, 0, :, 0:self.K - 1], 0.0)
        pool.memset(k.upad[:, 1, :, 0:self.K - 1], 0.0).then_inc(self.pad_ready.sem, 1)
        pool.wait_ge(*self.started.upto(1))
        with pool.Fori(0, self.N // 2) as i:
            for q in range(2):
                n = 2 * i + q
                for c in range(2):
                    pool.wait_ge(*self.scanned[c].upto(n + 1))
                    last = k.s[c][:, :].rearrange("p (b t) -> p b t", t=S)[:, :, S - 1]
                    pool.tensor_tensor(k.s_last[:, c, :], k.s_last[:, c, :], last, ALU.add)
                    pool.wait_ge(*self.c_ready.upto(n + 1))
                    pool.wait_ge(*self.y_done[c].upto(n))
                    pool.tensor_tensor(k.sC[c][:, :], k.s[c][:, :], k.cb[q][:, :], ALU.mult)\
                        .then_inc(self.sc_ready[c].sem, 1)


class WideCross:

    H, DH, T = 16, 64, M + 1

    def __init__(self, k, norm, turn):
        self.k, self.norm, self.turn = k, norm, turn
        sig = k.sig
        self.clear = sig["wc_clear"].take(1)
        self.cT_ready = sig["at_xT_ready"].take(B)
        self.q_done = sig["wc_q_done"].take(B)
        self.k_done = sig["wc_k_done"].take(B)
        self.v_done = sig["at_qkv_done"].take(B)
        self.q_ready = sig["at_kv_ready"].take(B)
        self.k_ready = sig["wc_k_ready"].take(B)
        self.v_ready = sig["at_v_ready"].take(B)
        self.s_done = sig["at_s_done"].take(4 * B)
        self.max_ready = sig["at_max_ready"].take(4 * B)
        self.p_ready = sig["at_p_ready"].take(4 * B)
        self.pt_done = sig["at_pt_done"].take(4 * B)
        self.ptv_ready = sig["at_ptv_ready"].take(2 * B)
        self.pta_ready = sig["at_pta_ready"].take(2 * B)
        self.av_done = sig["wc_av_done"].take(4 * B)
        self.o_ready = sig["wc_o_ready"].take(4 * B)
        self.oT_done = sig["wc_oT_done"].take(2 * B)
        self.oT_ready = sig["wc_oT_ready"].take(2 * B)
        self.y_done = sig["at_y_done"].take(B)
        self.y_ready = sig["at_res_done"].take(B)

    def sync(self, sp, null_v):
        k = self.k
        sp.wait_ge(*self.clear.upto(1))
        for p in range(2):
            dst = k.wv[p][M:M + 1, :].rearrange("o (h w) -> o h w", h=self.H)[:, :, 0:self.DH]
            sp.dma_start(dst, bcast(null_v, 1, self.H)).then_inc(k.loads["null_v"], 16)

    def pool(self, pool):
        k = self.k
        pool.wait_ge(*self.turn.xT_ready.upto(2))
        k.arrived(pool, "null_k")
        for p in range(2):
            pool.tensor_copy(k.kT[p][:, :, M], k.null_k[:, 0:1].to_broadcast([P, 8]))
            t = pool.memset(k.wv[p], 1.0)
        t.then_inc(self.clear.sem, 1)
        with pool.Fori(0, B // 2) as i:
            for p in range(2):
                pool.wait_ge(*self.v_done.upto(2 * i))
                for c in range(2):
                    t = pool.tensor_copy(k.cT[p][:, c, :], k.ctxT[:, c, bass.ts(2 * i + p, M)])
                t.then_inc(self.cT_ready.sem, 1)

    def tensor(self, pe):
        k = self.k
        pe.wait_ge(*self.turn.xT_ready.upto(2))
        pe.wait_ge(*self.clear.upto(1))
        k.arrived(pe, "wide_cross")
        k.arrived(pe, "null_v")
        with pe.Fori(0, B // 2) as i:
            for p in range(2):
                self.project(pe, i, p)
            for u in range(4):
                self.scores(pe, i, 0, u)
            self.values(pe, i, 0)
            self.scores(pe, i, 1, 0)
            self.turn_out(pe, i, 0, 0)
            self.scores(pe, i, 1, 1)
            self.scores(pe, i, 1, 2)
            self.turn_out(pe, i, 0, 1)
            self.scores(pe, i, 1, 3)
            self.values(pe, i, 1)
            self.turn_out(pe, i, 1, 0)
            self.turn_out(pe, i, 1, 1)
            self.out(pe, i, 1)

    def project(self, pe, i, p):
        k = self.k
        b = 2 * i + p
        pe.wait_ge(*self.p_ready.upto(8 * i))
        pe.wait_ge(*self.q_ready.upto(b))
        for c in range(8):
            m = pe.matmul(k.ps[:, c // 4, c % 4 * P:(c % 4 + 1) * P], k.wq[:, c * P:(c + 1) * P],
                          k.xnT[:, bass.ts(b, P)], start=True, stop=True)
        m.then_inc(self.q_done.sem, 1)
        pe.wait_ge(*self.cT_ready.upto(b + 1))
        pe.wait_ge(*self.k_ready.upto(b))
        for c in range(8):
            for e in range(2):
                m = pe.matmul(k.ps[:, 2 + c // 4, c % 4 * P:c % 4 * P + M], k.wkv[:, e, c * P:(c + 1) * P],
                              k.cT[p][:, e, :], start=e == 0, stop=e == 1)
        m.then_inc(self.k_done.sem, 1)
        pe.wait_ge(*self.v_ready.upto(b))
        pe.wait_ge(*self.pta_ready.upto(4 * i))
        pe.wait_ge(*self.ptv_ready.upto(4 * i))
        for h in range(2):
            for e in range(2):
                m = pe.matmul(k.ps[0:M, 4 + h, :], k.cT[p][:, e, :], k.wkv[:, e, 1024 + h * HALF:1024 + (h + 1) * HALF],
                              start=e == 0, stop=e == 1)
        m.then_inc(self.v_done.sem, 1)

    def scores(self, pe, i, p, u):
        k = self.k
        b = 2 * i + p
        if u == 0:
            pe.wait_ge(*self.q_ready.upto(2 * i + 2))
            pe.wait_ge(*self.k_ready.upto(2 * i + 2))
            pe.wait_ge(*self.v_ready.upto(2 * i + 2))
        if p:
            pe.wait_ge(*self.p_ready.upto(8 * i + u + 1))
        r = slice(64 * (u % 2), 64 * (u % 2) + 64)
        for j in range(4):
            c = 4 * (u // 2) + j
            m = pe.matmul(k.ps[:, u, j * P:j * P + self.T], k.qT[p][r, c, :], k.kT[p][r, c, :], start=True, stop=True)
        m.then_inc(self.s_done.sem, 1)

    def values(self, pe, i, p):
        k = self.k
        b = 2 * i + p

        def turn(u):
            pe.wait_ge(*self.p_ready.upto(4 * b + u + 1))
            ready = self.pta_ready if u % 2 else self.ptv_ready
            pe.wait_ge(*ready.upto(2 * b + u // 2))
            for j in range(4):
                t = pe.transpose(k.ps[0:self.T, PT0 + u % 2, j * P:(j + 1) * P], k.p[p][:, 4 * u + j, 0:self.T], k.ident)
            t.then_inc(self.pt_done.sem, 1)

        def times_v(u):
            ready = self.pta_ready if u % 2 else self.ptv_ready
            pe.wait_ge(*ready.upto(2 * b + u // 2 + 1))
            pe.wait_ge(*self.o_ready.upto(4 * b + u))
            w = self.DH + 1
            for j in range(4):
                h = 2 * (4 * (u // 2) + j) + u % 2
                m = pe.matmul(k.ps[:, OB, j * w:(j + 1) * w], k.pT[u % 2][0:self.T, j, :],
                              k.wv[p][0:self.T, h * w:(h + 1) * w], start=True, stop=True)
            m.then_inc(self.av_done.sem, 1)

        turn(0)
        turn(1)
        if p:
            self.out(pe, i, 0)
        times_v(0)
        turn(2)
        times_v(1)
        turn(3)
        times_v(2)
        times_v(3)

    def turn_out(self, pe, i, p, half):
        k = self.k
        b = 2 * i + p
        pe.wait_ge(*self.o_ready.upto(4 * b + 2 * half + 2))
        pe.wait_ge(*self.oT_ready.upto(2 * b + half))
        for j in range(4):
            t = pe.transpose(k.ps[:, MB, j * P:(j + 1) * P], k.wo_in[:, (4 * half + j) * P:(4 * half + j + 1) * P], k.ident)
        t.then_inc(self.oT_done.sem, 1)

    def out(self, pe, i, p):
        k = self.k
        b = 2 * i + p
        pe.wait_ge(*self.oT_ready.upto(2 * b + 2))
        pe.wait_ge(*self.y_ready.upto(b))
        pe.wait_ge(*self.o_ready.upto(4 * b + 4))
        for c in range(8):
            m = pe.matmul(k.ps[:, OB, 3 * P:4 * P], k.woT[:, c, :], k.wout[:, c, :], start=c == 0, stop=c == 7)
        m.then_inc(self.y_done.sem, 1)

    def vector(self, dve):
        k, c = self.k, self.k.dchain
        with dve.Fori(0, B // 2) as i:
            c.enter(i, 2 * (1 + 4 + 4))
            for p in range(2):
                b = 2 * i + p
                dve.wait_ge(*self.q_done.upto(b + 1))
                dve.wait_ge(*self.s_done.upto(8 * i))
                f = k.qT[p][:, :, :].rearrange("p c t -> p (c t)")
                c.step(dve.tensor_copy(f[:, 0:HALF], k.ps[:, 0, :]))
                dve.tensor_copy(f[:, HALF:], k.ps[:, 1, :]).then_inc(self.q_ready.sem, 1)
            for p in range(2):
                b = 2 * i + p
                for u in range(4):
                    dve.wait_ge(*self.s_done.upto(4 * b + u + 1))
                    hs = slice(4 * u, 4 * u + 4)
                    src = k.ps[:, u, :].rearrange("q (h t) -> q h t", t=P)[:, :, 0:self.T]
                    c.link(dve.tensor_reduce(k.mx[p][:, hs], src, AX.X, ALU.max))
                    dve.tensor_scalar(k.nmx[p][:, hs], k.mx[p][:, hs], -0.125, None, ALU.mult)\
                        .then_inc(self.max_ready.sem, 1)
                if p:
                    self.collect(dve, 2 * i)
                self.turned(dve, b, 0)
                self.outputs(dve, b, 0)
                self.turned(dve, b, 2)
                for u in range(1, 4):
                    self.outputs(dve, b, u)
                if p:
                    self.collect(dve, b)
        c.leave(B // 2)
        dve.wait_ge(*self.y_ready.upto(B))
        token_stats(k, dve, k.r, range(B))

    def turned(self, dve, b, u):
        k = self.k
        dve.wait_ge(*self.pt_done.upto(4 * b + u + 1))
        dve.wait_ge(*self.av_done.upto(4 * b + max(u - 1, 0)))
        dve.tensor_copy(k.pT[0][0:self.T, :, :].rearrange("t h q -> t (h q)"), k.ps[0:self.T, PT0, :])\
            .then_inc(self.ptv_ready.sem, 1)

    def outputs(self, dve, b, u):
        k, c = self.k, self.k.dchain
        w = self.DH + 1
        dve.wait_ge(*self.av_done.upto(4 * b + u + 1))
        dve.wait_ge(*self.oT_done.upto(2 * b))
        O = k.ps[:, OB, 0:4 * w].rearrange("q (h w) -> q h w", w=w)
        c.link(dve.reciprocal(k.rec[:, 0:4], O[:, :, self.DH]))
        dst = k.wo_in[:, :].rearrange("q (c r d) -> q c r d", r=2, d=self.DH)[:, 4 * (u // 2):4 * (u // 2) + 4, u % 2, :]
        dve.tensor_tensor(dst, O[:, :, 0:self.DH], bcast(k.rec[:, 0:4], 2, self.DH), ALU.mult)\
            .then_inc(self.o_ready.sem, 1)
        dve.wait_ge(*self.o_ready.upto(4 * b + u + 1))

    def collect(self, dve, b):
        k = self.k
        dve.wait_ge(*self.y_done.upto(b + 1))
        dve.tensor_copy(k.r[:, b, :], k.ps[:, OB, 3 * P:4 * P]).then_inc(self.y_ready.sem, 1)

    def scalar(self, act):
        k = self.k
        w = self.DH + 1
        act.wait_ge(*self.clear.upto(1))
        with act.Fori(0, B // 2) as i:
            for p in range(2):
                b = 2 * i + p
                act.wait_ge(*self.k_done.upto(b + 1))
                act.wait_ge(*self.s_done.upto(8 * i))
                for h in range(2):
                    e = act.activation(k.kT[p][:, 4 * h:4 * h + 4, 0:M],
                                       k.ps[:, 2 + h, :].rearrange("p (c t) -> p c t", t=P)[:, :, 0:M], ACT.Copy)
                e.then_inc(self.k_ready.sem, 1)
                act.wait_ge(*self.v_done.upto(b + 1))
                act.wait_ge(*self.av_done.upto(8 * i))
                for h in range(2):
                    e = act.activation(k.wv[p][0:M, 8 * h * w:8 * (h + 1) * w].rearrange("t (h w) -> t h w", w=w)[:, :, 0:self.DH],
                                       k.ps[0:M, 4 + h, :].rearrange("t (h d) -> t h d", d=self.DH), ACT.Copy)
                e.then_inc(self.v_ready.sem, 1)
            for p in range(2):
                b = 2 * i + p
                for u in range(4):
                    act.wait_ge(*self.max_ready.upto(4 * b + u + 1))
                    act.wait_ge(*self.pt_done.upto(8 * i))
                    for j in range(4):
                        h = 4 * u + j
                        e = act.activation(k.p[p][:, h, 0:self.T], k.ps[:, u, j * P:j * P + self.T], ACT.Exp,
                                           bias=k.nmx[p][:, h:h + 1], scale=0.125)
                    e.then_inc(self.p_ready.sem, 1)
                    if p and u == 0:
                        self.turned_out(act, 2 * i, 0)
                    if p and u == 2:
                        self.turned_out(act, 2 * i, 1)
                for u in (1, 3):
                    act.wait_ge(*self.pt_done.upto(4 * b + u + 1))
                    act.wait_ge(*self.av_done.upto(4 * b + u - 1))
                    act.activation(k.pT[1][0:self.T, :, :].rearrange("t h q -> t (h q)"), k.ps[0:self.T, PT0 + 1, :],
                                   ACT.Copy).then_inc(self.pta_ready.sem, 1)
                if p:
                    self.turned_out(act, b, 0)
                    self.turned_out(act, b, 1)

    def turned_out(self, act, b, half):
        k = self.k
        act.wait_ge(*self.oT_done.upto(2 * b + half + 1))
        act.wait_ge(*self.y_done.upto(b))
        act.activation(k.woT[:, 4 * half:4 * half + 4, :].rearrange("p c t -> p (c t)"), k.ps[:, MB, :], ACT.Copy)\
            .then_inc(self.oT_ready.sem, 1)


ROWS = [("relu_b1", 32), ("gelu_b1", 32), ("gate_b1", 32), ("dense_b1", 4), ("g_res0", 1), ("g_res3", 1),
        ("gamma", 1), ("beta", 1), ("conv_b", 2), ("b_dt", 2), ("ssm_d", 2), ("ln1_g", 1), ("ln1_b", 1)]
COL = {name: sum(n for _, n in ROWS[:j]) for j, (name, _) in enumerate(ROWS)}
NROWS = sum(n for _, n in ROWS)
WIDE = ["ln1_g", "ln1_b", "ln2_g", "ln2_b", "dense_b2", "b_in0", "b_in3", "g_init0", "g_init3", "ln_scale", "ln_bias"]
LOADS = {"x": 1, "first": 1, "l0": 6, "lens": 1, "rows": len(ROWS), "routers": 3, "gates": 2, "pool_consts": 1,
         "lower": 1, "masks": 1, "ctx": 1, "keys": 2, "wide": len(WIDE) + 4, "b2": 24, "bit": 11, "l3": 2, "mamba": 6, "null_k": 2,
         "wide_cross": 3, "null_v": 2}


def constants():
    f = np.float32
    theta = (f(1.0) / f(10000.0) ** (np.arange(0, 8, 2, dtype=f) / f(8))).astype(f)
    angle = np.outer(np.arange(S, dtype=f), theta).astype(f)
    angle = np.tile(np.concatenate([angle, angle], axis=1), (1, 16)).T
    group = np.arange(P) % 32
    decay = -np.expm1(-DEPOOL_EPS)
    lag = np.arange(M)[None, :] - np.arange(M)[:, None]
    filt = np.zeros((P, P))
    filt[:M, :M] = np.where(lag >= 0, np.exp(-DEPOOL_EPS) * decay ** np.maximum(lag, 0), 0.0)
    lower = np.broadcast_to((np.arange(8)[None, :] < np.arange(8)[:, None]).reshape(1, 64), (P, 64))
    early = np.concatenate([np.eye(P), np.cos(angle), np.sin(angle), group[:, None] // 8 == np.arange(4),
                            group[:, None] // 16 == np.arange(2)], axis=1)
    late = np.concatenate([np.arange(P)[:, None] <= np.arange(P), np.broadcast_to(np.arange(P), (P, P)), filt, lower], axis=1)
    off = np.arange(S)[:, None] - np.arange(S)[None, :]
    causal = np.where(off >= 0, 0.0, NEG)
    band = np.where(np.abs(off) <= 32, 0.0, NEG)
    select = np.zeros((P, 32, P))
    for part in range(3):
        select[32 * part + np.arange(32), np.arange(32)] = 1.0
    half = np.concatenate([np.eye(P), causal, band, select.reshape(P, 32 * P)], axis=1)
    return early.astype(f), late.astype(f), (half.astype(f).view(np.uint32) >> 16).astype(np.uint16)


class Setup:

    def __init__(self, k):
        self.k = k
        t = lambda name, n: k.sig["su_" + name].take(n)
        self.w_turned = t("w_turned", 2)
        self.w_ready = t("w_ready", 2)
        self.flipped = t("flipped", 1)
        self.small_turned = t("small_turned", 2)
        self.small_ready = t("small_ready", 2)
        self.idx_ready = t("idx_ready", 1)
        self.idx_turned = t("idx_turned", 1)
        self.idxT_ready = t("idxT_ready", 1)
        self.edges_ready = t("edges_ready", 1)
        self.count_done = t("count_done", 1)
        self.edge_ready = t("edge_ready", 1)
        self.plug_done = t("plug_done", 1)
        self.plug_ready = t("plug_ready", 1)
        self.pick_ready = t("pick_ready", 1)
        self.pick_turned = t("pick_turned", 2)
        self.pickT_ready = t("pickT_ready", 2)
        self.ctx_turned = t("ctx_turned", 4)
        self.ctxT_ready = t("ctxT_ready", 4)
        self.ms_ready = t("ms_ready", 1)
        self.ctxn_ready = t("ctxn_ready", 1)
        self.spread_done = t("spread_done", 2)
        self.spread_ready = t("spread_ready", 2)
        self.pooled_done = t("pooled_done", 2)
        self.pooled_in = t("pooled_in", 2)
        self.keyrow = t("keyrow", 1)

    def tensor_first(self, pe):
        k = self.k
        k.arrived(pe, "first")
        k.arrived(pe, "l0")
        for j in range(6):
            t = pe.transpose(k.ps[:, PT0 + j // 4, j % 4 * P:(j % 4 + 1) * P], k.w_raw[:, j, :], k.ident)
            if j in (3, 5):
                t.then_inc(self.w_turned.sem, 1)
        k.arrived(pe, "rows")
        pe.transpose(k.ps[:, 0, 0:NROWS], k.rows[0:NROWS, :], k.ident[0:NROWS, 0:NROWS]).then_inc(self.small_turned.sem, 1)
        k.arrived(pe, "routers")
        pe.transpose(k.ps[:, 6, 0:20], k.router_rows[0:20, :], k.ident[0:20, 0:20]).then_inc(self.small_turned.sem, 1)
        pe.wait_ge(*self.idx_ready.upto(1))
        pe.transpose(k.ps[0:M, 1, 0:B], k.idx[0:B, :], k.ident[0:B, 0:B]).then_inc(self.idx_turned.sem, 1)
        pe.wait_ge(*self.edges_ready.upto(1))
        for b in range(B):
            m = pe.matmul(k.ps[:, 2, 2 * b:2 * b + 1], k.edges[0:M, b, :], k.ones[0:M, 0:1], start=True, stop=True)
        m.then_inc(self.count_done.sem, 1)
        k.arrived(pe, "pool_consts")
        pe.wait_ge(*self.edge_ready.upto(1))
        pe.matmul(k.ps[:, 3, 0:B], k.upto_here, k.edge[:, :], start=True, stop=True).then_inc(self.plug_done.sem, 1)
        pe.wait_ge(*self.w_ready.upto(2))
        pe.wait_ge(*self.small_ready.upto(2))
        pe.wait_ge(*self.plug_ready.upto(1))
        pe.wait_ge(*self.flipped.upto(1))

    def scalar_first(self, act):
        k = self.k
        for j in range(2):
            act.wait_ge(*self.w_turned.upto(j + 1))
            n = 4 - 2 * j
            act.activation(k.wT[:, 4 * j:4 * j + n, :].rearrange("p j e -> p (j e)"), k.ps[:, PT0 + j, 0:n * P],
                           ACT.Copy).then_inc(self.w_ready.sem, 1)
        act.wait_ge(*self.small_turned.upto(1))
        act.activation(k.cols[:, :], k.ps[:, 0, 0:NROWS], ACT.Copy).then_inc(self.small_ready.sem, 1)
        act.wait_ge(*self.small_turned.upto(2))
        act.activation(k.routerT[:, :], k.ps[:, 6, 0:20], ACT.Copy).then_inc(self.small_ready.sem, 1)
        act.wait_ge(*self.idx_turned.upto(1))
        act.activation(k.idxT[0:M, :], k.ps[0:M, 1, 0:B], ACT.Copy).then_inc(self.idxT_ready.sem, 1)

    def vector_first(self, dve):
        k, c = self.k, self.k.dchain
        k.arrived(dve, "lens")
        c.link(dve.tensor_copy(k.lens[:, :], k.lens_i[:, :]))
        c.link(dve.tensor_tensor_scan(k.cum[:, :], k.ones[0:B, 0:M], k.lens[:, :], 0.0, ALU.mult, ALU.add))
        c.link(dve.tensor_scalar(k.cum[:, :], k.cum[:, :], -1.0, None, ALU.add))
        c.link(dve.tensor_scalar(k.lens[:, :], k.cum[:, :], 0.0, float(S), ALU.is_lt, ALU.mult))
        dve.tensor_tensor(k.idx[:, :], k.cum[:, :], k.lens[:, :], ALU.add).then_inc(self.idx_ready.sem, 1)
        dve.wait_ge(*self.w_ready.upto(1))
        for j in range(2):
            src = k.wT[:, j, :].rearrange("p (h j) -> p h j", j=8)
            dst = k.w_flip[:, j, :].rearrange("p (h j) -> p h j", j=8)
            c.step(dve.tensor_scalar(dst[:, :, 0:4], src[:, :, 4:8], -1.0, None, ALU.mult))
            t = dve.tensor_copy(dst[:, :, 4:8], src[:, :, 0:4])
            c.step(t) if j == 0 else t.then_inc(self.flipped.sem, 1)
        dve.wait_ge(*self.count_done.upto(1))
        dve.tensor_scalar(k.edge[:, :], k.ps[:, 2, 0:2 * B].rearrange("p (b o) -> p b o", o=2)[:, :, 0], 1.0, None, ALU.min)\
            .then_inc(self.edge_ready.sem, 1)
        dve.wait_ge(*self.plug_done.upto(1))
        c.link(dve.tensor_scalar(k.plug[:, :], k.ps[:, 3, 0:B], -1.0, 0.0, ALU.add, ALU.max))
        dve.tensor_scalar(k.plug[:, :], k.plug[:, :], float(M - 1), None, ALU.min).then_inc(self.plug_ready.sem, 1)
        k.arrived(dve, "ctx")
        for b in range(B):
            c.step(dve.bn_stats(k.bn[0:M, b, :], k.ctx[0:M, b * CTX:(b + 1) * CTX]))
        c.settle()
        for b in range(B):
            c.step(dve.bn_aggr(k.ctx_mv[0:M, b, :], k.bn[0:M, b, :]))
        c.settle()
        c.link(dve.tensor_tensor(k.ctx_ms[0:M, :], k.ctx_mv[0:M, :, 0], k.ctx_mv[0:M, :, 0], ALU.mult))
        dve.scalar_tensor_tensor(k.ctx_ms[0:M, :], k.ctx_ms[0:M, :], LN_EPS, k.ctx_mv[0:M, :, 1], ALU.add, ALU.add)\
            .then_inc(self.ms_ready.sem, 1)
        k.arrived(dve, "keys")
        c.link(dve.tensor_copy(k.key_row[0:1, :], k.key_mask[:, :]))
        c.link(dve.tensor_scalar(k.key_row[0:1, :], k.key_row[0:1, :], -1.0, -NEG, ALU.add, ALU.mult))
        dve.tensor_scalar(k.key_row[0:1, :], k.key_row[0:1, :], k.key_b[0:1, 0:1], None, ALU.add)\
            .then_inc(self.keyrow.sem, 1)

    def pool_first(self, pool):
        k, c = self.k, self.k.pchain
        k.arrived(pool, "pool_consts")
        pool.wait_ge(*self.idxT_ready.upto(1))
        for b in range(B):
            t = pool.tensor_scalar(k.edges[0:M, b, :], k.iota[0:M, :], k.idxT[0:M, b:b + 1], None, ALU.is_equal)
        t.then_inc(self.edges_ready.sem, 1)
        pool.wait_ge(*self.plug_ready.upto(1))
        for b in range(B):
            t = pool.tensor_scalar(k.pick[:, b, :], k.iota[:, 0:M], k.plug[:, b:b + 1], None, ALU.is_equal)
        t.then_inc(self.pick_ready.sem, 1)
        pool.wait_ge(*self.ms_ready.upto(1))
        c.link(pool.tensor_tensor(k.ctx_ms[0:M, :], k.ctx_ms[0:M, :], bcast(k.minus_half[0:M, 0], 1, B), ALU.pow))
        t = pool.tensor_tensor(k.ctx_n[0:M, :, :], k.ctx[0:M, :].rearrange("p (b c) -> p b c", c=CTX)[:, :, 0:D],
                               bcast(k.ctx_ms[0:M, :], 2, D), ALU.mult)
        t.then_inc(self.ctxn_ready.sem, 1)

    def tensor_second(self, pe):
        k = self.k
        k.arrived(pe, "ctx")
        for b in range(B):
            for c in range(2):
                j = 2 * b + c
                if j >= 8 and j % 4 == 0:
                    pe.wait_ge(*self.ctxT_ready.upto(j // 4 - 1))
                t = pe.transpose(k.ps[:, j // 4 % 2, j % 4 * P:j % 4 * P + M],
                                 k.ctx[0:M, b * CTX + c * P:b * CTX + (c + 1) * P], k.ident[0:M, 0:M])
                if j % 4 == 3:
                    t.then_inc(self.ctx_turned.sem, 1)
        pe.wait_ge(*self.pick_ready.upto(1))
        for b in range(B):
            t = pe.transpose(k.ps[0:M, 2 + b // 4, b % 4 * P:(b % 4 + 1) * P], k.pick[:, b, :], k.ident)
            if b % 4 == 3:
                t.then_inc(self.pick_turned.sem, 1)
        pe.wait_ge(*self.ctxn_ready.upto(1))
        for h in range(2):
            pe.matmul(k.ps[0:M, PT0 + h, :], k.filter[0:M, 0:M],
                      k.ctx_n[0:M, 4 * h:4 * h + 4, :].rearrange("p b d -> p (b d)"), start=True, stop=True)\
                .then_inc(self.spread_done.sem, 1)
        for b in range(B):
            pe.wait_ge(*self.pickT_ready.upto(b // 4 + 1))
            pe.wait_ge(*self.spread_ready.upto(b // 4 + 1))
            m = pe.matmul(k.ps[:, 6 + b // 4, b % 4 * P:(b % 4 + 1) * P], k.pickT[0:M, b * P:(b + 1) * P],
                          k.patches[0:M, b * D:(b + 1) * D], start=True, stop=True)
            if b % 4 == 3:
                m.then_inc(self.pooled_done.sem, 1)

    def scalar_second(self, act):
        k = self.k
        for j in range(4):
            act.wait_ge(*self.ctx_turned.upto(j + 1))
            src = k.ps[:, j % 2, :].rearrange("p (b c t) -> p c b t", b=2, c=2)[:, :, :, 0:M]
            dst = k.ctxT[:, :, 2 * j * M:2 * (j + 1) * M].rearrange("p c (b t) -> p c b t", t=M)
            for c in range(2):
                t = act.activation(dst[:, c], src[:, c], ACT.Copy)
            t.then_inc(self.ctxT_ready.sem, 1)
        for h in range(2):
            act.wait_ge(*self.pick_turned.upto(h + 1))
            act.activation(k.pickT[0:M, h * HALF:(h + 1) * HALF], k.ps[0:M, 2 + h, :], ACT.Copy)\
                .then_inc(self.pickT_ready.sem, 1)
        for h in range(2):
            act.wait_ge(*self.spread_done.upto(h + 1))
            act.activation(k.patches[0:M, h * HALF:(h + 1) * HALF], k.ps[0:M, PT0 + h, :], ACT.Copy)\
                .then_inc(self.spread_ready.sem, 1)
        for h in range(2):
            act.wait_ge(*self.pooled_done.upto(h + 1))
            act.activation(k.pooled_raw[:, 4 * h:4 * h + 4, :].rearrange("p b d -> p (b d)"), k.ps[:, 6 + h, :], ACT.Copy)\
                .then_inc(self.pooled_in.sem, 1)

    def pool_second(self, pool):
        k, c = self.k, self.k.pchain
        k.arrived(pool, "wide")
        pool.wait_ge(*self.pooled_in.upto(2))
        c.link(pool.tensor_tensor(k.pooled0[:, :, :], k.pooled_raw[:, :, :], bcast(k.wide["g_init0"], 1, B), ALU.mult))
        pool.tensor_tensor(k.pooled0[:, :, :], k.pooled0[:, :, :], bcast(k.wide["b_in0"], 1, B), ALU.add)\
            .then_inc(k.pooled_ready.sem, 1)

    def pool_third(self, pool):
        k, c = self.k, self.k.pchain
        c.link(pool.tensor_tensor(k.pooled3[:, :, :], k.pooled_raw[:, :, :], bcast(k.wide["g_init3"], 1, B), ALU.mult))
        pool.tensor_tensor(k.pooled3[:, :, :], k.pooled3[:, :, :], bcast(k.wide["b_in3"], 1, B), ALU.add)\
            .then_inc(k.pooled_ready.sem, 1)


class BitWeights:

    def __init__(self, k):
        self.k = k
        t = lambda name, n: k.sig["bw_" + name].take(n)
        self.scale_ready = t("scale_ready", 1)
        self.rounded = t("rounded", 1)
        self.turned = t("turned", 9)
        self.in_sbuf = t("in_sbuf", 9)

    def vector(self, dve):
        k, c = self.k, self.k.dchain
        k.arrived(dve, "bit")
        for j, (raw, n, width) in enumerate(((k.bit_raw1, 18, P), (k.bit_raw2, 9, 2 * P))):
            sc = k.bit_scale[:, 18 * j:18 * j + n]
            c.link(dve.tensor_reduce(sc, raw[:, :, :], AX.X, ALU.add, apply_absolute_value=True))
            c.link(dve.tensor_scalar(sc, sc, 1.0 / width, 1e-5, ALU.mult, ALU.max))
        c.step(dve.tensor_scalar(k.bit_half[:, :], k.bit_scale[:, :], 0.5, None, ALU.mult))
        dve.tensor_scalar(k.bit_mhalf[:, :], k.bit_scale[:, :], -0.5, None, ALU.mult).then_inc(self.scale_ready.sem, 1)

    def pool(self, pool):
        k, c = self.k, self.k.pchain
        pool.wait_ge(*self.scale_ready.upto(1))
        for j, (raw, n, width) in enumerate(((k.bit_raw1, 18, P), (k.bit_raw2, 9, 2 * P))):
            for t in range(n):
                q = slice(18 * j + t, 18 * j + t + 1)
                c.step(pool.tensor_scalar(k.bit_up[:, 0:width], raw[:, t, :], k.bit_half[:, q], k.bit_scale[:, q],
                                          ALU.is_gt, ALU.mult))
                c.link(pool.tensor_scalar(k.bit_down[:, 0:width], raw[:, t, :], k.bit_mhalf[:, q], k.bit_scale[:, q],
                                          ALU.is_lt, ALU.mult))
                last = pool.tensor_tensor(raw[:, t, :], k.bit_up[:, 0:width], k.bit_down[:, 0:width], ALU.subtract)
                if j == 1 and t == n - 1:
                    last.then_inc(self.rounded.sem, 1)
                else:
                    c.link(last)

    def tensor(self, pe):
        k = self.k
        pe.wait_ge(*self.rounded.upto(1))
        for e in range(9):
            if e >= 2:
                pe.wait_ge(*self.in_sbuf.upto(e - 1))
            for c in range(2):
                pe.transpose(k.ps[:, e % 2, c * P:(c + 1) * P], k.bit_raw1[:, 2 * e + c, :], k.ident)
            for c in range(2):
                t = pe.transpose(k.ps[:, e % 2, (2 + c) * P:(3 + c) * P], k.bit_raw2[:, e, c * P:(c + 1) * P], k.ident)
            t.then_inc(self.turned.sem, 1)

    def scalar(self, act):
        k = self.k
        for e in range(9):
            act.wait_ge(*self.turned.upto(e + 1))
            act.activation(k.bit_w1T[:, e * 256:(e + 1) * 256], k.ps[:, e % 2, 0:256], ACT.Copy)
            act.activation(k.bit_w2T[:, e * 256:(e + 1) * 256], k.ps[:, e % 2, 256:512], ACT.Copy)\
                .then_inc(self.in_sbuf.sem, 1)


class Arena:

    def __init__(self, tensor):
        self.tensor, self.at, self.most = tensor, 0, 0

    def take(self, *shape, dtype=F32):
        n = int(np.prod(shape))
        words = n if dtype == F32 else (n + 1) // 2
        v = self.tensor[:, self.at:self.at + words]
        if dtype == BF16:
            v = v.bitcast(BF16)
        self.at += (words + 7) // 8 * 8
        self.most = max(self.most, self.at)
        assert self.at <= self.tensor.shape[1], (self.at, self.tensor.shape)
        if len(shape) == 2:
            v = v.rearrange("p (a b) -> p a b", a=shape[0])
        elif len(shape) == 3:
            v = v.rearrange("p (a b c) -> p a b c", a=shape[0], b=shape[1])
        return v

    def rewind(self, at):
        self.at = at


class Kit:

    def arrived(self, eng, group):
        eng.wait_ge(self.loads[group], 16 * LOADS[group])


SIGNALS = """result at_v_clear wc_clear var_ready rstd_ready xn_ready x_turned xnT_ready
at_xT_ready at_kv_ready at_v_ready at_s_done at_max_ready at_p_ready at_pt_done at_ptv_ready at_pta_ready
at_av_even at_av_odd at_o_ready at_qkv_done at_oT_done at_oT_ready at_y_done at_res_done
ff_h_done ff_h_ready ff_o_done ff_acc_done ff_router_done ff_w_ready ff_w_turned ff_wT_ready ff_b2_done
ff_l_ready ff_e_ready dp_pooled_in dp_y_done an_bias_in dense_start
mb_in_done mb_u_in mb_gate_ready mb_conv_done mb_u_ready mb_dl_done mb_dl_ready mb_bc_done mb_bc_ready mb_dt_done
mb_z_ready mb_lg_ready mb_du_ready mb_a_exp mb_started mb_pad_ready mb_b_done mb_c_done mb_c_ready mb_dA_ready0 mb_dA_ready1
mb_dbu_done mb_scanned0 mb_scanned1 mb_sc_ready0 mb_sc_ready1 mb_y_done0 mb_y_done1 mb_yg_ready mb_out_done
wc_q_done wc_k_done wc_k_ready wc_av_done wc_o_ready wc_oT_done wc_oT_ready
su_w_turned su_w_ready su_flipped su_small_turned su_small_ready su_idx_ready su_idx_turned su_idxT_ready
su_edges_ready su_count_done su_edge_ready su_plug_done su_plug_ready su_pick_ready su_pick_turned su_pickT_ready
su_ctx_turned su_ctxT_ready su_ms_ready su_ctxn_ready su_spread_done su_spread_ready su_pooled_done su_pooled_in
su_keyrow su_pooled_ready bw_scale_ready bw_rounded bw_turned bw_in_sbuf""".split()


CREDITS = {
    "tensor": {"ff_o_done": 2, "at_s_done": 1, "at_pt_done": 1, "at_av_even": 1, "at_av_odd": 1, "at_qkv_done": 1,
               "at_oT_done": 1, "at_y_done": 1, "mb_y_done0": 1, "mb_y_done1": 1, "wc_av_done": 1, "wc_oT_done": 1},
    "scalar": {"ff_h_ready": 4, "at_v_ready": 1, "at_p_ready": 1, "at_pta_ready": 1, "at_oT_ready": 1, "mb_c_ready": 1,
               "wc_k_ready": 1, "wc_oT_ready": 1},
    "vector": {"ff_acc_done": 1, "at_kv_ready": 1, "at_ptv_ready": 1, "at_o_ready": 1, "at_res_done": 1,
               "mb_dbu_done": 1, "mb_scanned0": 1, "mb_scanned1": 1, "wc_o_ready": 1},
    "pool": {"mb_sc_ready0": 1, "mb_sc_ready1": 1},
}
KEEP_WORDS, WORK_WORDS = 38300, 14880
PRESETS = 6


def decoder(nc, a, out):
    ctx = ExitStack()
    with ctx:
        k = Kit()
        k.sig = {n: Signal(ctx.enter_context(nc.semaphore(n))) for n in SIGNALS}
        k.loads = {n: ctx.enter_context(nc.semaphore("ld_" + n)) for n in LOADS}
        k.ring_loaded = [Signal(ctx.enter_context(nc.semaphore(f"ring_loaded{p}"))) for p in range(2)]
        k.ring_copied = [Signal(ctx.enter_context(nc.semaphore(f"ring_copied{p}"))) for p in range(2)]
        preset = ctx.enter_context(nc.semaphore("preset"))
        stored = ctx.enter_context(nc.semaphore("stored"))
        chains = [ctx.enter_context(nc.semaphore(n)) for n in ("vector_chain", "scalar_chain", "pool_chain")]
        for credits in CREDITS.values():
            for name, n in credits.items():
                k.sig[name].take(n)
        k.pooled_ready = k.sig["su_pooled_ready"].take(2)

        keep = Arena(ctx.enter_context(nc.sbuf_tensor("keep", [P, KEEP_WORDS], F32)))
        work = Arena(ctx.enter_context(nc.sbuf_tensor("work", [P, WORK_WORDS], F32)))
        k.ps = ctx.enter_context(nc.psum_tensor("banks", [P, 8, HALF], F32))
        early = keep.take(3 * P + 6)
        k.ident, k.cosT, k.sinT = (early[:, j * P:(j + 1) * P] for j in range(3))
        k.head_of4, k.head_of2 = early[:, 3 * P:3 * P + 4], early[:, 3 * P + 4:3 * P + 6]
        lower = keep.take(64)
        k.lower = lower.rearrange("p (a b) -> p a b", a=8)
        halves = keep.take(35 * P, dtype=BF16)
        k.ident16, k.causal, k.band = (halves[:, j * P:(j + 1) * P] for j in range(3))
        k.sel = halves[0:96, 3 * P:35 * P]
        k.x, k.xn, k.r = (keep.take(B, D) for _ in range(3))
        k.xnT = keep.take(TOK)
        k.mv, k.bn = keep.take(B, 2), keep.take(B, 6)
        k.var_eps, k.rstd, k.root1, k.root2, k.ms = (keep.take(B) for _ in range(5))
        k.minus_half, k.ones = keep.take(1), keep.take(P)
        k.one_col = k.ones[:, 0:1]
        k.cols, k.rows, k.col = keep.take(NROWS), keep.take(P), COL
        k.router_rows, k.routerT = keep.take(P), keep.take(20)
        gates = keep.take(2, 8)
        k.router = {"relu": gates[:, 0, :], "gate": gates[:, 1, :], "gelu": k.routerT[:, 0:12], "bit": k.routerT[:, 12:20]}
        wide = keep.take(len(WIDE), D)
        k.wide = {n: wide[:, j, :] for j, n in enumerate(WIDE)}
        k.ln1_g, k.ln1_b, k.dense_b2 = k.wide["ln1_g"], k.wide["ln1_b"], k.wide["dense_b2"]
        bias = keep.take(36)
        k.router_b = {"relu": bias[:, 0:8], "gelu": bias[:, 8:16], "gate": bias[:, 16:24], "bit": bias[:, 28:36]}
        k.lang_b = bias[:, 24:28]
        k.wT, k.w_flip = keep.take(6, P), keep.take(2, P)
        k.l0_qk = [k.wT[:, 0, :], k.w_flip[:, 0, :], k.wT[:, 1, :], k.w_flip[:, 1, :]]
        k.l0_wvT, k.l0_woT = k.wT[:, 2, :], k.wT[:, 3, :]
        l3_qkv, k.l3_wo = keep.take(3 * D), keep.take(D)
        k.l3_qk, k.l3_wv = [l3_qkv[:, 0:D], l3_qkv[:, D:2 * D]], l3_qkv[:, 2 * D:3 * D]
        blocks = keep.take(3, TOK)
        k.b2_blocks = {n: blocks[0:64, j, :] for j, n in enumerate(("relu", "gelu", "gate"))}
        k.ctx, k.ctxT = keep.take(B * CTX), keep.take(2, B * M)
        k.pooled_raw = keep.take(B, D)
        k.key_row, k.key_b, k.null_k = keep.take(B * M), keep.take(1), keep.take(1)
        k.bit_w1T, k.bit_w2T = keep.take(9 * 256), keep.take(9 * 256)
        k.mb_win, k.mb_conv, k.mb_wx, k.wx3 = keep.take(4 * P), keep.take(8, 2 * P), keep.take(2, 96), keep.take(2, 96)
        k.mb_wdt, k.mb_wout = keep.take(2 * P)[0:64, :], keep.take(2, D)
        k.a_log, k.a_exp, k.a_neg, k.s_last = keep.take(2, 16), keep.take(2, 16), keep.take(32), keep.take(2, B)
        k.w, k.logit, k.lang, k.lp = keep.take(64), keep.take(B, 8), keep.take(B, 4), keep.take(B, 5)
        k.peak, k.rank, k.wT_route = keep.take(B), keep.take(B, 8), keep.take(P)
        k.more, k.same = keep.take(B, 8, 8), keep.take(B, 8, 8)
        k.w1 = [keep.take(HALF) for _ in range(2)]
        k.w2 = [keep.take(4, D) for _ in range(2)]
        k.bit_scale, k.bit_half, k.bit_mhalf = (keep.take(27) for _ in range(3))
        k.bit_up, k.bit_down = keep.take(2 * P), keep.take(2 * P)
        at = keep.at
        k.bit_raw1, k.bit_raw2 = keep.take(18, P), keep.take(9, 2 * P)
        keep.rewind(at)
        k.wq, k.wkv, k.wout = keep.take(8 * P), keep.take(2, 2048), keep.take(8, D)

        k.p = [work.take(16, P) for _ in range(2)]
        k.pT = [work.take(4, P) for _ in range(2)]
        k.mx, k.nmx = ([work.take(16) for _ in range(2)] for _ in range(2))
        k.rec = work.take(16)
        at = work.at
        k.xT, k.q, k.t1, k.t2, k.t3, k.t4 = ([work.take(P) for _ in range(2)] for _ in range(6))
        k.kb = [work.take(4, P) for _ in range(2)]
        k.o, k.oT = work.take(P), work.take(P)
        k.v16 = [work.take(16 * 9) for _ in range(2)]
        k.v8 = [work.take(8 * 17) for _ in range(2)]
        after_attention = work.at
        k.hT = [work.take(4, HALF) for _ in range(2)]
        work.rewind(after_attention)
        k.w_raw = work.take(6, P)
        late = work.take(3 * P)
        k.upto_here, k.iota, k.filter = (late[:, j * P:(j + 1) * P] for j in range(3))
        k.lens, k.cum, k.idx = (work.take(M)[0:B, :] for _ in range(3))
        k.lens_i = work.take(M)[0:B, :].bitcast(I32)
        k.key_mask = work.take(B * M)[0:1, :].bitcast(I32)
        k.idxT, k.edge, k.plug = work.take(B), work.take(B), work.take(B)
        k.ctx_mv, k.ctx_ms = work.take(B, 2), work.take(B)
        k.edges, k.pick = work.take(B, S), work.take(B, M)
        k.pickT, k.patches = (v.rearrange("p h t -> p (h t)")[:, 0:TOK] for v in k.p)
        k.ctx_n = work.take(B, D)
        k.pooled0, k.pooled3 = k.edges, k.pooled_raw
        work.rewind(at)
        k.qT = [work.take(8, P) for _ in range(2)]
        k.kT = [work.take(8, M + 1) for _ in range(2)]
        k.wv = [work.take(16 * 65) for _ in range(2)]
        k.cT = [work.take(2, M) for _ in range(2)]
        k.wo_in, k.woT = work.take(1024), work.take(8, P)
        work.rewind(0)
        k.gate, k.u = work.take(2, TOK), work.take(2, TOK)
        k.delta, k.du, k_sC = work.take(2, TOK), work.take(2, TOK), work.take(2, TOK)
        at = work.at
        k.sp, s2 = work.take(2, TOK), work.take(2, TOK)
        end = work.at
        work.rewind(at)
        k.upad = work.take(2, 8, 131)
        work.rewind(end)
        k.bc3 = work.take(TOK, dtype=BF16)[0:96, :]
        k.dA = [k.u[:, c, :].rearrange("p (b t) -> p b t", t=S) for c in range(2)]
        k.yg, k.dbu = k.du, [k.sp[:, c, :] for c in range(2)]
        k.s, k.sC = [s2[:, c, :] for c in range(2)], [k_sC[:, c, :] for c in range(2)]
        k.dlT, k.rest = s2[0:64, 0, :], s2[0:96, 1, :]
        k.cb = [k.xnT, k.r[:, :, :].rearrange("p b d -> p (b d)")]
        k.zeros = k.cb[1][:, 0:HALF]
        k.wT_small = k.wT_route[0:64, :]

        setup = Setup(k)
        bits = BitWeights(k)
        n0 = Norm(k)
        t0 = Turn(k, n0)
        l0_attn = Attention(k, n0, t0, "rope")
        n1 = Norm(k, again=True)
        t1 = Turn(k, n1)
        l0_cross = Depool(k, n1, t1, k.wT[:, 4, :], k.pooled0, 1)
        n2 = Norm(k)
        t2 = Turn(k, n2)
        l0_ffn = Experts(k, n2, t2, "relu")
        n3 = Norm(k)
        t3 = Turn(k, n3)
        l1_attn = Attention(k, n3, t3, "self")
        n4 = Norm(k, src=k.r)
        t4 = Turn(k, n4)
        l1_start = DenseStart(k, n4)
        l1_dense = Experts(k, n4, t4, "dense")
        n5 = Norm(k, src=k.r)
        l1_after = AfterNorm(k, n5, k.wide["ln2_g"], k.wide["ln2_b"])
        n6 = Norm(k)
        t6 = Turn(k, n6)
        l1_cross = Attention(k, n6, t6, "context")
        n7 = Norm(k)
        t7 = Turn(k, n7)
        l1_ffn = Experts(k, n7, t7, "gelu")
        n8 = Norm(k)
        t8 = Turn(k, n8)
        l2_mamba = Mamba(k, n8, t8)
        n9 = Norm(k)
        t9 = Turn(k, n9)
        l2_cross = WideCross(k, n9, t9)
        n10 = Norm(k, src=k.r, eps=1e-6)
        l2_after = AfterNorm(k, n10, k.wide["ln_scale"], k.wide["ln_bias"])
        n11 = Norm(k, again=True)
        t11 = Turn(k, n11)
        l2_ffn = Experts(k, n11, t11, "bit")
        n12 = Norm(k)
        t12 = Turn(k, n12)
        l3_attn = Attention(k, n12, t12, "packed")
        n13 = Norm(k, again=True)
        t13 = Turn(k, n13)
        l3_cross = Depool(k, n13, t13, k.wT[:, 5, :], k.pooled3, 2)
        n14 = Norm(k)
        t14 = Turn(k, n14)
        l3_ffn = Experts(k, n14, t14, "gate")

        col = lambda name: k.cols[:, COL[name]:COL[name] + 1]

        def credit(eng, name):
            for signal, n in CREDITS[name].items():
                eng.sem_inc(k.sig[signal].sem, n)

        block = ctx.enter_context(nc.Block())

        @block.sync
        def _(sp):
            issued = dict.fromkeys(LOADS, 0)

            def load(group, dst, src):
                sp.dma_start(dst, src).then_inc(k.loads[group], 16)
                issued[group] += 1

            def on_all(v):
                return bcast(v, 0, P)

            load("x", k.x, a["x"].rearrange("b s d -> s b d"))
            load("first", early, a["early"])
            for j, name in enumerate(("L0_attn_W_Q", "L0_attn_W_K", "L0_attn_W_V", "L0_attn_W_O", "L0_xattn_W_in",
                                      "L3_xattn_W_in")):
                load("l0", k.w_raw[:, j, :], a[name])
            load("lens", k.lens_i, a["mask_BxS2_if0"])
            row = lambda name, v, n: load("rows", k.rows[COL[name]:COL[name] + n, :], v)
            for name, v in (("relu_b1", "L0_ffn_b1"), ("gelu_b1", "L1_ffn_b1"), ("gate_b1", "L3_ffn_b1")):
                row(name, a[v].rearrange("e (c p) -> (e c) p", p=P), 32)
            for name, v, n in (("dense_b1", "L1_attn_b1", 4), ("g_res0", "L0_xattn_g_res", 1),
                               ("g_res3", "L3_xattn_g_res", 1), ("gamma", "L2_ffn_ln_gamma", 1),
                               ("beta", "L2_ffn_ln_beta", 1), ("conv_b", "L2_attn_conv_b", 2),
                               ("b_dt", "L2_attn_b_dt", 2), ("ssm_d", "L2_attn_D", 2),
                               ("ln1_g", "L1_attn_ln1_g", 1), ("ln1_b", "L1_attn_ln1_b", 1)):
                row(name, a[v].rearrange("(c p) -> c p", p=P), n)
            load("routers", k.router_rows[0:8, :], a["L1_ffn_router_w"])
            load("routers", k.router_rows[8:12, :], a["L1_ffn_lang_w"])
            load("routers", k.router_rows[12:20, :], a["L2_ffn_router_w"])
            load("pool_consts", late, a["late"][:, 0:3 * P])
            load("lower", lower, a["late"][:, 3 * P:3 * P + 64])
            load("masks", halves.bitcast(U16), a["halves"])
            load("ctx", k.ctx[0:M, :].rearrange("s (b c) -> s b c", c=CTX), a["ctx_2048"].rearrange("b s c -> s b c"))
            load("keys", k.key_mask, a["mask_BxS2_ik0"].rearrange("b s -> (b s)").unsqueeze(0))
            load("keys", k.key_b[0:1, :], a["L1_xattn_b"].unsqueeze(0))
            load("gates", gates[:, 0, :], a["L0_ffn_gate_w"])
            load("gates", gates[:, 1, :], a["L3_ffn_Wg"])
            for at, n, name in ((0, 8, "L0_ffn_gate_b"), (8, 8, "L1_ffn_router_b"), (16, 8, "L3_ffn_bg"),
                                (24, 4, "L1_ffn_lang_b")):
                load("wide", bias[:, at:at + n], on_all(a[name]))
            for name, v in (("ln1_g", "L1_attn_ln1_g"), ("ln1_b", "L1_attn_ln1_b"), ("ln2_g", "L1_attn_ln2_g"),
                            ("ln2_b", "L1_attn_ln2_b"), ("dense_b2", "L1_attn_b2"), ("b_in0", "L0_xattn_b_in"),
                            ("b_in3", "L3_xattn_b_in"), ("g_init0", "L0_xattn_g_init"), ("g_init3", "L3_xattn_g_init"),
                            ("ln_scale", "L2_xattn_ln_scale"), ("ln_bias", "L2_xattn_ln_bias")):
                load("wide", k.wide[name], on_all(a[v][0:D]))
            sp.wait_ge(preset, PRESETS)
            for j, name in enumerate(("L0_ffn_b2", "L1_ffn_b2", "L3_ffn_b2")):
                for t in range(B):
                    load("b2", blocks[8 * t:8 * t + 8, j, t * D:(t + 1) * D], a[name])
            load("bit", k.bit_raw1[:, 0:2, :], a["L2_ffn_shared_w1"].rearrange("(c p) d -> p c d", p=P))
            for e in range(8):
                load("bit", k.bit_raw1[:, 2 + 2 * e:4 + 2 * e, :],
                     a["L2_ffn_expert_w1"][e].rearrange("(c p) d -> p c d", p=P))
            load("bit", k.bit_raw2[:, 0, :], a["L2_ffn_shared_w2"])
            load("bit", k.bit_raw2[:, 1:9, :], a["L2_ffn_expert_w2"].rearrange("e d f -> d e f"))
            load("l3", l3_qkv, a["L3_attn_w_qkv"])
            load("l3", k.l3_wo, a["L3_attn_w_out"])
            load("mamba", k.mb_win, a["L2_attn_W_in"])
            load("mamba", k.mb_conv, a["L2_attn_conv_w"].rearrange("k (c p) o -> p (k c) o", p=P))
            load("mamba", k.mb_wx, a["L2_attn_W_x"].rearrange("(c p) f -> p c f", p=P))
            load("mamba", k.mb_wdt, a["L2_attn_W_dt"])
            load("mamba", k.mb_wout, a["L2_attn_W_out"].rearrange("(c p) d -> p c d", p=P))
            load("mamba", k.a_log, a["L2_attn_A_log"].rearrange("(c p) n -> p c n", p=P))
            for h in range(2):
                load("null_k", k.null_k[64 * h:64 * h + 64, :], a["L2_xattn_null_kv"][0].unsqueeze(1))
            l0_ffn.sync(sp, a["L0_ffn_w1"], a["L0_ffn_w2"])
            l1_dense.sync(sp, a["L1_attn_W1"], a["L1_attn_W2"])
            l1_ffn.sync(sp, a["L1_ffn_w1"], a["L1_ffn_w2"])
            sp.wait_ge(*bits.in_sbuf.upto(9))
            load("wide_cross", k.wq, a["L2_xattn_Wq"])
            load("wide_cross", k.wkv, a["L2_xattn_Wkv"].rearrange("(e p) f -> p e f", p=P))
            load("wide_cross", k.wout, a["L2_xattn_Wout"].rearrange("(c p) d -> p c d", p=P))
            l2_cross.sync(sp, a["L2_xattn_null_kv"][1:2])
            issued["null_v"] += 2
            l3_ffn.sync(sp, a["L3_ffn_W1"], a["L3_ffn_W2"])
            for h in range(2):
                sp.wait_ge(*l3_ffn.result.upto(h + 1))
                sp.dma_start(out[4 * h:4 * h + 4].rearrange("b s d -> s b d"), k.x[:, 4 * h:4 * h + 4, :])\
                    .then_inc(stored, 16)
            sp.wait_ge(stored, 32)
            assert issued == LOADS, (issued, LOADS)

        @block.tensor
        def _(pe):
            credit(pe, "tensor")
            pe.wait_ge(preset, PRESETS)
            setup.tensor_first(pe)
            t0.tensor(pe)
            k.arrived(pe, "masks")
            l0_attn.tensor(pe)
            pe.wait_ge(*l0_attn.res_done.upto(B))
            setup.tensor_second(pe)
            t1.tensor(pe)
            l0_cross.tensor(pe)
            t2.tensor(pe)
            k.arrived(pe, "gates")
            l0_ffn.tensor(pe)
            t3.tensor(pe)
            l1_attn.tensor(pe)
            t4.tensor(pe)
            l1_dense.tensor(pe)
            t6.tensor(pe)
            pe.wait_ge(*setup.keyrow.upto(1))
            l1_cross.tensor(pe)
            t7.tensor(pe)
            l1_ffn.tensor(pe)
            bits.tensor(pe)
            t8.tensor(pe)
            l2_mamba.tensor(pe)
            t9.tensor(pe)
            l2_cross.tensor(pe)
            t11.tensor(pe)
            l2_ffn.tensor(pe)
            t12.tensor(pe)
            k.arrived(pe, "l3")
            l3_attn.tensor(pe)
            t13.tensor(pe)
            l3_cross.tensor(pe)
            t14.tensor(pe)
            l3_ffn.tensor(pe)

        @block.vector
        def _(dve):
            k.dchain = Chain(dve, chains[0])
            credit(dve, "vector")
            dve.wait_ge(preset, PRESETS)
            k.arrived(dve, "x")
            token_stats(k, dve, k.x, range(B))
            n0.vector(dve)
            setup.vector_first(dve)
            l0_attn.vector(dve)
            n1.vector(dve)
            l0_cross.vector(dve)
            n2.vector(dve)
            k.arrived(dve, "wide")
            k.arrived(dve, "lower")
            l0_ffn.vector(dve, between=bits)
            n3.vector(dve)
            l1_attn.vector(dve)
            n4.vector(dve)
            l1_start.vector(dve)
            l1_dense.vector(dve)
            n5.vector(dve)
            l1_after.vector(dve)
            n6.vector(dve)
            l1_cross.vector(dve)
            n7.vector(dve)
            l1_ffn.vector(dve)
            n8.vector(dve)
            l2_mamba.vector(dve)
            n9.vector(dve)
            l2_cross.vector(dve)
            n10.vector(dve)
            l2_after.vector(dve)
            n11.vector(dve)
            l2_ffn.vector(dve)
            n12.vector(dve)
            l3_attn.vector(dve)
            n13.vector(dve)
            l3_cross.vector(dve)
            n14.vector(dve)
            l3_ffn.vector(dve, stats=False)

        @block.scalar
        def _(act):
            k.achain = Chain(act, chains[1])
            credit(act, "scalar")
            act.wait_ge(preset, PRESETS)
            setup.scalar_first(act)
            act.wait_ge(*setup.small_ready.upto(1))
            t0.scalar(act)
            l0_attn.scalar(act)
            setup.scalar_second(act)
            t1.scalar(act, scale=col("g_res0"))
            t2.scalar(act)
            l0_ffn.scalar(act)
            t3.scalar(act)
            l1_attn.scalar(act)
            t4.scalar(act, scale=col("ln1_g"), bias=col("ln1_b"))
            l1_dense.scalar(act)
            t6.scalar(act, scale=1.0 / np.sqrt(16.0))
            l1_cross.scalar(act)
            t7.scalar(act)
            l1_ffn.scalar(act)
            bits.scalar(act)
            t8.scalar(act)
            l2_mamba.scalar(act)
            t9.scalar(act)
            l2_cross.scalar(act)
            t11.scalar(act, scale=col("gamma"), bias=col("beta"))
            l2_ffn.scalar(act)
            t12.scalar(act)
            l3_attn.scalar(act)
            t13.scalar(act, scale=col("g_res3"))
            t14.scalar(act)
            l3_ffn.scalar(act)

        @block.gpsimd
        def _(pool):
            k.pchain = Chain(pool, chains[2])
            credit(pool, "pool")
            for v, value in ((k.minus_half, -0.5), (k.ones, 1.0), (k.key_row, 0.0), (bias[:, 28:36], 0.0),
                             (k.lp[:, :, 4], 0.0), (blocks[0:64, :, :], 0.0)):
                pool.memset(v, value).then_inc(preset, 1)
            pool.wait_ge(preset, PRESETS)
            n0.pool(pool)
            setup.pool_first(pool)
            l0_attn.pool(pool)
            setup.pool_second(pool)
            n1.pool(pool)
            l0_cross.pool(pool)
            n2.pool(pool)
            bits.pool(pool)
            n3.pool(pool)
            l1_attn.pool(pool)
            setup.pool_third(pool)
            n4.pool(pool)
            l1_start.pool(pool)
            n5.pool(pool)
            l1_after.pool(pool)
            n6.pool(pool)
            l1_cross.pool(pool)
            n7.pool(pool)
            n8.pool(pool)
            l2_mamba.pool(pool)
            n9.pool(pool)
            l2_cross.pool(pool)
            n10.pool(pool)
            l2_after.pool(pool)
            n11.pool(pool)
            l2_ffn.pool(pool)
            n12.pool(pool)
            l3_attn.pool(pool)
            n13.pool(pool)
            l3_cross.pool(pool)
            n14.pool(pool)


def kernel(**inputs):
    import concourse.bacc as _bacc
    from concourse.bass_utils import run_bass_kernel_spmd as _run

    arrays = {f"in_{name}_dram": np.ascontiguousarray(v) for name, v in inputs.items()}
    arrays.update({f"in_{name}_dram": v for name, v in zip(("early", "late", "halves"), constants())})
    nc = _bacc.Bacc("TRN2", target_bir_lowering=False, num_devices=1)
    args = {}
    for name, v in arrays.items():
        args[name[3:-5]] = nc.dram_tensor(name, v.shape, mybir.dt.from_np(v.dtype), kind="ExternalInput").ap()
    out = nc.dram_tensor("out_0_dram", (B, S, D), F32, kind="ExternalOutput").ap()
    decoder(nc, args, out)
    return _run(nc, [arrays], core_ids=[0]).results[0]["out_0_dram"]
```

```python
from contextlib import ExitStack

import numpy as np

import concourse.bass as bass
from concourse import mybir

F32 = mybir.dt.float32
BF16 = mybir.dt.bfloat16
I32 = mybir.dt.int32
U16 = mybir.dt.uint16
ACT = mybir.ActivationFunctionType
ALU = mybir.AluOpType
AX = mybir.AxisListType

P = 128
B, S, D = 8, 128, 128
TOK = B * S
M, CTX = 120, 256
LN_EPS = 1e-5
HALF = 512
DEPOOL_EPS = 0.001
NEG = -1e30

PT0, OB, MB = 4, 6, 7


class Signal:

    def __init__(self, sem):
        self.sem, self.total = sem, 0

    def take(self, count):
        base = self.total
        self.total += count
        return Share(self.sem, base)


class Share:
    def __init__(self, sem, base):
        self.sem, self.base = sem, base

    def upto(self, n):
        return self.sem, n + self.base


class Chain:

    def __init__(self, eng, sem):
        self.eng, self.sem, self.base, self.n = eng, sem, 0, 0
        self.i, self.per = None, 0

    def step(self, ins):
        ins.then_inc(self.sem, 1)
        self.n += 1

    def settle(self):
        if self.i is None:
            if self.base + self.n:
                self.eng.wait_ge(self.sem, self.base + self.n)
        else:
            self.eng.wait_ge(self.sem, self.i * self.per + (self.base + self.n))

    def link(self, ins):
        self.step(ins)
        self.settle()

    def enter(self, i, per):
        self.base, self.n, self.i, self.per = self.base + self.n, 0, i, per

    def leave(self, trips):
        assert self.n == self.per, (self.n, self.per)
        self.base, self.n, self.i = self.base + trips * self.per, 0, None


def strided(flat, n, step, width):
    return bass.AP(tensor=flat.tensor, offset=flat.offset, ap=[flat.ap[0], [step, n], [1, width]])


def bcast(ap, axis, n):
    new = ap.unsqueeze(axis)
    shape = list(new.shape)
    shape[axis] = n
    return new.to_broadcast(shape)


class Norm:

    def __init__(self, k, src=None, again=False, eps=LN_EPS):
        self.k, self.src, self.again, self.eps = k, k.x if src is None else src, again, eps
        self.var_ready = k.sig["var_ready"].take(1)
        self.rstd_ready = k.sig["rstd_ready"].take(1)
        self.xn_ready = k.sig["xn_ready"].take(B)

    def vector(self, dve):
        k = self.k
        k.dchain.settle()
        dve.tensor_scalar(k.var_eps[:, :], k.mv[:, :, 1], self.eps, None, ALU.add).then_inc(self.var_ready.sem, 1)
        dve.wait_ge(*self.rstd_ready.upto(1))
        for b in range(B):
            dve.tensor_scalar(k.xn[:, b, :], self.src[:, b, :], k.mv[:, b, 0:1], k.rstd[:, b:b + 1],
                              ALU.subtract, ALU.mult).then_inc(self.xn_ready.sem, 1)

    def pool(self, pool):
        k = self.k
        pool.wait_ge(*self.var_ready.upto(1))
        root = lambda out, v: pool.tensor_tensor(out, v, bcast(k.minus_half[:, 0], 1, B), ALU.pow)
        if not self.again:
            root(k.rstd[:, :], k.var_eps[:, :]).then_inc(self.rstd_ready.sem, 1)
            return
        k.pchain.link(root(k.root1[:, :], k.var_eps[:, :]))
        k.pchain.link(pool.tensor_tensor(k.ms[:, :], k.root1[:, :], k.root1[:, :], ALU.mult))
        k.pchain.link(pool.tensor_tensor(k.ms[:, :], k.ms[:, :], k.mv[:, :, 1], ALU.mult))
        k.pchain.link(pool.tensor_scalar(k.ms[:, :], k.ms[:, :], LN_EPS, None, ALU.add))
        k.pchain.link(root(k.root2[:, :], k.ms[:, :]))
        pool.tensor_tensor(k.rstd[:, :], k.root1[:, :], k.root2[:, :], ALU.mult).then_inc(self.rstd_ready.sem, 1)


def token_stats(k, dve, src, bs):
    for b in bs:
        k.dchain.step(dve.bn_stats(k.bn[:, b, :], src[:, b, :]))
    k.dchain.settle()
    for b in bs:
        k.dchain.step(dve.bn_aggr(k.mv[:, b, :], k.bn[:, b, :]))


class Turn:

    def __init__(self, k, norm):
        self.k, self.norm = k, norm
        self.turned = k.sig["x_turned"].take(2)
        self.xT_ready = k.sig["xnT_ready"].take(2)

    def tensor(self, pe):
        k = self.k
        for b in range(B):
            pe.wait_ge(*self.norm.xn_ready.upto(b + 1))
            t = pe.transpose(k.ps[:, PT0 + b // 4, b % 4 * P:(b % 4 + 1) * P], k.xn[:, b, :], k.ident)
            if b % 4 == 3:
                t.then_inc(self.turned.sem, 1)

    def scalar(self, act, scale=1.0, bias=0.0):
        k = self.k
        for h in range(2):
            act.wait_ge(*self.turned.upto(h + 1))
            act.activation(k.xnT[:, h * HALF:(h + 1) * HALF], k.ps[:, PT0 + h, :], ACT.Identity,
                           scale=scale, bias=bias).then_inc(self.xT_ready.sem, 1)


class Attention:

    UNITS = 4

    def __init__(self, k, norm, turn, kind):
        self.k, self.norm, self.turn, self.kind = k, norm, turn, kind
        self.H = 8 if kind == "context" else 16
        self.dh = D // self.H
        self.per = self.H // self.UNITS
        self.T = M if kind == "context" else S
        self.scale = 1.0 / np.sqrt(8.0) if kind in ("rope", "packed") else 1.0
        self.proj = kind in ("rope", "packed")
        self.v = k.ctx.rearrange("t (b n) -> t b n", b=B)[:, :, P:CTX] if kind == "context" else k.v_tok if self.proj else k.xn
        self.q_all = k.q_all if self.proj else k.xnT
        self.k_all = k.k_all if self.proj else k.ctxT[:, 0, :] if kind == "context" else k.xnT
        sig = k.sig
        self.vb_ready = sig["at_vb_ready"].take(B)
        self.kv_ready = sig["at_kv_ready"].take(B)
        self.s_done = sig["at_s_done"].take(4 * B)
        self.max_ready = sig["at_max_ready"].take(4 * B)
        self.p_ready = sig["at_p_ready"].take(4 * B)
        self.rec_ready = sig["at_rec_ready"].take(4 * B)
        self.pn_ready = sig["at_pn_ready"].take(4 * B)
        self.pt_done = sig["at_pt_done"].take(4 * B)
        self.ptv_ready = sig["at_ptv_ready"].take(2 * B)
        self.pta_ready = sig["at_pta_ready"].take(2 * B)
        self.av_even = sig["at_av_even"].take(2 * B)
        self.av_odd = sig["at_av_odd"].take(2 * B)
        self.oT_ready = sig["at_oT_ready"].take(B)
        self.y_done = sig["at_y_done"].take(B)
        self.res_done = sig["at_res_done"].take(B)
        if self.proj:
            self.v_ready = sig["at_v_ready"].take(2)
            self.vp_done = sig["at_vp_done"].take(2)
            self.qk_done = sig["at_qk_done"].take(8 if kind == "rope" else 4)
            self.turned_qk = sig["at_turned_qk"].take(4)
            self.q_ready = sig["at_q_ready"].take(2 if kind == "packed" else 0)

    def each(self, eng, step):
        step(0, 0)
        with eng.Fori(0, B // 2 - 1) as i:
            step(i, 1)
            step(i + 1, 0)
        step(B // 2 - 1, 1)

    def place(self, i, p):
        fixed = isinstance(i, int)
        return fixed and p == 0, fixed and p == 1, (i, 1) if p == 0 else (i + 1, 0)

    def tensor(self, pe):
        if self.proj:
            self.project(pe)
        for u in range(4):
            self.scores(pe, 0, 0, u)

        def sequence(i, p):
            first, last, nxt = self.place(i, p)
            for u in range(4):
                if not last:
                    self.scores(pe, *nxt, u)
                self.turn_weights(pe, i, p, u)
                if u:
                    self.times_v(pe, i, p, u - 1)
                if u == 0 and not first:
                    self.out(pe, i, p)
            self.times_v(pe, i, p, 3)

        self.each(pe, sequence)
        self.out(pe, B // 2, 0)

    def project(self, pe):
        k = self.k
        pe.wait_ge(*self.turn.xT_ready.upto(2))
        wv = k.l0_wvT if self.kind == "rope" else k.l3_wv
        for b in range(B):
            m = pe.matmul(k.ps[:, 6 + b // 4, b % 4 * P:(b % 4 + 1) * P], k.xnT[:, b * P:(b + 1) * P], wv,
                          start=True, stop=True)
            if b % 4 == 3:
                m.then_inc(self.vp_done.sem, 1)
        weights = k.l0_qk if self.kind == "rope" else k.l3_qk
        for h in range(2):
            for j, w in enumerate(weights):
                bank = len(weights) * h + j
                if bank >= 6:
                    pe.wait_ge(*self.v_ready.upto(bank - 5))
                pe.matmul(k.ps[:, bank, :], w, k.xnT[:, h * HALF:(h + 1) * HALF], start=True, stop=True)\
                    .then_inc(self.qk_done.sem, 1)
        pe.wait_ge(*self.turned_qk.upto(4))
        if self.kind == "packed":
            pe.wait_ge(*self.q_ready.upto(2))

    def scores(self, pe, i, p, u):
        k = self.k
        b = 2 * i + p
        if u == 0:
            pe.wait_ge(*self.kv_ready.upto(b + 1))
        pe.wait_ge(*self.p_ready.upto(0 if isinstance(b, int) and b == 0 else 8 * i + (4 * p + u - 3)))
        out = k.ps[:, u, :].rearrange("q (h t) -> q h t", t=P)[:, 0:self.per, 0:self.T]
        g = slice(32 * u, 32 * u + 32)
        mask = self.kind != "packed"
        if self.kind == "context":
            pe.matmul(out, k.ones, bcast(k.key_row[:, bass.ts(b, M)], 1, self.per), start=True, stop=False)
        elif mask:
            pe.matmul(out, k.ident16, bcast(k.causal if self.kind == "rope" else k.band, 1, self.per),
                      start=True, stop=False)
        pe.matmul(out, k.q[p][g, :], k.kb[p][g, 0:self.per, 0:self.T], start=not mask, stop=True)\
            .then_inc(self.s_done.sem, 1)

    def turn_weights(self, pe, i, p, u):
        k = self.k
        b = 2 * i + p
        pe.wait_ge(*self.pn_ready.upto(4 * b + u + 1))
        ready = self.pta_ready if u % 2 else self.ptv_ready
        pe.wait_ge(*ready.upto(2 * b + u // 2))
        for j in range(self.per):
            t = pe.transpose(k.ps[0:self.T, PT0 + u % 2, j * P:(j + 1) * P],
                             k.p[p][:, u * self.per + j, 0:self.T], k.ident)
        t.then_inc(self.pt_done.sem, 1)

    def times_v(self, pe, i, p, u):
        k = self.k
        b = 2 * i + p
        if u == 0:
            pe.wait_ge(*self.oT_ready.upto(b))
            pe.wait_ge(*self.vb_ready.upto(b + 1))
        ready = self.pta_ready if u % 2 else self.ptv_ready
        pe.wait_ge(*ready.upto(2 * b + u // 2 + 1))
        for j in range(self.per):
            h = u * self.per + j
            m = pe.matmul(k.ps[:, OB, 0:P], k.v_block[p][0:self.T, h, :], k.pT[u % 2][0:self.T, j, :],
                          start=h == 0, stop=h == self.H - 1)
        m.then_inc((self.av_odd if u % 2 else self.av_even).sem, 1)

    def out(self, pe, i, p):
        k = self.k
        b = 2 * i + p
        pe.wait_ge(*self.oT_ready.upto(b))
        pe.wait_ge(*self.res_done.upto(b - 1))
        if self.proj:
            y = pe.matmul(k.ps[:, MB, 0:P], k.oT, k.l0_woT if self.kind == "rope" else k.l3_wo, start=True, stop=True)
        else:
            y = pe.transpose(k.ps[:, MB, 0:P], k.oT, k.ident)
        y.then_inc(self.y_done.sem, 1)

    def vector(self, dve):
        k, c = self.k, self.k.dchain
        if self.proj:
            self.keys(dve)
        for u in range(4):
            self.maxima(dve, 0, 0, u)
            if u:
                self.sums(dve, 0, 0, u - 1)
        self.sequence_vector(dve, 0, 0)
        with dve.Fori(0, B // 2 - 1) as i:
            c.enter(i, 2 * (4 + 4))
            self.sequence_vector(dve, i, 1)
            self.sequence_vector(dve, i + 1, 0)
        c.leave(B // 2 - 1)
        self.sequence_vector(dve, B // 2 - 1, 1)
        self.residual(dve, B // 2, 0)
        dve.wait_ge(*self.res_done.upto(B))
        token_stats(k, dve, k.r if self.kind == "self" else k.x, range(B))

    def sequence_vector(self, dve, i, p):
        first, last, nxt = self.place(i, p)
        for u in range(4):
            if not last:
                self.maxima(dve, *nxt, u)
            if u == 0:
                self.sums(dve, i, p, 3)
            elif not last:
                self.sums(dve, *nxt, u - 1)
            if u % 2 == 0:
                self.turned_weights(dve, i, p, u)
            if u == 1 and not first:
                self.residual(dve, i, p)

    def keys(self, dve):
        k = self.k
        if self.kind == "packed":
            for h in range(2):
                dve.wait_ge(*self.qk_done.upto(2 * h + 2))
                dve.tensor_copy(k.k_all[:, h * HALF:(h + 1) * HALF], k.ps[:, 2 * h + 1, :])\
                    .then_inc(self.turned_qk.sem, 2)
            return
        four = lambda v: v.rearrange("p (b t) -> p b t", t=S)
        for h in range(2):
            for j in range(2):
                q = slice((2 * j) * HALF, (2 * j + 1) * HALF)
                r = slice((2 * j + 1) * HALF, (2 * j + 2) * HALF)
                dve.wait_ge(*self.qk_done.upto(4 * h + 2 * j + 2))
                k.dchain.step(dve.tensor_tensor(four(k.terms[h][:, q]), four(k.ps[:, 4 * h + 2 * j, :]),
                                                bcast(k.cosT, 1, 4), ALU.mult))
                dve.tensor_tensor(four(k.terms[h][:, r]), four(k.ps[:, 4 * h + 2 * j + 1, :]),
                                  bcast(k.sinT, 1, 4), ALU.mult).then_inc(self.turned_qk.sem, 1)

    def maxima(self, dve, i, p, u):
        k, c = self.k, self.k.dchain
        dve.wait_ge(*self.s_done.upto(4 * (2 * i + p) + u + 1))
        hs = slice(u * self.per, (u + 1) * self.per)
        src = k.ps[:, u, :].rearrange("q (h t) -> q h t", t=P)[:, 0:self.per, 0:self.T]
        c.link(dve.tensor_reduce(k.mx[p][:, hs], src, AX.X, ALU.max))
        dve.tensor_scalar(k.nmx[p][:, hs], k.mx[p][:, hs], -self.scale, None, ALU.mult)\
            .then_inc(self.max_ready.sem, 1)

    def turned_weights(self, dve, i, p, u):
        k = self.k
        b = 2 * i + p
        dve.wait_ge(*self.pt_done.upto(4 * b + u + 1))
        dve.wait_ge(*self.av_even.upto(2 * b + u // 2))
        n = self.per * P
        dve.tensor_copy(k.pT[0][0:self.T, :, :].rearrange("t h q -> t (h q)")[:, 0:n],
                        k.ps[0:self.T, PT0, 0:n]).then_inc(self.ptv_ready.sem, 1)

    def sums(self, dve, i, p, u):
        k, c = self.k, self.k.dchain
        dve.wait_ge(*self.p_ready.upto(4 * (2 * i + p) + u + 1))
        hs = slice(u * self.per, (u + 1) * self.per)
        c.link(dve.tensor_reduce(k.total[p][:, hs], k.p[p][:, hs, 0:self.T], AX.X, ALU.add))
        dve.reciprocal(k.rec[p][:, hs], k.total[p][:, hs]).then_inc(self.rec_ready.sem, 1)

    def residual(self, dve, i, p):
        k = self.k
        b = 2 * i + p
        base, dst = (k.xn, k.r) if self.kind == "self" else (k.x, k.x)
        dve.wait_ge(*self.y_done.upto(b))
        dve.tensor_tensor(dst[:, b - 1, :], base[:, b - 1, :], k.ps[:, MB, 0:P], ALU.add).then_inc(self.res_done.sem, 1)

    def pool(self, pool):
        k, c = self.k, self.k.pchain
        pool.wait_ge(*self.turn.xT_ready.upto(1))
        for p in range(2):
            c.step(pool.memset(k.v_block[p][:, 0:self.H, :], 0.0))
        pool.wait_ge(*self.turn.xT_ready.upto(2))
        if self.kind == "rope":
            for h in range(2):
                for j, dst in enumerate((k.q_all, k.k_all)):
                    pool.wait_ge(*self.turned_qk.upto(2 * h + j + 1))
                    c.step(pool.tensor_tensor(dst[:, h * HALF:(h + 1) * HALF],
                                              k.terms[h][:, 2 * j * HALF:(2 * j + 1) * HALF],
                                              k.terms[h][:, (2 * j + 1) * HALF:(2 * j + 2) * HALF], ALU.add))
        elif self.kind == "packed":
            pool.wait_ge(*self.turned_qk.upto(4))
            pool.wait_ge(*self.q_ready.upto(2))
        c.settle()
        self.keys_of(pool, 0, 0)
        if self.proj:
            pool.wait_ge(*self.v_ready.upto(2))
        self.values_of(pool, 0, 0)

        def sequence(i, p):
            first, last, nxt = self.place(i, p)
            if not last:
                self.keys_of(pool, *nxt)
            for u in range(4):
                self.normalise(pool, i, p, u)
            if not last:
                self.values_of(pool, *nxt)

        self.each(pool, sequence)

    def keys_of(self, pool, i, p):
        k = self.k
        b = 2 * i + p
        hm = k.head_of4 if self.per == 4 else k.head_of2
        pool.wait_ge(*self.s_done.upto(0 if isinstance(b, int) and b == 0 else 8 * i + (4 * p - 4)))
        pool.tensor_copy(k.q[p], self.q_all[:, bass.ts(b, P)])
        pool.tensor_tensor(k.kb[p][:, 0:self.per, 0:self.T], bcast(self.k_all[:, bass.ts(b, self.T)], 1, self.per),
                           bcast(hm, 2, self.T), ALU.mult).then_inc(self.kv_ready.sem, 1)

    def values_of(self, pool, i, p):
        k = self.k
        b = 2 * i + p
        pool.wait_ge(*self.av_odd.upto(0 if isinstance(b, int) and b == 0 else 4 * i + (2 * p - 2)))
        flat = k.v_block[p].rearrange("t h f -> t (h f)")
        dst = strided(flat[0:self.T, :], self.H, P + self.dh, self.dh)
        src = self.v[0:self.T, bass.ds(b, 1), :].rearrange("t o (h d) -> t (o h) d", d=self.dh)
        pool.tensor_copy(dst, src).then_inc(self.vb_ready.sem, 1)

    def normalise(self, pool, i, p, u):
        k = self.k
        pool.wait_ge(*self.rec_ready.upto(4 * (2 * i + p) + u + 1))
        hs = slice(u * self.per, (u + 1) * self.per)
        w = k.p[p][:, hs, 0:self.T]
        pool.tensor_tensor(w, w, bcast(k.rec[p][:, hs], 2, self.T), ALU.mult).then_inc(self.pn_ready.sem, 1)

    def scalar(self, act):
        if self.proj:
            self.values(act)
        if self.kind == "packed":
            self.queries(act)
        for u in range(4):
            self.weights(act, 0, 0, u)

        def sequence(i, p):
            first, last, nxt = self.place(i, p)
            for u in range(4):
                if u % 2:
                    self.turned_weights_odd(act, i, p, u)
                if not last:
                    self.weights(act, *nxt, u)
            self.outputs(act, i, p)

        self.each(act, sequence)

    def values(self, act):
        k = self.k
        for h in range(2):
            act.wait_ge(*self.vp_done.upto(h + 1))
            act.activation(k.v_tok[:, 4 * h:4 * h + 4, :], k.ps[:, 6 + h, :].rearrange("t (b n) -> t b n", b=4), ACT.Copy)\
                .then_inc(self.v_ready.sem, 1)

    def queries(self, act):
        k = self.k
        for h in range(2):
            act.wait_ge(*self.qk_done.upto(2 * h + 1))
            act.activation(k.q_all[:, h * HALF:(h + 1) * HALF], k.ps[:, 2 * h, :], ACT.Copy).then_inc(self.q_ready.sem, 1)

    def weights(self, act, i, p, u):
        k = self.k
        b = 2 * i + p
        act.wait_ge(*self.max_ready.upto(4 * b + u + 1))
        if u == 0:
            act.wait_ge(*self.pt_done.upto(0 if isinstance(b, int) and b == 0 else 8 * i + (4 * p - 4)))
        for j in range(self.per):
            h = u * self.per + j
            e = act.activation(k.p[p][:, h, 0:self.T], k.ps[:, u, j * P:j * P + self.T], ACT.Exp,
                               bias=k.nmx[p][:, h:h + 1], scale=float(self.scale))
        e.then_inc(self.p_ready.sem, 1)

    def turned_weights_odd(self, act, i, p, u):
        k = self.k
        b = 2 * i + p
        act.wait_ge(*self.pt_done.upto(4 * b + u + 1))
        act.wait_ge(*self.av_odd.upto(2 * b + u // 2))
        n = self.per * P
        act.activation(k.pT[1][0:self.T, :, :].rearrange("t h q -> t (h q)")[:, 0:n],
                       k.ps[0:self.T, PT0 + 1, 0:n], ACT.Copy).then_inc(self.pta_ready.sem, 1)

    def outputs(self, act, i, p):
        k = self.k
        b = 2 * i + p
        act.wait_ge(*self.av_odd.upto(2 * b + 2))
        act.wait_ge(*self.y_done.upto(b))
        act.activation(k.oT, k.ps[:, OB, 0:P], ACT.Copy).then_inc(self.oT_ready.sem, 1)


class Experts:

    def __init__(self, k, norm, turn, kind):
        self.k, self.norm, self.turn, self.kind = k, norm, turn, kind
        self.nf = 2 if kind == "bit" else 4
        self.func = {"gelu": ACT.Gelu, "bit": ACT.Silu}.get(kind, ACT.Relu)
        self.routed = kind != "dense"
        self.b2 = kind in ("relu", "gelu", "gate")
        self.first = {"dense": -2, "bit": 2}.get(kind, 0)
        self.items = {"dense": 2, "bit": 18}.get(kind, 16)
        sig = k.sig
        self.h_done = sig["ff_h_done"].take(self.items * self.nf)
        self.h_ready = sig["ff_h_ready"].take(self.items * self.nf)
        self.o_done = sig["ff_o_done"].take(self.items)
        self.acc_done = sig["ff_acc_done"].take(self.items)
        if self.routed:
            self.router_done = sig["ff_router_done"].take(1)
        if kind in ("relu", "gelu", "gate"):
            self.loaded = [s.take(4 * 32) for s in k.ring_loaded]
        elif kind == "bit":
            self.loaded = [s.take(4) for s in k.ring_copied]
        else:
            self.loaded = [None, k.ring_loaded[1].take(32)]
        if self.b2:
            self.w_ready = sig["ff_w_ready"].take(1)
            self.w_turned = sig["ff_w_turned"].take(1)
            self.wT_ready = sig["ff_wT_ready"].take(1)
            self.b2_done = sig["ff_b2_done"].take(1)
        if kind == "gate":
            self.result = sig["result"].take(2)
        if kind in ("gelu", "gate", "bit"):
            self.l_ready = sig["ff_l_ready"].take(2 if kind == "gelu" else 1)
            self.e_ready = sig["ff_e_ready"].take(2 if kind == "gelu" else 1)

    def weights_in(self, p):
        if self.kind == "bit":
            return lambda i: self.loaded[p].upto(i + 1)
        return lambda i: self.loaded[p].upto(32 * (i + 1))

    def sync(self, sp, w1, w2):
        k = self.k
        if self.kind == "dense":
            sp.wait_ge(*self.o_done.upto(0))
            sp.dma_start(k.w1[1][:, :], w1).then_inc(self.loaded[1].sem, 16)
            sp.dma_start(k.w2[1][:, :, :], w2.rearrange("(c p) d -> p c d", p=P)).then_inc(self.loaded[1].sem, 16)
            return
        with sp.Fori(0, 4) as i:
            for p in range(2):
                e = 2 * i + p
                sp.wait_ge(*self.o_done.upto(2 * e - 2))
                sp.dma_start(k.w1[p][:, :], w1[bass.ds(e, 1)].rearrange("o d f -> d (o f)"))\
                    .then_inc(self.loaded[p].sem, 16)
                sp.dma_start(k.w2[p][:, :, :], w2[bass.ds(e, 1)].rearrange("o (c p) d -> p (o c) d", p=P))\
                    .then_inc(self.loaded[p].sem, 16)

    def pool(self, pool):
        k = self.k
        with pool.Fori(0, 4) as i:
            for p in range(2):
                e = 2 * i + p
                pool.wait_ge(*self.o_done.upto(2 * e))
                pool.tensor_copy(k.w1[p][:, 0:256], k.bit_w1T[:, bass.ts(e + 1, 256)])
                pool.tensor_copy(k.w2[p][:, 0:2, :].rearrange("f c d -> f (c d)"), k.bit_w2T[:, bass.ts(e + 1, 256)])\
                    .then_inc(self.loaded[p].sem, 1)

    def tensor(self, pe):
        k = self.k
        if self.routed:
            R = {"gelu": 12}.get(self.kind, 8)
            for t in range(B):
                pe.wait_ge(*self.turn.xT_ready.upto(t // 4 + 1))
                m = pe.matmul(k.ps[:, 6, 16 * t:16 * t + R], k.xnT[:, t * P:(t + 1) * P], k.router[self.kind],
                              start=True, stop=True)
            m.then_inc(self.router_done.sem, 1)
        else:
            pe.wait_ge(*self.turn.xT_ready.upto(2))
        if self.kind == "dense":
            self.block(pe, 0, [1])
        else:
            if self.kind == "bit":
                self.block(pe, 0, ["shared"])
            with pe.Fori(0, 4) as i:
                self.block(pe, i, [0, 1])
        if self.b2:
            pe.wait_ge(*self.w_ready.upto(1))
            pe.wait_ge(*self.h_ready.upto(self.items * self.nf))
            pe.transpose(k.ps[0:64, 0, 0:P], k.w[:, :], k.ident).then_inc(self.w_turned.sem, 1)
            pe.wait_ge(*self.wT_ready.upto(1))
            k.arrived(pe, "b2")
            for h in range(2):
                m = pe.matmul(k.ps[:, 6 + h, :], k.wT_small, k.b2_blocks[self.kind][:, h * HALF:(h + 1) * HALF],
                              start=True, stop=True)
            m.then_inc(self.b2_done.sem, 1)

    def item(self, i, p, h):
        return h if p == "shared" else self.first + 4 * i + 2 * p + h

    def block(self, pe, i, ps):
        items = [(p, h) for p in ps for h in range(2)]
        self.layer1(pe, i, *items[0])
        for n, it in enumerate(items):
            if n + 1 < len(items):
                self.layer1(pe, i, *items[n + 1])
            self.layer2(pe, i, *it)

    def layer1(self, pe, i, p, h):
        k = self.k
        n = self.item(i, p, h)
        shared = p == "shared"
        if h == 0 and not shared:
            pe.wait_ge(*self.weights_in(p)(i))
        w1 = k.bit_w1T[:, 0:256] if shared else k.w1[p][:, :]
        for c in range(self.nf):
            pe.wait_ge(*self.h_ready.upto(self.nf * (n - 1) + c + 1))
            pe.matmul(k.ps[:, c, :], w1[:, c * P:(c + 1) * P], k.xnT[:, h * HALF:(h + 1) * HALF],
                      start=True, stop=True).then_inc(self.h_done.sem, 1)

    def layer2(self, pe, i, p, h):
        k = self.k
        n = self.item(i, p, h)
        pe.wait_ge(*self.acc_done.upto(n - 1))
        pe.wait_ge(*self.h_ready.upto(self.nf * (n + 1)))
        for j in range(4):
            for c in range(self.nf):
                w2 = k.bit_w2T[:, c * P:(c + 1) * P] if p == "shared" else k.w2[p][:, c, :]
                m = pe.matmul(k.ps[:, 4 + h, j * P:(j + 1) * P], k.hT[h][:, c, j * P:(j + 1) * P], w2,
                              start=c == 0, stop=c == self.nf - 1)
        m.then_inc(self.o_done.sem, 1)

    def scalar(self, act):
        k = self.k
        if self.kind in ("gelu", "gate", "bit"):
            for r in range({"gelu": 2}.get(self.kind, 1)):
                act.wait_ge(*self.l_ready.upto(r + 1))
                arg = k.lang if self.kind == "gelu" and r == 0 else k.logit
                act.activation(arg[:, :, :], arg[:, :, :], ACT.Exp, scale=-1.0 if self.kind == "gate" else 1.0)\
                    .then_inc(self.e_ready.sem, 1)
        if self.kind == "dense":
            self.hidden(act, 0, [1])
        else:
            if self.kind == "bit":
                self.hidden(act, 0, ["shared"])
            with act.Fori(0, 4) as i:
                self.hidden(act, i, [0, 1])
        if self.b2:
            act.wait_ge(*self.w_turned.upto(1))
            act.activation(k.wT_small, k.ps[0:64, 0, 0:P], ACT.Copy).then_inc(self.wT_ready.sem, 1)

    def hidden(self, act, i, ps):
        k = self.k
        for p in ps:
            for h in range(2):
                n = self.item(i, p, h)
                act.wait_ge(*self.o_done.upto(n - 1))
                for c in range(self.nf):
                    act.wait_ge(*self.h_done.upto(self.nf * n + c + 1))
                    if self.kind == "bit":
                        bias = 0.0
                    elif self.kind == "dense":
                        bias = k.cols[:, k.col["dense_b1"] + c:k.col["dense_b1"] + c + 1]
                    else:
                        j = k.col[self.kind + "_b1"] + c
                        bias = k.cols[:, bass.ds((2 * i + p) * 4 + j if h == 0 else i * 8 + (4 * p + j), 1)]
                    act.activation(k.hT[h][:, c, :], k.ps[:, c, :], self.func, bias=bias)\
                        .then_inc(self.h_ready.sem, 1)

    def vector(self, dve, stats=True, between=None):
        k, c = self.k, self.k.dchain
        if self.routed:
            self.route(dve)
        if between is not None:
            between.vector(dve)
        if self.kind == "dense":
            self.add(dve, 0, 1, k.r)
        elif self.kind == "bit":
            self.add(dve, 0, "shared", k.x)
            with dve.Fori(0, 4) as i:
                for p in range(2):
                    self.add(dve, i, p, k.x)
        else:
            with dve.Fori(0, 4) as i:
                for p in range(2):
                    self.add(dve, i, p, k.x)
        dve.wait_ge(*self.acc_done.upto(self.items))
        acc = k.r if self.kind == "dense" else k.x
        for h in range(2):
            if self.b2:
                dve.wait_ge(*self.b2_done.upto(1))
                total = dve.tensor_tensor(k.x[:, 4 * h:4 * h + 4, :], k.x[:, 4 * h:4 * h + 4, :],
                                          k.ps[:, 6 + h, :].rearrange("s (b d) -> s b d", d=D), ALU.add)
                if stats:
                    c.link(total)
                else:
                    total.then_inc(self.result.sem, 1)
            if stats:
                token_stats(k, dve, acc, range(4 * h, 4 * h + 4))

    def add(self, dve, i, p, acc):
        k = self.k
        for h in range(2):
            n = self.item(i, p, h)
            dve.wait_ge(*self.o_done.upto(n + 1))
            dve.wait_ge(*self.acc_done.upto(n - 1))
            if p == "shared" or self.kind == "dense":
                ins = dve.tensor_tensor(acc[:, 4 * h:4 * h + 4, :], acc[:, 4 * h:4 * h + 4, :],
                                        k.ps[:, 4 + h, :].rearrange("s (b d) -> s b d", d=D), ALU.add)
            else:
                for j in range(4):
                    t = 4 * h + j
                    ins = dve.scalar_tensor_tensor(acc[:, t, :], k.ps[:, 4 + h, j * P:(j + 1) * P],
                                                   k.w[:, bass.ds(2 * i + (8 * t + p), 1)], acc[:, t, :],
                                                   ALU.mult, ALU.add)
            ins.then_inc(self.acc_done.sem, 1)

    def route(self, dve):
        k, c = self.k, self.k.dchain
        dve.wait_ge(*self.router_done.upto(1))
        G = k.ps[:, 6, 0:16 * B].rearrange("s (t r) -> s t r", r=16)
        L = k.logit[:, :, :]
        W = k.w[:, :].rearrange("s (t e) -> s t e", e=8)

        def exponentials(r):
            dve.wait_ge(*self.e_ready.upto(r + 1))

        c.link(dve.tensor_tensor(L, G[:, :, 0:8], bcast(k.router_b[self.kind], 1, B), ALU.add))
        if self.kind == "gate":
            dve.tensor_scalar(W, L, 0.0, None, ALU.is_gt).then_inc(self.l_ready.sem, 1)
            exponentials(0)
            c.link(dve.tensor_scalar(L, L, 1.0, None, ALU.add))
            c.link(dve.reciprocal(L, L))
            dve.tensor_tensor(W, W, L, ALU.mult).then_inc(self.w_ready.sem, 1)
            dve.wait_ge(*self.w_ready.upto(1))
            return
        if self.kind == "gelu":
            G4 = k.lang[:, :, :]
            c.link(dve.tensor_tensor(G4, G[:, :, 8:12], bcast(k.lang_b, 1, B), ALU.add))
            c.link(dve.tensor_reduce(k.peak[:, :], G4, AX.X, ALU.max))
            dve.tensor_tensor(G4, G4, bcast(k.peak[:, :], 2, 4), ALU.subtract).then_inc(self.l_ready.sem, 1)
            exponentials(0)
            c.link(dve.tensor_reduce(k.peak[:, :], G4, AX.X, ALU.add))
            c.link(dve.reciprocal(k.peak[:, :], k.peak[:, :]))
            c.link(dve.tensor_tensor(k.lp[:, :, 0:4], G4, bcast(k.peak[:, :], 2, 4), ALU.mult))
            c.link(dve.tensor_tensor(G4, k.lp[:, :, 0:4], k.lp[:, :, 1:5], ALU.add))
            for half in range(2):
                v = k.logit[:, :, 4 * half:4 * half + 4]
                c.link(dve.scalar_tensor_tensor(v, G4, 0.1, v, ALU.mult, ALU.add))
        c.link(dve.tensor_reduce(k.peak[:, :], L, AX.X, ALU.max))
        c.link(dve.tensor_tensor(L, L, bcast(k.peak[:, :], 2, 8), ALU.subtract))
        c.link(dve.tensor_scalar(L, L, -104.0, None, ALU.max))
        mine, other = bcast(L, 3, 8), bcast(L, 2, 8)
        c.step(dve.tensor_tensor(k.more[:, :, :, :], other, mine, ALU.is_gt))
        c.link(dve.tensor_tensor(k.same[:, :, :, :], other, mine, ALU.is_equal))
        c.link(dve.tensor_tensor(k.same[:, :, :, :], k.same[:, :, :, :], bcast(k.lower, 1, B), ALU.mult))
        c.link(dve.tensor_tensor(k.more[:, :, :, :], k.more[:, :, :, :], k.same[:, :, :, :], ALU.add))
        last = dve.tensor_reduce(k.rank[:, :, :], k.more[:, :, :, :], AX.X, ALU.add)
        if self.kind == "relu":
            c.link(last)
            dve.tensor_scalar(W, k.rank[:, :, :], 2.0, None, ALU.is_lt).then_inc(self.w_ready.sem, 1)
            dve.wait_ge(*self.w_ready.upto(1))
            return
        last.then_inc(self.l_ready.sem, 1)
        r = 1 if self.kind == "gelu" else 0
        exponentials(r)
        c.link(dve.tensor_scalar(W, k.rank[:, :, :], 2.0 if self.kind == "gelu" else 1.0, None, ALU.is_lt))
        if self.kind == "gelu":
            c.link(dve.tensor_tensor(L, L, W, ALU.mult))
        c.link(dve.tensor_reduce(k.peak[:, :], L, AX.X, ALU.add))
        c.link(dve.reciprocal(k.peak[:, :], k.peak[:, :]))
        if self.kind == "gelu":
            dve.tensor_tensor(W, L, bcast(k.peak[:, :], 2, 8), ALU.mult).then_inc(self.w_ready.sem, 1)
            dve.wait_ge(*self.w_ready.upto(1))
        else:
            c.link(dve.tensor_tensor(W, W, bcast(k.peak[:, :], 2, 8), ALU.mult))


class Depool:

    def __init__(self, k, norm, turn, w_inT, pooled, nth):
        self.k, self.norm, self.turn, self.w_inT, self.pooled, self.nth = k, norm, turn, w_inT, pooled, nth
        self.pooled_in = k.sig["dp_pooled_in"].take(1)
        self.y_done = k.sig["dp_y_done"].take(2)

    def pool(self, pool):
        k = self.k
        pool.wait_ge(*self.norm.xn_ready.upto(B))
        pool.wait_ge(*k.pooled_ready.upto(self.nth))
        pool.tensor_tensor(k.x[:, :, :], k.x[:, :, :], self.pooled[:, :, :], ALU.add).then_inc(self.pooled_in.sem, 1)

    def tensor(self, pe):
        k = self.k
        for b in range(B):
            pe.wait_ge(*self.turn.xT_ready.upto(b // 4 + 1))
            m = pe.matmul(k.ps[:, b // 4, b % 4 * P:(b % 4 + 1) * P], k.xnT[:, b * P:(b + 1) * P], self.w_inT,
                          start=True, stop=True)
            if b % 4 == 3:
                m.then_inc(self.y_done.sem, 1)

    def vector(self, dve):
        k = self.k
        dve.wait_ge(*self.pooled_in.upto(1))
        for h in range(2):
            dve.wait_ge(*self.y_done.upto(h + 1))
            k.dchain.link(dve.tensor_tensor(k.x[:, 4 * h:4 * h + 4, :], k.x[:, 4 * h:4 * h + 4, :],
                                            k.ps[:, h, :].rearrange("s (b d) -> s b d", d=D), ALU.add))
            token_stats(k, dve, k.x, range(4 * h, 4 * h + 4))


class AfterNorm:

    def __init__(self, k, norm, gain, bias):
        self.k, self.norm, self.gain, self.bias = k, norm, gain, bias
        self.bias_in = k.sig["an_bias_in"].take(1)

    def pool(self, pool):
        k = self.k
        pool.tensor_tensor(k.x[:, :, :], k.x[:, :, :], bcast(self.bias, 1, B), ALU.add).then_inc(self.bias_in.sem, 1)

    def vector(self, dve):
        k, c = self.k, self.k.dchain
        dve.wait_ge(*self.norm.xn_ready.upto(B))
        dve.wait_ge(*self.bias_in.upto(1))
        for h in range(2):
            q = slice(4 * h, 4 * h + 4)
            c.link(dve.tensor_tensor(k.xn[:, q, :], k.xn[:, q, :], bcast(self.gain, 1, 4), ALU.mult))
            c.link(dve.tensor_tensor(k.x[:, q, :], k.x[:, q, :], k.xn[:, q, :], ALU.add))
            token_stats(k, dve, k.x, range(4 * h, 4 * h + 4))


class DenseStart:

    def __init__(self, k, norm):
        self.k, self.norm = k, norm
        self.ready = k.sig["dense_start"].take(1)

    def pool(self, pool):
        k = self.k
        pool.wait_ge(*self.norm.xn_ready.upto(B))
        k.pchain.link(pool.tensor_tensor(k.r[:, :, :], k.xn[:, :, :], bcast(k.ln1_g, 1, B), ALU.mult))
        k.pchain.link(pool.tensor_tensor(k.r[:, :, :], k.r[:, :, :], bcast(k.ln1_b, 1, B), ALU.add))
        pool.tensor_tensor(k.r[:, :, :], k.r[:, :, :], bcast(k.dense_b2, 1, B), ALU.add).then_inc(self.ready.sem, 1)

    def vector(self, dve):
        dve.wait_ge(*self.ready.upto(1))


class Mamba:

    N, K, C = 16, 4, 2

    def __init__(self, k, norm, turn):
        self.k, self.norm, self.turn = k, norm, turn
        sig = k.sig
        t = lambda name, n: sig["mb_" + name].take(n)
        self.pad_ready = t("pad_ready", 1)
        self.started = t("started", 1)
        self.in_done = t("in_done", 8)
        self.u_in = t("u_in", 4)
        self.gate_ready = t("gate_ready", 4)
        self.conv_done = t("conv_done", 4)
        self.u_ready = t("u_ready", 4)
        self.dl_done = t("dl_done", 2)
        self.dl_ready = t("dl_ready", 2)
        self.bc_done = t("bc_done", 2)
        self.bc_ready = t("bc_ready", 1)
        self.dt_done = t("dt_done", 4)
        self.z_ready = t("z_ready", 2)
        self.lg_ready = t("lg_ready", 2)
        self.du_ready = t("du_ready", 2)
        self.a_exp = t("a_exp", 1)
        self.b_done = t("b_done", self.N)
        self.c_done = t("c_done", self.N)
        self.c_ready = t("c_ready", self.N)
        self.dA_ready = [t(f"dA_ready{c}", self.N) for c in range(2)]
        self.dbu_done = t("dbu_done", 2 * self.N)
        self.scanned = [t(f"scanned{c}", self.N) for c in range(2)]
        self.sc_ready = [t(f"sc_ready{c}", self.N) for c in range(2)]
        self.y_done = [t(f"y_done{c}", self.N) for c in range(2)]
        self.yg_ready = t("yg_ready", 2)
        self.out_done = t("out_done", 2)

    def tensor(self, pe):
        k = self.k
        pe.wait_ge(*self.turn.xT_ready.upto(2))
        k.arrived(pe, "mamba")
        k.arrived(pe, "masks")
        for c in range(4):
            for h in range(2):
                pe.matmul(k.ps[:, 2 * c + h, :], k.mb_win[:, c * P:(c + 1) * P], k.xnT[:, h * HALF:(h + 1) * HALF],
                          start=True, stop=True).then_inc(self.in_done.sem, 1)
        pe.wait_ge(*self.u_in.upto(4))
        pe.wait_ge(*self.pad_ready.upto(1))
        for o in range(2):
            for h in range(2):
                for n, (tap, c) in enumerate((tap, c) for tap in range(self.K) for c in range(2)):
                    m = pe.matmul(k.ps[:, 2 * o + h, :], k.mb_conv[:, 2 * tap + c, o * P:(o + 1) * P],
                                  k.upad[:, c, 4 * h:4 * h + 4, tap:tap + P], start=n == 0, stop=n == 2 * self.K - 1)
                m.then_inc(self.conv_done.sem, 1)
        pe.wait_ge(*self.gate_ready.upto(4))
        pe.wait_ge(*self.u_ready.upto(4))
        for out, w, rows, sig in ((4, k.mb_wx[:, :, 0:64], 64, self.dl_done), (6, k.wx3[:, :, :], 96, self.bc_done)):
            for h in range(2):
                for c in range(2):
                    m = pe.matmul(k.ps[0:rows, out + h, :], w[:, c, :], k.u[:, c, h * HALF:(h + 1) * HALF],
                                  start=c == 0, stop=c == 1)
                m.then_inc(sig.sem, 1)
        pe.wait_ge(*self.dl_ready.upto(2))
        for c in range(2):
            for h in range(2):
                pe.matmul(k.ps[:, 2 * c + h, :], k.mb_wdt[:, c * P:(c + 1) * P], k.dlT[:, h * HALF:(h + 1) * HALF],
                          start=True, stop=True).then_inc(self.dt_done.sem, 1)
        pe.wait_ge(*self.bc_ready.upto(1))
        for bank in range(4, 8):
            pe.matmul(k.ps[:, bank, :], k.ident, k.zeros, start=True, stop=False)
        pe.wait_ge(*self.du_ready.upto(2))
        self.spread(pe, 0)
        with pe.Fori(0, self.N // 2 - 1) as i:
            for q in range(2):
                self.spread(pe, 2 * i + (q + 1))
                self.sum_up(pe, 2 * i + q, False)
        self.spread(pe, self.N - 1)
        self.sum_up(pe, self.N - 2, False)
        self.sum_up(pe, self.N - 1, True)
        pe.wait_ge(*self.yg_ready.upto(2))
        for b in range(B):
            for c in range(2):
                m = pe.matmul(k.ps[:, b // 4, b % 4 * P:(b % 4 + 1) * P], k.yg[:, c, b * P:(b + 1) * P],
                              k.mb_wout[:, c, :], start=c == 0, stop=c == 1)
            if b % 4 == 3:
                m.then_inc(self.out_done.sem, 1)

    def spread(self, pe, n):
        k = self.k
        pe.wait_ge(*self.dbu_done.upto(2 * n))
        for h in range(2):
            m = pe.matmul(k.ps[:, h, :], k.sel[:, bass.ts(n, P)], k.bc3[:, h * HALF:(h + 1) * HALF],
                          start=True, stop=True)
        m.then_inc(self.b_done.sem, 1)
        pe.wait_ge(*self.c_ready.upto(n))
        for h in range(2):
            m = pe.matmul(k.ps[:, 2 + h, :], k.sel[:, bass.ts(n + self.N, P)], k.bc3[:, h * HALF:(h + 1) * HALF],
                          start=True, stop=True)
        m.then_inc(self.c_done.sem, 1)

    def sum_up(self, pe, n, last):
        k = self.k
        for c in range(2):
            pe.wait_ge(*self.sc_ready[c].upto(n + 1))
            for h in range(2):
                m = pe.matmul(k.ps[:, 4 + 2 * c + h, :], k.ident, k.sC[c][:, h * HALF:(h + 1) * HALF],
                              start=False, stop=last)
            m.then_inc(self.y_done[c].sem, 1)

    def scalar(self, act):
        k = self.k
        for c in range(2):
            for h in range(2):
                act.wait_ge(*self.in_done.upto(2 * c + h + 1))
                act.activation(k.upad[:, c, 4 * h:4 * h + 4, self.K - 1:self.K - 1 + P],
                               k.ps[:, 2 * c + h, :].rearrange("p (b t) -> p b t", t=P), ACT.Copy)\
                    .then_inc(self.u_in.sem, 1)
        for c in range(2):
            for h in range(2):
                act.wait_ge(*self.in_done.upto(4 + 2 * c + h + 1))
                act.activation(k.gate[:, c, h * HALF:(h + 1) * HALF], k.ps[:, 4 + 2 * c + h, :], ACT.Silu)\
                    .then_inc(self.gate_ready.sem, 1)
        for o in range(2):
            for h in range(2):
                act.wait_ge(*self.conv_done.upto(2 * o + h + 1))
                j = k.col["conv_b"] + o
                act.activation(k.u[:, o, h * HALF:(h + 1) * HALF], k.ps[:, 2 * o + h, :], ACT.Silu,
                               bias=k.cols[:, j:j + 1]).then_inc(self.u_ready.sem, 1)
        for h in range(2):
            act.wait_ge(*self.dl_done.upto(h + 1))
            act.activation(k.dlT[:, h * HALF:(h + 1) * HALF], k.ps[0:64, 4 + h, :], ACT.Copy)\
                .then_inc(self.dl_ready.sem, 1)
        k.arrived(act, "mamba")
        act.activation(k.a_exp[:, :, :], k.a_log[:, :, :], ACT.Exp).then_inc(self.a_exp.sem, 1)
        for c in range(2):
            act.wait_ge(*self.z_ready.upto(c + 1))
            k.achain.link(act.activation(k.sp[:, c, :], k.sp[:, c, :], ACT.Exp))
            act.activation(k.sp[:, c, :], k.sp[:, c, :], ACT.Ln, bias=k.one_col).then_inc(self.lg_ready.sem, 1)
        with act.Fori(0, self.N // 2) as i:
            for q in range(2):
                n = 2 * i + q
                for c in range(2):
                    act.wait_ge(*self.scanned[c].upto(n))
                    act.wait_ge(*self.started.upto(1))
                    act.activation(k.dA[c][:, :, 1:S], k.delta[:, c, :].rearrange("p (b t) -> p b t", t=S)[:, :, 1:S],
                                   ACT.Exp, scale=k.a_neg[:, bass.ds(n + 16 * c, 1)]).then_inc(self.dA_ready[c].sem, 1)
                    if c == 0:
                        act.wait_ge(*self.c_done.upto(n + 1))
                        act.wait_ge(*self.sc_ready[1].upto(n - 1))
                        act.activation(k.cb[q][:, :], k.ps[:, 2:4, :].rearrange("p a n -> p (a n)"), ACT.Copy)\
                            .then_inc(self.c_ready.sem, 1)

    def vector(self, dve):
        k, c_ = self.k, self.k.dchain
        dve.wait_ge(*self.bc_done.upto(2))
        src = k.ps[:, 6:8, :].rearrange("p a n -> p (a n)")
        c_.link(dve.tensor_copy(k.bc3[0:96, :], src[0:96, :]))
        c_.link(dve.tensor_tensor(k.rest[:, :], src[0:96, :], k.bc3[0:96, :], ALU.subtract))
        c_.step(dve.tensor_copy(k.bc3[32:64, :], k.rest[32:64, :]))
        c_.link(dve.tensor_copy(k.bc3[64:96, :], k.rest[64:96, :]))
        c_.link(dve.tensor_tensor(k.rest[64:96, :], k.rest[64:96, :], k.bc3[64:96, :], ALU.subtract))
        dve.tensor_copy(k.bc3[64:96, :], k.rest[64:96, :]).then_inc(self.bc_ready.sem, 1)
        dve.wait_ge(*self.a_exp.upto(1))
        c_.step(dve.tensor_scalar(k.a_neg[:, :], k.a_exp[:, :, :].rearrange("p c n -> p (c n)"), -1.0, None, ALU.mult))
        for c in range(2):
            dve.wait_ge(*self.dt_done.upto(2 * c + 2))
            z = k.ps[:, 2 * c:2 * c + 2, :].rearrange("p a n -> p (a n)")
            j = k.col["b_dt"] + c
            c_.link(dve.tensor_scalar(k.delta[:, c, :], z, k.cols[:, j:j + 1], None, ALU.add))
            dve.scalar_tensor_tensor(k.sp[:, c, :], k.delta[:, c, :], -1.0, k.delta[:, c, :], ALU.mult, ALU.min)\
                .then_inc(self.z_ready.sem, 1)
        for c in range(2):
            dve.wait_ge(*self.lg_ready.upto(c + 1))
            c_.link(dve.scalar_tensor_tensor(k.delta[:, c, :], k.delta[:, c, :], 0.0, k.sp[:, c, :], ALU.max, ALU.add))
            dve.wait_ge(*self.u_ready.upto(4))
            dve.tensor_tensor(k.du[:, c, :], k.delta[:, c, :], k.u[:, c, :], ALU.mult).then_inc(self.du_ready.sem, 1)
        dve.wait_ge(*self.du_ready.upto(2))
        for c in range(2):
            c_.step(dve.memset(k.dA[c][:, :, 0:1], 0.0))
        dve.memset(k.s_last[:, :, :], 0.0).then_inc(self.started.sem, 1)
        dve.wait_ge(*self.started.upto(1))
        with dve.Fori(0, self.N) as n:
            for c in range(2):
                dve.wait_ge(*self.b_done.upto(n + 1))
                dve.wait_ge(*self.scanned[c].upto(n))
                dve.tensor_tensor(k.dbu[c][:, :], k.ps[:, 0:2, :].rearrange("p a n -> p (a n)"), k.du[:, c, :],
                                  ALU.mult).then_inc(self.dbu_done.sem, 1)
                dve.wait_ge(*self.dbu_done.upto(2 * n + (c + 1)))
                dve.wait_ge(*self.dA_ready[c].upto(n + 1))
                dve.wait_ge(*self.sc_ready[c].upto(n))
                dve.tensor_tensor_scan(k.s[c][:, :], k.dA[c][:, :, :].rearrange("p b t -> p (b t)"), k.dbu[c][:, :],
                                       0.0, ALU.mult, ALU.add).then_inc(self.scanned[c].sem, 1)
        for c in range(2):
            j = k.col["ssm_d"] + c
            dve.wait_ge(*self.y_done[c].upto(self.N))
            dve.wait_ge(*self.sc_ready[c].upto(self.N))
            c_.link(dve.tensor_scalar(k.s_last[:, c, :], k.s_last[:, c, :], k.cols[:, j:j + 1], None, ALU.mult))
            y = k.ps[:, 4 + 2 * c:6 + 2 * c, :].rearrange("p a (b t) -> p (a b) t", t=S)
            c_.link(dve.tensor_tensor(k.yg[:, c, :].rearrange("p (b t) -> p b t", t=S), y,
                                      bcast(k.s_last[:, c, :], 2, S), ALU.add))
            dve.wait_ge(*self.gate_ready.upto(4))
            dve.tensor_tensor(k.yg[:, c, :], k.yg[:, c, :], k.gate[:, c, :], ALU.mult).then_inc(self.yg_ready.sem, 1)
        for h in range(2):
            dve.wait_ge(*self.out_done.upto(h + 1))
            c_.link(dve.tensor_tensor(k.x[:, 4 * h:4 * h + 4, :], k.x[:, 4 * h:4 * h + 4, :],
                                      k.ps[:, h, :].rearrange("s (b d) -> s b d", d=D), ALU.add))
            token_stats(k, dve, k.x, range(4 * h, 4 * h + 4))

    def pool(self, pool):
        k = self.k
        pool.wait_ge(*self.turn.xT_ready.upto(2))
        k.arrived(pool, "mamba")
        for j in range(3):
            pool.tensor_copy(k.wx3[:, :, 32 * j:32 * j + 32], k.mb_wx[:, :, 64:96])
        pool.memset(k.zeros, 0.0)
        pool.memset(k.upad[:, 0, :, 0:self.K - 1], 0.0)
        pool.memset(k.upad[:, 1, :, 0:self.K - 1], 0.0).then_inc(self.pad_ready.sem, 1)
        pool.wait_ge(*self.started.upto(1))
        with pool.Fori(0, self.N // 2) as i:
            for q in range(2):
                n = 2 * i + q
                for c in range(2):
                    pool.wait_ge(*self.scanned[c].upto(n + 1))
                    last = k.s[c][:, :].rearrange("p (b t) -> p b t", t=S)[:, :, S - 1]
                    pool.tensor_tensor(k.s_last[:, c, :], k.s_last[:, c, :], last, ALU.add)
                    pool.wait_ge(*self.c_ready.upto(n + 1))
                    pool.wait_ge(*self.y_done[c].upto(n))
                    pool.tensor_tensor(k.sC[c][:, :], k.s[c][:, :], k.cb[q][:, :], ALU.mult)\
                        .then_inc(self.sc_ready[c].sem, 1)


class WideCross:

    H, DH, T = 16, 64, M + 1

    def __init__(self, k, norm, turn):
        self.k, self.norm, self.turn = k, norm, turn
        sig = k.sig
        self.clear = sig["wc_clear"].take(1)
        self.cT_ready = sig["at_xT_ready"].take(B)
        self.q_done = sig["wc_q_done"].take(B)
        self.k_done = sig["wc_k_done"].take(B)
        self.v_done = sig["at_qkv_done"].take(B)
        self.q_ready = sig["at_kv_ready"].take(B)
        self.k_ready = sig["wc_k_ready"].take(B)
        self.v_ready = sig["at_v_ready"].take(B)
        self.s_done = sig["at_s_done"].take(4 * B)
        self.max_ready = sig["at_max_ready"].take(4 * B)
        self.p_ready = sig["at_p_ready"].take(4 * B)
        self.pt_done = sig["at_pt_done"].take(4 * B)
        self.ptv_ready = sig["at_ptv_ready"].take(2 * B)
        self.pta_ready = sig["at_pta_ready"].take(2 * B)
        self.av_done = sig["wc_av_done"].take(4 * B)
        self.o_ready = sig["wc_o_ready"].take(4 * B)
        self.oT_done = sig["wc_oT_done"].take(2 * B)
        self.oT_ready = sig["wc_oT_ready"].take(2 * B)
        self.y_done = sig["at_y_done"].take(B)
        self.y_ready = sig["at_res_done"].take(B)

    def sync(self, sp, null_v):
        k = self.k
        sp.wait_ge(*self.clear.upto(1))
        for p in range(2):
            dst = k.wv[p][M:M + 1, :].rearrange("o (h w) -> o h w", h=self.H)[:, :, 0:self.DH]
            sp.dma_start(dst, bcast(null_v, 1, self.H)).then_inc(k.loads["null_v"], 16)

    def pool(self, pool):
        k = self.k
        pool.wait_ge(*self.turn.xT_ready.upto(2))
        k.arrived(pool, "null_k")
        for p in range(2):
            pool.tensor_copy(k.kT[p][:, :, M], k.null_k[:, 0:1].to_broadcast([P, 8]))
            t = pool.memset(k.wv[p], 1.0)
        t.then_inc(self.clear.sem, 1)
        with pool.Fori(0, B // 2) as i:
            for p in range(2):
                pool.wait_ge(*self.v_done.upto(2 * i))
                for c in range(2):
                    t = pool.tensor_copy(k.cT[p][:, c, :], k.ctxT[:, c, bass.ts(2 * i + p, M)])
                t.then_inc(self.cT_ready.sem, 1)

    def tensor(self, pe):
        k = self.k
        pe.wait_ge(*self.turn.xT_ready.upto(2))
        pe.wait_ge(*self.clear.upto(1))
        k.arrived(pe, "wide_cross")
        k.arrived(pe, "null_v")
        with pe.Fori(0, B // 2) as i:
            for p in range(2):
                self.project(pe, i, p)
            for u in range(4):
                self.scores(pe, i, 0, u)
            self.values(pe, i, 0)
            self.scores(pe, i, 1, 0)
            self.turn_out(pe, i, 0, 0)
            self.scores(pe, i, 1, 1)
            self.scores(pe, i, 1, 2)
            self.turn_out(pe, i, 0, 1)
            self.scores(pe, i, 1, 3)
            self.values(pe, i, 1)
            self.turn_out(pe, i, 1, 0)
            self.turn_out(pe, i, 1, 1)
            self.out(pe, i, 1)

    def project(self, pe, i, p):
        k = self.k
        b = 2 * i + p
        pe.wait_ge(*self.p_ready.upto(8 * i))
        pe.wait_ge(*self.q_ready.upto(b))
        for c in range(8):
            m = pe.matmul(k.ps[:, c // 4, c % 4 * P:(c % 4 + 1) * P], k.wq[:, c * P:(c + 1) * P],
                          k.xnT[:, bass.ts(b, P)], start=True, stop=True)
        m.then_inc(self.q_done.sem, 1)
        pe.wait_ge(*self.cT_ready.upto(b + 1))
        pe.wait_ge(*self.k_ready.upto(b))
        for c in range(8):
            for e in range(2):
                m = pe.matmul(k.ps[:, 2 + c // 4, c % 4 * P:c % 4 * P + M], k.wkv[:, e, c * P:(c + 1) * P],
                              k.cT[p][:, e, :], start=e == 0, stop=e == 1)
        m.then_inc(self.k_done.sem, 1)
        pe.wait_ge(*self.v_ready.upto(b))
        pe.wait_ge(*self.pta_ready.upto(4 * i))
        pe.wait_ge(*self.ptv_ready.upto(4 * i))
        for h in range(2):
            for e in range(2):
                m = pe.matmul(k.ps[0:M, 4 + h, :], k.cT[p][:, e, :], k.wkv[:, e, 1024 + h * HALF:1024 + (h + 1) * HALF],
                              start=e == 0, stop=e == 1)
        m.then_inc(self.v_done.sem, 1)

    def scores(self, pe, i, p, u):
        k = self.k
        b = 2 * i + p
        if u == 0:
            pe.wait_ge(*self.q_ready.upto(2 * i + 2))
            pe.wait_ge(*self.k_ready.upto(2 * i + 2))
            pe.wait_ge(*self.v_ready.upto(2 * i + 2))
        if p:
            pe.wait_ge(*self.p_ready.upto(8 * i + u + 1))
        r = slice(64 * (u % 2), 64 * (u % 2) + 64)
        for j in range(4):
            c = 4 * (u // 2) + j
            m = pe.matmul(k.ps[:, u, j * P:j * P + self.T], k.qT[p][r, c, :], k.kT[p][r, c, :], start=True, stop=True)
        m.then_inc(self.s_done.sem, 1)

    def values(self, pe, i, p):
        k = self.k
        b = 2 * i + p

        def turn(u):
            pe.wait_ge(*self.p_ready.upto(4 * b + u + 1))
            ready = self.pta_ready if u % 2 else self.ptv_ready
            pe.wait_ge(*ready.upto(2 * b + u // 2))
            for j in range(4):
                t = pe.transpose(k.ps[0:self.T, PT0 + u % 2, j * P:(j + 1) * P], k.p[p][:, 4 * u + j, 0:self.T], k.ident)
            t.then_inc(self.pt_done.sem, 1)

        def times_v(u):
            ready = self.pta_ready if u % 2 else self.ptv_ready
            pe.wait_ge(*ready.upto(2 * b + u // 2 + 1))
            pe.wait_ge(*self.o_ready.upto(4 * b + u))
            w = self.DH + 1
            for j in range(4):
                h = 2 * (4 * (u // 2) + j) + u % 2
                m = pe.matmul(k.ps[:, OB, j * w:(j + 1) * w], k.pT[u % 2][0:self.T, j, :],
                              k.wv[p][0:self.T, h * w:(h + 1) * w], start=True, stop=True)
            m.then_inc(self.av_done.sem, 1)

        turn(0)
        turn(1)
        if p:
            self.out(pe, i, 0)
        times_v(0)
        turn(2)
        times_v(1)
        turn(3)
        times_v(2)
        times_v(3)

    def turn_out(self, pe, i, p, half):
        k = self.k
        b = 2 * i + p
        pe.wait_ge(*self.o_ready.upto(4 * b + 2 * half + 2))
        pe.wait_ge(*self.oT_ready.upto(2 * b + half))
        for j in range(4):
            t = pe.transpose(k.ps[:, MB, j * P:(j + 1) * P], k.wo_in[:, (4 * half + j) * P:(4 * half + j + 1) * P], k.ident)
        t.then_inc(self.oT_done.sem, 1)

    def out(self, pe, i, p):
        k = self.k
        b = 2 * i + p
        pe.wait_ge(*self.oT_ready.upto(2 * b + 2))
        pe.wait_ge(*self.y_ready.upto(b))
        pe.wait_ge(*self.o_ready.upto(4 * b + 4))
        for c in range(8):
            m = pe.matmul(k.ps[:, OB, 3 * P:4 * P], k.woT[:, c, :], k.wout[:, c, :], start=c == 0, stop=c == 7)
        m.then_inc(self.y_done.sem, 1)

    def vector(self, dve):
        k, c = self.k, self.k.dchain
        with dve.Fori(0, B // 2) as i:
            c.enter(i, 2 * (1 + 4 + 4))
            for p in range(2):
                b = 2 * i + p
                dve.wait_ge(*self.q_done.upto(b + 1))
                dve.wait_ge(*self.s_done.upto(8 * i))
                f = k.qT[p][:, :, :].rearrange("p c t -> p (c t)")
                c.step(dve.tensor_copy(f[:, 0:HALF], k.ps[:, 0, :]))
                dve.tensor_copy(f[:, HALF:], k.ps[:, 1, :]).then_inc(self.q_ready.sem, 1)
            for p in range(2):
                b = 2 * i + p
                for u in range(4):
                    dve.wait_ge(*self.s_done.upto(4 * b + u + 1))
                    hs = slice(4 * u, 4 * u + 4)
                    src = k.ps[:, u, :].rearrange("q (h t) -> q h t", t=P)[:, :, 0:self.T]
                    c.link(dve.tensor_reduce(k.mx[p][:, hs], src, AX.X, ALU.max))
                    dve.tensor_scalar(k.nmx[p][:, hs], k.mx[p][:, hs], -0.125, None, ALU.mult)\
                        .then_inc(self.max_ready.sem, 1)
                if p:
                    self.collect(dve, 2 * i)
                self.turned(dve, b, 0)
                self.outputs(dve, b, 0)
                self.turned(dve, b, 2)
                for u in range(1, 4):
                    self.outputs(dve, b, u)
                if p:
                    self.collect(dve, b)
        c.leave(B // 2)
        dve.wait_ge(*self.y_ready.upto(B))
        token_stats(k, dve, k.r, range(B))

    def turned(self, dve, b, u):
        k = self.k
        dve.wait_ge(*self.pt_done.upto(4 * b + u + 1))
        dve.wait_ge(*self.av_done.upto(4 * b + max(u - 1, 0)))
        dve.tensor_copy(k.pT[0][0:self.T, :, :].rearrange("t h q -> t (h q)"), k.ps[0:self.T, PT0, :])\
            .then_inc(self.ptv_ready.sem, 1)

    def outputs(self, dve, b, u):
        k, c = self.k, self.k.dchain
        w = self.DH + 1
        dve.wait_ge(*self.av_done.upto(4 * b + u + 1))
        dve.wait_ge(*self.oT_done.upto(2 * b))
        O = k.ps[:, OB, 0:4 * w].rearrange("q (h w) -> q h w", w=w)
        c.link(dve.reciprocal(k.rec[0][:, 0:4], O[:, :, self.DH]))
        dst = k.wo_in[:, :].rearrange("q (c r d) -> q c r d", r=2, d=self.DH)[:, 4 * (u // 2):4 * (u // 2) + 4, u % 2, :]
        dve.tensor_tensor(dst, O[:, :, 0:self.DH], bcast(k.rec[0][:, 0:4], 2, self.DH), ALU.mult)\
            .then_inc(self.o_ready.sem, 1)
        dve.wait_ge(*self.o_ready.upto(4 * b + u + 1))

    def collect(self, dve, b):
        k = self.k
        dve.wait_ge(*self.y_done.upto(b + 1))
        dve.tensor_copy(k.r[:, b, :], k.ps[:, OB, 3 * P:4 * P]).then_inc(self.y_ready.sem, 1)

    def scalar(self, act):
        k = self.k
        w = self.DH + 1
        act.wait_ge(*self.clear.upto(1))
        with act.Fori(0, B // 2) as i:
            for p in range(2):
                b = 2 * i + p
                act.wait_ge(*self.k_done.upto(b + 1))
                act.wait_ge(*self.s_done.upto(8 * i))
                for h in range(2):
                    e = act.activation(k.kT[p][:, 4 * h:4 * h + 4, 0:M],
                                       k.ps[:, 2 + h, :].rearrange("p (c t) -> p c t", t=P)[:, :, 0:M], ACT.Copy)
                e.then_inc(self.k_ready.sem, 1)
                act.wait_ge(*self.v_done.upto(b + 1))
                act.wait_ge(*self.av_done.upto(8 * i))
                for h in range(2):
                    e = act.activation(k.wv[p][0:M, 8 * h * w:8 * (h + 1) * w].rearrange("t (h w) -> t h w", w=w)[:, :, 0:self.DH],
                                       k.ps[0:M, 4 + h, :].rearrange("t (h d) -> t h d", d=self.DH), ACT.Copy)
                e.then_inc(self.v_ready.sem, 1)
            for p in range(2):
                b = 2 * i + p
                for u in range(4):
                    act.wait_ge(*self.max_ready.upto(4 * b + u + 1))
                    act.wait_ge(*self.pt_done.upto(8 * i))
                    for j in range(4):
                        h = 4 * u + j
                        e = act.activation(k.p[p][:, h, 0:self.T], k.ps[:, u, j * P:j * P + self.T], ACT.Exp,
                                           bias=k.nmx[p][:, h:h + 1], scale=0.125)
                    e.then_inc(self.p_ready.sem, 1)
                    if p and u == 0:
                        self.turned_out(act, 2 * i, 0)
                    if p and u == 2:
                        self.turned_out(act, 2 * i, 1)
                for u in (1, 3):
                    act.wait_ge(*self.pt_done.upto(4 * b + u + 1))
                    act.wait_ge(*self.av_done.upto(4 * b + u - 1))
                    act.activation(k.pT[1][0:self.T, :, :].rearrange("t h q -> t (h q)"), k.ps[0:self.T, PT0 + 1, :],
                                   ACT.Copy).then_inc(self.pta_ready.sem, 1)
                if p:
                    self.turned_out(act, b, 0)
                    self.turned_out(act, b, 1)

    def turned_out(self, act, b, half):
        k = self.k
        act.wait_ge(*self.oT_done.upto(2 * b + half + 1))
        act.wait_ge(*self.y_done.upto(b))
        act.activation(k.woT[:, 4 * half:4 * half + 4, :].rearrange("p c t -> p (c t)"), k.ps[:, MB, :], ACT.Copy)\
            .then_inc(self.oT_ready.sem, 1)


ROWS = [("relu_b1", 32), ("gelu_b1", 32), ("gate_b1", 32), ("dense_b1", 4), ("g_res0", 1), ("g_res3", 1),
        ("gamma", 1), ("beta", 1), ("conv_b", 2), ("b_dt", 2), ("ssm_d", 2), ("ln1_g", 1), ("ln1_b", 1)]
COL = {name: sum(n for _, n in ROWS[:j]) for j, (name, _) in enumerate(ROWS)}
NROWS = sum(n for _, n in ROWS)
WIDE = ["ln1_g", "ln1_b", "ln2_g", "ln2_b", "dense_b2", "b_in0", "b_in3", "g_init0", "g_init3", "ln_scale", "ln_bias"]
LOADS = {"x": 1, "first": 1, "l0": 6, "lens": 1, "rows": len(ROWS), "routers": 3, "gates": 2, "pool_consts": 1,
         "lower": 1, "masks": 1, "ctx": 1, "keys": 2, "wide": len(WIDE) + 4, "b2": 24, "bit": 11, "l3": 2, "mamba": 6, "null_k": 2,
         "wide_cross": 3, "null_v": 2}


def constants():
    f = np.float32
    theta = (f(1.0) / f(10000.0) ** (np.arange(0, 8, 2, dtype=f) / f(8))).astype(f)
    angle = np.outer(np.arange(S, dtype=f), theta).astype(f)
    angle = np.tile(np.concatenate([angle, angle], axis=1), (1, 16)).T
    group = np.arange(P) % 32
    decay = -np.expm1(-DEPOOL_EPS)
    lag = np.arange(M)[None, :] - np.arange(M)[:, None]
    filt = np.zeros((P, P))
    filt[:M, :M] = np.where(lag >= 0, np.exp(-DEPOOL_EPS) * decay ** np.maximum(lag, 0), 0.0)
    lower = np.broadcast_to((np.arange(8)[None, :] < np.arange(8)[:, None]).reshape(1, 64), (P, 64))
    early = np.concatenate([np.eye(P), np.cos(angle), np.sin(angle), group[:, None] // 8 == np.arange(4),
                            group[:, None] // 16 == np.arange(2)], axis=1)
    late = np.concatenate([np.arange(P)[:, None] <= np.arange(P), np.broadcast_to(np.arange(P), (P, P)), filt, lower], axis=1)
    off = np.arange(S)[:, None] - np.arange(S)[None, :]
    causal = np.where(off >= 0, 0.0, NEG)
    band = np.where(np.abs(off) <= 32, 0.0, NEG)
    select = np.zeros((P, 32, P))
    for part in range(3):
        select[32 * part + np.arange(32), np.arange(32)] = 1.0
    half = np.concatenate([np.eye(P), causal, band, select.reshape(P, 32 * P)], axis=1)
    return early.astype(f), late.astype(f), (half.astype(f).view(np.uint32) >> 16).astype(np.uint16)


class Setup:

    def __init__(self, k):
        self.k = k
        t = lambda name, n: k.sig["su_" + name].take(n)
        self.w_turned = t("w_turned", 2)
        self.w_ready = t("w_ready", 2)
        self.flipped = t("flipped", 1)
        self.small_turned = t("small_turned", 2)
        self.small_ready = t("small_ready", 2)
        self.idx_ready = t("idx_ready", 1)
        self.idx_turned = t("idx_turned", 1)
        self.idxT_ready = t("idxT_ready", 1)
        self.edges_ready = t("edges_ready", 1)
        self.count_done = t("count_done", 1)
        self.edge_ready = t("edge_ready", 1)
        self.plug_done = t("plug_done", 1)
        self.plug_ready = t("plug_ready", 1)
        self.pick_ready = t("pick_ready", 1)
        self.pick_turned = t("pick_turned", 2)
        self.pickT_ready = t("pickT_ready", 2)
        self.ctx_turned = t("ctx_turned", 4)
        self.ctxT_ready = t("ctxT_ready", 4)
        self.ms_ready = t("ms_ready", 1)
        self.ctxn_ready = t("ctxn_ready", 1)
        self.spread_done = t("spread_done", 2)
        self.spread_ready = t("spread_ready", 2)
        self.pooled_done = t("pooled_done", 2)
        self.pooled_in = t("pooled_in", 2)
        self.keyrow = t("keyrow", 1)

    def tensor_first(self, pe):
        k = self.k
        k.arrived(pe, "first")
        k.arrived(pe, "l0")
        for j in range(6):
            t = pe.transpose(k.ps[:, PT0 + j // 4, j % 4 * P:(j % 4 + 1) * P], k.w_raw[:, j, :], k.ident)
            if j in (3, 5):
                t.then_inc(self.w_turned.sem, 1)
        k.arrived(pe, "rows")
        pe.transpose(k.ps[:, 0, 0:NROWS], k.rows[0:NROWS, :], k.ident[0:NROWS, 0:NROWS]).then_inc(self.small_turned.sem, 1)
        k.arrived(pe, "routers")
        pe.transpose(k.ps[:, 6, 0:20], k.router_rows[0:20, :], k.ident[0:20, 0:20]).then_inc(self.small_turned.sem, 1)
        pe.wait_ge(*self.idx_ready.upto(1))
        pe.transpose(k.ps[0:M, 1, 0:B], k.idx[0:B, :], k.ident[0:B, 0:B]).then_inc(self.idx_turned.sem, 1)
        pe.wait_ge(*self.edges_ready.upto(1))
        for b in range(B):
            m = pe.matmul(k.ps[:, 2, 2 * b:2 * b + 1], k.edges[0:M, b, :], k.ones[0:M, 0:1], start=True, stop=True)
        m.then_inc(self.count_done.sem, 1)
        k.arrived(pe, "pool_consts")
        pe.wait_ge(*self.edge_ready.upto(1))
        pe.matmul(k.ps[:, 3, 0:B], k.upto_here, k.edge[:, :], start=True, stop=True).then_inc(self.plug_done.sem, 1)
        pe.wait_ge(*self.w_ready.upto(2))
        pe.wait_ge(*self.small_ready.upto(2))
        pe.wait_ge(*self.plug_ready.upto(1))
        pe.wait_ge(*self.flipped.upto(1))

    def scalar_first(self, act):
        k = self.k
        for j in range(2):
            act.wait_ge(*self.w_turned.upto(j + 1))
            n = 4 - 2 * j
            act.activation(k.wT[:, 4 * j:4 * j + n, :].rearrange("p j e -> p (j e)"), k.ps[:, PT0 + j, 0:n * P],
                           ACT.Copy).then_inc(self.w_ready.sem, 1)
        act.wait_ge(*self.small_turned.upto(1))
        act.activation(k.cols[:, :], k.ps[:, 0, 0:NROWS], ACT.Copy).then_inc(self.small_ready.sem, 1)
        act.wait_ge(*self.small_turned.upto(2))
        act.activation(k.routerT[:, :], k.ps[:, 6, 0:20], ACT.Copy).then_inc(self.small_ready.sem, 1)
        act.wait_ge(*self.idx_turned.upto(1))
        act.activation(k.idxT[0:M, :], k.ps[0:M, 1, 0:B], ACT.Copy).then_inc(self.idxT_ready.sem, 1)

    def vector_first(self, dve):
        k, c = self.k, self.k.dchain
        k.arrived(dve, "lens")
        c.link(dve.tensor_copy(k.lens[:, :], k.lens_i[:, :]))
        c.link(dve.tensor_tensor_scan(k.cum[:, :], k.ones[0:B, 0:M], k.lens[:, :], 0.0, ALU.mult, ALU.add))
        c.link(dve.tensor_scalar(k.cum[:, :], k.cum[:, :], -1.0, None, ALU.add))
        c.link(dve.tensor_scalar(k.lens[:, :], k.cum[:, :], 0.0, float(S), ALU.is_lt, ALU.mult))
        dve.tensor_tensor(k.idx[:, :], k.cum[:, :], k.lens[:, :], ALU.add).then_inc(self.idx_ready.sem, 1)
        dve.wait_ge(*self.w_ready.upto(1))
        for j in range(2):
            src = k.wT[:, j, :].rearrange("p (h j) -> p h j", j=8)
            dst = k.w_flip[:, j, :].rearrange("p (h j) -> p h j", j=8)
            c.step(dve.tensor_scalar(dst[:, :, 0:4], src[:, :, 4:8], -1.0, None, ALU.mult))
            t = dve.tensor_copy(dst[:, :, 4:8], src[:, :, 0:4])
            c.step(t) if j == 0 else t.then_inc(self.flipped.sem, 1)
        dve.wait_ge(*self.count_done.upto(1))
        dve.tensor_scalar(k.edge[:, :], k.ps[:, 2, 0:2 * B].rearrange("p (b o) -> p b o", o=2)[:, :, 0], 1.0, None, ALU.min)\
            .then_inc(self.edge_ready.sem, 1)
        dve.wait_ge(*self.plug_done.upto(1))
        c.link(dve.tensor_scalar(k.plug[:, :], k.ps[:, 3, 0:B], -1.0, 0.0, ALU.add, ALU.max))
        dve.tensor_scalar(k.plug[:, :], k.plug[:, :], float(M - 1), None, ALU.min).then_inc(self.plug_ready.sem, 1)
        k.arrived(dve, "ctx")
        for b in range(B):
            c.step(dve.bn_stats(k.bn[0:M, b, :], k.ctx[0:M, b * CTX:(b + 1) * CTX]))
        c.settle()
        for b in range(B):
            c.step(dve.bn_aggr(k.ctx_mv[0:M, b, :], k.bn[0:M, b, :]))
        c.settle()
        c.link(dve.tensor_tensor(k.ctx_ms[0:M, :], k.ctx_mv[0:M, :, 0], k.ctx_mv[0:M, :, 0], ALU.mult))
        dve.scalar_tensor_tensor(k.ctx_ms[0:M, :], k.ctx_ms[0:M, :], LN_EPS, k.ctx_mv[0:M, :, 1], ALU.add, ALU.add)\
            .then_inc(self.ms_ready.sem, 1)
        k.arrived(dve, "keys")
        c.link(dve.tensor_copy(k.key_row[0:1, :], k.key_mask[:, :]))
        c.link(dve.tensor_scalar(k.key_row[0:1, :], k.key_row[0:1, :], -1.0, -NEG, ALU.add, ALU.mult))
        dve.tensor_scalar(k.key_row[0:1, :], k.key_row[0:1, :], k.key_b[0:1, 0:1], None, ALU.add)\
            .then_inc(self.keyrow.sem, 1)

    def pool_first(self, pool):
        k, c = self.k, self.k.pchain
        k.arrived(pool, "pool_consts")
        pool.wait_ge(*self.idxT_ready.upto(1))
        for b in range(B):
            t = pool.tensor_scalar(k.edges[0:M, b, :], k.iota[0:M, :], k.idxT[0:M, b:b + 1], None, ALU.is_equal)
        t.then_inc(self.edges_ready.sem, 1)
        pool.wait_ge(*self.plug_ready.upto(1))
        for b in range(B):
            t = pool.tensor_scalar(k.pick[:, b, :], k.iota[:, 0:M], k.plug[:, b:b + 1], None, ALU.is_equal)
        t.then_inc(self.pick_ready.sem, 1)
        pool.wait_ge(*self.ms_ready.upto(1))
        c.link(pool.tensor_tensor(k.ctx_ms[0:M, :], k.ctx_ms[0:M, :], bcast(k.minus_half[0:M, 0], 1, B), ALU.pow))
        t = pool.tensor_tensor(k.ctx_n[0:M, :, :], k.ctx[0:M, :].rearrange("p (b c) -> p b c", c=CTX)[:, :, 0:D],
                               bcast(k.ctx_ms[0:M, :], 2, D), ALU.mult)
        t.then_inc(self.ctxn_ready.sem, 1)

    def tensor_second(self, pe):
        k = self.k
        k.arrived(pe, "ctx")
        for b in range(B):
            for c in range(2):
                j = 2 * b + c
                if j >= 8 and j % 4 == 0:
                    pe.wait_ge(*self.ctxT_ready.upto(j // 4 - 1))
                t = pe.transpose(k.ps[:, j // 4 % 2, j % 4 * P:j % 4 * P + M],
                                 k.ctx[0:M, b * CTX + c * P:b * CTX + (c + 1) * P], k.ident[0:M, 0:M])
                if j % 4 == 3:
                    t.then_inc(self.ctx_turned.sem, 1)
        pe.wait_ge(*self.pick_ready.upto(1))
        for b in range(B):
            t = pe.transpose(k.ps[0:M, 2 + b // 4, b % 4 * P:(b % 4 + 1) * P], k.pick[:, b, :], k.ident)
            if b % 4 == 3:
                t.then_inc(self.pick_turned.sem, 1)
        pe.wait_ge(*self.ctxn_ready.upto(1))
        for h in range(2):
            pe.matmul(k.ps[0:M, PT0 + h, :], k.filter[0:M, 0:M],
                      k.ctx_n[0:M, 4 * h:4 * h + 4, :].rearrange("p b d -> p (b d)"), start=True, stop=True)\
                .then_inc(self.spread_done.sem, 1)
        for b in range(B):
            pe.wait_ge(*self.pickT_ready.upto(b // 4 + 1))
            pe.wait_ge(*self.spread_ready.upto(b // 4 + 1))
            m = pe.matmul(k.ps[:, 6 + b // 4, b % 4 * P:(b % 4 + 1) * P], k.pickT[0:M, b * P:(b + 1) * P],
                          k.patches[0:M, b * D:(b + 1) * D], start=True, stop=True)
            if b % 4 == 3:
                m.then_inc(self.pooled_done.sem, 1)

    def scalar_second(self, act):
        k = self.k
        for j in range(4):
            act.wait_ge(*self.ctx_turned.upto(j + 1))
            src = k.ps[:, j % 2, :].rearrange("p (b c t) -> p c b t", b=2, c=2)[:, :, :, 0:M]
            dst = k.ctxT[:, :, 2 * j * M:2 * (j + 1) * M].rearrange("p c (b t) -> p c b t", t=M)
            for c in range(2):
                t = act.activation(dst[:, c], src[:, c], ACT.Copy)
            t.then_inc(self.ctxT_ready.sem, 1)
        for h in range(2):
            act.wait_ge(*self.pick_turned.upto(h + 1))
            act.activation(k.pickT[0:M, h * HALF:(h + 1) * HALF], k.ps[0:M, 2 + h, :], ACT.Copy)\
                .then_inc(self.pickT_ready.sem, 1)
        for h in range(2):
            act.wait_ge(*self.spread_done.upto(h + 1))
            act.activation(k.patches[0:M, h * HALF:(h + 1) * HALF], k.ps[0:M, PT0 + h, :], ACT.Copy)\
                .then_inc(self.spread_ready.sem, 1)
        for h in range(2):
            act.wait_ge(*self.pooled_done.upto(h + 1))
            act.activation(k.pooled_raw[:, 4 * h:4 * h + 4, :].rearrange("p b d -> p (b d)"), k.ps[:, 6 + h, :], ACT.Copy)\
                .then_inc(self.pooled_in.sem, 1)

    def pool_second(self, pool):
        k, c = self.k, self.k.pchain
        k.arrived(pool, "wide")
        pool.wait_ge(*self.pooled_in.upto(2))
        c.link(pool.tensor_tensor(k.pooled0[:, :, :], k.pooled_raw[:, :, :], bcast(k.wide["g_init0"], 1, B), ALU.mult))
        pool.tensor_tensor(k.pooled0[:, :, :], k.pooled0[:, :, :], bcast(k.wide["b_in0"], 1, B), ALU.add)\
            .then_inc(k.pooled_ready.sem, 1)

    def pool_third(self, pool):
        k, c = self.k, self.k.pchain
        c.link(pool.tensor_tensor(k.pooled3[:, :, :], k.pooled_raw[:, :, :], bcast(k.wide["g_init3"], 1, B), ALU.mult))
        pool.tensor_tensor(k.pooled3[:, :, :], k.pooled3[:, :, :], bcast(k.wide["b_in3"], 1, B), ALU.add)\
            .then_inc(k.pooled_ready.sem, 1)


class BitWeights:

    def __init__(self, k):
        self.k = k
        t = lambda name, n: k.sig["bw_" + name].take(n)
        self.scale_ready = t("scale_ready", 1)
        self.rounded = t("rounded", 1)
        self.turned = t("turned", 9)
        self.in_sbuf = t("in_sbuf", 9)

    def vector(self, dve):
        k, c = self.k, self.k.dchain
        k.arrived(dve, "bit")
        for j, (raw, n, width) in enumerate(((k.bit_raw1, 18, P), (k.bit_raw2, 9, 2 * P))):
            sc = k.bit_scale[:, 18 * j:18 * j + n]
            c.link(dve.tensor_reduce(sc, raw[:, :, :], AX.X, ALU.add, apply_absolute_value=True))
            c.link(dve.tensor_scalar(sc, sc, 1.0 / width, 1e-5, ALU.mult, ALU.max))
        c.step(dve.tensor_scalar(k.bit_half[:, :], k.bit_scale[:, :], 0.5, None, ALU.mult))
        dve.tensor_scalar(k.bit_mhalf[:, :], k.bit_scale[:, :], -0.5, None, ALU.mult).then_inc(self.scale_ready.sem, 1)

    def pool(self, pool):
        k, c = self.k, self.k.pchain
        pool.wait_ge(*self.scale_ready.upto(1))
        for j, (raw, n, width) in enumerate(((k.bit_raw1, 18, P), (k.bit_raw2, 9, 2 * P))):
            for t in range(n):
                q = slice(18 * j + t, 18 * j + t + 1)
                c.step(pool.tensor_scalar(k.bit_up[:, 0:width], raw[:, t, :], k.bit_half[:, q], k.bit_scale[:, q],
                                          ALU.is_gt, ALU.mult))
                c.link(pool.tensor_scalar(k.bit_down[:, 0:width], raw[:, t, :], k.bit_mhalf[:, q], k.bit_scale[:, q],
                                          ALU.is_lt, ALU.mult))
                last = pool.tensor_tensor(raw[:, t, :], k.bit_up[:, 0:width], k.bit_down[:, 0:width], ALU.subtract)
                if j == 1 and t == n - 1:
                    last.then_inc(self.rounded.sem, 1)
                else:
                    c.link(last)

    def tensor(self, pe):
        k = self.k
        pe.wait_ge(*self.rounded.upto(1))
        for e in range(9):
            if e >= 2:
                pe.wait_ge(*self.in_sbuf.upto(e - 1))
            for c in range(2):
                pe.transpose(k.ps[:, e % 2, c * P:(c + 1) * P], k.bit_raw1[:, 2 * e + c, :], k.ident)
            for c in range(2):
                t = pe.transpose(k.ps[:, e % 2, (2 + c) * P:(3 + c) * P], k.bit_raw2[:, e, c * P:(c + 1) * P], k.ident)
            t.then_inc(self.turned.sem, 1)

    def scalar(self, act):
        k = self.k
        for e in range(9):
            act.wait_ge(*self.turned.upto(e + 1))
            act.activation(k.bit_w1T[:, e * 256:(e + 1) * 256], k.ps[:, e % 2, 0:256], ACT.Copy)
            act.activation(k.bit_w2T[:, e * 256:(e + 1) * 256], k.ps[:, e % 2, 256:512], ACT.Copy)\
                .then_inc(self.in_sbuf.sem, 1)


class Arena:

    def __init__(self, tensor):
        self.tensor, self.at, self.most = tensor, 0, 0

    def take(self, *shape, dtype=F32):
        n = int(np.prod(shape))
        words = n if dtype == F32 else (n + 1) // 2
        v = self.tensor[:, self.at:self.at + words]
        if dtype == BF16:
            v = v.bitcast(BF16)
        self.at += (words + 7) // 8 * 8
        self.most = max(self.most, self.at)
        assert self.at <= self.tensor.shape[1], (self.at, self.tensor.shape)
        if len(shape) == 2:
            v = v.rearrange("p (a b) -> p a b", a=shape[0])
        elif len(shape) == 3:
            v = v.rearrange("p (a b c) -> p a b c", a=shape[0], b=shape[1])
        return v

    def rewind(self, at):
        self.at = at


class Kit:

    def arrived(self, eng, group):
        eng.wait_ge(self.loads[group], 16 * LOADS[group])


SIGNALS = """at_vb_ready at_rec_ready at_pn_ready at_vp_done at_qk_done at_turned_qk at_q_ready result at_v_clear wc_clear var_ready rstd_ready xn_ready x_turned xnT_ready
at_xT_ready at_kv_ready at_v_ready at_s_done at_max_ready at_p_ready at_pt_done at_ptv_ready at_pta_ready
at_av_even at_av_odd at_o_ready at_qkv_done at_oT_done at_oT_ready at_y_done at_res_done
ff_h_done ff_h_ready ff_o_done ff_acc_done ff_router_done ff_w_ready ff_w_turned ff_wT_ready ff_b2_done
ff_l_ready ff_e_ready dp_pooled_in dp_y_done an_bias_in dense_start
mb_in_done mb_u_in mb_gate_ready mb_conv_done mb_u_ready mb_dl_done mb_dl_ready mb_bc_done mb_bc_ready mb_dt_done
mb_z_ready mb_lg_ready mb_du_ready mb_a_exp mb_started mb_pad_ready mb_b_done mb_c_done mb_c_ready mb_dA_ready0 mb_dA_ready1
mb_dbu_done mb_scanned0 mb_scanned1 mb_sc_ready0 mb_sc_ready1 mb_y_done0 mb_y_done1 mb_yg_ready mb_out_done
wc_q_done wc_k_done wc_k_ready wc_av_done wc_o_ready wc_oT_done wc_oT_ready
su_w_turned su_w_ready su_flipped su_small_turned su_small_ready su_idx_ready su_idx_turned su_idxT_ready
su_edges_ready su_count_done su_edge_ready su_plug_done su_plug_ready su_pick_ready su_pick_turned su_pickT_ready
su_ctx_turned su_ctxT_ready su_ms_ready su_ctxn_ready su_spread_done su_spread_ready su_pooled_done su_pooled_in
su_keyrow su_pooled_ready bw_scale_ready bw_rounded bw_turned bw_in_sbuf""".split()


CREDITS = {
    "tensor": {"ff_o_done": 2, "at_s_done": 1, "at_pt_done": 5, "at_av_even": 1, "at_av_odd": 1, "at_qkv_done": 1,
               "at_oT_done": 1, "at_y_done": 1, "mb_y_done0": 1, "mb_y_done1": 1, "wc_av_done": 1, "wc_oT_done": 1},
    "scalar": {"ff_h_ready": 4, "at_v_ready": 1, "at_p_ready": 1, "at_pta_ready": 1, "at_oT_ready": 1, "mb_c_ready": 1,
               "wc_k_ready": 1, "wc_oT_ready": 1},
    "vector": {"ff_acc_done": 1, "at_kv_ready": 1, "at_ptv_ready": 1, "at_o_ready": 1, "at_res_done": 1,
               "mb_dbu_done": 1, "mb_scanned0": 1, "mb_scanned1": 1, "wc_o_ready": 1},
    "pool": {"mb_sc_ready0": 1, "mb_sc_ready1": 1},
}
KEEP_WORDS, WORK_WORDS = 38000, 15200
PRESETS = 6


def decoder(nc, a, out):
    ctx = ExitStack()
    with ctx:
        k = Kit()
        k.sig = {n: Signal(ctx.enter_context(nc.semaphore(n))) for n in SIGNALS}
        k.loads = {n: ctx.enter_context(nc.semaphore("ld_" + n)) for n in LOADS}
        k.ring_loaded = [Signal(ctx.enter_context(nc.semaphore(f"ring_loaded{p}"))) for p in range(2)]
        k.ring_copied = [Signal(ctx.enter_context(nc.semaphore(f"ring_copied{p}"))) for p in range(2)]
        preset = ctx.enter_context(nc.semaphore("preset"))
        stored = ctx.enter_context(nc.semaphore("stored"))
        chains = [ctx.enter_context(nc.semaphore(n)) for n in ("vector_chain", "scalar_chain", "pool_chain")]
        for credits in CREDITS.values():
            for name, n in credits.items():
                k.sig[name].take(n)
        k.pooled_ready = k.sig["su_pooled_ready"].take(2)

        keep = Arena(ctx.enter_context(nc.sbuf_tensor("keep", [P, KEEP_WORDS], F32)))
        work = Arena(ctx.enter_context(nc.sbuf_tensor("work", [P, WORK_WORDS], F32)))
        k.ps = ctx.enter_context(nc.psum_tensor("banks", [P, 8, HALF], F32))
        early = keep.take(3 * P + 6)
        k.ident, k.cosT, k.sinT = (early[:, j * P:(j + 1) * P] for j in range(3))
        k.head_of4, k.head_of2 = early[:, 3 * P:3 * P + 4], early[:, 3 * P + 4:3 * P + 6]
        lower = keep.take(64)
        k.lower = lower.rearrange("p (a b) -> p a b", a=8)
        halves = keep.take(35 * P, dtype=BF16)
        k.ident16, k.causal, k.band = (halves[:, j * P:(j + 1) * P] for j in range(3))
        k.sel = halves[0:96, 3 * P:35 * P]
        k.x, k.xn, k.r = (keep.take(B, D) for _ in range(3))
        k.xnT = keep.take(TOK)
        k.mv, k.bn = keep.take(B, 2), keep.take(B, 6)
        k.var_eps, k.rstd, k.root1, k.root2, k.ms = (keep.take(B) for _ in range(5))
        k.minus_half, k.ones = keep.take(1), keep.take(P)
        k.one_col = k.ones[:, 0:1]
        k.cols, k.rows, k.col = keep.take(NROWS), keep.take(P), COL
        k.router_rows, k.routerT = keep.take(P), keep.take(20)
        gates = keep.take(2, 8)
        k.router = {"relu": gates[:, 0, :], "gate": gates[:, 1, :], "gelu": k.routerT[:, 0:12], "bit": k.routerT[:, 12:20]}
        wide = keep.take(len(WIDE), D)
        k.wide = {n: wide[:, j, :] for j, n in enumerate(WIDE)}
        k.ln1_g, k.ln1_b, k.dense_b2 = k.wide["ln1_g"], k.wide["ln1_b"], k.wide["dense_b2"]
        bias = keep.take(36)
        k.router_b = {"relu": bias[:, 0:8], "gelu": bias[:, 8:16], "gate": bias[:, 16:24], "bit": bias[:, 28:36]}
        k.lang_b = bias[:, 24:28]
        k.wT, k.w_flip = keep.take(6, P), keep.take(2, P)
        k.l0_qk = [k.wT[:, 0, :], k.w_flip[:, 0, :], k.wT[:, 1, :], k.w_flip[:, 1, :]]
        k.l0_wvT, k.l0_woT = k.wT[:, 2, :], k.wT[:, 3, :]
        l3_qkv, k.l3_wo = keep.take(3 * D), keep.take(D)
        k.l3_qk, k.l3_wv = [l3_qkv[:, 0:D], l3_qkv[:, D:2 * D]], l3_qkv[:, 2 * D:3 * D]
        blocks = keep.take(3, TOK)
        k.b2_blocks = {n: blocks[0:64, j, :] for j, n in enumerate(("relu", "gelu", "gate"))}
        k.ctx, k.ctxT = keep.take(B * CTX), keep.take(2, B * M)
        k.pooled_raw = keep.take(B, D)
        k.key_row, k.key_b, k.null_k = keep.take(B * M), keep.take(1), keep.take(1)
        k.bit_w1T, k.bit_w2T = keep.take(9 * 256), keep.take(9 * 256)
        k.mb_win, k.mb_conv, k.mb_wx, k.wx3 = keep.take(4 * P), keep.take(8, 2 * P), keep.take(2, 96), keep.take(2, 96)
        k.mb_wdt, k.mb_wout = keep.take(2 * P)[0:64, :], keep.take(2, D)
        k.a_log, k.a_exp, k.a_neg, k.s_last = keep.take(2, 16), keep.take(2, 16), keep.take(32), keep.take(2, B)
        k.w, k.logit, k.lang, k.lp = keep.take(64), keep.take(B, 8), keep.take(B, 4), keep.take(B, 5)
        k.peak, k.rank, k.wT_route = keep.take(B), keep.take(B, 8), keep.take(P)
        k.more, k.same = keep.take(B, 8, 8), keep.take(B, 8, 8)
        k.w1 = [keep.take(HALF) for _ in range(2)]
        k.w2 = [keep.take(4, D) for _ in range(2)]
        k.bit_scale, k.bit_half, k.bit_mhalf = (keep.take(27) for _ in range(3))
        k.bit_up, k.bit_down = keep.take(2 * P), keep.take(2 * P)
        at = keep.at
        k.bit_raw1, k.bit_raw2 = keep.take(18, P), keep.take(9, 2 * P)
        keep.rewind(at)
        k.wq, k.wkv, k.wout = keep.take(8 * P), keep.take(2, 2048), keep.take(8, D)

        k.p = [work.take(16, P) for _ in range(2)]
        k.pT = [work.take(4, P) for _ in range(2)]
        k.mx, k.nmx = ([work.take(16) for _ in range(2)] for _ in range(2))
        k.total, k.rec = ([work.take(16) for _ in range(2)] for _ in range(2))
        at = work.at
        k.terms = [v.rearrange("p h t -> p (h t)") for v in k.p]
        k.q = [work.take(P) for _ in range(2)]
        k.q_all, k.k_all, k.v_tok = work.take(TOK), work.take(TOK), work.take(B, D)
        k.kb = [work.take(4, P) for _ in range(2)]
        k.oT = work.take(P)
        late = work.take(3 * P)
        k.upto_here, k.iota, k.filter = (late[:, j * P:(j + 1) * P] for j in range(3))
        k.idxT, k.edge, k.plug = work.take(B), work.take(B), work.take(B)
        k.ctx_mv, k.ctx_ms = work.take(B, 2), work.take(B)
        k.w_raw = k.terms[0][:, TOK:TOK + 6 * P].rearrange("p (a b) -> p a b", a=6)
        k.edges = k.terms[1][:, TOK:2 * TOK].rearrange("p (b t) -> p b t", b=B)
        k.pickT, k.patches = (v[:, 0:TOK] for v in k.terms)
        k.lens, k.cum, k.idx, lens = (k.k_all[0:B, j * M:(j + 1) * M] for j in range(4))
        k.lens_i, k.key_mask = lens.bitcast(I32), k.q_all[0:1, 0:B * M].bitcast(I32)
        k.pick = k.pooled_raw.rearrange("p b t -> p (b t)")[:, 0:B * M].rearrange("p (b t) -> p b t", b=B)
        k.ctx_n = k.r
        k.pooled0, k.pooled3 = k.edges, k.pooled_raw
        after_attention = work.at
        k.v_block = [work.take(16, P) for _ in range(2)]
        work.rewind(after_attention)
        k.hT = [work.take(4, HALF) for _ in range(2)]
        work.rewind(at)
        k.qT = [work.take(8, P) for _ in range(2)]
        k.kT = [work.take(8, M + 1) for _ in range(2)]
        k.wv = [work.take(16 * 65) for _ in range(2)]
        k.cT = [work.take(2, M) for _ in range(2)]
        k.wo_in, k.woT = work.take(1024), work.take(8, P)
        work.rewind(0)
        k.gate, k.u = work.take(2, TOK), work.take(2, TOK)
        k.delta, k.du, k_sC = work.take(2, TOK), work.take(2, TOK), work.take(2, TOK)
        at = work.at
        k.sp, s2 = work.take(2, TOK), work.take(2, TOK)
        end = work.at
        work.rewind(at)
        k.upad = work.take(2, 8, 131)
        work.rewind(end)
        k.bc3 = work.take(TOK, dtype=BF16)[0:96, :]
        k.dA = [k.u[:, c, :].rearrange("p (b t) -> p b t", t=S) for c in range(2)]
        k.yg, k.dbu = k.du, [k.sp[:, c, :] for c in range(2)]
        k.s, k.sC = [s2[:, c, :] for c in range(2)], [k_sC[:, c, :] for c in range(2)]
        k.dlT, k.rest = s2[0:64, 0, :], s2[0:96, 1, :]
        k.cb = [k.xnT, k.r[:, :, :].rearrange("p b d -> p (b d)")]
        k.zeros = k.cb[1][:, 0:HALF]
        k.wT_small = k.wT_route[0:64, :]

        setup = Setup(k)
        bits = BitWeights(k)
        n0 = Norm(k)
        t0 = Turn(k, n0)
        l0_attn = Attention(k, n0, t0, "rope")
        n1 = Norm(k, again=True)
        t1 = Turn(k, n1)
        l0_cross = Depool(k, n1, t1, k.wT[:, 4, :], k.pooled0, 1)
        n2 = Norm(k)
        t2 = Turn(k, n2)
        l0_ffn = Experts(k, n2, t2, "relu")
        n3 = Norm(k)
        t3 = Turn(k, n3)
        l1_attn = Attention(k, n3, t3, "self")
        n4 = Norm(k, src=k.r)
        t4 = Turn(k, n4)
        l1_start = DenseStart(k, n4)
        l1_dense = Experts(k, n4, t4, "dense")
        n5 = Norm(k, src=k.r)
        l1_after = AfterNorm(k, n5, k.wide["ln2_g"], k.wide["ln2_b"])
        n6 = Norm(k)
        t6 = Turn(k, n6)
        l1_cross = Attention(k, n6, t6, "context")
        n7 = Norm(k)
        t7 = Turn(k, n7)
        l1_ffn = Experts(k, n7, t7, "gelu")
        n8 = Norm(k)
        t8 = Turn(k, n8)
        l2_mamba = Mamba(k, n8, t8)
        n9 = Norm(k)
        t9 = Turn(k, n9)
        l2_cross = WideCross(k, n9, t9)
        n10 = Norm(k, src=k.r, eps=1e-6)
        l2_after = AfterNorm(k, n10, k.wide["ln_scale"], k.wide["ln_bias"])
        n11 = Norm(k, again=True)
        t11 = Turn(k, n11)
        l2_ffn = Experts(k, n11, t11, "bit")
        n12 = Norm(k)
        t12 = Turn(k, n12)
        l3_attn = Attention(k, n12, t12, "packed")
        n13 = Norm(k, again=True)
        t13 = Turn(k, n13)
        l3_cross = Depool(k, n13, t13, k.wT[:, 5, :], k.pooled3, 2)
        n14 = Norm(k)
        t14 = Turn(k, n14)
        l3_ffn = Experts(k, n14, t14, "gate")

        col = lambda name: k.cols[:, COL[name]:COL[name] + 1]

        def credit(eng, name):
            for signal, n in CREDITS[name].items():
                eng.sem_inc(k.sig[signal].sem, n)

        block = ctx.enter_context(nc.Block())

        @block.sync
        def _(sp):
            issued = dict.fromkeys(LOADS, 0)

            def load(group, dst, src):
                sp.dma_start(dst, src).then_inc(k.loads[group], 16)
                issued[group] += 1

            def on_all(v):
                return bcast(v, 0, P)

            load("x", k.x, a["x"].rearrange("b s d -> s b d"))
            load("first", early, a["early"])
            for j, name in enumerate(("L0_attn_W_Q", "L0_attn_W_K", "L0_attn_W_V", "L0_attn_W_O", "L0_xattn_W_in",
                                      "L3_xattn_W_in")):
                load("l0", k.w_raw[:, j, :], a[name])
            load("lens", k.lens_i, a["mask_BxS2_if0"])
            row = lambda name, v, n: load("rows", k.rows[COL[name]:COL[name] + n, :], v)
            for name, v in (("relu_b1", "L0_ffn_b1"), ("gelu_b1", "L1_ffn_b1"), ("gate_b1", "L3_ffn_b1")):
                row(name, a[v].rearrange("e (c p) -> (e c) p", p=P), 32)
            for name, v, n in (("dense_b1", "L1_attn_b1", 4), ("g_res0", "L0_xattn_g_res", 1),
                               ("g_res3", "L3_xattn_g_res", 1), ("gamma", "L2_ffn_ln_gamma", 1),
                               ("beta", "L2_ffn_ln_beta", 1), ("conv_b", "L2_attn_conv_b", 2),
                               ("b_dt", "L2_attn_b_dt", 2), ("ssm_d", "L2_attn_D", 2),
                               ("ln1_g", "L1_attn_ln1_g", 1), ("ln1_b", "L1_attn_ln1_b", 1)):
                row(name, a[v].rearrange("(c p) -> c p", p=P), n)
            load("routers", k.router_rows[0:8, :], a["L1_ffn_router_w"])
            load("routers", k.router_rows[8:12, :], a["L1_ffn_lang_w"])
            load("routers", k.router_rows[12:20, :], a["L2_ffn_router_w"])
            load("pool_consts", late, a["late"][:, 0:3 * P])
            load("lower", lower, a["late"][:, 3 * P:3 * P + 64])
            load("masks", halves.bitcast(U16), a["halves"])
            load("ctx", k.ctx[0:M, :].rearrange("s (b c) -> s b c", c=CTX), a["ctx_2048"].rearrange("b s c -> s b c"))
            load("keys", k.key_mask, a["mask_BxS2_ik0"].rearrange("b s -> (b s)").unsqueeze(0))
            load("keys", k.key_b[0:1, :], a["L1_xattn_b"].unsqueeze(0))
            load("gates", gates[:, 0, :], a["L0_ffn_gate_w"])
            load("gates", gates[:, 1, :], a["L3_ffn_Wg"])
            for at, n, name in ((0, 8, "L0_ffn_gate_b"), (8, 8, "L1_ffn_router_b"), (16, 8, "L3_ffn_bg"),
                                (24, 4, "L1_ffn_lang_b")):
                load("wide", bias[:, at:at + n], on_all(a[name]))
            for name, v in (("ln1_g", "L1_attn_ln1_g"), ("ln1_b", "L1_attn_ln1_b"), ("ln2_g", "L1_attn_ln2_g"),
                            ("ln2_b", "L1_attn_ln2_b"), ("dense_b2", "L1_attn_b2"), ("b_in0", "L0_xattn_b_in"),
                            ("b_in3", "L3_xattn_b_in"), ("g_init0", "L0_xattn_g_init"), ("g_init3", "L3_xattn_g_init"),
                            ("ln_scale", "L2_xattn_ln_scale"), ("ln_bias", "L2_xattn_ln_bias")):
                load("wide", k.wide[name], on_all(a[v][0:D]))
            sp.wait_ge(preset, PRESETS)
            for j, name in enumerate(("L0_ffn_b2", "L1_ffn_b2", "L3_ffn_b2")):
                for t in range(B):
                    load("b2", blocks[8 * t:8 * t + 8, j, t * D:(t + 1) * D], a[name])
            load("bit", k.bit_raw1[:, 0:2, :], a["L2_ffn_shared_w1"].rearrange("(c p) d -> p c d", p=P))
            for e in range(8):
                load("bit", k.bit_raw1[:, 2 + 2 * e:4 + 2 * e, :],
                     a["L2_ffn_expert_w1"][e].rearrange("(c p) d -> p c d", p=P))
            load("bit", k.bit_raw2[:, 0, :], a["L2_ffn_shared_w2"])
            load("bit", k.bit_raw2[:, 1:9, :], a["L2_ffn_expert_w2"].rearrange("e d f -> d e f"))
            load("l3", l3_qkv, a["L3_attn_w_qkv"])
            load("l3", k.l3_wo, a["L3_attn_w_out"])
            load("mamba", k.mb_win, a["L2_attn_W_in"])
            load("mamba", k.mb_conv, a["L2_attn_conv_w"].rearrange("k (c p) o -> p (k c) o", p=P))
            load("mamba", k.mb_wx, a["L2_attn_W_x"].rearrange("(c p) f -> p c f", p=P))
            load("mamba", k.mb_wdt, a["L2_attn_W_dt"])
            load("mamba", k.mb_wout, a["L2_attn_W_out"].rearrange("(c p) d -> p c d", p=P))
            load("mamba", k.a_log, a["L2_attn_A_log"].rearrange("(c p) n -> p c n", p=P))
            for h in range(2):
                load("null_k", k.null_k[64 * h:64 * h + 64, :], a["L2_xattn_null_kv"][0].unsqueeze(1))
            l0_ffn.sync(sp, a["L0_ffn_w1"], a["L0_ffn_w2"])
            l1_dense.sync(sp, a["L1_attn_W1"], a["L1_attn_W2"])
            l1_ffn.sync(sp, a["L1_ffn_w1"], a["L1_ffn_w2"])
            sp.wait_ge(*bits.in_sbuf.upto(9))
            load("wide_cross", k.wq, a["L2_xattn_Wq"])
            load("wide_cross", k.wkv, a["L2_xattn_Wkv"].rearrange("(e p) f -> p e f", p=P))
            load("wide_cross", k.wout, a["L2_xattn_Wout"].rearrange("(c p) d -> p c d", p=P))
            l2_cross.sync(sp, a["L2_xattn_null_kv"][1:2])
            issued["null_v"] += 2
            l3_ffn.sync(sp, a["L3_ffn_W1"], a["L3_ffn_W2"])
            for h in range(2):
                sp.wait_ge(*l3_ffn.result.upto(h + 1))
                sp.dma_start(out[4 * h:4 * h + 4].rearrange("b s d -> s b d"), k.x[:, 4 * h:4 * h + 4, :])\
                    .then_inc(stored, 16)
            sp.wait_ge(stored, 32)
            assert issued == LOADS, (issued, LOADS)

        @block.tensor
        def _(pe):
            credit(pe, "tensor")
            pe.wait_ge(preset, PRESETS)
            setup.tensor_first(pe)
            t0.tensor(pe)
            k.arrived(pe, "masks")
            l0_attn.tensor(pe)
            pe.wait_ge(*l0_attn.res_done.upto(B))
            setup.tensor_second(pe)
            t1.tensor(pe)
            l0_cross.tensor(pe)
            t2.tensor(pe)
            k.arrived(pe, "gates")
            l0_ffn.tensor(pe)
            t3.tensor(pe)
            l1_attn.tensor(pe)
            t4.tensor(pe)
            l1_dense.tensor(pe)
            t6.tensor(pe)
            pe.wait_ge(*setup.keyrow.upto(1))
            l1_cross.tensor(pe)
            t7.tensor(pe)
            l1_ffn.tensor(pe)
            bits.tensor(pe)
            t8.tensor(pe)
            l2_mamba.tensor(pe)
            t9.tensor(pe)
            l2_cross.tensor(pe)
            t11.tensor(pe)
            l2_ffn.tensor(pe)
            t12.tensor(pe)
            k.arrived(pe, "l3")
            l3_attn.tensor(pe)
            t13.tensor(pe)
            l3_cross.tensor(pe)
            t14.tensor(pe)
            l3_ffn.tensor(pe)

        @block.vector
        def _(dve):
            k.dchain = Chain(dve, chains[0])
            credit(dve, "vector")
            dve.wait_ge(preset, PRESETS)
            k.arrived(dve, "x")
            token_stats(k, dve, k.x, range(B))
            n0.vector(dve)
            setup.vector_first(dve)
            l0_attn.vector(dve)
            n1.vector(dve)
            l0_cross.vector(dve)
            n2.vector(dve)
            k.arrived(dve, "wide")
            k.arrived(dve, "lower")
            l0_ffn.vector(dve, between=bits)
            n3.vector(dve)
            l1_attn.vector(dve)
            n4.vector(dve)
            l1_start.vector(dve)
            l1_dense.vector(dve)
            n5.vector(dve)
            l1_after.vector(dve)
            n6.vector(dve)
            l1_cross.vector(dve)
            n7.vector(dve)
            l1_ffn.vector(dve)
            n8.vector(dve)
            l2_mamba.vector(dve)
            n9.vector(dve)
            l2_cross.vector(dve)
            n10.vector(dve)
            l2_after.vector(dve)
            n11.vector(dve)
            l2_ffn.vector(dve)
            n12.vector(dve)
            l3_attn.vector(dve)
            n13.vector(dve)
            l3_cross.vector(dve)
            n14.vector(dve)
            l3_ffn.vector(dve, stats=False)

        @block.scalar
        def _(act):
            k.achain = Chain(act, chains[1])
            credit(act, "scalar")
            act.wait_ge(preset, PRESETS)
            setup.scalar_first(act)
            act.wait_ge(*setup.small_ready.upto(1))
            t0.scalar(act)
            l0_attn.scalar(act)
            setup.scalar_second(act)
            t1.scalar(act, scale=col("g_res0"))
            t2.scalar(act)
            l0_ffn.scalar(act)
            t3.scalar(act)
            l1_attn.scalar(act)
            t4.scalar(act, scale=col("ln1_g"), bias=col("ln1_b"))
            l1_dense.scalar(act)
            t6.scalar(act, scale=1.0 / np.sqrt(16.0))
            l1_cross.scalar(act)
            t7.scalar(act)
            l1_ffn.scalar(act)
            bits.scalar(act)
            t8.scalar(act)
            l2_mamba.scalar(act)
            t9.scalar(act)
            l2_cross.scalar(act)
            t11.scalar(act, scale=col("gamma"), bias=col("beta"))
            l2_ffn.scalar(act)
            t12.scalar(act)
            l3_attn.scalar(act)
            t13.scalar(act, scale=col("g_res3"))
            t14.scalar(act)
            l3_ffn.scalar(act)

        @block.gpsimd
        def _(pool):
            k.pchain = Chain(pool, chains[2])
            credit(pool, "pool")
            for v, value in ((k.minus_half, -0.5), (k.ones, 1.0), (k.key_row, 0.0), (bias[:, 28:36], 0.0),
                             (k.lp[:, :, 4], 0.0), (blocks[0:64, :, :], 0.0)):
                pool.memset(v, value).then_inc(preset, 1)
            pool.wait_ge(preset, PRESETS)
            n0.pool(pool)
            setup.pool_first(pool)
            l0_attn.pool(pool)
            setup.pool_second(pool)
            n1.pool(pool)
            l0_cross.pool(pool)
            n2.pool(pool)
            bits.pool(pool)
            n3.pool(pool)
            l1_attn.pool(pool)
            setup.pool_third(pool)
            n4.pool(pool)
            l1_start.pool(pool)
            n5.pool(pool)
            l1_after.pool(pool)
            n6.pool(pool)
            l1_cross.pool(pool)
            n7.pool(pool)
            n8.pool(pool)
            l2_mamba.pool(pool)
            n9.pool(pool)
            l2_cross.pool(pool)
            n10.pool(pool)
            l2_after.pool(pool)
            n11.pool(pool)
            l2_ffn.pool(pool)
            n12.pool(pool)
            l3_attn.pool(pool)
            n13.pool(pool)
            l3_cross.pool(pool)
            n14.pool(pool)


def kernel(**inputs):
    import concourse.bacc as _bacc
    from concourse.bass_utils import run_bass_kernel_spmd as _run

    arrays = {f"in_{name}_dram": np.ascontiguousarray(v) for name, v in inputs.items()}
    arrays.update({f"in_{name}_dram": v for name, v in zip(("early", "late", "halves"), constants())})
    nc = _bacc.Bacc("TRN2", target_bir_lowering=False, num_devices=1)
    args = {}
    for name, v in arrays.items():
        args[name[3:-5]] = nc.dram_tensor(name, v.shape, mybir.dt.from_np(v.dtype), kind="ExternalInput").ap()
    out = nc.dram_tensor("out_0_dram", (B, S, D), F32, kind="ExternalOutput").ap()
    decoder(nc, args, out)
    return _run(nc, [arrays], core_ids=[0]).results[0]["out_0_dram"]
```

```python
from contextlib import ExitStack

import numpy as np

import concourse.bass as bass
from concourse import mybir

F32 = mybir.dt.float32
F32R = mybir.dt.float32r
BF16 = mybir.dt.bfloat16
I32 = mybir.dt.int32
U16 = mybir.dt.uint16
ACT = mybir.ActivationFunctionType
ALU = mybir.AluOpType
AX = mybir.AxisListType

P = 128
B, S, D = 8, 128, 128
TOK = B * S
M, CTX = 120, 256
LN_EPS = 1e-5
HALF = 512
DEPOOL_EPS = 0.001
NEG = -1e30

PT0, OB, MB = 4, 6, 7


class Signal:

    def __init__(self, sem):
        self.sem, self.total = sem, 0

    def take(self, count):
        base = self.total
        self.total += count
        return Share(self.sem, base)


class Share:
    def __init__(self, sem, base):
        self.sem, self.base = sem, base

    def upto(self, n):
        return self.sem, n + self.base


class Chain:

    def __init__(self, eng, sem):
        self.eng, self.sem, self.base, self.n = eng, sem, 0, 0
        self.i, self.per = None, 0

    def step(self, ins):
        ins.then_inc(self.sem, 1)
        self.n += 1

    def settle(self):
        if self.i is None:
            if self.base + self.n:
                self.eng.wait_ge(self.sem, self.base + self.n)
        else:
            self.eng.wait_ge(self.sem, self.i * self.per + (self.base + self.n))

    def link(self, ins):
        self.step(ins)
        self.settle()

    def enter(self, i, per):
        self.base, self.n, self.i, self.per = self.base + self.n, 0, i, per

    def leave(self, trips):
        assert self.n == self.per, (self.n, self.per)
        self.base, self.n, self.i = self.base + trips * self.per, 0, None


def strided(flat, n, step, width):
    return bass.AP(tensor=flat.tensor, offset=flat.offset, ap=[flat.ap[0], [step, n], [1, width]])


def bcast(ap, axis, n):
    new = ap.unsqueeze(axis)
    shape = list(new.shape)
    shape[axis] = n
    return new.to_broadcast(shape)


class Norm:

    def __init__(self, k, src=None, again=False, eps=LN_EPS):
        self.k, self.src, self.again, self.eps = k, k.x if src is None else src, again, eps
        self.var_ready = k.sig["var_ready"].take(1)
        self.rstd_ready = k.sig["rstd_ready"].take(1)
        self.xn_ready = k.sig["xn_ready"].take(B)

    def vector(self, dve):
        k = self.k
        k.dchain.settle()
        if self.again:
            total = dve.tensor_scalar(k.var_eps[:, :], k.mv[:, :, 1], 1.0 + self.eps, self.eps ** 2, ALU.mult, ALU.add)
        else:
            total = dve.tensor_scalar(k.var_eps[:, :], k.mv[:, :, 1], self.eps, None, ALU.add)
        total.then_inc(self.var_ready.sem, 1)
        dve.wait_ge(*self.rstd_ready.upto(1))
        for b in range(B):
            dve.tensor_scalar(k.xn[:, b, :], self.src[:, b, :], k.mv[:, b, 0:1], k.rstd[:, b:b + 1],
                              ALU.subtract, ALU.mult).then_inc(self.xn_ready.sem, 1)

    def pool(self, pool):
        k = self.k
        pool.wait_ge(*self.var_ready.upto(1))
        pool.tensor_tensor(k.rstd[:, :], k.var_eps[:, :], bcast(k.minus_half[:, 0], 1, B), ALU.pow)\
            .then_inc(self.rstd_ready.sem, 1)


def token_stats(k, dve, src, bs):
    for b in bs:
        k.dchain.step(dve.bn_stats(k.bn[:, b, :], src[:, b, :]))
    k.dchain.settle()
    for b in bs:
        k.dchain.step(dve.bn_aggr(k.mv[:, b, :], k.bn[:, b, :]))


class Turn:

    def __init__(self, k, norm):
        self.k, self.norm = k, norm
        self.turned = k.sig["x_turned"].take(2)
        self.xT_ready = k.sig["xnT_ready"].take(2)

    def tensor(self, pe):
        k = self.k
        for b in range(B):
            pe.wait_ge(*self.norm.xn_ready.upto(b + 1))
            t = pe.transpose(k.ps[:, PT0 + b // 4, b % 4 * P:(b % 4 + 1) * P], k.xn[:, b, :], k.ident)
            if b % 4 == 3:
                t.then_inc(self.turned.sem, 1)

    def scalar(self, act, scale=1.0, bias=0.0):
        k = self.k
        for h in range(2):
            act.wait_ge(*self.turned.upto(h + 1))
            act.activation(k.xnT[:, h * HALF:(h + 1) * HALF], k.ps[:, PT0 + h, :], ACT.Identity,
                           scale=scale, bias=bias).then_inc(self.xT_ready.sem, 1)


class Attention:

    UNITS = 4

    def __init__(self, k, norm, turn, kind, setup=None):
        self.k, self.norm, self.turn, self.kind = k, norm, turn, kind
        self.setup = setup
        self.H = 8 if kind == "context" else 16
        self.dh = D // self.H
        self.per = self.H // self.UNITS
        self.T = M if kind == "context" else S
        self.scale = 1.0 / np.sqrt(8.0) if kind in ("rope", "packed") else 1.0
        self.proj = kind in ("rope", "packed")
        self.v = k.ctx.rearrange("t (b n) -> t b n", b=B)[:, :, P:CTX] if kind == "context" else k.v_tok if self.proj else k.xn
        self.q_all = k.q_all if self.proj else k.xnT
        self.k_all = k.k_all if self.proj else k.ctxT[:, 0, :] if kind == "context" else k.xnT
        sig = k.sig
        self.vb_ready = sig["at_vb_ready"].take(B)
        self.kv_ready = sig["at_kv_ready"].take(B)
        self.s_done = sig["at_s_done"].take(4 * B)
        self.max_ready = sig["at_max_ready"].take(4 * B)
        self.p_ready = sig["at_p_ready"].take(4 * B)
        self.rec_ready = sig["at_rec_ready"].take(4 * B)
        self.pn_ready = sig["at_pn_ready"].take(4 * B)
        self.pt_done = sig["at_pt_done"].take(4 * B)
        self.ptv_ready = sig["at_ptv_ready"].take(2 * B)
        self.pta_ready = sig["at_pta_ready"].take(2 * B)
        self.av_even = sig["at_av_even"].take(2 * B)
        self.av_odd = sig["at_av_odd"].take(2 * B)
        self.oT_ready = sig["at_oT_ready"].take(B)
        self.y_done = sig["at_y_done"].take(B)
        self.res_done = sig["at_res_done"].take(B)
        if self.proj:
            self.v_ready = sig["at_v_ready"].take(2)
            self.vp_done = sig["at_vp_done"].take(2)
            self.qk_done = sig["at_qk_done"].take(8 if kind == "rope" else 4)
            self.turned_qk = sig["at_turned_qk"].take(4)
            self.q_ready = sig["at_q_ready"].take(2 if kind == "packed" else 0)

    def each(self, eng, step, aside=None):
        step(0, 0)
        with eng.Fori(0, B // 2 - 1) as i:
            step(i, 1)
            step(i + 1, 0)
        if aside:
            aside(eng)
        step(B // 2 - 1, 1)

    def place(self, i, p):
        fixed = isinstance(i, int)
        return fixed and p == 0, fixed and p == 1, (i, 1) if p == 0 else (i + 1, 0)

    def tensor(self, pe):
        if self.proj:
            self.project(pe)
        if self.setup:
            self.setup.tensor_counts(pe)
        for u in range(4):
            self.scores(pe, 0, 0, u)

        def sequence(i, p):
            first, last, nxt = self.place(i, p)
            for u in range(4):
                if not last:
                    self.scores(pe, *nxt, u)
                self.turn_weights(pe, i, p, u)
                if u:
                    self.times_v(pe, i, p, u - 1)
                if u == 0 and not first:
                    self.out(pe, i, p)
            self.times_v(pe, i, p, 3)

        def aside(pe):
            pe.wait_ge(*self.p_ready.upto(4 * B))
            self.setup.tensor_second(pe)

        self.each(pe, sequence, aside if self.setup else None)
        self.out(pe, B // 2, 0)

    def project(self, pe):
        k = self.k
        pe.wait_ge(*self.turn.xT_ready.upto(2))
        wv = k.l0_wvT if self.kind == "rope" else k.l3_wv
        for b in range(B):
            m = pe.matmul(k.ps[:, 6 + b // 4, b % 4 * P:(b % 4 + 1) * P], k.xnT[:, b * P:(b + 1) * P], wv,
                          start=True, stop=True)
            if b % 4 == 3:
                m.then_inc(self.vp_done.sem, 1)
        weights = k.l0_qk if self.kind == "rope" else k.l3_qk
        for h in range(2):
            for j, w in enumerate(weights):
                bank = len(weights) * h + j
                if bank >= 6:
                    pe.wait_ge(*self.v_ready.upto(bank - 5))
                pe.matmul(k.ps[:, bank, :], w, k.xnT[:, h * HALF:(h + 1) * HALF], start=True, stop=True)\
                    .then_inc(self.qk_done.sem, 1)
        pe.wait_ge(*self.turned_qk.upto(4))
        if self.kind == "packed":
            pe.wait_ge(*self.q_ready.upto(2))

    def scores(self, pe, i, p, u):
        k = self.k
        b = 2 * i + p
        if u == 0:
            pe.wait_ge(*self.kv_ready.upto(b + 1))
        pe.wait_ge(*self.p_ready.upto(0 if isinstance(b, int) and b == 0 else 8 * i + (4 * p + u - 3)))
        out = k.ps[:, u, :].rearrange("q (h t) -> q h t", t=P)[:, 0:self.per, 0:self.T]
        g = slice(32 * u, 32 * u + 32)
        mask = self.kind != "packed"
        if self.kind == "context":
            pe.matmul(out, k.ones, bcast(k.key_row[:, bass.ts(b, M)], 1, self.per), start=True, stop=False)
        elif mask:
            pe.matmul(out, k.ident16, bcast(k.causal if self.kind == "rope" else k.band, 1, self.per),
                      start=True, stop=False)
        passes = ((k.q_high, k.kb_high), (k.q_low, k.kb_high), (k.q_high, k.kb_low))
        for j, (q, kb) in enumerate(passes):
            m = pe.matmul(out, q[p][g, :], kb[p][g, 0:self.per, 0:self.T], start=not mask and j == 0, stop=j == 2)
        m.then_inc(self.s_done.sem, 1)

    def turn_weights(self, pe, i, p, u):
        k = self.k
        b = 2 * i + p
        pe.wait_ge(*self.pn_ready.upto(4 * b + u + 1))
        ready = self.pta_ready if u % 2 else self.ptv_ready
        pe.wait_ge(*ready.upto(2 * b + u // 2))
        for j in range(self.per):
            t = pe.transpose(k.ps[0:self.T, PT0 + u % 2, j * P:(j + 1) * P],
                             k.p[p][:, u * self.per + j, 0:self.T], k.ident)
        t.then_inc(self.pt_done.sem, 1)

    def times_v(self, pe, i, p, u):
        k = self.k
        b = 2 * i + p
        if u == 0:
            pe.wait_ge(*self.oT_ready.upto(b))
            pe.wait_ge(*self.vb_ready.upto(b + 1))
        ready = self.pta_ready if u % 2 else self.ptv_ready
        pe.wait_ge(*ready.upto(2 * b + u // 2 + 1))
        for j in range(self.per):
            h = u * self.per + j
            m = pe.matmul(k.ps[:, OB, 0:P], k.v_block[p][0:self.T, h, :], k.pT[u % 2][0:self.T, j, :],
                          start=h == 0, stop=h == self.H - 1)
        m.then_inc((self.av_odd if u % 2 else self.av_even).sem, 1)

    def out(self, pe, i, p):
        k = self.k
        b = 2 * i + p
        pe.wait_ge(*self.oT_ready.upto(b))
        pe.wait_ge(*self.res_done.upto(b - 1))
        if self.proj:
            y = pe.matmul(k.ps[:, MB, 0:P], k.oT, k.l0_woT if self.kind == "rope" else k.l3_wo, start=True, stop=True)
        else:
            y = pe.transpose(k.ps[:, MB, 0:P], k.oT, k.ident)
        y.then_inc(self.y_done.sem, 1)

    def vector(self, dve):
        k, c = self.k, self.k.dchain
        if self.proj:
            self.keys(dve)
        if self.kind == "rope":
            self.setup.vector_counts(dve)
        else:
            dve.wait_ge(*self.turn.xT_ready.upto(1))
            if self.kind == "packed":
                dve.wait_ge(*self.q_ready.upto(2))
                dve.wait_ge(*self.turned_qk.upto(4))
            self.query_key_parts(dve, c, 0, 0)
            self.key_blocks(dve, 0, 0)
        for u in range(4):
            self.maxima(dve, 0, 0, u)
            if u:
                self.sums(dve, 0, 0, u - 1)
        self.sequence_vector(dve, 0, 0)
        with dve.Fori(0, B // 2 - 1) as i:
            c.enter(i, 2 * (4 + 4))
            self.sequence_vector(dve, i, 1)
            self.sequence_vector(dve, i + 1, 0)
        c.leave(B // 2 - 1)
        src = k.r if self.kind == "self" else k.x
        dve.wait_ge(*self.res_done.upto(B - 2))
        if self.setup:
            self.setup.vector_second(dve)
        token_stats(k, dve, src, range(B - 2))
        self.sequence_vector(dve, B // 2 - 1, 1)
        self.residual(dve, B // 2, 0)
        dve.wait_ge(*self.res_done.upto(B))
        token_stats(k, dve, src, range(B - 2, B))

    def sequence_vector(self, dve, i, p):
        first, last, nxt = self.place(i, p)
        for u in range(4):
            if not last:
                self.maxima(dve, *nxt, u)
            if u % 2 == 0:
                self.turned_weights(dve, i, p, u)
            if u == 0:
                self.sums(dve, i, p, 3)
            elif not last:
                self.sums(dve, *nxt, u - 1)
            if u == 1 and not first:
                self.residual(dve, i, p)

    def keys(self, dve):
        k = self.k
        if self.kind == "packed":
            for h in range(2):
                dve.wait_ge(*self.qk_done.upto(2 * h + 2))
                dve.tensor_copy(k.k_all[:, h * HALF:(h + 1) * HALF], k.ps[:, 2 * h + 1, :])\
                    .then_inc(self.turned_qk.sem, 2)
            return
        four = lambda v: v.rearrange("p (b t) -> p b t", t=S)
        for h in range(2):
            for j in range(2):
                q = slice((2 * j) * HALF, (2 * j + 1) * HALF)
                r = slice((2 * j + 1) * HALF, (2 * j + 2) * HALF)
                dve.wait_ge(*self.qk_done.upto(4 * h + 2 * j + 2))
                k.dchain.step(dve.tensor_tensor(four(k.terms[h][:, q]), four(k.ps[:, 4 * h + 2 * j, :]),
                                                bcast(k.cosT, 1, 4), ALU.mult))
                dve.tensor_tensor(four(k.terms[h][:, r]), four(k.ps[:, 4 * h + 2 * j + 1, :]),
                                  bcast(k.sinT, 1, 4), ALU.mult).then_inc(self.turned_qk.sem, 1)

    def maxima(self, dve, i, p, u):
        k, c = self.k, self.k.dchain
        dve.wait_ge(*self.s_done.upto(4 * (2 * i + p) + u + 1))
        hs = slice(u * self.per, (u + 1) * self.per)
        src = k.ps[:, u, :].rearrange("q (h t) -> q h t", t=P)[:, 0:self.per, 0:self.T]
        c.link(dve.tensor_reduce(k.mx[p][:, hs], src, AX.X, ALU.max))
        dve.tensor_scalar(k.nmx[p][:, hs], k.mx[p][:, hs], -self.scale, None, ALU.mult)\
            .then_inc(self.max_ready.sem, 1)

    def turned_weights(self, dve, i, p, u):
        k = self.k
        b = 2 * i + p
        dve.wait_ge(*self.pt_done.upto(4 * b + u + 1))
        dve.wait_ge(*self.av_even.upto(2 * b + u // 2))
        n = self.per * P
        dve.tensor_copy(k.pT[0][0:self.T, :, :].rearrange("t h q -> t (h q)")[:, 0:n],
                        k.ps[0:self.T, PT0, 0:n]).then_inc(self.ptv_ready.sem, 1)

    def sums(self, dve, i, p, u):
        k, c = self.k, self.k.dchain
        dve.wait_ge(*self.p_ready.upto(4 * (2 * i + p) + u + 1))
        hs = slice(u * self.per, (u + 1) * self.per)
        c.link(dve.tensor_reduce(k.total[p][:, hs], k.p[p][:, hs, 0:self.T], AX.X, ALU.add))
        dve.reciprocal(k.rec[p][:, hs], k.total[p][:, hs]).then_inc(self.rec_ready.sem, 1)

    def residual(self, dve, i, p):
        k = self.k
        b = 2 * i + p
        base, dst = (k.xn, k.r) if self.kind == "self" else (k.x, k.x)
        dve.wait_ge(*self.y_done.upto(b))
        dve.tensor_tensor(dst[:, b - 1, :], base[:, b - 1, :], k.ps[:, MB, 0:P], ALU.add).then_inc(self.res_done.sem, 1)

    def pool(self, pool):
        k, c = self.k, self.k.pchain
        pool.wait_ge(*self.turn.xT_ready.upto(1))
        for p in range(2):
            c.step(pool.memset(k.v_block[p][:, 0:self.H, :], 0.0))
        if self.kind == "rope":
            pool.wait_ge(*self.turn.xT_ready.upto(2))
            for h in range(2):
                for j, dst in enumerate((k.q_all, k.k_all)):
                    pool.wait_ge(*self.turned_qk.upto(2 * h + j + 1))
                    c.step(pool.tensor_tensor(dst[:, h * HALF:(h + 1) * HALF],
                                              k.terms[h][:, 2 * j * HALF:(2 * j + 1) * HALF],
                                              k.terms[h][:, (2 * j + 1) * HALF:(2 * j + 2) * HALF], ALU.add))
        c.settle()
        if self.kind == "rope":
            self.query_key_parts(pool, c, 0, 0)
            self.key_blocks(pool, 0, 0)
            self.setup.pool_counts(pool)
        else:
            pool.wait_ge(*self.kv_ready.upto(1))
        self.query_key_parts(pool, c, 0, 1)
        self.key_blocks(pool, 0, 1)
        if self.proj:
            pool.wait_ge(*self.v_ready.upto(2))
        self.values_of(pool, 0, 0)

        def sequence(i, p, keys=True, values=True):
            self.normalise(pool, i, p, 0)
            if keys:
                self.query_key_parts(pool, c, i + 1, p)
            self.normalise(pool, i, p, 1)
            if keys:
                self.key_blocks(pool, i + 1, p)
            self.normalise(pool, i, p, 2)
            if values:
                self.values_of(pool, *((i, 1) if p == 0 else (i + 1, 0)))
            self.normalise(pool, i, p, 3)

        sequence(0, 0)
        with pool.Fori(0, B // 2 - 2) as i:
            c.enter(i, 2 * 2 * (1 if self.k_all is self.q_all else 2))
            sequence(i, 1)
            sequence(i + 1, 0)
        c.leave(B // 2 - 2)
        sequence(B // 2 - 2, 1)
        for p in range(2):
            sequence(B // 2 - 1, p, keys=False, values=p == 0)

    def query_key_parts(self, eng, c, i, p):
        k = self.k
        b = 2 * i + p
        eng.wait_ge(*self.s_done.upto(0 if isinstance(b, int) and b == 0 else 8 * i + (4 * p - 4)))
        self.parts(eng, c, i, p, self.q_all, P, k.q_high[p], k.q_low[p])
        if self.k_all is not self.q_all:
            self.parts(eng, c, i, p, self.k_all, self.T, k.k_high, k.k_low)

    def key_blocks(self, eng, i, p):
        k = self.k
        hm = k.head_of4 if self.per == 4 else k.head_of2
        high, low = (k.q_high[p], k.q_low[p]) if self.k_all is self.q_all else (k.k_high[:, 0:self.T], k.k_low[:, 0:self.T])
        for part, block in ((high, k.kb_high[p]), (low, k.kb_low[p])):
            t = eng.tensor_tensor(block[:, 0:self.per, 0:self.T], bcast(part.bitcast(F32), 1, self.per),
                                   bcast(hm, 2, self.T), ALU.mult)
        t.then_inc(self.kv_ready.sem, 1)

    def parts(self, eng, c, i, p, v, n, high, low):
        c.link(eng.tensor_copy(high[:, 0:n], v[:, bass.ts(2 * i + p, n)]))
        c.link(eng.tensor_tensor(low[:, 0:n], v[:, bass.ds(i * (2 * n) + p * n, n)], high[:, 0:n].bitcast(F32), ALU.subtract))

    def values_of(self, pool, i, p):
        k = self.k
        b = 2 * i + p
        pool.wait_ge(*self.av_odd.upto(0 if isinstance(b, int) and b == 0 else 4 * i + (2 * p - 2)))
        flat = k.v_block[p].rearrange("t h f -> t (h f)")
        dst = strided(flat[0:self.T, :], self.H, P + self.dh, self.dh)
        src = self.v[0:self.T, bass.ds(b, 1), :].rearrange("t o (h d) -> t (o h) d", d=self.dh)
        pool.tensor_copy(dst, src).then_inc(self.vb_ready.sem, 1)

    def normalise(self, pool, i, p, u):
        k = self.k
        pool.wait_ge(*self.rec_ready.upto(4 * (2 * i + p) + u + 1))
        hs = slice(u * self.per, (u + 1) * self.per)
        w = k.p[p][:, hs, 0:self.T]
        pool.tensor_tensor(w, w, bcast(k.rec[p][:, hs], 2, self.T), ALU.mult).then_inc(self.pn_ready.sem, 1)

    def scalar(self, act):
        if self.proj:
            self.values(act)
        if self.kind == "packed":
            self.queries(act)
        if self.setup:
            self.setup.scalar_counts(act)
        for u in range(4):
            self.weights(act, 0, 0, u)

        def sequence(i, p):
            first, last, nxt = self.place(i, p)
            for u in range(4):
                if u % 2:
                    self.turned_weights_odd(act, i, p, u)
                if not last:
                    self.weights(act, *nxt, u)
            self.outputs(act, i, p)

        self.each(act, sequence, self.setup.scalar_second if self.setup else None)

    def values(self, act):
        k = self.k
        for h in range(2):
            act.wait_ge(*self.vp_done.upto(h + 1))
            act.activation(k.v_tok[:, 4 * h:4 * h + 4, :], k.ps[:, 6 + h, :].rearrange("t (b n) -> t b n", b=4), ACT.Copy)\
                .then_inc(self.v_ready.sem, 1)

    def queries(self, act):
        k = self.k
        for h in range(2):
            act.wait_ge(*self.qk_done.upto(2 * h + 1))
            act.activation(k.q_all[:, h * HALF:(h + 1) * HALF], k.ps[:, 2 * h, :], ACT.Copy).then_inc(self.q_ready.sem, 1)

    def weights(self, act, i, p, u):
        k = self.k
        b = 2 * i + p
        act.wait_ge(*self.max_ready.upto(4 * b + u + 1))
        if u == 0:
            act.wait_ge(*self.pt_done.upto(0 if isinstance(b, int) and b == 0 else 8 * i + (4 * p - 4)))
        for j in range(self.per):
            h = u * self.per + j
            e = act.activation(k.p[p][:, h, 0:self.T], k.ps[:, u, j * P:j * P + self.T], ACT.Exp,
                               bias=k.nmx[p][:, h:h + 1], scale=float(self.scale))
        e.then_inc(self.p_ready.sem, 1)

    def turned_weights_odd(self, act, i, p, u):
        k = self.k
        b = 2 * i + p
        act.wait_ge(*self.pt_done.upto(4 * b + u + 1))
        act.wait_ge(*self.av_odd.upto(2 * b + u // 2))
        n = self.per * P
        act.activation(k.pT[1][0:self.T, :, :].rearrange("t h q -> t (h q)")[:, 0:n],
                       k.ps[0:self.T, PT0 + 1, 0:n], ACT.Copy).then_inc(self.pta_ready.sem, 1)

    def outputs(self, act, i, p):
        k = self.k
        b = 2 * i + p
        act.wait_ge(*self.av_odd.upto(2 * b + 2))
        act.wait_ge(*self.y_done.upto(b))
        act.activation(k.oT, k.ps[:, OB, 0:P], ACT.Copy).then_inc(self.oT_ready.sem, 1)


class Experts:

    def __init__(self, k, norm, turn, kind):
        self.k, self.norm, self.turn, self.kind = k, norm, turn, kind
        self.nf = 2 if kind == "bit" else 4
        self.func = {"gelu": ACT.Gelu, "bit": ACT.Silu}.get(kind, ACT.Relu)
        self.routed = kind != "dense"
        self.b2 = kind in ("relu", "gelu", "gate")
        self.first = {"dense": -2, "bit": 2}.get(kind, 0)
        self.items = {"dense": 2, "bit": 18}.get(kind, 16)
        sig = k.sig
        self.h_done = sig["ff_h_done"].take(self.items * self.nf)
        self.h_ready = sig["ff_h_ready"].take(self.items * self.nf)
        self.o_done = sig["ff_o_done"].take(self.items)
        self.acc_done = sig["ff_acc_done"].take(self.items)
        if self.routed:
            self.router_done = sig["ff_router_done"].take(1)
        if kind in ("relu", "gelu", "gate"):
            self.loaded = [s.take(4 * 32) for s in k.ring_loaded]
        elif kind == "bit":
            self.loaded = [s.take(4) for s in k.signs_copied]
        else:
            self.loaded = [None, k.ring_loaded[1].take(32)]
        self.x_high, self.x_low = k.bit_x_parts if kind == "bit" else k.x_parts
        self.x_split = sig["ff_x_split"].take(2)
        if kind != "bit":
            self.w1_split = [sig[f"ff_w1_split{p}"].take(4 if self.routed else p) for p in range(2)]
        if self.b2:
            self.w_ready = sig["ff_w_ready"].take(1)
            self.w_turned = sig["ff_w_turned"].take(1)
            self.wT_ready = sig["ff_wT_ready"].take(1)
            self.b2_done = sig["ff_b2_done"].take(1)
        if kind in ("gelu", "gate", "bit"):
            self.l_ready = sig["ff_l_ready"].take(2 if kind == "gelu" else 1)
            self.e_ready = sig["ff_e_ready"].take(2 if kind == "gelu" else 1)

    def weights_in(self, p):
        return lambda i: (self.loaded if self.kind == "bit" else self.w1_split)[p].upto(i + 1)

    def sync(self, sp, w1, w2):
        k = self.k
        if self.kind == "dense":
            sp.wait_ge(*self.o_done.upto(0))
            sp.dma_start(k.w1[1][:, :], w1).then_inc(self.loaded[1].sem, 16)
            sp.dma_start(k.w2[1][:, :, :], w2.rearrange("(c p) d -> p c d", p=P)).then_inc(self.loaded[1].sem, 16)
            return
        with sp.Fori(0, 4) as i:
            for p in range(2):
                e = 2 * i + p
                sp.wait_ge(*self.o_done.upto(2 * e - 2))
                sp.dma_start(k.w1[p][:, :], w1[bass.ds(e, 1)].rearrange("o d f -> d (o f)"))\
                    .then_inc(self.loaded[p].sem, 16)
                sp.dma_start(k.w2[p][:, :, :], w2[bass.ds(e, 1)].rearrange("o (c p) d -> p (o c) d", p=P))\
                    .then_inc(self.loaded[p].sem, 16)

    def pool(self, pool):
        k = self.k
        with pool.Fori(0, 4) as i:
            for p in range(2):
                e = 2 * i + p
                pool.wait_ge(*self.o_done.upto(2 * e))
                pool.tensor_copy(k.signs[p], k.bit_w1T[:, bass.ts(e + 1, 256)]).then_inc(self.loaded[p].sem, 1)

    def tensor(self, pe):
        k = self.k
        if self.routed:
            R = {"gelu": 12}.get(self.kind, 8)
            for t in range(B):
                pe.wait_ge(*self.turn.xT_ready.upto(t // 4 + 1))
                m = pe.matmul(k.ps[:, 6, 16 * t:16 * t + R], k.xnT[:, t * P:(t + 1) * P], k.router[self.kind],
                              start=True, stop=True)
            m.then_inc(self.router_done.sem, 1)
        else:
            pe.wait_ge(*self.turn.xT_ready.upto(2))
        if self.kind == "dense":
            self.block(pe, 0, [1])
        else:
            if self.kind == "bit":
                self.block(pe, 0, ["shared"])
            if self.b2:
                self.block(pe, 0, [0, 1])
                self.biases(pe)
            with pe.Fori(1 if self.b2 else 0, 4) as i:
                self.block(pe, i, [0, 1])

    def biases(self, pe):
        k = self.k
        pe.wait_ge(*self.w_ready.upto(1))
        pe.transpose(k.ps[0:64, 7, 0:P], k.w[:, :], k.ident).then_inc(self.w_turned.sem, 1)
        pe.wait_ge(*self.wT_ready.upto(1))
        k.arrived(pe, "b2")
        for h in range(2):
            m = pe.matmul(k.ps[:, 6 + h, :], k.wT_small, k.b2_blocks[self.kind][:, h * HALF:(h + 1) * HALF],
                          start=True, stop=True)
        m.then_inc(self.b2_done.sem, 1)

    def item(self, i, p, h):
        return h if p == "shared" else self.first + 4 * i + 2 * p + h

    def block(self, pe, i, ps):
        items = [(p, h) for p in ps for h in range(2)]
        self.layer1(pe, i, *items[0])
        for n, it in enumerate(items):
            if n + 1 < len(items):
                self.layer1(pe, i, *items[n + 1])
            self.layer2(pe, i, *it)

    def layer1(self, pe, i, p, h):
        k = self.k
        n = self.item(i, p, h)
        shared = p == "shared"
        if h == 0 and not shared:
            pe.wait_ge(*self.weights_in(p)(i))
        if isinstance(i, int) and i == 0:
            pe.wait_ge(*self.x_split.upto(h + 1))
        if self.kind == "bit":
            signs = k.bit_w1T if shared else k.signs[p]
            parts = [(signs, self.x_high), (signs, self.x_low)]
        else:
            parts = [(k.w1_high[p], self.x_high), (k.w1_low[p], self.x_high), (k.w1_high[p], self.x_low)]
        for c in range(self.nf):
            pe.wait_ge(*self.h_ready.upto(self.nf * (n - 1) + c + 1))
            for j, (w, x) in enumerate(parts):
                m = pe.matmul(k.ps[:, c, :], w[:, c * P:(c + 1) * P], x[:, h * HALF:(h + 1) * HALF],
                              start=j == 0, stop=j == len(parts) - 1)
            m.then_inc(self.h_done.sem, 1)

    def layer2(self, pe, i, p, h):
        k = self.k
        n = self.item(i, p, h)
        pe.wait_ge(*self.acc_done.upto(n - 1))
        pe.wait_ge(*self.h_ready.upto(self.nf * (n + 1)))
        for j in range(4):
            for c in range(self.nf):
                w2 = k.w2[p][:, c, :] if self.kind != "bit" else \
                    k.bit_w2T[:, bass.ds(c * P if p == "shared" else i * 512 + ((p + 1) * 256 + c * P), P)]
                m = pe.matmul(k.ps[:, 4 + h, j * P:(j + 1) * P], k.hT[h][:, c, j * P:(j + 1) * P], w2,
                              start=c == 0, stop=c == self.nf - 1)
        m.then_inc(self.o_done.sem, 1)

    def scalar(self, act):
        k = self.k
        if self.kind in ("gelu", "gate", "bit"):
            for r in range({"gelu": 2}.get(self.kind, 1)):
                act.wait_ge(*self.l_ready.upto(r + 1))
                arg = k.lang if self.kind == "gelu" and r == 0 else k.logit
                act.activation(arg[:, :, :], arg[:, :, :], ACT.Exp, scale=-1.0 if self.kind == "gate" else 1.0)\
                    .then_inc(self.e_ready.sem, 1)
        if self.kind == "dense":
            self.hidden(act, 0, [1])
        else:
            if self.kind == "bit":
                self.hidden(act, 0, ["shared"])
            if self.b2:
                self.hidden(act, 0, [0, 1])
                act.wait_ge(*self.w_turned.upto(1))
                act.activation(k.wT_small, k.ps[0:64, 7, 0:P], ACT.Copy).then_inc(self.wT_ready.sem, 1)
            with act.Fori(1 if self.b2 else 0, 4) as i:
                self.hidden(act, i, [0, 1])

    def hidden(self, act, i, ps):
        k = self.k
        for p in ps:
            for h in range(2):
                n = self.item(i, p, h)
                act.wait_ge(*self.o_done.upto(n - 1))
                for c in range(self.nf):
                    act.wait_ge(*self.h_done.upto(self.nf * n + c + 1))
                    bias, scale = 0.0, 1.0
                    if p == "shared":
                        scale = k.bit_scale[:, c:c + 1]
                    elif self.kind == "bit":
                        scale = k.bit_scale[:, bass.ds((2 * i + p) * 2 + (2 + c) if h == 0 else i * 4 + (2 * p + 2 + c), 1)]
                    elif self.kind == "dense":
                        bias = k.cols[:, k.col["dense_b1"] + c:k.col["dense_b1"] + c + 1]
                    else:
                        j = k.col[self.kind + "_b1"] + c
                        bias = k.cols[:, bass.ds((2 * i + p) * 4 + j if h == 0 else i * 8 + (4 * p + j), 1)]
                    act.activation(k.hT[h][:, c, :], k.ps[:, c, :], self.func, bias=bias, scale=scale)\
                        .then_inc(self.h_ready.sem, 1)

    def vector(self, dve, stats=True, between=None):
        k, c = self.k, self.k.dchain
        if self.kind != "bit":
            for p in (0, 1) if self.routed else (1,):
                self.split_w1(dve, 0, p)
        for h in range(2):
            dve.wait_ge(*self.turn.xT_ready.upto(h + 1))
            self.split(dve, k.xnT, self.x_high, self.x_low, h * HALF).then_inc(self.x_split.sem, 1)
        if self.routed:
            self.route(dve)
        if between is not None:
            between.vector(dve)
        if self.kind == "dense":
            for h in range(2):
                self.add(dve, 0, 1, h, k.r)
        elif self.kind == "bit":
            for h in range(2):
                self.add(dve, 0, "shared", h, k.x)
            with dve.Fori(0, 4) as i:
                for p in range(2):
                    for h in range(2):
                        self.add(dve, i, p, h, k.x)
        else:
            for p, h in ((0, 0), (0, 1), (1, 0)):
                self.add(dve, 0, p, h, k.x)
            dve.wait_ge(*self.b2_done.upto(1))
            dve.wait_ge(*self.acc_done.upto(3))
            for h in range(2):
                c.link(dve.tensor_tensor(k.x[:, 4 * h:4 * h + 4, :], k.x[:, 4 * h:4 * h + 4, :],
                                         k.ps[:, 6 + h, :].rearrange("s (b d) -> s b d", d=D), ALU.add))
            with dve.Fori(1, 4) as i:
                c.enter(i - 1, 2)
                self.split_w1(dve, i, 0)
                self.add(dve, i, -1, 1, k.x)
                self.split_w1(dve, i, 1)
                for p, h in ((0, 0), (0, 1), (1, 0)):
                    self.add(dve, i, p, h, k.x)
            c.leave(3)
            self.add(dve, 4, -1, 1, k.x)
        if stats:
            for h in range(2):
                dve.wait_ge(*self.acc_done.upto(self.items - 1 + h))
                token_stats(k, dve, k.r if self.kind == "dense" else k.x, range(4 * h, 4 * h + 4))

    def split(self, dve, v, high, low, at):
        cols = slice(at, at + HALF)
        self.k.dchain.link(dve.tensor_copy(high[:, cols], v[:, cols]))
        return dve.tensor_tensor(low[:, cols], v[:, cols], high[:, cols].bitcast(F32), ALU.subtract)

    def split_w1(self, dve, i, p):
        k = self.k
        dve.wait_ge(*self.loaded[p].upto(32 * (i + 1)))
        self.split(dve, k.w1[p], k.w1_high[p], k.w1_low[p], 0).then_inc(self.w1_split[p].sem, 1)

    def add(self, dve, i, p, h, acc):
        k = self.k
        n = self.item(i, p, h)
        dve.wait_ge(*self.o_done.upto(n + 1))
        dve.wait_ge(*self.acc_done.upto(n - 1))
        if p == "shared" or self.kind == "dense":
            ins = dve.tensor_tensor(acc[:, 4 * h:4 * h + 4, :], acc[:, 4 * h:4 * h + 4, :],
                                    k.ps[:, 4 + h, :].rearrange("s (b d) -> s b d", d=D), ALU.add)
        else:
            for j in range(4):
                t = 4 * h + j
                ins = dve.scalar_tensor_tensor(acc[:, t, :], k.ps[:, 4 + h, j * P:(j + 1) * P],
                                               k.w[:, bass.ds(2 * i + (8 * t + p), 1)], acc[:, t, :],
                                               ALU.mult, ALU.add)
        ins.then_inc(self.acc_done.sem, 1)

    def route(self, dve):
        k, c = self.k, self.k.dchain
        dve.wait_ge(*self.router_done.upto(1))
        G = k.ps[:, 6, 0:16 * B].rearrange("s (t r) -> s t r", r=16)
        L = k.logit[:, :, :]
        W = k.w[:, :].rearrange("s (t e) -> s t e", e=8)

        def exponentials(r):
            dve.wait_ge(*self.e_ready.upto(r + 1))

        c.link(dve.tensor_tensor(L, G[:, :, 0:8], bcast(k.router_b[self.kind], 1, B), ALU.add))
        if self.kind == "gate":
            dve.tensor_scalar(W, L, 0.0, None, ALU.is_gt).then_inc(self.l_ready.sem, 1)
            exponentials(0)
            c.link(dve.tensor_scalar(L, L, 1.0, None, ALU.add))
            c.link(dve.reciprocal(L, L))
            dve.tensor_tensor(W, W, L, ALU.mult).then_inc(self.w_ready.sem, 1)
            dve.wait_ge(*self.w_ready.upto(1))
            return
        if self.kind == "gelu":
            G4 = k.lang[:, :, :]
            c.link(dve.tensor_tensor(G4, G[:, :, 8:12], bcast(k.lang_b, 1, B), ALU.add))
            c.link(dve.tensor_reduce(k.peak[:, :], G4, AX.X, ALU.max))
            dve.tensor_tensor(G4, G4, bcast(k.peak[:, :], 2, 4), ALU.subtract).then_inc(self.l_ready.sem, 1)
            exponentials(0)
            c.link(dve.tensor_reduce(k.peak[:, :], G4, AX.X, ALU.add))
            c.link(dve.reciprocal(k.peak[:, :], k.peak[:, :]))
            c.link(dve.tensor_tensor(k.lp[:, :, 0:4], G4, bcast(k.peak[:, :], 2, 4), ALU.mult))
            c.link(dve.tensor_tensor(G4, k.lp[:, :, 0:4], k.lp[:, :, 1:5], ALU.add))
            for half in range(2):
                v = k.logit[:, :, 4 * half:4 * half + 4]
                c.link(dve.scalar_tensor_tensor(v, G4, 0.1, v, ALU.mult, ALU.add))
        c.link(dve.tensor_reduce(k.peak[:, :], L, AX.X, ALU.max))
        c.link(dve.tensor_tensor(L, L, bcast(k.peak[:, :], 2, 8), ALU.subtract))
        c.link(dve.tensor_scalar(L, L, -104.0, None, ALU.max))
        mine, other = bcast(L, 3, 8), bcast(L, 2, 8)
        c.step(dve.tensor_tensor(k.more[:, :, :, :], other, mine, ALU.is_gt))
        c.link(dve.tensor_tensor(k.same[:, :, :, :], other, mine, ALU.is_equal))
        c.link(dve.tensor_tensor(k.same[:, :, :, :], k.same[:, :, :, :], bcast(k.lower, 1, B), ALU.mult))
        c.link(dve.tensor_tensor(k.more[:, :, :, :], k.more[:, :, :, :], k.same[:, :, :, :], ALU.add))
        last = dve.tensor_reduce(k.rank[:, :, :], k.more[:, :, :, :], AX.X, ALU.add)
        if self.kind == "relu":
            c.link(last)
            dve.tensor_scalar(W, k.rank[:, :, :], 2.0, None, ALU.is_lt).then_inc(self.w_ready.sem, 1)
            dve.wait_ge(*self.w_ready.upto(1))
            return
        last.then_inc(self.l_ready.sem, 1)
        r = 1 if self.kind == "gelu" else 0
        exponentials(r)
        c.link(dve.tensor_scalar(W, k.rank[:, :, :], 2.0 if self.kind == "gelu" else 1.0, None, ALU.is_lt))
        if self.kind == "gelu":
            c.link(dve.tensor_tensor(L, L, W, ALU.mult))
        c.link(dve.tensor_reduce(k.peak[:, :], L, AX.X, ALU.add))
        c.link(dve.reciprocal(k.peak[:, :], k.peak[:, :]))
        if self.kind == "gelu":
            dve.tensor_tensor(W, L, bcast(k.peak[:, :], 2, 8), ALU.mult).then_inc(self.w_ready.sem, 1)
            dve.wait_ge(*self.w_ready.upto(1))
        else:
            c.link(dve.tensor_tensor(W, W, bcast(k.peak[:, :], 2, 8), ALU.mult))


class Depool:

    def __init__(self, k, norm, turn, w_inT, setup=None):
        self.k, self.norm, self.turn, self.w_inT, self.setup = k, norm, turn, w_inT, setup
        self.y_done = k.sig["dp_y_done"].take(2)

    def tensor(self, pe):
        k = self.k
        for h in range(2):
            if self.setup:
                for b in range(4 * h, 4 * h + 4):
                    self.setup.pick(pe, h, b, k.patches0)
            else:
                pe.wait_ge(*k.pooled_ready.upto(h + 1))
                pe.matmul(k.ps[:, h, :], k.ident, k.pooled3[:, 4 * h:4 * h + 4, :].rearrange("p b d -> p (b d)"),
                          start=True, stop=True)
        self.turn.tensor(pe)
        for b in range(B):
            pe.wait_ge(*self.turn.xT_ready.upto(b // 4 + 1))
            m = pe.matmul(k.ps[:, b // 4, b % 4 * P:(b % 4 + 1) * P], k.xnT[:, b * P:(b + 1) * P], self.w_inT,
                          start=False, stop=True, skip_group_check=True)
            if b % 4 == 3:
                m.then_inc(self.y_done.sem, 1)

    def vector(self, dve):
        k = self.k
        for h in range(2):
            dve.wait_ge(*self.y_done.upto(h + 1))
            k.dchain.link(dve.tensor_tensor(k.x[:, 4 * h:4 * h + 4, :], k.x[:, 4 * h:4 * h + 4, :],
                                            k.ps[:, h, :].rearrange("s (b d) -> s b d", d=D), ALU.add))
            token_stats(k, dve, k.x, range(4 * h, 4 * h + 4))


class AfterNorm:

    def __init__(self, k, gain, bias, eps=LN_EPS):
        self.k, self.gain, self.bias, self.eps = k, gain, bias, eps
        self.var_ready = k.sig["var_ready"].take(1)
        self.rstd_ready = k.sig["rstd_ready"].take(1)
        self.bias_in = k.sig["an_bias_in"].take(1)

    def pool(self, pool):
        k = self.k
        pool.tensor_tensor(k.x[:, :, :], k.x[:, :, :], bcast(self.bias, 1, B), ALU.add).then_inc(self.bias_in.sem, 1)
        pool.wait_ge(*self.var_ready.upto(1))
        pool.tensor_tensor(k.rstd[:, :], k.var_eps[:, :], bcast(k.minus_half[:, 0], 1, B), ALU.pow)\
            .then_inc(self.rstd_ready.sem, 1)

    def vector(self, dve):
        k, c = self.k, self.k.dchain
        c.settle()
        dve.tensor_scalar(k.var_eps[:, :], k.mv[:, :, 1], self.eps, None, ALU.add).then_inc(self.var_ready.sem, 1)
        for b in range(B):
            c.step(dve.scalar_tensor_tensor(k.xn[:, b, :], k.r[:, b, :], k.mv[:, b, 0:1], self.gain, ALU.subtract, ALU.mult))
        dve.wait_ge(*self.rstd_ready.upto(1))
        dve.wait_ge(*self.bias_in.upto(1))
        c.settle()
        for b in range(B):
            c.step(dve.scalar_tensor_tensor(k.x[:, b, :], k.xn[:, b, :], k.rstd[:, b:b + 1], k.x[:, b, :], ALU.mult, ALU.add))
        c.settle()
        token_stats(k, dve, k.x, range(B))


class DenseStart:

    def __init__(self, k, norm):
        self.k, self.norm = k, norm
        self.ready = k.sig["dense_start"].take(1)

    def pool(self, pool):
        k = self.k
        pool.wait_ge(*self.norm.xn_ready.upto(B))
        k.pchain.link(pool.tensor_tensor(k.r[:, :, :], k.xn[:, :, :], bcast(k.ln1_g, 1, B), ALU.mult))
        k.pchain.link(pool.tensor_tensor(k.r[:, :, :], k.r[:, :, :], bcast(k.ln1_b, 1, B), ALU.add))
        pool.tensor_tensor(k.r[:, :, :], k.r[:, :, :], bcast(k.dense_b2, 1, B), ALU.add).then_inc(self.ready.sem, 1)

    def vector(self, dve):
        dve.wait_ge(*self.ready.upto(1))


class Mamba:

    N, K, C = 16, 4, 2

    def __init__(self, k, norm, turn):
        self.k, self.norm, self.turn = k, norm, turn
        sig = k.sig
        t = lambda name, n: sig["mb_" + name].take(n)
        self.pad_ready = t("pad_ready", 1)
        self.started = t("started", 1)
        self.in_done = t("in_done", 8)
        self.u_in = t("u_in", 4)
        self.gate_ready = t("gate_ready", 4)
        self.conv_done = t("conv_done", 4)
        self.u_ready = t("u_ready", 4)
        self.dl_done = t("dl_done", 2)
        self.dl_ready = t("dl_ready", 2)
        self.bc_done = t("bc_done", 2)
        self.bc_ready = t("bc_ready", 1)
        self.bc_rounded = t("bc_rounded", 1)
        self.dt_done = t("dt_done", 4)
        self.z_ready = t("z_ready", 2)
        self.lg_ready = t("lg_ready", 2)
        self.du_ready = t("du_ready", 2)
        self.a_exp = t("a_exp", 1)
        self.b_done = t("b_done", self.N)
        self.c_done = t("c_done", self.N)
        self.c_ready = t("c_ready", self.N)
        self.dA_ready = [t(f"dA_ready{c}", self.N) for c in range(2)]
        self.dbu_done = t("dbu_done", 2 * self.N)
        self.scanned = [t(f"scanned{c}", self.N) for c in range(2)]
        self.sc_ready = [t(f"sc_ready{c}", self.N) for c in range(2)]
        self.y_done = [t(f"y_done{c}", self.N) for c in range(2)]
        self.lasts_ready = t("lasts_ready", 2)
        self.yg_ready = t("yg_ready", 2)
        self.out_done = t("out_done", 2)

    def tensor(self, pe, beside):
        k = self.k
        pe.wait_ge(*self.turn.xT_ready.upto(2))
        k.arrived(pe, "mamba")
        k.arrived(pe, "masks")
        for c in range(4):
            for h in range(2):
                pe.matmul(k.ps[:, 2 * c + h, :], k.mb_win[:, c * P:(c + 1) * P], k.xnT[:, h * HALF:(h + 1) * HALF],
                          start=True, stop=True).then_inc(self.in_done.sem, 1)
        pe.wait_ge(*self.u_in.upto(4))
        pe.wait_ge(*self.pad_ready.upto(1))
        for o in range(2):
            for h in range(2):
                for n, (tap, c) in enumerate((tap, c) for tap in range(self.K) for c in range(2)):
                    m = pe.matmul(k.ps[:, 2 * o + h, :], k.mb_conv[:, 2 * tap + c, o * P:(o + 1) * P],
                                  k.upad[:, c, 4 * h:4 * h + 4, tap:tap + P], start=n == 0, stop=n == 2 * self.K - 1)
                m.then_inc(self.conv_done.sem, 1)
        pe.wait_ge(*self.gate_ready.upto(4))
        pe.wait_ge(*self.u_ready.upto(4))
        self.narrow(pe, 4, k.mb_wx[:, :, 0:64], 64, self.dl_done)
        for c in range(2):
            for h in range(2):
                pe.wait_ge(*self.dl_ready.upto(h + 1))
                pe.matmul(k.ps[:, 2 * c + h, :], k.mb_wdt[:, c * P:(c + 1) * P], k.dlT[:, h * HALF:(h + 1) * HALF],
                          start=True, stop=True).then_inc(self.dt_done.sem, 1)
        self.narrow(pe, 6, k.wx3, 96, self.bc_done)
        pe.wait_ge(*self.bc_ready.upto(1))
        for bank in range(4, 8):
            pe.matmul(k.ps[:, bank, :], k.ident, k.zeros, start=True, stop=False)
        pe.wait_ge(*self.z_ready.upto(2))
        self.spread(pe, 0)
        with pe.Fori(0, self.N // 2 - 1) as i:
            for q in range(2):
                self.spread(pe, 2 * i + (q + 1))
                self.sum_up(pe, 2 * i + q, False)
        self.spread(pe, self.N - 1)
        self.sum_up(pe, self.N - 2, False)
        self.sum_up(pe, self.N - 1, True)
        pe.wait_ge(*self.c_ready.upto(self.N))
        beside.first_keys(pe, 0)
        pe.wait_ge(*self.yg_ready.upto(2))
        for b in range(B):
            for c in range(2):
                m = pe.matmul(k.ps[:, b // 4, b % 4 * P:(b % 4 + 1) * P], k.yg[:, c, b * P:(b + 1) * P],
                              k.mb_wout[:, c, :], start=c == 0, stop=c == 1)
            if b % 4 == 3:
                m.then_inc(self.out_done.sem, 1)
        beside.first_keys(pe, 1)
        beside.first_values(pe)

    def narrow(self, pe, bank, w, rows, done):
        k = self.k
        for h in range(2):
            for c in range(2):
                m = pe.matmul(k.ps[0:rows, bank + h, :], w[:, c, :], k.u[:, c, h * HALF:(h + 1) * HALF],
                              start=c == 0, stop=c == 1)
            m.then_inc(done.sem, 1)

    def spread(self, pe, n):
        k = self.k
        pe.wait_ge(*self.dbu_done.upto(2 * n))
        for h in range(2):
            m = pe.matmul(k.ps[:, h, :], k.sel[:, bass.ts(n, P)], k.bc3[:, h * HALF:(h + 1) * HALF],
                          start=True, stop=True)
        m.then_inc(self.b_done.sem, 1)
        pe.wait_ge(*self.c_ready.upto(n))
        for h in range(2):
            m = pe.matmul(k.ps[:, 2 + h, :], k.sel[:, bass.ts(n + self.N, P)], k.bc3[:, h * HALF:(h + 1) * HALF],
                          start=True, stop=True)
        m.then_inc(self.c_done.sem, 1)

    def sum_up(self, pe, n, last):
        k = self.k
        for c in range(2):
            pe.wait_ge(*self.sc_ready[c].upto(n + 1))
            for h in range(2):
                m = pe.matmul(k.ps[:, 4 + 2 * c + h, :], k.ident, k.sC[c][:, h * HALF:(h + 1) * HALF],
                              start=False, stop=last)
            m.then_inc(self.y_done[c].sem, 1)

    def scalar(self, act):
        k = self.k
        for c in range(2):
            for h in range(2):
                act.wait_ge(*self.in_done.upto(2 * c + h + 1))
                act.activation(k.upad[:, c, 4 * h:4 * h + 4, self.K - 1:self.K - 1 + P],
                               k.ps[:, 2 * c + h, :].rearrange("p (b t) -> p b t", t=P), ACT.Copy)\
                    .then_inc(self.u_in.sem, 1)
        for c in range(2):
            for h in range(2):
                act.wait_ge(*self.in_done.upto(4 + 2 * c + h + 1))
                act.activation(k.gate[:, c, h * HALF:(h + 1) * HALF], k.ps[:, 4 + 2 * c + h, :], ACT.Silu)\
                    .then_inc(self.gate_ready.sem, 1)
        for o in range(2):
            for h in range(2):
                act.wait_ge(*self.conv_done.upto(2 * o + h + 1))
                j = k.col["conv_b"] + o
                act.activation(k.u[:, o, h * HALF:(h + 1) * HALF], k.ps[:, 2 * o + h, :], ACT.Silu,
                               bias=k.cols[:, j:j + 1]).then_inc(self.u_ready.sem, 1)
        for h in range(2):
            act.wait_ge(*self.dl_done.upto(h + 1))
            act.activation(k.dlT[:, h * HALF:(h + 1) * HALF], k.ps[0:64, 4 + h, :], ACT.Copy)\
                .then_inc(self.dl_ready.sem, 1)
        k.arrived(act, "mamba")
        act.activation(k.a_exp[:, :, :], k.a_log[:, :, :], ACT.Exp).then_inc(self.a_exp.sem, 1)
        for c in range(2):
            act.wait_ge(*self.z_ready.upto(c + 1))
            k.achain.step(act.activation(k.sp[:, c, :], k.sp[:, c, :], ACT.Exp))
        act.wait_ge(*self.bc_done.upto(2))
        act.activation(k.bc3[0:96, :], k.ps[0:96, 6:8, :].rearrange("p a n -> p (a n)"), ACT.Copy)\
            .then_inc(self.bc_rounded.sem, 1)
        k.achain.settle()
        for c in range(2):
            act.activation(k.sp[:, c, :], k.sp[:, c, :], ACT.Ln, bias=k.one_col).then_inc(self.lg_ready.sem, 1)
        with act.Fori(0, self.N // 2) as i:
            for q in range(2):
                n = 2 * i + q
                for c in range(2):
                    act.wait_ge(*self.scanned[c].upto(n))
                    act.wait_ge(*self.started.upto(1))
                    act.activation(k.s_lasts[:, c, bass.ds(n, 1), :].rearrange("p o b -> p (o b)"), self.last_of(c), ACT.Copy)
                    act.activation(k.dA[c][:, :, 1:S], k.delta[:, c, :].rearrange("p (b t) -> p b t", t=S)[:, :, 1:S],
                                   ACT.Exp, scale=k.a_neg[:, bass.ds(n + 16 * c, 1)]).then_inc(self.dA_ready[c].sem, 1)
                    if c == 0:
                        act.wait_ge(*self.c_done.upto(n + 1))
                        act.wait_ge(*self.sc_ready[1].upto(n - 1))
                        act.activation(k.cb[q][:, :], k.ps[:, 2:4, :].rearrange("p a n -> p (a n)"), ACT.Copy)\
                            .then_inc(self.c_ready.sem, 1)

        for c in range(2):
            act.wait_ge(*self.scanned[c].upto(self.N))
            act.activation(k.s_lasts[:, c, self.N, :], self.last_of(c), ACT.Copy).then_inc(self.lasts_ready.sem, 1)

    def last_of(self, c):
        return self.k.s[c][:, :].rearrange("p (b t) -> p b t", t=S)[:, :, S - 1]

    def vector(self, dve):
        k, c_ = self.k, self.k.dchain
        dve.wait_ge(*self.a_exp.upto(1))
        c_.step(dve.tensor_scalar(k.a_neg[:, :], k.a_exp[:, :, :].rearrange("p c n -> p (c n)"), -1.0, None, ALU.mult))
        for c in range(2):
            dve.wait_ge(*self.dt_done.upto(2 * c + 2))
            z = k.ps[:, 2 * c:2 * c + 2, :].rearrange("p a n -> p (a n)")
            j = k.col["b_dt"] + c
            c_.link(dve.tensor_scalar(k.delta[:, c, :], z, k.cols[:, j:j + 1], None, ALU.add))
            dve.scalar_tensor_tensor(k.sp[:, c, :], k.delta[:, c, :], -1.0, k.delta[:, c, :], ALU.mult, ALU.min)\
                .then_inc(self.z_ready.sem, 1)
        dve.wait_ge(*self.bc_rounded.upto(1))
        src = k.ps[:, 6:8, :].rearrange("p a n -> p (a n)")
        c_.link(dve.tensor_tensor(k.rest[:, :], src[0:96, :], k.bc3[0:96, :], ALU.subtract))
        c_.step(dve.tensor_copy(k.bc3[32:64, :], k.rest[32:64, :]))
        c_.link(dve.tensor_copy(k.bc3[64:96, :], k.rest[64:96, :]))
        c_.link(dve.tensor_tensor(k.rest[64:96, :], k.rest[64:96, :], k.bc3[64:96, :], ALU.subtract))
        dve.tensor_copy(k.bc3[64:96, :], k.rest[64:96, :]).then_inc(self.bc_ready.sem, 1)
        for c in range(2):
            dve.wait_ge(*self.lg_ready.upto(c + 1))
            c_.link(dve.scalar_tensor_tensor(k.delta[:, c, :], k.delta[:, c, :], 0.0, k.sp[:, c, :], ALU.max, ALU.add))
            dve.wait_ge(*self.u_ready.upto(4))
            dve.tensor_tensor(k.du[:, c, :], k.delta[:, c, :], k.u[:, c, :], ALU.mult).then_inc(self.du_ready.sem, 1)
        dve.wait_ge(*self.du_ready.upto(2))
        for c in range(2):
            c_.step(dve.memset(k.dA[c][:, :, 0:1], 0.0))
            c_.step(dve.memset(self.last_of(c), 0.0))
        c_.settle()
        dve.sem_inc(self.started.sem, 1)
        dve.wait_ge(*self.started.upto(1))
        with dve.Fori(0, self.N) as n:
            for c in range(2):
                dve.wait_ge(*self.b_done.upto(n + 1))
                dve.wait_ge(*self.scanned[c].upto(n))
                dve.tensor_tensor(k.dbu[c][:, :], k.ps[:, 0:2, :].rearrange("p a n -> p (a n)"), k.du[:, c, :],
                                  ALU.mult).then_inc(self.dbu_done.sem, 1)
                dve.wait_ge(*self.dbu_done.upto(2 * n + (c + 1)))
                dve.wait_ge(*self.dA_ready[c].upto(n + 1))
                dve.wait_ge(*self.sc_ready[c].upto(n))
                dve.tensor_tensor_scan(k.s[c][:, :], k.dA[c][:, :, :].rearrange("p b t -> p (b t)"), k.dbu[c][:, :],
                                       0.0, ALU.mult, ALU.add).then_inc(self.scanned[c].sem, 1)
        for c in range(2):
            j = k.col["ssm_d"] + c
            dve.wait_ge(*self.y_done[c].upto(self.N))
            dve.wait_ge(*self.lasts_ready.upto(c + 1))
            c_.link(dve.tensor_reduce(k.s_last[:, c, :], k.s_lasts[:, c, :, :].rearrange("p n b -> p b n"), AX.X, ALU.add))
            c_.link(dve.tensor_scalar(k.s_last[:, c, :], k.s_last[:, c, :], k.cols[:, j:j + 1], None, ALU.mult))
            y = k.ps[:, 4 + 2 * c:6 + 2 * c, :].rearrange("p a (b t) -> p (a b) t", t=S)
            c_.link(dve.tensor_tensor(k.yg[:, c, :].rearrange("p (b t) -> p b t", t=S), y,
                                      bcast(k.s_last[:, c, :], 2, S), ALU.add))
            dve.wait_ge(*self.gate_ready.upto(4))
            dve.tensor_tensor(k.yg[:, c, :], k.yg[:, c, :], k.gate[:, c, :], ALU.mult).then_inc(self.yg_ready.sem, 1)
        for h in range(2):
            dve.wait_ge(*self.out_done.upto(h + 1))
            c_.link(dve.tensor_tensor(k.x[:, 4 * h:4 * h + 4, :], k.x[:, 4 * h:4 * h + 4, :],
                                      k.ps[:, h, :].rearrange("s (b d) -> s b d", d=D), ALU.add))
            token_stats(k, dve, k.x, range(4 * h, 4 * h + 4))

    def pool(self, pool):
        k = self.k
        pool.wait_ge(*self.turn.xT_ready.upto(2))
        k.arrived(pool, "mamba")
        for j in range(3):
            pool.tensor_copy(k.wx3[:, :, 32 * j:32 * j + 32], k.mb_wx[:, :, 64:96])
        pool.memset(k.zeros, 0.0)
        pool.memset(k.upad[:, 0, :, 0:self.K - 1], 0.0)
        pool.memset(k.upad[:, 1, :, 0:self.K - 1], 0.0).then_inc(self.pad_ready.sem, 1)
        with pool.Fori(0, self.N // 2) as i:
            for q in range(2):
                n = 2 * i + q
                for c in range(2):
                    pool.wait_ge(*self.scanned[c].upto(n + 1))
                    pool.wait_ge(*self.c_ready.upto(n + 1))
                    pool.wait_ge(*self.y_done[c].upto(n))
                    pool.tensor_tensor(k.sC[c][:, :], k.s[c][:, :], k.cb[q][:, :], ALU.mult)\
                        .then_inc(self.sc_ready[c].sem, 1)


class WideCross:

    H, DH, T = 16, 64, M + 1
    SHARED = 7
    KEYS0, VALUES0, QUERIES0 = (2, 3), (6, 7), (7, 6)

    def __init__(self, k, norm, turn):
        self.k, self.norm, self.turn = k, norm, turn
        sig = k.sig
        self.clear = sig["wc_clear"].take(1)
        self.cT_ready = sig["wc_cT_ready"].take(B)
        self.q_done = sig["wc_q_done"].take(2 * B)
        self.k_done = sig["wc_k_done"].take(2 * B)
        self.v_done = sig["wc_v_done"].take(2 * B)
        self.q_ready = sig["wc_q_ready"].take(2 * B)
        self.k_ready = sig["wc_k_ready"].take(2 * B)
        self.v_ready = sig["wc_v_ready"].take(2 * B)
        self.s_done = sig["at_s_done"].take(4 * B)
        self.max_ready = sig["at_max_ready"].take(4 * B)
        self.p_ready = sig["at_p_ready"].take(4 * B)
        self.rec_ready = sig["at_rec_ready"].take(4 * B)
        self.pn_ready = sig["at_pn_ready"].take(4 * B)
        self.pt_done = sig["at_pt_done"].take(4 * B)
        self.ptv_ready = sig["at_ptv_ready"].take(2 * B)
        self.pta_ready = sig["at_pta_ready"].take(2 * B)
        self.av_done = sig["wc_av_done"].take(4 * B)
        self.o_ready = sig["wc_o_ready"].take(2 * B)
        self.y_done = sig["at_y_done"].take(B)
        self.y_ready = sig["at_res_done"].take(B)

    def sync(self, sp, null_v):
        k = self.k
        sp.wait_ge(*self.turn.xT_ready.upto(2))
        sp.dma_start(k.wv[M:M + 1, :].rearrange("o (h d) -> o h d", h=self.H), bcast(null_v, 1, self.H))\
            .then_inc(k.loads["null_v"], 16)

    def pool(self, pool):
        k = self.k
        pool.wait_ge(*self.turn.xT_ready.upto(2))
        k.arrived(pool, "null_k")
        pool.tensor_copy(k.kT[:, :, M], k.null_k[:, 0:1].to_broadcast([P, 8])).then_inc(self.clear.sem, 1)
        for u in range(4):
            self.normalise(pool, 0, u)
        with pool.Fori(0, B - 1) as b:
            self.context(pool, b + 1)
            for u in range(4):
                self.normalise(pool, b + 1, u)

    def context(self, pool, n):
        k = self.k
        if not isinstance(n, int):
            pool.wait_ge(*self.v_done.upto(2 * n))
        for c in range(2):
            t = pool.tensor_copy(k.cT[:, c, :], k.ctxT[:, c, bass.ts(n, M)])
        t.then_inc(self.cT_ready.sem, 1)

    def normalise(self, pool, n, u):
        k = self.k
        pool.wait_ge(*self.rec_ready.upto(4 * n + u + 1))
        w = k.p[0][:, 4 * u:4 * u + 4, 0:self.T]
        pool.tensor_tensor(w, w, bcast(k.rec[0][:, 4 * u:4 * u + 4], 2, self.T), ALU.mult).then_inc(self.pn_ready.sem, 1)

    def tensor(self, pe):
        k = self.k
        pe.wait_ge(*self.turn.xT_ready.upto(2))
        pe.wait_ge(*self.clear.upto(1))
        pe.wait_ge(*self.v_ready.upto(2))
        for h in range(2):
            self.queries(pe, 0, h, self.QUERIES0[h])
        for u in range(4):
            self.scores(pe, 0, u)
        k.arrived(pe, "null_v")
        with pe.Fori(0, B - 1) as b:
            self.turn_weights(pe, b, 0)
            pe.wait_ge(*self.y_ready.upto(b))
            self.queries(pe, b + 1, 0)
            self.turn_weights(pe, b, 1)
            self.times_v(pe, b, 0)
            self.keys(pe, b + 1, 0)
            self.turn_weights(pe, b, 2)
            self.times_v(pe, b, 1)
            self.scores(pe, b + 1, 0)
            self.queries(pe, b + 1, 1)
            self.turn_weights(pe, b, 3)
            self.times_v(pe, b, 2)
            self.keys(pe, b + 1, 1)
            self.scores(pe, b + 1, 1)
            self.times_v(pe, b, 3)
            self.values(pe, b + 1, 0)
            self.scores(pe, b + 1, 2)
            self.values(pe, b + 1, 1)
            self.scores(pe, b + 1, 3)
            pe.wait_ge(*self.v_ready.upto(2 * b + 4))
            self.out(pe, b)
        last = B - 1
        self.turn_weights(pe, last, 0)
        self.turn_weights(pe, last, 1)
        for u in range(4):
            self.times_v(pe, last, u)
            if u < 2:
                self.turn_weights(pe, last, u + 2)
        pe.wait_ge(*self.y_ready.upto(last))
        self.out(pe, last)

    def first_keys(self, pe, h):
        k = self.k
        k.arrived(pe, "wide_cross")
        self.project_keys(pe, 0, h, self.KEYS0[h])

    def first_values(self, pe):
        pe.wait_ge(*self.cT_ready.upto(1))
        for h in range(2):
            self.project_values(pe, h, self.VALUES0[h])

    def queries(self, pe, n, h, bank=SHARED):
        k = self.k
        if h:
            pe.wait_ge(*self.k_ready.upto(2 * n + 1))
        for j in range(4):
            c = 4 * h + j
            m = pe.matmul(k.ps[:, bank, j * P:(j + 1) * P], k.wq[:, c * P:(c + 1) * P], k.xnT[:, bass.ts(n, P)],
                          start=True, stop=True)
        m.then_inc(self.q_done.sem, 1)

    def keys(self, pe, n, h):
        pe.wait_ge(*self.q_ready.upto(2 * n + h + 1))
        self.project_keys(pe, n, h, self.SHARED)

    def project_keys(self, pe, n, h, bank):
        k = self.k
        for j in range(4):
            c = 4 * h + j
            for e in range(2):
                m = pe.matmul(k.ps[:, bank, j * P:j * P + M], k.wkv[:, e, c * P:(c + 1) * P],
                              k.ctxT[:, e, bass.ts(n, M)], start=e == 0, stop=e == 1)
        m.then_inc(self.k_done.sem, 1)

    def values(self, pe, n, h):
        pe.wait_ge(*self.cT_ready.upto(n + 1))
        if h:
            pe.wait_ge(*self.v_ready.upto(2 * n + 1))
        else:
            pe.wait_ge(*self.k_ready.upto(2 * n + 2))
        self.project_values(pe, h, self.SHARED)

    def project_values(self, pe, h, bank):
        k = self.k
        for e in range(2):
            m = pe.matmul(k.ps[0:M, bank, :], k.cT[:, e, :], k.wkv[:, e, 1024 + h * HALF:1024 + (h + 1) * HALF],
                          start=e == 0, stop=e == 1)
        m.then_inc(self.v_done.sem, 1)

    def scores(self, pe, n, u):
        k = self.k
        if u % 2 == 0:
            pe.wait_ge(*self.q_ready.upto(2 * n + u // 2 + 1))
            pe.wait_ge(*self.k_ready.upto(2 * n + u // 2 + 1))
        pe.wait_ge(*self.p_ready.upto(0 if isinstance(n, int) else 4 * n + (u - 3)))
        r = slice(64 * (u % 2), 64 * (u % 2) + 64)
        for j in range(4):
            c = 4 * (u // 2) + j
            m = pe.matmul(k.ps[:, u, j * P:j * P + self.T], k.qT[r, c, :], k.kT[r, c, :], start=True, stop=True)
        m.then_inc(self.s_done.sem, 1)

    def turn_weights(self, pe, b, u):
        k = self.k
        pe.wait_ge(*self.pn_ready.upto(4 * b + u + 1))
        ready = self.pta_ready if u % 2 else self.ptv_ready
        pe.wait_ge(*ready.upto(2 * b + u // 2))
        for j in range(4):
            t = pe.transpose(k.ps[0:self.T, PT0 + u % 2, j * P:(j + 1) * P], k.p[0][:, 4 * u + j, 0:self.T], k.ident)
        t.then_inc(self.pt_done.sem, 1)

    def times_v(self, pe, b, u):
        k = self.k
        ready = self.pta_ready if u % 2 else self.ptv_ready
        pe.wait_ge(*ready.upto(2 * b + u // 2 + 1))
        if u == 0:
            pe.wait_ge(*self.v_ready.upto(2 * b + 2))
        if u % 2 == 0:
            pe.wait_ge(*self.o_ready.upto(2 * b + u // 2))
        r = u % 2
        for j in range(4):
            h = 2 * (4 * (u // 2) + j) + r
            m = pe.matmul(k.ps[64 * r:64 * r + 64, OB, j * P:(j + 1) * P], k.wv[0:self.T, h * self.DH:(h + 1) * self.DH],
                          k.pT[r][0:self.T, j, :], start=True, stop=True)
        m.then_inc(self.av_done.sem, 1)

    def out(self, pe, b):
        k = self.k
        pe.wait_ge(*self.o_ready.upto(2 * b + 2))
        for c in range(8):
            m = pe.matmul(k.ps[:, self.SHARED, 0:P], k.woT[:, c, :], k.wout[:, c, :], start=c == 0, stop=c == 7)
        m.then_inc(self.y_done.sem, 1)

    def vector(self, dve):
        k, c = self.k, self.k.dchain
        for h in range(2):
            self.queries_in(dve, 0, h, self.QUERIES0[h])
        for u in range(4):
            self.maxima(dve, 0, u)
            if u:
                self.sums(dve, 0, u - 1)
        with dve.Fori(0, B - 1) as b:
            c.enter(b, 4 + 4)
            self.turned_even(dve, b, 0)
            self.sums(dve, b, 3)
            self.queries_in(dve, b + 1, 0)
            self.turned_even(dve, b, 2)
            self.maxima(dve, b + 1, 0)
            self.queries_in(dve, b + 1, 1)
            self.sums(dve, b + 1, 0)
            self.maxima(dve, b + 1, 1)
            self.maxima(dve, b + 1, 2)
            self.sums(dve, b + 1, 1)
            self.maxima(dve, b + 1, 3)
            self.sums(dve, b + 1, 2)
            self.collect(dve, b)
        c.leave(B - 1)
        last = B - 1
        self.sums(dve, last, 3)
        self.turned_even(dve, last, 0)
        self.turned_even(dve, last, 2)
        dve.wait_ge(*self.y_ready.upto(last))
        token_stats(k, dve, k.r, range(last))
        self.collect(dve, last)
        dve.wait_ge(*self.y_ready.upto(B))
        token_stats(k, dve, k.r, range(last, B))

    def queries_in(self, dve, n, h, bank=SHARED):
        k = self.k
        dve.wait_ge(*self.q_done.upto(2 * n + h + 1))
        dve.tensor_copy(k.qT[:, 4 * h:4 * h + 4, :].rearrange("p c t -> p (c t)"), k.ps[:, bank, :])\
            .then_inc(self.q_ready.sem, 1)

    def maxima(self, dve, n, u):
        k = self.k
        dve.wait_ge(*self.s_done.upto(4 * n + u + 1))
        hs = slice(4 * u, 4 * u + 4)
        src = k.ps[:, u, :].rearrange("q (h t) -> q h t", t=P)[:, :, 0:self.T]
        k.dchain.link(dve.tensor_reduce(k.mx[0][:, hs], src, AX.X, ALU.max))
        dve.tensor_scalar(k.nmx[0][:, hs], k.mx[0][:, hs], -0.125, None, ALU.mult).then_inc(self.max_ready.sem, 1)

    def sums(self, dve, n, u):
        k = self.k
        dve.wait_ge(*self.p_ready.upto(4 * n + u + 1))
        hs = slice(4 * u, 4 * u + 4)
        k.dchain.link(dve.tensor_reduce(k.total[0][:, hs], k.p[0][:, hs, 0:self.T], AX.X, ALU.add))
        dve.reciprocal(k.rec[0][:, hs], k.total[0][:, hs]).then_inc(self.rec_ready.sem, 1)

    def turned_even(self, dve, b, u):
        k = self.k
        dve.wait_ge(*self.pt_done.upto(4 * b + u + 1))
        if u:
            dve.wait_ge(*self.av_done.upto(4 * b + u - 1))
        dve.tensor_copy(k.pT[0][0:self.T, :, :].rearrange("t h q -> t (h q)"), k.ps[0:self.T, PT0, :])\
            .then_inc(self.ptv_ready.sem, 1)

    def collect(self, dve, b):
        k = self.k
        dve.wait_ge(*self.y_done.upto(b + 1))
        dve.tensor_copy(k.r[:, bass.ds(b, 1), :].rearrange("q o d -> q (o d)"), k.ps[:, self.SHARED, 0:P])\
            .then_inc(self.y_ready.sem, 1)

    def scalar_first(self, act):
        for h in range(2):
            self.keys_in(act, 0, h, self.KEYS0[h])
        for h in range(2):
            self.values_in(act, 0, h, self.VALUES0[h])

    def scalar(self, act):
        for u in range(4):
            self.weights(act, 0, u)
        with act.Fori(0, B - 1) as b:
            self.turned_odd(act, b, 1)
            self.keys_in(act, b + 1, 0)
            self.outputs(act, b, 0)
            self.weights(act, b + 1, 0)
            self.turned_odd(act, b, 3)
            self.keys_in(act, b + 1, 1)
            self.weights(act, b + 1, 1)
            self.values_in(act, b + 1, 0)
            self.outputs(act, b, 1)
            self.weights(act, b + 1, 2)
            self.values_in(act, b + 1, 1)
            self.weights(act, b + 1, 3)
        last = B - 1
        self.turned_odd(act, last, 1)
        self.outputs(act, last, 0)
        self.turned_odd(act, last, 3)
        self.outputs(act, last, 1)

    def keys_in(self, act, n, h, bank=SHARED):
        k = self.k
        act.wait_ge(*self.k_done.upto(2 * n + h + 1))
        act.activation(k.kT[:, 4 * h:4 * h + 4, 0:M], k.ps[:, bank, :].rearrange("p (c t) -> p c t", t=P)[:, :, 0:M],
                       ACT.Copy).then_inc(self.k_ready.sem, 1)

    def values_in(self, act, n, h, bank=SHARED):
        k = self.k
        act.wait_ge(*self.v_done.upto(2 * n + h + 1))
        act.activation(k.wv[0:M, h * HALF:(h + 1) * HALF], k.ps[0:M, bank, :], ACT.Copy).then_inc(self.v_ready.sem, 1)

    def weights(self, act, n, u):
        k = self.k
        act.wait_ge(*self.max_ready.upto(4 * n + u + 1))
        for j in range(4):
            h = 4 * u + j
            e = act.activation(k.p[0][:, h, 0:self.T], k.ps[:, u, j * P:j * P + self.T], ACT.Exp,
                               bias=k.nmx[0][:, h:h + 1], scale=0.125)
        e.then_inc(self.p_ready.sem, 1)

    def turned_odd(self, act, b, u):
        k = self.k
        act.wait_ge(*self.pt_done.upto(4 * b + u + 1))
        if u > 1:
            act.wait_ge(*self.av_done.upto(4 * b + u - 1))
        act.activation(k.pT[1][0:self.T, :, :].rearrange("t h q -> t (h q)"), k.ps[0:self.T, PT0 + 1, :], ACT.Copy)\
            .then_inc(self.pta_ready.sem, 1)

    def outputs(self, act, b, h):
        k = self.k
        act.wait_ge(*self.av_done.upto(4 * b + 2 * h + 2))
        act.activation(k.woT[:, 4 * h:4 * h + 4, :].rearrange("p c t -> p (c t)"), k.ps[:, OB, :], ACT.Copy)\
            .then_inc(self.o_ready.sem, 1)


ROWS = [("relu_b1", 32), ("gelu_b1", 32), ("gate_b1", 32), ("dense_b1", 4), ("g_res0", 1), ("g_res3", 1),
        ("gamma", 1), ("beta", 1), ("conv_b", 2), ("b_dt", 2), ("ssm_d", 2), ("ln1_g", 1), ("ln1_b", 1)]
COL = {name: sum(n for _, n in ROWS[:j]) for j, (name, _) in enumerate(ROWS)}
NROWS = sum(n for _, n in ROWS)
WIDE = ["ln1_g", "ln1_b", "ln2_g", "ln2_b", "dense_b2", "b_in0", "b_in3", "g_init0", "g_init3", "ln_scale", "ln_bias"]
LOADS = {"x": 1, "first": 1, "l0": 6, "lens": 1, "rows": len(ROWS), "routers": 3, "gates": 2, "pool_consts": 1,
         "lower": 1, "masks": 1, "ctx": 1, "keys": 2, "wide": len(WIDE) + 4, "b2": 24, "bit": 11, "l3": 2, "mamba": 6, "null_k": 2,
         "wide_cross": 3, "null_v": 1}


def constants():
    f = np.float32
    theta = (f(1.0) / f(10000.0) ** (np.arange(0, 8, 2, dtype=f) / f(8))).astype(f)
    angle = np.outer(np.arange(S, dtype=f), theta).astype(f)
    angle = np.tile(np.concatenate([angle, angle], axis=1), (1, 16)).T
    group = np.arange(P) % 32
    decay = -np.expm1(-DEPOOL_EPS)
    lag = np.arange(M)[None, :] - np.arange(M)[:, None]
    filt = np.zeros((P, P))
    filt[:M, :M] = np.where(lag >= 0, np.exp(-DEPOOL_EPS) * decay ** np.maximum(lag, 0), 0.0)
    lower = np.broadcast_to((np.arange(8)[None, :] < np.arange(8)[:, None]).reshape(1, 64), (P, 64))
    early = np.concatenate([np.eye(P), np.cos(angle), np.sin(angle), group[:, None] // 8 == np.arange(4),
                            group[:, None] // 16 == np.arange(2)], axis=1)
    late = np.concatenate([np.arange(P)[:, None] <= np.arange(P), np.broadcast_to(np.arange(P), (P, P)), filt, lower], axis=1)
    off = np.arange(S)[:, None] - np.arange(S)[None, :]
    causal = np.where(off >= 0, 0.0, NEG)
    band = np.where(np.abs(off) <= 32, 0.0, NEG)
    select = np.zeros((P, 32, P))
    for part in range(3):
        select[32 * part + np.arange(32), np.arange(32)] = 1.0
    half = np.concatenate([np.eye(P), causal, band, select.reshape(P, 32 * P)], axis=1)
    return early.astype(f), late.astype(f), (half.astype(f).view(np.uint32) >> 16).astype(np.uint16)


class Setup:

    def __init__(self, k):
        self.k = k
        t = lambda name, n: k.sig["su_" + name].take(n)
        self.w_turned = t("w_turned", 2)
        self.w_ready = t("w_ready", 2)
        self.flipped = t("flipped", 1)
        self.small_turned = t("small_turned", 2)
        self.small_ready = t("small_ready", 2)
        self.idx_ready = t("idx_ready", 1)
        self.idx_turned = t("idx_turned", 1)
        self.idxT_ready = t("idxT_ready", 1)
        self.edges_ready = t("edges_ready", 1)
        self.count_done = t("count_done", 1)
        self.edge_ready = t("edge_ready", 1)
        self.plug_done = t("plug_done", 1)
        self.plug_ready = t("plug_ready", 1)
        self.pick_ready = t("pick_ready", 1)
        self.pick_turned = t("pick_turned", 2)
        self.pickT_ready = t("pickT_ready", 2)
        self.ctx_turned = t("ctx_turned", 4)
        self.ctxT_ready = t("ctxT_ready", 4)
        self.ms_ready = t("ms_ready", 1)
        self.ctxn_ready = t("ctxn_ready", 1)
        self.spread_done = t("spread_done", 2)
        self.spread_ready = t("spread_ready", 1)
        self.pooled_done = t("pooled_done", 2)
        self.keyrow = t("keyrow", 1)

    def tensor_first(self, pe):
        k = self.k
        k.arrived(pe, "first")
        k.arrived(pe, "l0")
        for j in range(6):
            t = pe.transpose(k.ps[:, PT0 + j // 4, j % 4 * P:(j % 4 + 1) * P], k.w_raw[:, j, :], k.ident)
            if j in (3, 5):
                t.then_inc(self.w_turned.sem, 1)
        pe.wait_ge(*self.idx_ready.upto(1))
        pe.transpose(k.ps[0:M, 1, 0:B], k.idx[0:B, :], k.ident[0:B, 0:B]).then_inc(self.idx_turned.sem, 1)
        pe.wait_ge(*self.w_ready.upto(2))
        pe.wait_ge(*self.idxT_ready.upto(1))
        pe.wait_ge(*self.flipped.upto(1))

    def scalar_first(self, act):
        k = self.k
        for j in range(2):
            act.wait_ge(*self.w_turned.upto(j + 1))
            n = 4 - 2 * j
            act.activation(k.wT[:, 4 * j:4 * j + n, :].rearrange("p j e -> p (j e)"), k.ps[:, PT0 + j, 0:n * P],
                           ACT.Copy).then_inc(self.w_ready.sem, 1)
        act.wait_ge(*self.idx_turned.upto(1))
        act.activation(k.idxT[0:M, :], k.ps[0:M, 1, 0:B], ACT.Copy).then_inc(self.idxT_ready.sem, 1)

    def vector_first(self, dve):
        k, c = self.k, self.k.dchain
        k.arrived(dve, "lens")
        c.link(dve.tensor_copy(k.lens[:, :], k.lens_i[:, :]))
        c.link(dve.tensor_tensor_scan(k.cum[:, :], k.ones[0:B, 0:M], k.lens[:, :], 0.0, ALU.mult, ALU.add))
        c.link(dve.tensor_scalar(k.cum[:, :], k.cum[:, :], -1.0, None, ALU.add))
        c.link(dve.tensor_scalar(k.lens[:, :], k.cum[:, :], 0.0, float(S), ALU.is_lt, ALU.mult))
        dve.tensor_tensor(k.idx[:, :], k.cum[:, :], k.lens[:, :], ALU.add).then_inc(self.idx_ready.sem, 1)
        dve.wait_ge(*self.w_ready.upto(1))
        for j in range(2):
            src = k.wT[:, j, :].rearrange("p (h j) -> p h j", j=8)
            dst = k.w_flip[:, j, :].rearrange("p (h j) -> p h j", j=8)
            c.step(dve.tensor_scalar(dst[:, :, 0:4], src[:, :, 4:8], -1.0, None, ALU.mult))
            t = dve.tensor_copy(dst[:, :, 4:8], src[:, :, 0:4])
            c.step(t) if j == 0 else t.then_inc(self.flipped.sem, 1)
        k.arrived(dve, "keys")
        c.link(dve.tensor_copy(k.key_row[0:1, :], k.key_mask[:, :]))
        c.link(dve.tensor_scalar(k.key_row[0:1, :], k.key_row[0:1, :], -1.0, -NEG, ALU.add, ALU.mult))
        dve.tensor_scalar(k.key_row[0:1, :], k.key_row[0:1, :], k.key_b[0:1, 0:1], None, ALU.add)\
            .then_inc(self.keyrow.sem, 1)

    def tensor_counts(self, pe):
        k = self.k
        k.arrived(pe, "rows")
        pe.transpose(k.ps[:, 0, 0:NROWS], k.rows[0:NROWS, :], k.ident[0:NROWS, 0:NROWS]).then_inc(self.small_turned.sem, 1)
        k.arrived(pe, "routers")
        pe.transpose(k.ps[:, 6, 0:20], k.router_rows[0:20, :], k.ident[0:20, 0:20]).then_inc(self.small_turned.sem, 1)
        pe.wait_ge(*self.edges_ready.upto(1))
        for b in range(B):
            m = pe.matmul(k.ps[:, 2, 2 * b:2 * b + 1], k.edges[0:M, b, :], k.ones[0:M, 0:1], start=True, stop=True)
        m.then_inc(self.count_done.sem, 1)
        k.arrived(pe, "pool_consts")
        pe.wait_ge(*self.edge_ready.upto(1))
        pe.matmul(k.ps[:, 3, 0:B], k.upto_here, k.edge[:, :], start=True, stop=True).then_inc(self.plug_done.sem, 1)
        pe.wait_ge(*self.small_ready.upto(2))
        pe.wait_ge(*self.plug_ready.upto(1))

    def scalar_counts(self, act):
        k = self.k
        act.wait_ge(*self.small_turned.upto(1))
        act.activation(k.cols[:, :], k.ps[:, 0, 0:NROWS], ACT.Copy).then_inc(self.small_ready.sem, 1)
        act.wait_ge(*self.small_turned.upto(2))
        act.activation(k.routerT[:, :], k.ps[:, 6, 0:20], ACT.Copy).then_inc(self.small_ready.sem, 1)

    def vector_counts(self, dve):
        k, c = self.k, self.k.dchain
        k.arrived(dve, "pool_consts")
        dve.wait_ge(*self.idxT_ready.upto(1))
        for b in range(B):
            t = dve.tensor_scalar(k.edges[0:M, b, :], k.iota[0:M, :], k.idxT[0:M, b:b + 1], None, ALU.is_equal)
        t.then_inc(self.edges_ready.sem, 1)
        k.arrived(dve, "ctx")
        for b in range(B):
            c.step(dve.bn_stats(k.bn[0:M, b, :], k.ctx[0:M, b * CTX:(b + 1) * CTX]))
        c.settle()
        for b in range(B):
            c.step(dve.bn_aggr(k.ctx_mv[0:M, b, :], k.bn[0:M, b, :]))
        dve.wait_ge(*self.count_done.upto(1))
        dve.tensor_scalar(k.edge[:, :], k.ps[:, 2, 0:2 * B].rearrange("p (b o) -> p b o", o=2)[:, :, 0], 1.0, None, ALU.min)\
            .then_inc(self.edge_ready.sem, 1)
        c.settle()
        c.link(dve.tensor_tensor(k.ctx_ms[0:M, :], k.ctx_mv[0:M, :, 0], k.ctx_mv[0:M, :, 0], ALU.mult))
        dve.scalar_tensor_tensor(k.ctx_ms[0:M, :], k.ctx_ms[0:M, :], LN_EPS, k.ctx_mv[0:M, :, 1], ALU.add, ALU.add)\
            .then_inc(self.ms_ready.sem, 1)
        dve.wait_ge(*self.plug_done.upto(1))
        c.link(dve.tensor_scalar(k.plug[:, :], k.ps[:, 3, 0:B], -1.0, 0.0, ALU.add, ALU.max))
        dve.tensor_scalar(k.plug[:, :], k.plug[:, :], float(M - 1), None, ALU.min).then_inc(self.plug_ready.sem, 1)
        dve.wait_ge(*self.plug_ready.upto(1))
        for b in range(B):
            t = dve.tensor_scalar(k.pick[:, b, :], k.iota[:, 0:M], k.plug[:, b:b + 1], None, ALU.is_equal)
        t.then_inc(self.pick_ready.sem, 1)

    def pool_counts(self, pool):
        k, c = self.k, self.k.pchain
        pool.wait_ge(*self.ms_ready.upto(1))
        c.link(pool.tensor_tensor(k.ctx_ms[0:M, :], k.ctx_ms[0:M, :], bcast(k.minus_half[0:M, 0], 1, B), ALU.pow))
        pool.tensor_tensor(k.ctx_n[0:M, :, :], k.ctx[0:M, :].rearrange("p (b c) -> p b c", c=CTX)[:, :, 0:D],
                           bcast(k.ctx_ms[0:M, :], 2, D), ALU.mult).then_inc(self.ctxn_ready.sem, 1)

    def tensor_second(self, pe):
        k = self.k
        k.arrived(pe, "ctx")
        for b in range(B):
            for c in range(2):
                j = 2 * b + c
                if j >= 8 and j % 4 == 0:
                    pe.wait_ge(*self.ctxT_ready.upto(j // 4 - 1))
                t = pe.transpose(k.ps[:, j // 4 % 2, j % 4 * P:j % 4 * P + M],
                                 k.ctx[0:M, b * CTX + c * P:b * CTX + (c + 1) * P], k.ident[0:M, 0:M])
                if j % 4 == 3:
                    t.then_inc(self.ctx_turned.sem, 1)
        pe.wait_ge(*self.pick_ready.upto(1))
        for b in range(B):
            t = pe.transpose(k.ps[0:M, 2 + b // 4, b % 4 * P:(b % 4 + 1) * P], k.pick[:, b, :], k.ident)
            if b % 4 == 3:
                t.then_inc(self.pick_turned.sem, 1)
        pe.wait_ge(*self.ctxn_ready.upto(1))
        pe.wait_ge(*self.ctxT_ready.upto(4))
        for h in range(2):
            pe.matmul(k.ps[0:M, h, :], k.filter[0:M, 0:M],
                      k.ctx_n[0:M, 4 * h:4 * h + 4, :].rearrange("p b d -> p (b d)"), start=True, stop=True)\
                .then_inc(self.spread_done.sem, 1)
        pe.wait_ge(*self.pickT_ready.upto(2))
        pe.wait_ge(*self.spread_ready.upto(1))
        for b in range(B):
            m = self.pick(pe, 2 + b // 4, b, k.patches3)
            if b % 4 == 3:
                m.then_inc(self.pooled_done.sem, 1)

    def pick(self, pe, bank, b, patches):
        k = self.k
        return pe.matmul(k.ps[:, bank, b % 4 * P:(b % 4 + 1) * P], k.pickT[0:M, b * P:(b + 1) * P],
                         patches[0:M, b * D:(b + 1) * D], start=b % 4 == 0, stop=True, skip_group_check=True)

    def scalar_second(self, act):
        k = self.k
        for j in range(4):
            act.wait_ge(*self.ctx_turned.upto(j + 1))
            src = k.ps[:, j % 2, :].rearrange("p (b c t) -> p c b t", b=2, c=2)[:, :, :, 0:M]
            dst = k.ctxT[:, :, 2 * j * M:2 * (j + 1) * M].rearrange("p c (b t) -> p c b t", t=M)
            for c in range(2):
                t = act.activation(dst[:, c], src[:, c], ACT.Copy)
            t.then_inc(self.ctxT_ready.sem, 1)
        for h in range(2):
            act.wait_ge(*self.pick_turned.upto(h + 1))
            act.activation(k.pickT[0:M, h * HALF:(h + 1) * HALF], k.ps[0:M, 2 + h, :], ACT.Copy)\
                .then_inc(self.pickT_ready.sem, 1)
        for h in range(2):
            act.wait_ge(*self.pooled_done.upto(h + 1))
            act.activation(k.pooled3[:, 4 * h:4 * h + 4, :].rearrange("p b d -> p (b d)"), k.ps[:, 2 + h, :], ACT.Copy)\
                .then_inc(k.pooled_ready.sem, 1)

    def vector_second(self, dve):
        k, c = self.k, self.k.dchain
        k.arrived(dve, "wide")
        four = lambda v: v[0:M].rearrange("p (b d) -> p b d", d=D)
        for h in range(2):
            q = slice(h * HALF, (h + 1) * HALF)
            dve.wait_ge(*self.spread_done.upto(h + 1))
            for dst, g in ((k.patches0, "g_init0"), (k.patches3, "g_init3")):
                c.step(dve.tensor_tensor(four(dst[:, q]), four(k.ps[:, h, :]), bcast(k.wide[g][0:M], 1, 4), ALU.mult))
        c.settle()
        for dst, bias in ((k.patches0, "b_in0"), (k.patches3, "b_in3")):
            t = dve.tensor_tensor(four(dst), four(dst), bcast(k.wide[bias][0:M], 1, B), ALU.add)
            if bias == "b_in0":
                c.step(t)
            else:
                t.then_inc(self.spread_ready.sem, 1)


class BitWeights:

    def __init__(self, k):
        self.k = k
        t = lambda name, n: k.sig["bw_" + name].take(n)
        self.scale_ready = t("scale_ready", 1)
        self.rounded = t("rounded", 1)
        self.turned = t("turned", 9)
        self.in_sbuf = t("in_sbuf", 9)

    def vector(self, dve):
        k, c = self.k, self.k.dchain
        k.arrived(dve, "bit")
        for j, (raw, n, width) in enumerate(((k.bit_raw1, 18, P), (k.bit_raw2, 9, 2 * P))):
            sc = k.bit_scale[:, 18 * j:18 * j + n]
            c.link(dve.tensor_reduce(sc, raw[:, :, :], AX.X, ALU.add, apply_absolute_value=True))
            c.link(dve.tensor_scalar(sc, sc, 1.0 / width, 1e-5, ALU.mult, ALU.max))
        c.step(dve.tensor_scalar(k.bit_half[:, :], k.bit_scale[:, :], 0.5, None, ALU.mult))
        dve.tensor_scalar(k.bit_mhalf[:, :], k.bit_scale[:, :], -0.5, None, ALU.mult).then_inc(self.scale_ready.sem, 1)

    def pool(self, pool):
        k, c = self.k, self.k.pchain
        pool.wait_ge(*self.scale_ready.upto(1))
        for j, (raw, n, width) in enumerate(((k.bit_raw1, 18, P), (k.bit_raw2, 9, 2 * P))):
            for t in range(n):
                q = slice(18 * j + t, 18 * j + t + 1)
                scale, times = (k.bit_scale[:, q], ALU.mult) if j else (1.0, ALU.mult)
                c.step(pool.tensor_scalar(k.bit_up[:, 0:width], raw[:, t, :], k.bit_half[:, q], scale, ALU.is_gt, times))
                c.link(pool.tensor_scalar(k.bit_down[:, 0:width], raw[:, t, :], k.bit_mhalf[:, q], scale, ALU.is_lt, times))
                last = pool.tensor_tensor(raw[:, t, :], k.bit_up[:, 0:width], k.bit_down[:, 0:width], ALU.subtract)
                if j == 1 and t == n - 1:
                    last.then_inc(self.rounded.sem, 1)
                else:
                    c.link(last)

    def tensor(self, pe):
        k = self.k
        pe.wait_ge(*self.rounded.upto(1))
        for e in range(9):
            if e >= 2:
                pe.wait_ge(*self.in_sbuf.upto(e - 1))
            for c in range(2):
                pe.transpose(k.ps[:, e % 2, c * P:(c + 1) * P], k.bit_raw1[:, 2 * e + c, :], k.ident)
            for c in range(2):
                t = pe.transpose(k.ps[:, e % 2, (2 + c) * P:(3 + c) * P], k.bit_raw2[:, e, c * P:(c + 1) * P], k.ident)
            t.then_inc(self.turned.sem, 1)

    def scalar(self, act):
        k = self.k
        for e in range(9):
            act.wait_ge(*self.turned.upto(e + 1))
            act.activation(k.bit_w1T[:, e * 256:(e + 1) * 256], k.ps[:, e % 2, 0:256], ACT.Copy)
            act.activation(k.bit_w2T[:, e * 256:(e + 1) * 256], k.ps[:, e % 2, 256:512], ACT.Copy)\
                .then_inc(self.in_sbuf.sem, 1)


class Arena:

    def __init__(self, tensor):
        self.tensor, self.at, self.most = tensor, 0, 0

    def take(self, *shape, dtype=F32):
        n = int(np.prod(shape))
        words = n if dtype == F32 else (n + 1) // 2
        v = self.tensor[:, self.at:self.at + words]
        if dtype == BF16:
            v = v.bitcast(BF16)
        self.at += (words + 7) // 8 * 8
        self.most = max(self.most, self.at)
        assert self.at <= self.tensor.shape[1], (self.at, self.tensor.shape)
        if len(shape) == 2:
            v = v.rearrange("p (a b) -> p a b", a=shape[0])
        elif len(shape) == 3:
            v = v.rearrange("p (a b c) -> p a b c", a=shape[0], b=shape[1])
        return v

    def rewind(self, at):
        self.at = at


class Kit:

    def arrived(self, eng, group):
        eng.wait_ge(self.loads[group], 16 * LOADS[group])


SIGNALS = """at_vb_ready at_rec_ready at_pn_ready at_vp_done at_qk_done at_turned_qk at_q_ready at_v_clear wc_clear var_ready rstd_ready xn_ready x_turned xnT_ready
at_xT_ready at_kv_ready at_v_ready at_s_done at_max_ready at_p_ready at_pt_done at_ptv_ready at_pta_ready
at_av_even at_av_odd at_o_ready at_qkv_done at_oT_done at_oT_ready at_y_done at_res_done
ff_h_done ff_h_ready ff_o_done ff_acc_done ff_router_done ff_w_ready ff_w_turned ff_wT_ready ff_b2_done
ff_l_ready ff_e_ready ff_x_split ff_w1_split0 ff_w1_split1 dp_y_done an_bias_in dense_start
mb_in_done mb_u_in mb_gate_ready mb_conv_done mb_u_ready mb_dl_done mb_dl_ready mb_bc_done mb_bc_ready mb_bc_rounded mb_dt_done
mb_z_ready mb_lg_ready mb_du_ready mb_a_exp mb_started mb_pad_ready mb_b_done mb_c_done mb_c_ready mb_dA_ready0 mb_dA_ready1
mb_dbu_done mb_scanned0 mb_scanned1 mb_sc_ready0 mb_sc_ready1 mb_y_done0 mb_y_done1 mb_lasts_ready mb_yg_ready mb_out_done
wc_q_done wc_k_done wc_k_ready wc_av_done wc_o_ready wc_cT_ready wc_v_done wc_q_ready wc_v_ready
su_w_turned su_w_ready su_flipped su_small_turned su_small_ready su_idx_ready su_idx_turned su_idxT_ready
su_edges_ready su_count_done su_edge_ready su_plug_done su_plug_ready su_pick_ready su_pick_turned su_pickT_ready
su_ctx_turned su_ctxT_ready su_ms_ready su_ctxn_ready su_spread_done su_spread_ready su_pooled_done
su_keyrow su_pooled_ready bw_scale_ready bw_rounded bw_turned bw_in_sbuf""".split()


CREDITS = {
    "tensor": {"ff_o_done": 2, "at_s_done": 1, "at_pt_done": 5, "at_av_even": 1, "at_av_odd": 1, "at_qkv_done": 1,
               "at_oT_done": 1, "at_y_done": 1, "mb_y_done0": 1, "mb_y_done1": 1, "wc_av_done": 1},
    "scalar": {"ff_h_ready": 4, "at_v_ready": 1, "at_p_ready": 1, "at_pta_ready": 1, "at_oT_ready": 1, "mb_c_ready": 1,
               "wc_o_ready": 1},
    "vector": {"ff_acc_done": 1, "at_kv_ready": 1, "at_ptv_ready": 1, "at_o_ready": 1, "at_res_done": 1,
               "mb_dbu_done": 1, "mb_scanned0": 1, "mb_scanned1": 1},
    "pool": {"mb_sc_ready0": 1, "mb_sc_ready1": 1},
}
ROUNDED_WORDS = 9 * 256 + 5 * 512
WORK_WORDS = 14848
KEEP_WORDS = 53200 - WORK_WORDS - ROUNDED_WORDS
PRESETS = 6


def decoder(nc, a, out):
    ctx = ExitStack()
    with ctx:
        k = Kit()
        k.sig = {n: Signal(ctx.enter_context(nc.semaphore(n))) for n in SIGNALS}
        k.loads = {n: ctx.enter_context(nc.semaphore("ld_" + n)) for n in LOADS}
        k.ring_loaded = [Signal(ctx.enter_context(nc.semaphore(f"ring_loaded{p}"))) for p in range(2)]
        k.signs_copied = [Signal(ctx.enter_context(nc.semaphore(f"signs_copied{p}"))) for p in range(2)]
        preset = ctx.enter_context(nc.semaphore("preset"))
        stored = ctx.enter_context(nc.semaphore("stored"))
        chains = [ctx.enter_context(nc.semaphore(n)) for n in ("vector_chain", "scalar_chain", "pool_chain")]
        for credits in CREDITS.values():
            for name, n in credits.items():
                k.sig[name].take(n)
        k.pooled_ready = k.sig["su_pooled_ready"].take(2)

        keep = Arena(ctx.enter_context(nc.sbuf_tensor("keep", [P, KEEP_WORDS], F32)))
        work = Arena(ctx.enter_context(nc.sbuf_tensor("work", [P, WORK_WORDS], F32)))
        k.ps = ctx.enter_context(nc.psum_tensor("banks", [P, 8, HALF], F32))
        early = keep.take(3 * P + 6)
        k.ident, k.cosT, k.sinT = (early[:, j * P:(j + 1) * P] for j in range(3))
        k.head_of4, k.head_of2 = early[:, 3 * P:3 * P + 4], early[:, 3 * P + 4:3 * P + 6]
        lower = keep.take(64)
        k.lower = lower.rearrange("p (a b) -> p a b", a=8)
        halves = keep.take(35 * P, dtype=BF16)
        k.ident16, k.causal, k.band = (halves[:, j * P:(j + 1) * P] for j in range(3))
        k.sel = halves[0:96, 3 * P:35 * P]
        k.x, k.xn, k.r = (keep.take(B, D) for _ in range(3))
        k.xnT = keep.take(TOK)
        k.mv, k.bn = keep.take(B, 2), keep.take(B, 6)
        k.var_eps, k.rstd = keep.take(B), keep.take(B)
        k.minus_half, k.ones = keep.take(1), keep.take(P)
        k.one_col = k.ones[:, 0:1]
        k.cols, k.col = keep.take(NROWS), COL
        k.routerT = keep.take(20)
        gates = keep.take(2, 8)
        k.router = {"relu": gates[:, 0, :], "gate": gates[:, 1, :], "gelu": k.routerT[:, 0:12], "bit": k.routerT[:, 12:20]}
        wide = keep.take(len(WIDE), D)
        k.wide = {n: wide[:, j, :] for j, n in enumerate(WIDE)}
        k.ln1_g, k.ln1_b, k.dense_b2 = k.wide["ln1_g"], k.wide["ln1_b"], k.wide["dense_b2"]
        bias = keep.take(36)
        k.router_b = {"relu": bias[:, 0:8], "gelu": bias[:, 8:16], "gate": bias[:, 16:24], "bit": bias[:, 28:36]}
        k.lang_b = bias[:, 24:28]
        k.wT = keep.take(6, P)
        k.l0_wvT, k.l0_woT = k.wT[:, 2, :], k.wT[:, 3, :]
        l3_qkv, k.l3_wo = keep.take(3 * D), keep.take(D)
        k.l3_qk, k.l3_wv = [l3_qkv[:, 0:D], l3_qkv[:, D:2 * D]], l3_qkv[:, 2 * D:3 * D]
        blocks = keep.take(3, TOK)
        k.b2_blocks = {n: blocks[0:64, j, :] for j, n in enumerate(("relu", "gelu", "gate"))}
        k.ctx, k.ctxT = keep.take(B * CTX), keep.take(2, B * M)
        k.pooled_raw = keep.take(B, D)
        k.key_row, k.key_b, k.null_k = keep.take(B * M), keep.take(1), keep.take(1)
        k.bit_w2T = keep.take(9 * 256)
        k.mb_win, k.mb_conv, k.mb_wx, k.wx3 = keep.take(4 * P), keep.take(8, 2 * P), keep.take(2, 96), keep.take(2, 96)
        k.mb_wdt, k.mb_wout = keep.take(2 * P)[0:64, :], keep.take(2, D)
        k.a_log, k.a_exp, k.a_neg, k.s_last = keep.take(2, 16), keep.take(2, 16), keep.take(32), keep.take(2, B)
        k.w, k.logit, k.lang, k.lp = keep.take(64), keep.take(B, 8), keep.take(B, 4), keep.take(B, 5)
        k.peak = keep.take(B)
        k.w1 = [keep.take(HALF) for _ in range(2)]
        k.w2 = [keep.take(4, D) for _ in range(2)]
        k.bit_scale, k.bit_half, k.bit_mhalf = (keep.take(27) for _ in range(3))
        at = keep.at
        k.bit_raw1, k.bit_raw2 = keep.take(18, P), keep.take(9, 2 * P)
        keep.rewind(at)
        k.wq, k.wkv, k.wout = keep.take(8 * P), keep.take(2, 2048), keep.take(8, D)

        rounded = Arena(ctx.enter_context(nc.sbuf_tensor("rounded", [P, ROUNDED_WORDS], F32R)))
        k.bit_w1T, parts = rounded.take(9 * 256), rounded.take(4 * HALF)
        k.signs = [rounded.take(2 * P) for _ in range(2)]
        rounded.rewind(0)
        k.q_high, k.q_low = ([rounded.take(P) for _ in range(2)] for _ in range(2))
        k.kb_high, k.kb_low = ([rounded.take(4, P) for _ in range(2)] for _ in range(2))
        k.k_high, k.k_low = (rounded.take(P) for _ in range(2))
        k.w1_high, k.w1_low = ([parts[:, (2 * j + p) * HALF:(2 * j + p + 1) * HALF] for p in range(2)] for j in range(2))
        k.x_parts, k.bit_x_parts = ([v[:, j * TOK:(j + 1) * TOK] for j in range(2)] for v in (k.bit_w1T, parts))

        k.p = [work.take(16, P) for _ in range(2)]
        k.pT = [work.take(4, P) for _ in range(2)]
        k.mx, k.nmx = ([work.take(16) for _ in range(2)] for _ in range(2))
        k.total, k.rec = ([work.take(16) for _ in range(2)] for _ in range(2))
        at = work.at
        k.terms = [v.rearrange("p h t -> p (h t)") for v in k.p]
        k.q_all, k.k_all, k.v_tok = work.take(TOK), work.take(TOK), work.take(B, D)
        k.oT = work.take(P)
        late = work.take(3 * P)
        k.upto_here, k.iota, k.filter = (late[:, j * P:(j + 1) * P] for j in range(3))
        k.idxT, k.edge, k.plug = work.take(B), work.take(B), work.take(B)
        k.ctx_mv, k.ctx_ms = work.take(B, 2), work.take(B)
        k.w_raw = k.terms[0][:, TOK:TOK + 6 * P].rearrange("p (a b) -> p a b", a=6)
        k.rows, k.router_rows = k.pT[1][:, 0, :], k.pT[1][:, 1, :]
        k.w_flip = k.pT[0][:, 0:2, :]
        k.l0_qk = [k.wT[:, 0, :], k.w_flip[:, 0, :], k.wT[:, 1, :], k.w_flip[:, 1, :]]
        k.edges = k.xn
        k.lens, k.cum, k.idx, lens = (k.k_all[0:B, j * M:(j + 1) * M] for j in range(4))
        k.lens_i, k.key_mask = lens.bitcast(I32), k.q_all[0:1, 0:B * M].bitcast(I32)
        k.pick = k.pooled_raw.rearrange("p b t -> p (b t)")[:, 0:B * M].rearrange("p (b t) -> p b t", b=B)
        k.ctx_n, k.patches3 = k.r, k.r.rearrange("p b d -> p (b d)")
        k.pickT, k.patches0 = k.terms[0][:, 0:TOK], k.terms[0][:, TOK:2 * TOK]
        k.pooled3 = k.pooled_raw
        after_attention = work.at
        k.v_block = [work.take(16, P) for _ in range(2)]
        work.rewind(after_attention)
        k.hT = [work.take(4, HALF) for _ in range(2)]
        work.rewind(0)
        k.more, k.same, k.rank, k.wT_route = work.take(B, 8, 8), work.take(B, 8, 8), work.take(B, 8), work.take(P)
        k.bit_up, k.bit_down = work.take(2 * P), work.take(2 * P)
        work.rewind(at)
        k.cT, k.qT, k.woT = work.take(2, M), work.take(8, P), work.take(8, P)
        work.rewind(0)
        k.gate, k.u = work.take(2, TOK), work.take(2, TOK)
        k.delta, k.du, k_sC = work.take(2, TOK), work.take(2, TOK), work.take(2, TOK)
        at = work.at
        k.sp, s2 = work.take(2, TOK), work.take(2, TOK)
        end = work.at
        work.rewind(at)
        k.kT, k.wv = work.take(8, M + 1), work.take(16 * 64)
        work.rewind(at)
        k.upad = work.take(2, 8, 131)
        work.rewind(end)
        k.bc3 = work.take(TOK, dtype=BF16)[0:96, :]
        k.dA = [k.u[:, c, :].rearrange("p (b t) -> p b t", t=S) for c in range(2)]
        k.yg, k.dbu = k.du, [k.sp[:, c, :] for c in range(2)]
        k.s, k.sC = [s2[:, c, :] for c in range(2)], [k_sC[:, c, :] for c in range(2)]
        k.dlT, k.rest = s2[0:64, 0, :], s2[0:96, 1, :]
        k.cb = [k.xnT, k.r[:, :, :].rearrange("p b d -> p (b d)")]
        k.zeros = k.cb[1][:, 0:HALF]
        k.s_lasts = k.w1[0][:, 0:2 * 17 * B].rearrange("p (c n b) -> p c n b", c=2, b=B)
        k.wT_small = k.wT_route[0:64, :]

        setup = Setup(k)
        bits = BitWeights(k)
        n0 = Norm(k)
        t0 = Turn(k, n0)
        l0_attn = Attention(k, n0, t0, "rope", setup)
        n1 = Norm(k, again=True)
        t1 = Turn(k, n1)
        l0_cross = Depool(k, n1, t1, k.wT[:, 4, :], setup)
        n2 = Norm(k)
        t2 = Turn(k, n2)
        l0_ffn = Experts(k, n2, t2, "relu")
        n3 = Norm(k)
        t3 = Turn(k, n3)
        l1_attn = Attention(k, n3, t3, "self")
        n4 = Norm(k, src=k.r)
        t4 = Turn(k, n4)
        l1_start = DenseStart(k, n4)
        l1_dense = Experts(k, n4, t4, "dense")
        l1_after = AfterNorm(k, k.wide["ln2_g"], k.wide["ln2_b"])
        n6 = Norm(k)
        t6 = Turn(k, n6)
        l1_cross = Attention(k, n6, t6, "context")
        n7 = Norm(k)
        t7 = Turn(k, n7)
        l1_ffn = Experts(k, n7, t7, "gelu")
        n8 = Norm(k)
        t8 = Turn(k, n8)
        l2_mamba = Mamba(k, n8, t8)
        n9 = Norm(k)
        t9 = Turn(k, n9)
        l2_cross = WideCross(k, n9, t9)
        l2_after = AfterNorm(k, k.wide["ln_scale"], k.wide["ln_bias"], eps=1e-6)
        n11 = Norm(k, again=True)
        t11 = Turn(k, n11)
        l2_ffn = Experts(k, n11, t11, "bit")
        n12 = Norm(k)
        t12 = Turn(k, n12)
        l3_attn = Attention(k, n12, t12, "packed")
        n13 = Norm(k, again=True)
        t13 = Turn(k, n13)
        l3_cross = Depool(k, n13, t13, k.wT[:, 5, :])
        n14 = Norm(k)
        t14 = Turn(k, n14)
        l3_ffn = Experts(k, n14, t14, "gate")

        col = lambda name: k.cols[:, COL[name]:COL[name] + 1]

        def credit(eng, name):
            for signal, n in CREDITS[name].items():
                eng.sem_inc(k.sig[signal].sem, n)

        block = ctx.enter_context(nc.Block())

        @block.sync
        def _(sp):
            issued = dict.fromkeys(LOADS, 0)

            def load(group, dst, src):
                sp.dma_start(dst, src).then_inc(k.loads[group], 16)
                issued[group] += 1

            def on_all(v):
                return bcast(v, 0, P)

            load("x", k.x, a["x"].rearrange("b s d -> s b d"))
            load("first", early, a["early"])
            for j, name in enumerate(("L0_attn_W_Q", "L0_attn_W_K", "L0_attn_W_V", "L0_attn_W_O", "L0_xattn_W_in",
                                      "L3_xattn_W_in")):
                load("l0", k.w_raw[:, j, :], a[name])
            load("lens", k.lens_i, a["mask_BxS2_if0"])
            row = lambda name, v, n: load("rows", k.rows[COL[name]:COL[name] + n, :], v)
            for name, v in (("relu_b1", "L0_ffn_b1"), ("gelu_b1", "L1_ffn_b1"), ("gate_b1", "L3_ffn_b1")):
                row(name, a[v].rearrange("e (c p) -> (e c) p", p=P), 32)
            for name, v, n in (("dense_b1", "L1_attn_b1", 4), ("g_res0", "L0_xattn_g_res", 1),
                               ("g_res3", "L3_xattn_g_res", 1), ("gamma", "L2_ffn_ln_gamma", 1),
                               ("beta", "L2_ffn_ln_beta", 1), ("conv_b", "L2_attn_conv_b", 2),
                               ("b_dt", "L2_attn_b_dt", 2), ("ssm_d", "L2_attn_D", 2),
                               ("ln1_g", "L1_attn_ln1_g", 1), ("ln1_b", "L1_attn_ln1_b", 1)):
                row(name, a[v].rearrange("(c p) -> c p", p=P), n)
            load("routers", k.router_rows[0:8, :], a["L1_ffn_router_w"])
            load("routers", k.router_rows[8:12, :], a["L1_ffn_lang_w"])
            load("routers", k.router_rows[12:20, :], a["L2_ffn_router_w"])
            load("pool_consts", late, a["late"][:, 0:3 * P])
            load("lower", lower, a["late"][:, 3 * P:3 * P + 64])
            load("masks", halves.bitcast(U16), a["halves"])
            load("ctx", k.ctx[0:M, :].rearrange("s (b c) -> s b c", c=CTX), a["ctx_2048"].rearrange("b s c -> s b c"))
            load("keys", k.key_mask, a["mask_BxS2_ik0"].rearrange("b s -> (b s)").unsqueeze(0))
            load("keys", k.key_b[0:1, :], a["L1_xattn_b"].unsqueeze(0))
            load("gates", gates[:, 0, :], a["L0_ffn_gate_w"])
            load("gates", gates[:, 1, :], a["L3_ffn_Wg"])
            for at, n, name in ((0, 8, "L0_ffn_gate_b"), (8, 8, "L1_ffn_router_b"), (16, 8, "L3_ffn_bg"),
                                (24, 4, "L1_ffn_lang_b")):
                load("wide", bias[:, at:at + n], on_all(a[name]))
            for name, v in (("ln1_g", "L1_attn_ln1_g"), ("ln1_b", "L1_attn_ln1_b"), ("ln2_g", "L1_attn_ln2_g"),
                            ("ln2_b", "L1_attn_ln2_b"), ("dense_b2", "L1_attn_b2"), ("b_in0", "L0_xattn_b_in"),
                            ("b_in3", "L3_xattn_b_in"), ("g_init0", "L0_xattn_g_init"), ("g_init3", "L3_xattn_g_init"),
                            ("ln_scale", "L2_xattn_ln_scale"), ("ln_bias", "L2_xattn_ln_bias")):
                load("wide", k.wide[name], on_all(a[v][0:D]))
            sp.wait_ge(preset, PRESETS)
            for j, name in enumerate(("L0_ffn_b2", "L1_ffn_b2", "L3_ffn_b2")):
                for t in range(B):
                    load("b2", blocks[8 * t:8 * t + 8, j, t * D:(t + 1) * D], a[name])
            load("bit", k.bit_raw1[:, 0:2, :], a["L2_ffn_shared_w1"].rearrange("(c p) d -> p c d", p=P))
            for e in range(8):
                load("bit", k.bit_raw1[:, 2 + 2 * e:4 + 2 * e, :],
                     a["L2_ffn_expert_w1"][e].rearrange("(c p) d -> p c d", p=P))
            load("bit", k.bit_raw2[:, 0, :], a["L2_ffn_shared_w2"])
            load("bit", k.bit_raw2[:, 1:9, :], a["L2_ffn_expert_w2"].rearrange("e d f -> d e f"))
            load("l3", l3_qkv, a["L3_attn_w_qkv"])
            load("l3", k.l3_wo, a["L3_attn_w_out"])
            load("mamba", k.mb_win, a["L2_attn_W_in"])
            load("mamba", k.mb_conv, a["L2_attn_conv_w"].rearrange("k (c p) o -> p (k c) o", p=P))
            load("mamba", k.mb_wx, a["L2_attn_W_x"].rearrange("(c p) f -> p c f", p=P))
            load("mamba", k.mb_wdt, a["L2_attn_W_dt"])
            load("mamba", k.mb_wout, a["L2_attn_W_out"].rearrange("(c p) d -> p c d", p=P))
            load("mamba", k.a_log, a["L2_attn_A_log"].rearrange("(c p) n -> p c n", p=P))
            for h in range(2):
                load("null_k", k.null_k[64 * h:64 * h + 64, :], a["L2_xattn_null_kv"][0].unsqueeze(1))
            l0_ffn.sync(sp, a["L0_ffn_w1"], a["L0_ffn_w2"])
            l1_dense.sync(sp, a["L1_attn_W1"], a["L1_attn_W2"])
            l1_ffn.sync(sp, a["L1_ffn_w1"], a["L1_ffn_w2"])
            sp.wait_ge(*bits.in_sbuf.upto(9))
            load("wide_cross", k.wq, a["L2_xattn_Wq"])
            load("wide_cross", k.wkv, a["L2_xattn_Wkv"].rearrange("(e p) f -> p e f", p=P))
            load("wide_cross", k.wout, a["L2_xattn_Wout"].rearrange("(c p) d -> p c d", p=P))
            l2_cross.sync(sp, a["L2_xattn_null_kv"][1:2])
            issued["null_v"] += 1
            l3_ffn.sync(sp, a["L3_ffn_W1"], a["L3_ffn_W2"])
            for h in range(2):
                sp.wait_ge(*l3_ffn.acc_done.upto(l3_ffn.items - 1 + h))
                sp.dma_start(out[4 * h:4 * h + 4].rearrange("b s d -> s b d"), k.x[:, 4 * h:4 * h + 4, :])\
                    .then_inc(stored, 16)
            sp.wait_ge(stored, 32)
            assert issued == LOADS, (issued, LOADS)

        @block.tensor
        def _(pe):
            credit(pe, "tensor")
            pe.wait_ge(preset, PRESETS)
            setup.tensor_first(pe)
            t0.tensor(pe)
            k.arrived(pe, "masks")
            l0_attn.tensor(pe)
            l0_cross.tensor(pe)
            t2.tensor(pe)
            k.arrived(pe, "gates")
            l0_ffn.tensor(pe)
            t3.tensor(pe)
            l1_attn.tensor(pe)
            t4.tensor(pe)
            l1_dense.tensor(pe)
            t6.tensor(pe)
            pe.wait_ge(*setup.keyrow.upto(1))
            l1_cross.tensor(pe)
            t7.tensor(pe)
            l1_ffn.tensor(pe)
            bits.tensor(pe)
            t8.tensor(pe)
            l2_mamba.tensor(pe, l2_cross)
            t9.tensor(pe)
            l2_cross.tensor(pe)
            t11.tensor(pe)
            l2_ffn.tensor(pe)
            t12.tensor(pe)
            k.arrived(pe, "l3")
            l3_attn.tensor(pe)
            l3_cross.tensor(pe)
            t14.tensor(pe)
            l3_ffn.tensor(pe)

        @block.vector
        def _(dve):
            k.dchain = Chain(dve, chains[0])
            credit(dve, "vector")
            dve.wait_ge(preset, PRESETS)
            k.arrived(dve, "x")
            token_stats(k, dve, k.x, range(B))
            n0.vector(dve)
            setup.vector_first(dve)
            l0_attn.vector(dve)
            n1.vector(dve)
            l0_cross.vector(dve)
            n2.vector(dve)
            k.arrived(dve, "wide")
            k.arrived(dve, "lower")
            l0_ffn.vector(dve, between=bits)
            n3.vector(dve)
            l1_attn.vector(dve)
            n4.vector(dve)
            l1_dense.vector(dve, between=l1_start)
            l1_after.vector(dve)
            n6.vector(dve)
            l1_cross.vector(dve)
            n7.vector(dve)
            l1_ffn.vector(dve)
            n8.vector(dve)
            l2_mamba.vector(dve)
            n9.vector(dve)
            l2_cross.vector(dve)
            l2_after.vector(dve)
            n11.vector(dve)
            l2_ffn.vector(dve)
            n12.vector(dve)
            l3_attn.vector(dve)
            n13.vector(dve)
            l3_cross.vector(dve)
            n14.vector(dve)
            l3_ffn.vector(dve, stats=False)

        @block.scalar
        def _(act):
            k.achain = Chain(act, chains[1])
            credit(act, "scalar")
            act.wait_ge(preset, PRESETS)
            setup.scalar_first(act)
            t0.scalar(act)
            l0_attn.scalar(act)
            act.wait_ge(*setup.small_ready.upto(2))
            t1.scalar(act, scale=col("g_res0"))
            t2.scalar(act)
            l0_ffn.scalar(act)
            t3.scalar(act)
            l1_attn.scalar(act)
            t4.scalar(act, scale=col("ln1_g"), bias=col("ln1_b"))
            l1_dense.scalar(act)
            t6.scalar(act, scale=1.0 / np.sqrt(16.0))
            l1_cross.scalar(act)
            t7.scalar(act)
            l1_ffn.scalar(act)
            bits.scalar(act)
            t8.scalar(act)
            l2_mamba.scalar(act)
            l2_cross.scalar_first(act)
            t9.scalar(act)
            l2_cross.scalar(act)
            t11.scalar(act, scale=col("gamma"), bias=col("beta"))
            l2_ffn.scalar(act)
            t12.scalar(act)
            l3_attn.scalar(act)
            t13.scalar(act, scale=col("g_res3"))
            t14.scalar(act)
            l3_ffn.scalar(act)

        @block.gpsimd
        def _(pool):
            k.pchain = Chain(pool, chains[2])
            credit(pool, "pool")
            for v, value in ((k.minus_half, -0.5), (k.ones, 1.0), (k.key_row, 0.0), (bias[:, 28:36], 0.0),
                             (k.lp[:, :, 4], 0.0), (blocks[0:64, :, :], 0.0)):
                pool.memset(v, value).then_inc(preset, 1)
            pool.wait_ge(preset, PRESETS)
            n0.pool(pool)
            l0_attn.pool(pool)
            n1.pool(pool)
            n2.pool(pool)
            bits.pool(pool)
            n3.pool(pool)
            l1_attn.pool(pool)
            n4.pool(pool)
            l1_start.pool(pool)
            l1_after.pool(pool)
            n6.pool(pool)
            l1_cross.pool(pool)
            n7.pool(pool)
            n8.pool(pool)
            l2_mamba.pool(pool)
            l2_cross.context(pool, 0)
            n9.pool(pool)
            l2_cross.pool(pool)
            l2_after.pool(pool)
            n11.pool(pool)
            l2_ffn.pool(pool)
            n12.pool(pool)
            l3_attn.pool(pool)
            n13.pool(pool)
            n14.pool(pool)


def kernel(**inputs):
    import concourse.bacc as _bacc
    from concourse.bass_utils import run_bass_kernel_spmd as _run

    arrays = {f"in_{name}_dram": np.ascontiguousarray(v) for name, v in inputs.items()}
    arrays.update({f"in_{name}_dram": v for name, v in zip(("early", "late", "halves"), constants())})
    nc = _bacc.Bacc("TRN2", target_bir_lowering=False, num_devices=1)
    args = {}
    for name, v in arrays.items():
        args[name[3:-5]] = nc.dram_tensor(name, v.shape, mybir.dt.from_np(v.dtype), kind="ExternalInput").ap()
    out = nc.dram_tensor("out_0_dram", (B, S, D), F32, kind="ExternalOutput").ap()
    decoder(nc, args, out)
    return _run(nc, [arrays], core_ids=[0]).results[0]["out_0_dram"]
```
